# Optimizing a Trainium2 kernel written in Bass

```python
import numpy as np
import jax
import jax.numpy as jnp

def _softmax(x, axis=-1):
    return jax.nn.softmax(x, axis=axis)

def _gelu(x):
    return jax.nn.gelu(x, approximate=True)

def _silu(x):
    return jax.nn.silu(x)

def _sigmoid(x):
    return jax.nn.sigmoid(x)

def _layernorm(x, axis=-1, eps=1e-05):
    m = jnp.mean(x, axis=axis, keepdims=True)
    v = jnp.var(x, axis=axis, keepdims=True)
    return (x - m) / jnp.sqrt(v + eps)

def _scatter_add(tgt, idx, src, axis=0):
    return tgt.at[idx].add(src)

def _segment_sum(src, seg, n):
    return jax.ops.segment_sum(src, seg, n)
kernel_name = 'mk_adaln_attn_ffn_d4_seqx_r8_3d57d4'

def setup_inputs(seed: int=0):
    np.random.seed(seed)
    _w = jnp.asarray

    def _rec_inputs():
        import jax
        import jax.numpy as jnp
        _rk = jax.random.key(seed)
        x = -0.000125 + 0.9999 * jax.random.normal(jax.random.fold_in(_rk, 1), (8, 256, 128), jnp.float32)
        _lenS = 256 - jax.random.randint(jax.random.fold_in(_rk, 7), (8,), 0, max(1, 256 // 4) + 1, jnp.int32)
        _lenS2 = 256 - jax.random.randint(jax.random.fold_in(_rk, 8), (8,), 0, max(1, 256 // 4) + 1, jnp.int32)
        cond_1024 = 0.00782532 + 1.00527 * jax.random.normal(jax.random.fold_in(_rk, 11), (8, 128), jnp.float32)
        fside_Bx1x1024x16_0 = 0.00222621 + 0.99962 * jax.random.normal(jax.random.fold_in(_rk, 12), (8, 1, 128, 16), jnp.float32)
        return (x, cond_1024, fside_Bx1x1024x16_0)
    x, cond_1024, fside_Bx1x1024x16_0 = _rec_inputs()

    def _L0_cond_setup():
        import jax, jax.numpy as jnp
        import numpy as np
        INV_SQRT2 = 0.7071067811865476
        key = jax.random.key(seed)
        k1, k2, k3, k4 = jax.random.split(key, 4)
        B, N, d = (8, 512, 128)
        scale = 1.0 / np.sqrt(d)
        return {'v': jax.random.normal(k1, (B, N, d), dtype=jnp.float32), 'q_pool': jax.random.normal(k2, (B, d), dtype=jnp.float32), 'W1': jax.random.normal(k3, (d, d), dtype=jnp.float32) * scale, 'b1': jnp.zeros((d,), dtype=jnp.float32), 'W2': jax.random.normal(k4, (d, d), dtype=jnp.float32) * scale, 'b2': jnp.zeros((d,), dtype=jnp.float32)}
    _L0_cond_all = _L0_cond_setup()
    _L0_cond_in = {k: v for k, v in _L0_cond_all.items() if k in ('W1', 'b1', 'W2', 'b2')}
    del _L0_cond_all

    def _L0_attn_setup():
        import jax, jax.numpy as jnp
        import numpy as np
        B, S, D = (2, 256, 128)
        NH, KVH = (16, 4)
        HD = D // NH
        ROPE_BASE = 10000.0

        def rotate_half(x):
            half = x.shape[-1] // 2
            x1, x2 = (x[..., :half], x[..., half:])
            return jnp.concatenate((-x2, x1), axis=-1)

        def rope_cache(seq_len, head_dim, base, dtype):
            half = head_dim // 2
            inv_freq = 1.0 / base ** (jnp.arange(half, dtype=jnp.float32) / max(1, half))
            t = jnp.arange(seq_len, dtype=jnp.float32)
            freqs = jnp.einsum('i,j->ij', t, inv_freq)
            emb = jnp.concatenate((freqs, freqs), axis=-1)
            cos = jnp.cos(emb)[None, None].astype(dtype)
            sin = jnp.sin(emb)[None, None].astype(dtype)
            return (sin, cos)
        key = jax.random.key(seed)
        ks = jax.random.split(key, 5)
        s = 0.02
        return {'x': jax.random.normal(ks[0], (B, S, D), dtype=jnp.float32), 'Wq': jax.random.normal(ks[1], (D, D), dtype=jnp.float32) * s, 'Wk': jax.random.normal(ks[2], (D, KVH * HD), dtype=jnp.float32) * s, 'Wv': jax.random.normal(ks[3], (D, KVH * HD), dtype=jnp.float32) * s, 'Wo': jax.random.normal(ks[4], (D, D), dtype=jnp.float32) * s}
    _L0_attn_all = _L0_attn_setup()
    _L0_attn_in = {k: v for k, v in _L0_attn_all.items() if k in ('Wq', 'Wk', 'Wv', 'Wo')}
    del _L0_attn_all

    def _L0_cond2_setup():
        import jax, jax.numpy as jnp
        import numpy as np
        D = 128
        H = 128
        N = 64
        T = 64

        def _lstm(x, h0, Wx, Wh, b):
            xW = jnp.einsum('ntd,dk->tnk', x, Wx) + b
            c0 = jnp.zeros_like(h0)
            Hdim = h0.shape[1]

            def step(carry, xw_t):
                prev_h, prev_c = carry
                a = xw_t + prev_h @ Wh
                i = jax.nn.sigmoid(a[:, 0:Hdim])
                f = jax.nn.sigmoid(a[:, Hdim:2 * Hdim])
                o = jax.nn.sigmoid(a[:, 2 * Hdim:3 * Hdim])
                g = jnp.tanh(a[:, 3 * Hdim:4 * Hdim])
                next_c = f * prev_c + i * g
                next_h = o * jnp.tanh(next_c)
                return ((next_h, next_c), next_h)
            _, hs = jax.lax.scan(step, (h0, c0), xW)
            return jnp.transpose(hs, (1, 0, 2))
        key = jax.random.key(seed)
        k1, k2, k3, k4 = jax.random.split(key, 4)
        x = jax.random.normal(k1, (N, T, D), dtype=jnp.float32)
        h0 = jax.random.normal(k2, (N, H), dtype=jnp.float32)
        Wx = jax.random.normal(k3, (D, 4 * H), dtype=jnp.float32) / np.sqrt(D)
        Wh = jax.random.normal(k4, (H, 4 * H), dtype=jnp.float32) / np.sqrt(H)
        b = jnp.zeros((4 * H,), dtype=jnp.float32)
        return {'x': x, 'h0': h0, 'Wx': Wx, 'Wh': Wh, 'b': b}
    _L0_cond2_all = _L0_cond2_setup()
    _L0_cond2_in = {k: v for k, v in _L0_cond2_all.items() if k in ('Wx', 'Wh', 'b')}
    del _L0_cond2_all

    def _L0_ffn_setup():
        import jax, jax.numpy as jnp
        import numpy as np
        IN_FEATURES = 128
        OUT_FEATURES = 128
        B, S = (8, 512)
        key = jax.random.key(seed)
        kx, kw = jax.random.split(key)
        x = jax.random.normal(kx, (B, S, IN_FEATURES), dtype=jnp.float32)
        weight = jax.random.normal(kw, (OUT_FEATURES, IN_FEATURES), dtype=jnp.float32) * 0.1
        bias = jnp.zeros((OUT_FEATURES,), dtype=jnp.float32)
        return {'x': x, 'weight': weight, 'bias': bias}
    _L0_ffn_all = _L0_ffn_setup()
    _L0_ffn_in = {k: v for k, v in _L0_ffn_all.items() if k in ('weight', 'bias')}
    del _L0_ffn_all

    def _L1_cond_setup():
        import jax, jax.numpy as jnp
        import numpy as np
        TEMPERATURE = 2.0
        key = jax.random.key(seed)
        k1, k2 = jax.random.split(key)
        B, N, D = (16, 256, 128)
        x = jax.random.normal(k1, (B, N, D), dtype=jnp.float32)
        random_values = jax.random.uniform(k2, (B, D), dtype=jnp.float32)
        return {'x': x, 'random_values': random_values}
    _L1_cond_all = _L1_cond_setup()
    _L1_cond_in = {k: v for k, v in _L1_cond_all.items() if k in ()}
    del _L1_cond_all

    def _L1_attn_setup():
        import jax, jax.numpy as jnp
        import numpy as np
        N_HEAD = 16
        ROPE_BASE = 10000.0

        def _rotate_half(t):
            d = t.shape[-1] // 2
            return jnp.concatenate([-t[..., d:], t[..., :d]], axis=-1)

        def _rope_cos_sin(T, D, dtype):
            half = D // 2
            theta = 1.0 / ROPE_BASE ** (jnp.arange(half, dtype=dtype) / half)
            pos = jnp.arange(T, dtype=dtype)
            freqs = pos[:, None] * theta[None, :]
            cos = jnp.repeat(jnp.cos(freqs), 2, axis=-1)
            sin = jnp.repeat(jnp.sin(freqs), 2, axis=-1)
            return (cos, sin)
        key = jax.random.key(seed)
        k1, k2, k3 = jax.random.split(key, 3)
        B, T, C = (2, 256, 128)
        x = jax.random.normal(k1, (B, T, C), dtype=jnp.float32)
        w_qkv = jax.random.normal(k2, (C, 3 * C), dtype=jnp.float32) * C ** (-0.5)
        w_proj = jax.random.normal(k3, (C, C), dtype=jnp.float32) * C ** (-0.5)
        return {'x': x, 'w_qkv': w_qkv, 'w_proj': w_proj}
    _L1_attn_all = _L1_attn_setup()
    _L1_attn_in = {k: v for k, v in _L1_attn_all.items() if k in ('w_qkv', 'w_proj')}
    del _L1_attn_all

    def _L1_cond2_setup():
        import jax, jax.numpy as jnp
        import numpy as np
        TOP_K = 2
        N_EXPERTS = 8
        N_SHARED = 1
        EPS = 1e-09
        key = jax.random.key(seed)
        ks = jax.random.split(key, 10)
        B, T, d = (2, 256, 128)
        h_s, h_r, E = (256, 64, N_EXPERTS)
        return {'x': jax.random.normal(ks[0], (B, T, d), jnp.float32), 't_emb': jax.random.normal(ks[1], (B, d), jnp.float32), 'router_w': jax.random.normal(ks[2], (E, d), jnp.float32) * 0.01, 'router_t_w': jax.random.normal(ks[3], (E, d), jnp.float32) * 0.01, 'router_bias': jnp.zeros((E,), jnp.float32), 'sw1': jax.random.normal(ks[4], (h_s, d), jnp.float32) * 0.02, 'sw3': jax.random.normal(ks[5], (h_s, d), jnp.float32) * 0.02, 'sw2': jax.random.normal(ks[6], (d, h_s), jnp.float32) * 0.02, 'rw1': jax.random.normal(ks[7], (E, h_r, d), jnp.float32) * 0.02, 'rw2': jax.random.normal(ks[8], (E, d, h_r), jnp.float32) * 0.02}
    _L1_cond2_all = _L1_cond2_setup()
    _L1_cond2_in = {k: v for k, v in _L1_cond2_all.items() if k in ('router_w', 'router_t_w', 'router_bias', 'sw1', 'sw3', 'sw2', 'rw1', 'rw2')}
    del _L1_cond2_all

    def _L1_ffn_setup():
        import jax, jax.numpy as jnp
        import numpy as np
        NUM_EXPERTS = 8
        TOP_K = 2
        key = jax.random.key(seed)
        ks = jax.random.split(key, 6)
        B, S, D, H, E = (4, 128, 128, 256, NUM_EXPERTS)
        x = jax.random.normal(ks[0], (B, S, D), dtype=jnp.float32)
        Wg = jax.random.normal(ks[1], (D, E), dtype=jnp.float32) * 0.02
        W1 = jax.random.normal(ks[2], (E, D, H), dtype=jnp.float32) * 0.02
        b1 = jax.random.normal(ks[3], (E, H), dtype=jnp.float32) * 0.02
        W2 = jax.random.normal(ks[4], (E, H, D), dtype=jnp.float32) * 0.02
        b2 = jax.random.normal(ks[5], (E, D), dtype=jnp.float32) * 0.02
        return {'x': x, 'Wg': Wg, 'W1': W1, 'b1': b1, 'W2': W2, 'b2': b2}
    _L1_ffn_all = _L1_ffn_setup()
    _L1_ffn_in = {k: v for k, v in _L1_ffn_all.items() if k in ('Wg', 'W1', 'b1', 'W2', 'b2')}
    del _L1_ffn_all

    def _L2_cond_setup():
        import jax, jax.numpy as jnp
        import numpy as np
        import math
        D = 128
        H = 128
        key = jax.random.key(seed)
        k1, k2, k3, k4 = jax.random.split(key, 4)
        x = jax.random.normal(k1, (64, 64, D), dtype=jnp.float32)
        h0 = jax.random.normal(k2, (64, H), dtype=jnp.float32)
        Wx = jax.random.normal(k3, (D, 4 * H), dtype=jnp.float32) / math.sqrt(D)
        Wh = jax.random.normal(k4, (H, 4 * H), dtype=jnp.float32) / math.sqrt(H)
        b = jnp.zeros((4 * H,), dtype=jnp.float32)
        return {'x': x, 'h0': h0, 'Wx': Wx, 'Wh': Wh, 'b': b}
    _L2_cond_all = _L2_cond_setup()
    _L2_cond_in = {k: v for k, v in _L2_cond_all.items() if k in ('Wx', 'Wh', 'b')}
    del _L2_cond_all

    def _L2_attn_setup():
        import jax, jax.numpy as jnp
        import numpy as np
        B, T, D = (8, 256, 128)
        H, N = (8, 32)

        def _xavier(key, shape, fan_in, fan_out):
            lim = float(np.sqrt(6.0 / (fan_in + fan_out)))
            return jax.random.uniform(key, shape, jnp.float32, -lim, lim)

        def _reference_tuple_inner(x, W_in, W_k, W_v, W_q, W_beta, b_beta, W_out):
            b, t, d = x.shape
            h, n = b_beta.shape
            xp = jax.nn.silu(jnp.einsum('btd,ed->bte', x, W_in))

            def proj(W):
                return jnp.einsum('btd,md->btm', xp, W).reshape(b, t, h, n).transpose(1, 0, 2, 3)
            k_all = proj(W_k)
            v_all = proj(W_v)
            q_all = proj(W_q)
            beta_all = jax.nn.sigmoid(proj(W_beta) + b_beta)
            S0 = jnp.zeros((b, h, n, n), x.dtype)

            def step(S, inp):
                k, v, q, beta = inp
                kn = k / (jnp.linalg.norm(k, axis=-1, keepdims=True) + 1e-06)
                retrieved = jnp.einsum('bhij,bhj->bhi', S, kn)
                delta = v - retrieved
                S = jnp.tanh(beta[..., None] * S + delta[..., None] * kn[..., None, :])
                Sq = jnp.einsum('bhij,bhj->bhi', S, q)
                out = Sq * jax.nn.silu(Sq)
                return (S, out)
            S_final, outs = jax.lax.scan(step, S0, (k_all, v_all, q_all, beta_all))
            cell_out = outs.transpose(1, 0, 2, 3).reshape(b, t, h * n)
            y = jnp.einsum('btm,dm->btd', cell_out, W_out)
            return (y, S_final)
        key = jax.random.key(seed)
        ks = jax.random.split(key, 8)
        x = jax.random.normal(ks[0], (B, T, D), jnp.float32)
        W_in = _xavier(ks[1], (D, D), D, D)
        W_k = _xavier(ks[2], (H * N, D), N, D)
        W_v = _xavier(ks[3], (H * N, D), N, D)
        W_q = _xavier(ks[4], (H * N, D), N, D)
        W_beta = _xavier(ks[5], (H * N, D), N, D)
        b_beta = jnp.full((H, N), 2.0, jnp.float32)
        W_out = _xavier(ks[6], (D, H * N), H * N, D)
        return {'x': x, 'W_in': W_in, 'W_k': W_k, 'W_v': W_v, 'W_q': W_q, 'W_beta': W_beta, 'b_beta': b_beta, 'W_out': W_out}
    _L2_attn_all = _L2_attn_setup()
    _L2_attn_in = {k: v for k, v in _L2_attn_all.items() if k in ('W_in', 'W_k', 'W_v', 'W_q', 'W_beta', 'b_beta', 'W_out')}
    del _L2_attn_all

    def _L2_cond2_setup():
        import jax, jax.numpy as jnp
        import numpy as np
        import math
        N, T, D, H = (64, 64, 128, 128)
        key = jax.random.key(seed)
        k1, k2, k3, k4 = jax.random.split(key, 4)
        x = jax.random.normal(k1, (N, T, D), dtype=jnp.float32)
        h0 = jax.random.normal(k2, (N, H), dtype=jnp.float32)
        Wx = jax.random.normal(k3, (D, H), dtype=jnp.float32) / math.sqrt(D)
        Wh = jax.random.normal(k4, (H, H), dtype=jnp.float32) / math.sqrt(H)
        b = jnp.zeros((H,), dtype=jnp.float32)
        return {'x': x, 'h0': h0, 'Wx': Wx, 'Wh': Wh, 'b': b}
    _L2_cond2_all = _L2_cond2_setup()
    _L2_cond2_in = {k: v for k, v in _L2_cond2_all.items() if k in ('Wx', 'Wh', 'b')}
    del _L2_cond2_all

    def _L2_ffn_setup():
        import jax, jax.numpy as jnp
        import numpy as np
        HIDDEN = 128
        INNER = 512

        def _weight_quant(w):
            scale = 1.0 / jnp.clip(jnp.mean(jnp.abs(w)), 1e-05)
            wq = jnp.clip(jnp.round(w * scale), -1.0, 1.0) / scale
            return w + jax.lax.stop_gradient(wq - w)

        def _act_quant(x):
            scale = 127.0 / jnp.clip(jnp.max(jnp.abs(x), axis=-1, keepdims=True), 1e-05)
            xq = jnp.clip(jnp.round(x * scale), -128.0, 127.0) / scale
            return x + jax.lax.stop_gradient(xq - x)

        def _bitlinear(x, w):
            return jnp.einsum('bsi,oi->bso', _act_quant(x), _weight_quant(w))
        key = jax.random.key(seed)
        k0, k1, k2, k3 = jax.random.split(key, 4)
        x = jax.random.normal(k0, (4, 256, HIDDEN), dtype=jnp.float32)
        w_gate = jax.random.normal(k1, (INNER, HIDDEN), dtype=jnp.float32) / np.sqrt(HIDDEN)
        w_up = jax.random.normal(k2, (INNER, HIDDEN), dtype=jnp.float32) / np.sqrt(HIDDEN)
        w_down = jax.random.normal(k3, (HIDDEN, INNER), dtype=jnp.float32) / np.sqrt(INNER)
        return {'x': x, 'w_gate': w_gate, 'w_up': w_up, 'w_down': w_down}
    _L2_ffn_all = _L2_ffn_setup()
    _L2_ffn_in = {k: v for k, v in _L2_ffn_all.items() if k in ('w_gate', 'w_up', 'w_down')}
    del _L2_ffn_all

    def _L3_cond_setup():
        import jax, jax.numpy as jnp
        import numpy as np
        B, F_, IN, OUT, R = (32, 64, 128, 128, 16)
        key = jax.random.key(seed)
        ks = jax.random.split(key, 6)
        x = jax.random.normal(ks[0], (B, F_, IN), dtype=jnp.float32)
        u = jax.random.normal(ks[1], (B, 1, OUT, R), dtype=jnp.float32)
        v = jax.random.normal(ks[2], (B, 1, IN, R), dtype=jnp.float32)
        b = jax.random.normal(ks[3], (B, 1, OUT), dtype=jnp.float32)
        lim = 1.0 / np.sqrt(IN)
        W = jax.random.uniform(ks[4], (OUT, IN), minval=-lim, maxval=lim, dtype=jnp.float32)
        fc_bias = jax.random.uniform(ks[5], (OUT,), minval=-lim, maxval=lim, dtype=jnp.float32)
        return {'x': x, 'u': u, 'v': v, 'b': b, 'W': W, 'fc_bias': fc_bias}
    _L3_cond_all = _L3_cond_setup()
    _L3_cond_in = {k: v for k, v in _L3_cond_all.items() if k in ('W', 'fc_bias')}
    del _L3_cond_all

    def _L3_attn_setup():
        import jax, jax.numpy as jnp
        import numpy as np
        B, S, E, H = (2, 256, 128, 16)
        D = E // H
        EPS = 1e-06

        def _angle_decay():
            a = 1.0 / 10000.0 ** jnp.linspace(0.0, 1.0, D // 2)
            angle = jnp.repeat(a, 2)
            decay = jnp.log(1.0 - 2.0 ** (-5.0 - jnp.arange(H, dtype=jnp.float32)))
            return (angle, decay)

        def _rel_pos(slen):
            angle, decay = _angle_decay()
            idx = jnp.arange(slen, dtype=jnp.float32)
            sin = jnp.sin(idx[:, None] * angle[None, :])
            cos = jnp.cos(idx[:, None] * angle[None, :])
            diff = idx[:, None] - idx[None, :]
            tril = diff >= 0
            masked = jnp.where(tril, diff, jnp.inf)
            mask = jnp.exp(masked * decay[:, None, None])
            mask = jnp.nan_to_num(mask)
            mask = mask / jnp.sqrt(jnp.sum(mask, axis=-1, keepdims=True))
            return (sin, cos, mask)

        def _rotate_every_two(x):
            x1 = x[..., ::2]
            x2 = x[..., 1::2]
            return jnp.stack((-x2, x1), axis=-1).reshape(x.shape)

        def _theta_shift(x, sin, cos):
            return x * cos + _rotate_every_two(x) * sin
        key = jax.random.key(seed)
        ks = jax.random.split(key, 5)
        scale = 1.0 / np.sqrt(E)
        return {'x': jax.random.normal(ks[0], (B, S, E), dtype=jnp.float32), 'Wq': jax.random.normal(ks[1], (E, E), dtype=jnp.float32) * scale, 'Wk': jax.random.normal(ks[2], (E, E), dtype=jnp.float32) * scale, 'Wv': jax.random.normal(ks[3], (E, E), dtype=jnp.float32) * scale, 'Wg': jax.random.normal(ks[4], (E, E), dtype=jnp.float32) * scale}
    _L3_attn_all = _L3_attn_setup()
    _L3_attn_in = {k: v for k, v in _L3_attn_all.items() if k in ('Wq', 'Wk', 'Wv', 'Wg')}
    del _L3_attn_all

    def _L3_cond2_setup():
        import jax, jax.numpy as jnp
        import numpy as np
        N, T, D, H = (64, 64, 128, 128)

        def lstm_scan(x, h0, Wx, Wh, b):
            xW = jnp.einsum('ntd,dg->ntg', x, Wx) + b
            Hdim = h0.shape[1]
            c0 = jnp.zeros_like(h0)

            def step(carry, xw_t):
                prev_h, prev_c = carry
                a = xw_t + prev_h @ Wh
                i = jax.nn.sigmoid(a[:, :Hdim])
                f = jax.nn.sigmoid(a[:, Hdim:2 * Hdim])
                o = jax.nn.sigmoid(a[:, 2 * Hdim:3 * Hdim])
                g = jnp.tanh(a[:, 3 * Hdim:])
                next_c = f * prev_c + i * g
                next_h = o * jnp.tanh(next_c)
                return ((next_h, next_c), next_h)
            _, hs = jax.lax.scan(step, (h0, c0), jnp.swapaxes(xW, 0, 1))
            return jnp.swapaxes(hs, 0, 1)
        key = jax.random.key(seed)
        k1, k2, k3, k4 = jax.random.split(key, 4)
        x = jax.random.normal(k1, (N, T, D), dtype=jnp.float32)
        h0 = jax.random.normal(k2, (N, H), dtype=jnp.float32)
        Wx = jax.random.normal(k3, (D, 4 * H), dtype=jnp.float32) / np.sqrt(D)
        Wh = jax.random.normal(k4, (H, 4 * H), dtype=jnp.float32) / np.sqrt(H)
        b = jnp.zeros((4 * H,), dtype=jnp.float32)
        return {'x': x, 'h0': h0, 'Wx': Wx, 'Wh': Wh, 'b': b}
    _L3_cond2_all = _L3_cond2_setup()
    _L3_cond2_in = {k: v for k, v in _L3_cond2_all.items() if k in ('Wx', 'Wh', 'b')}
    del _L3_cond2_all

    def _L3_ffn_setup():
        import jax, jax.numpy as jnp
        import numpy as np
        D_MODEL, D_FF, N_EXPERTS, TOP_K = (128, 256, 8, 2)
        B, S = (2, 256)
        key = jax.random.key(seed)
        ks = jax.random.split(key, 6)
        sd = 1.0 / np.sqrt(D_MODEL)
        sf = 1.0 / np.sqrt(D_FF)
        return {'x': jax.random.normal(ks[0], (B, S, D_MODEL), jnp.float32), 'router_w': jax.random.normal(ks[1], (N_EXPERTS, D_MODEL), jnp.float32) * sd, 'gate_w': jax.random.normal(ks[2], (N_EXPERTS, D_MODEL, D_FF), jnp.float32) * sd, 'gate_b': jnp.zeros((N_EXPERTS, D_FF), jnp.float32), 'up_w': jax.random.normal(ks[3], (N_EXPERTS, D_MODEL, D_FF), jnp.float32) * sd, 'up_b': jnp.zeros((N_EXPERTS, D_FF), jnp.float32), 'down_w': jax.random.normal(ks[4], (N_EXPERTS, D_FF, D_MODEL), jnp.float32) * sf, 'down_b': jnp.zeros((N_EXPERTS, D_MODEL), jnp.float32)}
    _L3_ffn_all = _L3_ffn_setup()
    _L3_ffn_in = {k: v for k, v in _L3_ffn_all.items() if k in ('router_w', 'gate_w', 'gate_b', 'up_w', 'up_b', 'down_w', 'down_b')}
    del _L3_ffn_all
    return {'x': x, 'cond_1024': cond_1024, 'fside_Bx1x1024x16_0': fside_Bx1x1024x16_0, 'L0_cond_W1': _L0_cond_in['W1'], 'L0_cond_b1': _L0_cond_in['b1'], 'L0_cond_W2': _L0_cond_in['W2'], 'L0_cond_b2': _L0_cond_in['b2'], 'L0_attn_Wq': _L0_attn_in['Wq'], 'L0_attn_Wk': _L0_attn_in['Wk'], 'L0_attn_Wv': _L0_attn_in['Wv'], 'L0_attn_Wo': _L0_attn_in['Wo'], 'L0_cond2_Wx': _L0_cond2_in['Wx'], 'L0_cond2_Wh': _L0_cond2_in['Wh'], 'L0_cond2_b': _L0_cond2_in['b'], 'L0_ffn_weight': _L0_ffn_in['weight'], 'L0_ffn_bias': _L0_ffn_in['bias'], 'L1_attn_w_qkv': _L1_attn_in['w_qkv'], 'L1_attn_w_proj': _L1_attn_in['w_proj'], 'L1_cond2_router_w': _L1_cond2_in['router_w'], 'L1_cond2_router_t_w': _L1_cond2_in['router_t_w'], 'L1_cond2_router_bias': _L1_cond2_in['router_bias'], 'L1_cond2_sw1': _L1_cond2_in['sw1'], 'L1_cond2_sw3': _L1_cond2_in['sw3'], 'L1_cond2_sw2': _L1_cond2_in['sw2'], 'L1_cond2_rw1': _L1_cond2_in['rw1'], 'L1_cond2_rw2': _L1_cond2_in['rw2'], 'L1_ffn_Wg': _L1_ffn_in['Wg'], 'L1_ffn_W1': _L1_ffn_in['W1'], 'L1_ffn_b1': _L1_ffn_in['b1'], 'L1_ffn_W2': _L1_ffn_in['W2'], 'L1_ffn_b2': _L1_ffn_in['b2'], 'L2_cond_Wx': _L2_cond_in['Wx'], 'L2_cond_Wh': _L2_cond_in['Wh'], 'L2_cond_b': _L2_cond_in['b'], 'L2_attn_W_in': _L2_attn_in['W_in'], 'L2_attn_W_k': _L2_attn_in['W_k'], 'L2_attn_W_v': _L2_attn_in['W_v'], 'L2_attn_W_q': _L2_attn_in['W_q'], 'L2_attn_W_beta': _L2_attn_in['W_beta'], 'L2_attn_b_beta': _L2_attn_in['b_beta'], 'L2_attn_W_out': _L2_attn_in['W_out'], 'L2_cond2_Wx': _L2_cond2_in['Wx'], 'L2_cond2_Wh': _L2_cond2_in['Wh'], 'L2_cond2_b': _L2_cond2_in['b'], 'L2_ffn_w_gate': _L2_ffn_in['w_gate'], 'L2_ffn_w_up': _L2_ffn_in['w_up'], 'L2_ffn_w_down': _L2_ffn_in['w_down'], 'L3_cond_W': _L3_cond_in['W'], 'L3_cond_fc_bias': _L3_cond_in['fc_bias'], 'L3_attn_Wq': _L3_attn_in['Wq'], 'L3_attn_Wk': _L3_attn_in['Wk'], 'L3_attn_Wv': _L3_attn_in['Wv'], 'L3_attn_Wg': _L3_attn_in['Wg'], 'L3_cond2_Wx': _L3_cond2_in['Wx'], 'L3_cond2_Wh': _L3_cond2_in['Wh'], 'L3_cond2_b': _L3_cond2_in['b'], 'L3_ffn_router_w': _L3_ffn_in['router_w'], 'L3_ffn_gate_w': _L3_ffn_in['gate_w'], 'L3_ffn_gate_b': _L3_ffn_in['gate_b'], 'L3_ffn_up_w': _L3_ffn_in['up_w'], 'L3_ffn_up_b': _L3_ffn_in['up_b'], 'L3_ffn_down_w': _L3_ffn_in['down_w'], 'L3_ffn_down_b': _L3_ffn_in['down_b']}

def reference(x, cond_1024, fside_Bx1x1024x16_0, L0_cond_W1, L0_cond_b1, L0_cond_W2, L0_cond_b2, L0_attn_Wq, L0_attn_Wk, L0_attn_Wv, L0_attn_Wo, L0_cond2_Wx, L0_cond2_Wh, L0_cond2_b, L0_ffn_weight, L0_ffn_bias, L1_attn_w_qkv, L1_attn_w_proj, L1_cond2_router_w, L1_cond2_router_t_w, L1_cond2_router_bias, L1_cond2_sw1, L1_cond2_sw3, L1_cond2_sw2, L1_cond2_rw1, L1_cond2_rw2, L1_ffn_Wg, L1_ffn_W1, L1_ffn_b1, L1_ffn_W2, L1_ffn_b2, L2_cond_Wx, L2_cond_Wh, L2_cond_b, L2_attn_W_in, L2_attn_W_k, L2_attn_W_v, L2_attn_W_q, L2_attn_W_beta, L2_attn_b_beta, L2_attn_W_out, L2_cond2_Wx, L2_cond2_Wh, L2_cond2_b, L2_ffn_w_gate, L2_ffn_w_up, L2_ffn_w_down, L3_cond_W, L3_cond_fc_bias, L3_attn_Wq, L3_attn_Wk, L3_attn_Wv, L3_attn_Wg, L3_cond2_Wx, L3_cond2_Wh, L3_cond2_b, L3_ffn_router_w, L3_ffn_gate_w, L3_ffn_gate_b, L3_ffn_up_w, L3_ffn_up_b, L3_ffn_down_w, L3_ffn_down_b):
    import jax
    import jax.numpy as jnp

    def _L0_cond_ref(v, q_pool, W1, b1, W2, b2):
        import jax, jax.numpy as jnp
        import numpy as np
        INV_SQRT2 = 0.7071067811865476
        B, N, d = v.shape
        h = jax.nn.silu(q_pool @ W1.T + b1)
        gate = jax.nn.sigmoid(h @ W2.T + b2)[:, None, :]
        levels = int(np.log2(N))
        a = v
        details = []
        for _ in range(levels):
            e, o = (a[:, 0::2], a[:, 1::2])
            details.append((e - o) * INV_SQRT2)
            a = (e + o) * INV_SQRT2
        a = a * gate
        for dc in reversed(details):
            dc = dc * gate
            e = (a + dc) * INV_SQRT2
            o = (a - dc) * INV_SQRT2
            n = e.shape[1]
            a = jnp.stack([e, o], axis=2).reshape(B, 2 * n, d)
        return v + a

    def _L0_attn_ref(x, Wq, Wk, Wv, Wo):
        import jax, jax.numpy as jnp
        import numpy as np
        B, S, D = (2, 256, 128)
        NH, KVH = (16, 4)
        HD = D // NH
        ROPE_BASE = 10000.0

        def rotate_half(x):
            half = x.shape[-1] // 2
            x1, x2 = (x[..., :half], x[..., half:])
            return jnp.concatenate((-x2, x1), axis=-1)

        def rope_cache(seq_len, head_dim, base, dtype):
            half = head_dim // 2
            inv_freq = 1.0 / base ** (jnp.arange(half, dtype=jnp.float32) / max(1, half))
            t = jnp.arange(seq_len, dtype=jnp.float32)
            freqs = jnp.einsum('i,j->ij', t, inv_freq)
            emb = jnp.concatenate((freqs, freqs), axis=-1)
            cos = jnp.cos(emb)[None, None].astype(dtype)
            sin = jnp.sin(emb)[None, None].astype(dtype)
            return (sin, cos)
        bsz, seq_len, _ = x.shape
        scale = HD ** (-0.5)
        q = (x @ Wq).reshape(bsz, seq_len, NH, HD).transpose(0, 2, 1, 3)
        k = (x @ Wk).reshape(bsz, seq_len, KVH, HD).transpose(0, 2, 1, 3)
        v = (x @ Wv).reshape(bsz, seq_len, KVH, HD).transpose(0, 2, 1, 3)
        sin, cos = rope_cache(seq_len, HD, ROPE_BASE, q.dtype)
        q = q * cos + rotate_half(q) * sin
        k = k * cos + rotate_half(k) * sin
        rep = NH // KVH
        k = jnp.repeat(k, rep, axis=1)
        v = jnp.repeat(v, rep, axis=1)
        att = jnp.einsum('bhqd,bhkd->bhqk', q, k) * scale
        causal = jnp.tril(jnp.ones((seq_len, seq_len), dtype=bool))
        att = jnp.where(causal, att, jnp.finfo(att.dtype).min)
        att = jax.nn.softmax(att, axis=-1)
        y = jnp.einsum('bhqk,bhkd->bhqd', att, v)
        y = y.transpose(0, 2, 1, 3).reshape(bsz, seq_len, NH * HD)
        return y @ Wo

    def _L0_cond2_ref(x, h0, Wx, Wh, b):
        import jax, jax.numpy as jnp
        import numpy as np
        D = 128
        H = 128
        N = 64
        T = 64

        def _lstm(x, h0, Wx, Wh, b):
            xW = jnp.einsum('ntd,dk->tnk', x, Wx) + b
            c0 = jnp.zeros_like(h0)
            Hdim = h0.shape[1]

            def step(carry, xw_t):
                prev_h, prev_c = carry
                a = xw_t + prev_h @ Wh
                i = jax.nn.sigmoid(a[:, 0:Hdim])
                f = jax.nn.sigmoid(a[:, Hdim:2 * Hdim])
                o = jax.nn.sigmoid(a[:, 2 * Hdim:3 * Hdim])
                g = jnp.tanh(a[:, 3 * Hdim:4 * Hdim])
                next_c = f * prev_c + i * g
                next_h = o * jnp.tanh(next_c)
                return ((next_h, next_c), next_h)
            _, hs = jax.lax.scan(step, (h0, c0), xW)
            return jnp.transpose(hs, (1, 0, 2))
        return _lstm(x, h0, Wx, Wh, b)

    def _L0_ffn_ref(x, weight, bias):
        import jax, jax.numpy as jnp
        import numpy as np
        IN_FEATURES = 128
        OUT_FEATURES = 128
        B, S = (8, 512)
        w_scale = jnp.mean(jnp.abs(weight))
        q_weight = jnp.sign(weight) * (jnp.abs(weight) > 0.5 * w_scale).astype(weight.dtype)
        i_scale = jnp.max(jnp.abs(x)) / 127.0
        q_input = jnp.clip(jnp.round(x / i_scale), -128.0, 127.0)
        out = jnp.einsum('bsk,ok->bso', q_input, q_weight) * w_scale * i_scale
        out = out + bias
        return out

    def _L1_cond_ref(x, random_values):
        import jax, jax.numpy as jnp
        import numpy as np
        TEMPERATURE = 2.0
        ax = jnp.abs(x)
        p = ax / jnp.sum(ax, axis=1, keepdims=True)
        pi = jnp.exp(p * TEMPERATURE)
        thresholds = pi / jnp.sum(pi, axis=1, keepdims=True)
        cum = jnp.cumsum(thresholds, axis=1) + 0.001
        rv = random_values[:, None, :]
        chosen_idx = jnp.sum(cum <= rv, axis=1, keepdims=True)
        gathered = jnp.take_along_axis(ax, chosen_idx, axis=1)
        mask = ax >= gathered
        return x * mask

    def _L1_attn_ref(x, w_qkv, w_proj):
        import jax, jax.numpy as jnp
        import numpy as np
        N_HEAD = 16
        ROPE_BASE = 10000.0

        def _rotate_half(t):
            d = t.shape[-1] // 2
            return jnp.concatenate([-t[..., d:], t[..., :d]], axis=-1)

        def _rope_cos_sin(T, D, dtype):
            half = D // 2
            theta = 1.0 / ROPE_BASE ** (jnp.arange(half, dtype=dtype) / half)
            pos = jnp.arange(T, dtype=dtype)
            freqs = pos[:, None] * theta[None, :]
            cos = jnp.repeat(jnp.cos(freqs), 2, axis=-1)
            sin = jnp.repeat(jnp.sin(freqs), 2, axis=-1)
            return (cos, sin)
        B, T, C = x.shape
        H = N_HEAD
        D = C // H
        scale = D ** (-0.5)
        qkv = x @ w_qkv
        q, k, v = jnp.split(qkv, 3, axis=-1)
        to_heads = lambda t: t.reshape(B, T, H, D).transpose(0, 2, 1, 3)
        q, k, v = (to_heads(q), to_heads(k), to_heads(v))
        cos, sin = _rope_cos_sin(T, D, x.dtype)
        q = q * cos + _rotate_half(q) * sin
        k = k * cos + _rotate_half(k) * sin
        att = jnp.einsum('bhtd,bhsd->bhts', q, k) * scale
        causal = jnp.tril(jnp.ones((T, T), dtype=bool))
        att = jnp.where(causal, att, jnp.finfo(att.dtype).min)
        att = jax.nn.softmax(att, axis=-1)
        y = jnp.einsum('bhts,bhsd->bhtd', att, v)
        y = y.transpose(0, 2, 1, 3).reshape(B, T, C)
        return y @ w_proj

    def _L1_cond2_ref(x, t_emb, router_w, router_t_w, router_bias, sw1, sw3, sw2, rw1, rw2):
        import jax, jax.numpy as jnp
        import numpy as np
        TOP_K = 2
        N_EXPERTS = 8
        N_SHARED = 1
        EPS = 1e-09
        B, T, C = x.shape
        N = B * T
        x_flat = x.reshape(N, C)
        shared_out = jnp.einsum('nh,dh->nd', jax.nn.silu(x_flat @ sw1.T) * (x_flat @ sw3.T), sw2)
        t_bias = t_emb @ router_t_w.T
        t_bias_flat = jnp.broadcast_to(t_bias[:, None, :], (B, T, N_EXPERTS)).reshape(N, N_EXPERTS)
        s = jax.nn.sigmoid((x_flat @ router_w.T + t_bias_flat).astype(jnp.float32))
        sel_scores = s + router_bias
        _, topk_idx = jax.lax.top_k(sel_scores, TOP_K)
        s_sel = jnp.take_along_axis(s, topk_idx, axis=1)
        denom = jnp.sum(s_sel, axis=1, keepdims=True)
        gates = jnp.where(denom > EPS, s_sel / (denom + EPS), 1.0 / TOP_K).astype(x.dtype)
        combine = jnp.sum(gates[:, :, None] * jax.nn.one_hot(topk_idx, N_EXPERTS, dtype=x.dtype), axis=1)
        H = jax.nn.gelu(jnp.einsum('nd,ehd->enh', x_flat, rw1), approximate=False)
        O = jnp.einsum('enh,edh->end', H, rw2)
        routed_out = jnp.einsum('end,ne->nd', O, combine)
        out = (shared_out + routed_out) / (N_SHARED + TOP_K)
        return out.reshape(B, T, C)

    def _L1_ffn_ref(x, Wg, W1, b1, W2, b2):
        import jax, jax.numpy as jnp
        import numpy as np
        NUM_EXPERTS = 8
        TOP_K = 2
        B, S, D = x.shape
        E, _, H = W1.shape
        OUT = W2.shape[2]
        xm = x.reshape(-1, D)
        logits = xm @ Wg
        probs = jax.nn.softmax(logits, axis=-1)
        topk_p, topk_i = jax.lax.top_k(probs, TOP_K)
        flat_e = topk_i.reshape(-1)
        flat_p = topk_p.reshape(-1)
        order = jnp.argsort(flat_e)
        tok_idx = order // TOP_K
        e_sorted = flat_e[order]
        p_sorted = flat_p[order]
        xs = xm[tok_idx]
        y = jnp.zeros((xs.shape[0], OUT), dtype=xs.dtype)
        for e in range(E):
            h = jax.nn.relu(xs @ W1[e] + b1[e])
            ye = h @ W2[e] + b2[e]
            m = (e_sorted == e)[:, None].astype(xs.dtype)
            y = y + m * ye
        y = y * p_sorted[:, None]
        out = jnp.zeros((B * S, OUT), dtype=y.dtype).at[tok_idx].add(y)
        return out.reshape(B, S, OUT)

    def _L2_cond_ref(x, h0, Wx, Wh, b):
        import jax, jax.numpy as jnp
        import numpy as np
        import math
        D = 128
        H = 128
        xz = jnp.einsum('ntd,dk->ntk', x, Wx) + b
        c0 = jnp.zeros_like(h0)

        def step(carry, xz_t):
            prev_h, prev_c = carry
            z = xz_t + prev_h @ Wh
            ai, af, ao, ag = jnp.split(z, 4, axis=1)
            i = jax.nn.sigmoid(ai)
            f = jax.nn.sigmoid(af)
            o = jax.nn.sigmoid(ao)
            g = jnp.tanh(ag)
            next_c = f * prev_c + i * g
            next_h = o * jnp.tanh(next_c)
            return ((next_h, next_c), next_h)
        _, hs = jax.lax.scan(step, (h0, c0), jnp.swapaxes(xz, 0, 1))
        return jnp.swapaxes(hs, 0, 1)

    def _L2_attn_ref(x, W_in, W_k, W_v, W_q, W_beta, b_beta, W_out):
        import jax, jax.numpy as jnp
        import numpy as np
        B, T, D = (8, 256, 128)
        H, N = (8, 32)

        def _xavier(key, shape, fan_in, fan_out):
            lim = float(np.sqrt(6.0 / (fan_in + fan_out)))
            return jax.random.uniform(key, shape, jnp.float32, -lim, lim)

        def _reference_tuple_inner(x, W_in, W_k, W_v, W_q, W_beta, b_beta, W_out):
            b, t, d = x.shape
            h, n = b_beta.shape
            xp = jax.nn.silu(jnp.einsum('btd,ed->bte', x, W_in))

            def proj(W):
                return jnp.einsum('btd,md->btm', xp, W).reshape(b, t, h, n).transpose(1, 0, 2, 3)
            k_all = proj(W_k)
            v_all = proj(W_v)
            q_all = proj(W_q)
            beta_all = jax.nn.sigmoid(proj(W_beta) + b_beta)
            S0 = jnp.zeros((b, h, n, n), x.dtype)

            def step(S, inp):
                k, v, q, beta = inp
                kn = k / (jnp.linalg.norm(k, axis=-1, keepdims=True) + 1e-06)
                retrieved = jnp.einsum('bhij,bhj->bhi', S, kn)
                delta = v - retrieved
                S = jnp.tanh(beta[..., None] * S + delta[..., None] * kn[..., None, :])
                Sq = jnp.einsum('bhij,bhj->bhi', S, q)
                out = Sq * jax.nn.silu(Sq)
                return (S, out)
            S_final, outs = jax.lax.scan(step, S0, (k_all, v_all, q_all, beta_all))
            cell_out = outs.transpose(1, 0, 2, 3).reshape(b, t, h * n)
            y = jnp.einsum('btm,dm->btd', cell_out, W_out)
            return (y, S_final)
        return _reference_tuple_inner(x, W_in, W_k, W_v, W_q, W_beta, b_beta, W_out)[0]

    def _L2_cond2_ref(x, h0, Wx, Wh, b):
        import jax, jax.numpy as jnp
        import numpy as np
        import math
        N, T, D, H = (64, 64, 128, 128)
        xW = jnp.einsum('ntd,dh->nth', x, Wx) + b

        def step(prev_h, xw_t):
            next_h = jnp.tanh(prev_h @ Wh + xw_t)
            return (next_h, next_h)
        _, hs = jax.lax.scan(step, h0, jnp.swapaxes(xW, 0, 1))
        return jnp.swapaxes(hs, 0, 1)

    def _L2_ffn_ref(x, w_gate, w_up, w_down):
        import jax, jax.numpy as jnp
        import numpy as np
        HIDDEN = 128
        INNER = 512

        def _weight_quant(w):
            scale = 1.0 / jnp.clip(jnp.mean(jnp.abs(w)), 1e-05)
            wq = jnp.clip(jnp.round(w * scale), -1.0, 1.0) / scale
            return w + jax.lax.stop_gradient(wq - w)

        def _act_quant(x):
            scale = 127.0 / jnp.clip(jnp.max(jnp.abs(x), axis=-1, keepdims=True), 1e-05)
            xq = jnp.clip(jnp.round(x * scale), -128.0, 127.0) / scale
            return x + jax.lax.stop_gradient(xq - x)

        def _bitlinear(x, w):
            return jnp.einsum('bsi,oi->bso', _act_quant(x), _weight_quant(w))
        gate = jax.nn.silu(_bitlinear(x, w_gate))
        up = _bitlinear(x, w_up)
        return _bitlinear(gate * up, w_down)

    def _L3_cond_ref(x, u, v, b, W, fc_bias):
        import jax, jax.numpy as jnp
        import numpy as np
        B, F_, IN, OUT, R = (32, 64, 128, 128, 16)
        inch = x.shape[-1]
        r = v.shape[-1]
        z1 = jnp.einsum('bfi,bir->bfr', x, v[:, 0]) / inch
        z = jnp.einsum('bfr,bor->bfo', z1, u[:, 0]) / r
        y = jnp.einsum('bfi,oi->bfo', x, W) + fc_bias + z + b
        return jax.nn.gelu(y, approximate=False)

    def _L3_attn_ref(x, Wq, Wk, Wv, Wg):
        import jax, jax.numpy as jnp
        import numpy as np
        B, S, E, H = (2, 256, 128, 16)
        D = E // H
        EPS = 1e-06

        def _angle_decay():
            a = 1.0 / 10000.0 ** jnp.linspace(0.0, 1.0, D // 2)
            angle = jnp.repeat(a, 2)
            decay = jnp.log(1.0 - 2.0 ** (-5.0 - jnp.arange(H, dtype=jnp.float32)))
            return (angle, decay)

        def _rel_pos(slen):
            angle, decay = _angle_decay()
            idx = jnp.arange(slen, dtype=jnp.float32)
            sin = jnp.sin(idx[:, None] * angle[None, :])
            cos = jnp.cos(idx[:, None] * angle[None, :])
            diff = idx[:, None] - idx[None, :]
            tril = diff >= 0
            masked = jnp.where(tril, diff, jnp.inf)
            mask = jnp.exp(masked * decay[:, None, None])
            mask = jnp.nan_to_num(mask)
            mask = mask / jnp.sqrt(jnp.sum(mask, axis=-1, keepdims=True))
            return (sin, cos, mask)

        def _rotate_every_two(x):
            x1 = x[..., ::2]
            x2 = x[..., 1::2]
            return jnp.stack((-x2, x1), axis=-1).reshape(x.shape)

        def _theta_shift(x, sin, cos):
            return x * cos + _rotate_every_two(x) * sin
        bsz, tgt_len, _ = x.shape
        sin, cos, mask = _rel_pos(tgt_len)
        scaling = E ** (-0.5)
        q = x @ Wq
        k = x @ Wk * scaling
        v = x @ Wv
        g = x @ Wg
        q = q.reshape(bsz, tgt_len, H, D).transpose(0, 2, 1, 3)
        k = k.reshape(bsz, tgt_len, H, D).transpose(0, 2, 1, 3)
        vr = v.reshape(bsz, tgt_len, H, D).transpose(0, 2, 1, 3)
        qr = _theta_shift(q, sin, cos)
        kr = _theta_shift(k, sin, cos)
        qk = jnp.einsum('bhqd,bhkd->bhqk', qr, kr) * mask[None]
        denom = jax.lax.stop_gradient(jnp.clip(jnp.sum(jnp.abs(qk), axis=-1, keepdims=True), 1.0, 50000.0))
        out = jnp.einsum('bhqk,bhkd->bhqd', qk / denom, vr)
        out = out.transpose(0, 2, 1, 3)
        out = out * jax.lax.rsqrt(jnp.mean(out * out, axis=-1, keepdims=True) + EPS)
        out = out.reshape(bsz, tgt_len, E)
        return jax.nn.silu(g) * out

    def _L3_cond2_ref(x, h0, Wx, Wh, b):
        import jax, jax.numpy as jnp
        import numpy as np
        N, T, D, H = (64, 64, 128, 128)

        def lstm_scan(x, h0, Wx, Wh, b):
            xW = jnp.einsum('ntd,dg->ntg', x, Wx) + b
            Hdim = h0.shape[1]
            c0 = jnp.zeros_like(h0)

            def step(carry, xw_t):
                prev_h, prev_c = carry
                a = xw_t + prev_h @ Wh
                i = jax.nn.sigmoid(a[:, :Hdim])
                f = jax.nn.sigmoid(a[:, Hdim:2 * Hdim])
                o = jax.nn.sigmoid(a[:, 2 * Hdim:3 * Hdim])
                g = jnp.tanh(a[:, 3 * Hdim:])
                next_c = f * prev_c + i * g
                next_h = o * jnp.tanh(next_c)
                return ((next_h, next_c), next_h)
            _, hs = jax.lax.scan(step, (h0, c0), jnp.swapaxes(xW, 0, 1))
            return jnp.swapaxes(hs, 0, 1)
        return lstm_scan(x, h0, Wx, Wh, b)

    def _L3_ffn_ref(x, router_w, gate_w, gate_b, up_w, up_b, down_w, down_b):
        import jax, jax.numpy as jnp
        import numpy as np
        D_MODEL, D_FF, N_EXPERTS, TOP_K = (128, 256, 8, 2)
        B, S = (2, 256)
        b, s, d = x.shape
        xf = x.reshape(b * s, d)
        n = xf.shape[0]
        router_logits = xf @ router_w.T
        probs = jax.nn.softmax(router_logits, axis=-1)
        topv, topi = jax.lax.top_k(probs, TOP_K)
        mask = jnp.zeros_like(probs).at[jnp.arange(n)[:, None], topi].set(1.0)
        probs = probs * mask
        probs = probs / (probs.sum(axis=-1, keepdims=True) + 1e-09)
        g = jnp.einsum('nd,edf->nef', xf, gate_w) + gate_b
        u = jnp.einsum('nd,edf->nef', xf, up_w) + up_b
        h = jax.nn.silu(g) * u
        expert_out = jnp.einsum('nef,efd->ned', h, down_w) + down_b
        y = jnp.einsum('ne,ned->nd', probs, expert_out)
        return y.reshape(b, s, d)
    x = x + _L0_attn_ref(_L0_cond_ref(x, cond_1024, L0_cond_W1, L0_cond_b1, L0_cond_W2, L0_cond_b2), L0_attn_Wq, L0_attn_Wk, L0_attn_Wv, L0_attn_Wo)
    x = x + _L0_ffn_ref(_L0_cond2_ref(x, cond_1024, L0_cond2_Wx, L0_cond2_Wh, L0_cond2_b), L0_ffn_weight, L0_ffn_bias)
    x = x + _L1_attn_ref(_L1_cond_ref(x, cond_1024), L1_attn_w_qkv, L1_attn_w_proj)
    x = x + _L1_ffn_ref(_L1_cond2_ref(x, cond_1024, L1_cond2_router_w, L1_cond2_router_t_w, L1_cond2_router_bias, L1_cond2_sw1, L1_cond2_sw3, L1_cond2_sw2, L1_cond2_rw1, L1_cond2_rw2), L1_ffn_Wg, L1_ffn_W1, L1_ffn_b1, L1_ffn_W2, L1_ffn_b2)
    x = x + _L2_attn_ref(_L2_cond_ref(x, cond_1024, L2_cond_Wx, L2_cond_Wh, L2_cond_b), L2_attn_W_in, L2_attn_W_k, L2_attn_W_v, L2_attn_W_q, L2_attn_W_beta, L2_attn_b_beta, L2_attn_W_out)
    x = x + _L2_ffn_ref(_L2_cond2_ref(x, cond_1024, L2_cond2_Wx, L2_cond2_Wh, L2_cond2_b), L2_ffn_w_gate, L2_ffn_w_up, L2_ffn_w_down)
    x = x + _L3_attn_ref(_L3_cond_ref(x, fside_Bx1x1024x16_0, fside_Bx1x1024x16_0, cond_1024[:, None, :], L3_cond_W, L3_cond_fc_bias), L3_attn_Wq, L3_attn_Wk, L3_attn_Wv, L3_attn_Wg)
    x = x + _L3_ffn_ref(_L3_cond2_ref(x, cond_1024, L3_cond2_Wx, L3_cond2_Wh, L3_cond2_b), L3_ffn_router_w, L3_ffn_gate_w, L3_ffn_gate_b, L3_ffn_up_w, L3_ffn_up_b, L3_ffn_down_w, L3_ffn_down_b)
    return x

_drawn_inputs = setup_inputs


def setup_inputs(seed=0):
    import zlib

    import numpy as np

    out = dict(_drawn_inputs(seed))
    spreads = {'L0_cond_b1': (0.0, 0.1),
     'L0_cond_b2': (0.0, 0.1),
     'L0_cond2_b': (0.0, 0.1),
     'L0_ffn_bias': (0.0, 0.1),
     'L1_cond2_router_bias': (0.0, 0.1),
     'L2_cond_b': (0.0, 0.1),
     'L2_attn_b_beta': (2.0, 0.2),
     'L2_cond2_b': (0.0, 0.1),
     'L3_cond2_b': (0.0, 0.1),
     'L3_ffn_gate_b': (0.0, 0.1),
     'L3_ffn_up_b': (0.0, 0.1),
     'L3_ffn_down_b': (0.0, 0.1)}
    factors = {}
    for name, (base, spread) in spreads.items():
        noise = np.random.default_rng([zlib.crc32(name.encode()), seed]).standard_normal(out[name].shape)
        drawn = base * np.exp(spread * noise) if base else spread * noise
        out[name] = jnp.asarray(drawn.astype(out[name].dtype))
    for name, factor in factors.items():
        out[name] = (out[name] * factor).astype(out[name].dtype)
    return out
```

```python
from contextlib import ExitStack

import numpy as np

import concourse.bass as bass
from concourse import mybir

F32 = mybir.dt.float32
BF16 = mybir.dt.bfloat16
ALU = mybir.AluOpType
ACT = mybir.ActivationFunctionType
AX_X = mybir.AxisListType.X
RMAX = bass.bass_isa.ReduceOp.max
RADD = bass.bass_isa.ReduceOp.add

B, T, D = 8, 256, 128
TOK = B * T
P = 128
CHUNK = 512
NCHUNK = TOK // CHUNK


STAGE_SEMAPHORES = []


class Memory:

    def __init__(self, nc, stack, tag):
        self.nc, self.stack, self.tag = nc, stack, tag

    def sb(self, name, shape, dt=F32):
        return self.stack.enter_context(self.nc.sbuf_tensor(f"{self.tag}_{name}", shape, dt))

    def ps(self, name, shape, dt=F32):
        return self.stack.enter_context(self.nc.psum_tensor(f"{self.tag}_{name}", shape, dt))

    def sem(self, name):
        sem = self.nc.alloc_semaphore(f"{self.tag}_{name}")
        if self.tag != "main":
            STAGE_SEMAPHORES.append(sem)
        return sem
STEPS_IN_BODY = 4


def lstm_stage(nc, tag, src, dst, wx, wh, bias, h0, ident):
    with ExitStack() as stack:
        mem = Memory(nc, stack, tag)
        xw = mem.sb("xw", [P, T * 4 * B])
        gates = mem.sb("gates", [P, 3 * B])
        cand_cell = mem.sb("cand_cell", [P, 2 * B])
        both = mem.sb("both", [P, 2 * B])
        tanh_c = mem.sb("tanh_c", [P, B])
        h_ring = mem.sb("h_ring", [P, STEPS_IN_BODY, B])
        pre = mem.ps("pre", [P, 4, CHUNK])
        acc = mem.ps("acc", [P, 2, CHUNK])
        xw_psum = mem.sem("xw_psum")
        xw_act = mem.sem("xw_act")
        xw_dve = mem.sem("xw_dve")
        gates_psum = mem.sem("gates_psum")
        gates_ready = mem.sem("gates_ready")
        mul_ready = mem.sem("mul_ready")
        cell_ready = mem.sem("cell_ready")
        tanh_ready = mem.sem("tanh_ready")
        h_ready = mem.sem("h_ready")
        table_ready = mem.sem("table_ready")
        h_saved = mem.sem("h_saved")
        xw_by_gate = xw[:, :].rearrange("p (t g b) -> p g b t", g=4, b=B)
        dst_by_step = dst.rearrange("p (b t) -> p t b", t=T)
        U = STEPS_IN_BODY
        BC = CHUNK // T

        with nc.Block() as block:

            @block.tensor
            def _(pe):
                for c in range(NCHUNK):
                    for g in range(4):
                        if c >= 1 and g == 0:
                            pe.wait_ge(xw_act, 2 * c)
                        if c >= 1 and g == 2:
                            pe.wait_ge(xw_dve, 2 * c)
                        nc.tensor.matmul(pre[:, g, :], wx[:, g * P:(g + 1) * P], src[:, c * CHUNK:(c + 1) * CHUNK],
                                         start=True, stop=True).then_inc(xw_psum, 1)
                pe.wait_ge(xw_act, 2 * NCHUNK)
                pe.wait_ge(xw_dve, 2 * NCHUNK)
                with pe.Fori(0, T // U) as i:
                    for u in range(U):
                        s = i * U + u
                        bank = acc[:, u % 2, 0:4 * B]
                        nc.tensor.matmul(bank, ident, xw[:, bass.ds(s * 4 * B, 4 * B)], start=True, stop=False)
                        pe.wait_ge(h_ready, s + 1)
                        for g in range(4):
                            last = nc.tensor.matmul(acc[:, u % 2, g * B:(g + 1) * B], wh[:, g * P:(g + 1) * P],
                                                    h_ring[:, (u - 1) % U, :], start=False, stop=(g == 3))
                        last.then_inc(gates_psum, 1)

            @block.scalar
            def _(act):
                for c in range(NCHUNK):
                    for g in range(2):
                        act.wait_ge(xw_psum, 4 * c + g + 1)
                        nc.scalar.activation(xw_by_gate[:, g, BC * c:BC * (c + 1), :],
                                             pre[:, g, :].rearrange("p (b t) -> p b t", t=T), ACT.Identity,
                                             bias=bias[:, g:g + 1]).then_inc(xw_act, 1)
                act.wait_ge(cell_ready, 1)
                nc.scalar.activation(tanh_c[:, :], cand_cell[:, B:2 * B], ACT.Sigmoid).then_inc(table_ready, 1)
                act.wait_ge(table_ready, 1)
                with act.Fori(0, T // U) as i:
                    for u in range(U):
                        s = i * U + u
                        act.wait_ge(gates_psum, s + 1)
                        nc.scalar.activation(gates[:, :], acc[:, u % 2, 0:3 * B], ACT.Sigmoid)
                        nc.scalar.activation(cand_cell[:, 0:B], acc[:, u % 2, 3 * B:4 * B],
                                             ACT.Tanh).then_inc(gates_ready, 1)
                        act.wait_ge(cell_ready, s + 2)
                        nc.scalar.activation(tanh_c[:, :], cand_cell[:, B:2 * B], ACT.Tanh).then_inc(tanh_ready, 1)

            @block.vector
            def _(dve):
                nc.vector.tensor_copy(h_ring[:, U - 1, :], h0).then_inc(h_ready, 1)
                nc.vector.memset(cand_cell[:, B:2 * B], 0.0).then_inc(cell_ready, 1)
                for c in range(NCHUNK):
                    for g in range(2, 4):
                        dve.wait_ge(xw_psum, 4 * c + g + 1)
                        nc.vector.tensor_scalar(xw_by_gate[:, g, BC * c:BC * (c + 1), :],
                                                pre[:, g, :].rearrange("p (b t) -> p b t", t=T),
                                                bias[:, g:g + 1], None, ALU.add).then_inc(xw_dve, 1)
                dve.wait_ge(cell_ready, 1)
                with dve.Fori(0, T // U) as i:
                    for u in range(U):
                        s = i * U + u
                        dve.wait_ge(gates_ready, s + 1)
                        nc.vector.tensor_tensor(both[:, :], gates[:, 0:2 * B], cand_cell[:, :],
                                                ALU.mult).then_inc(mul_ready, 1)
                        dve.wait_ge(mul_ready, s + 1)
                        nc.vector.tensor_tensor(cand_cell[:, B:2 * B], both[:, 0:B], both[:, B:2 * B],
                                                ALU.add).then_inc(cell_ready, 1)
                        dve.wait_ge(h_saved, s + 1)
                        dve.wait_ge(tanh_ready, s + 1)
                        nc.vector.tensor_tensor(h_ring[:, u, :], gates[:, 2 * B:3 * B], tanh_c[:, :],
                                                ALU.mult).then_inc(h_ready, 1)

            @block.gpsimd
            def _(pool):
                pool.sem_inc(h_saved, U)
                with pool.Fori(0, T // U) as i:
                    for u in range(U):
                        s = i * U + u
                        pool.wait_ge(h_ready, s + 2)
                        nc.gpsimd.tensor_copy(dst_by_step[:, bass.ds(s, 1), :], h_ring[:, u:u + 1, :]).then_inc(h_saved, 1)


def rnn_stage(nc, tag, src, dst, wx, wh, bias, h0, ident):
    with ExitStack() as stack:
        mem = Memory(nc, stack, tag)
        xw = mem.sb("xw", [P, T * B])
        h_ring = mem.sb("h_ring", [P, STEPS_IN_BODY, B])
        pre = mem.ps("pre", [P, NCHUNK, CHUNK])
        acc = mem.ps("acc", [P, 2, CHUNK])
        xw_psum, xw_ready, table_ready = mem.sem("xw_psum"), mem.sem("xw_ready"), mem.sem("table_ready")
        h_psum, h_ready, h_saved = mem.sem("h_psum"), mem.sem("h_ready"), mem.sem("h_saved")
        xw_by_seq = xw[:, :].rearrange("p (t b) -> p b t", b=B)
        dst_by_step = dst.rearrange("p (b t) -> p t b", t=T)
        U = STEPS_IN_BODY
        BC = CHUNK // T

        with nc.Block() as block:

            @block.tensor
            def _(pe):
                for c in range(NCHUNK):
                    nc.tensor.matmul(pre[:, c, :], wx, src[:, c * CHUNK:(c + 1) * CHUNK],
                                     start=True, stop=True).then_inc(xw_psum, 1)
                pe.wait_ge(xw_ready, NCHUNK)
                with pe.Fori(0, T // U) as i:
                    for u in range(U):
                        s = i * U + u
                        bank = acc[:, u % 2, 0:B]
                        nc.tensor.matmul(bank, ident, xw[:, bass.ds(s * B, B)], start=True, stop=False)
                        pe.wait_ge(h_ready, s + 1)
                        nc.tensor.matmul(bank, wh, h_ring[:, (u - 1) % U, :], start=False, stop=True).then_inc(h_psum, 1)

            @block.scalar
            def _(act):
                nc.scalar.activation(h_ring[:, U - 1, :], h0, ACT.Identity).then_inc(h_ready, 1)
                act.wait_ge(h_ready, 1)
                nc.scalar.activation(h_ring[:, 0, :], h0, ACT.Tanh).then_inc(table_ready, 1)
                act.wait_ge(table_ready, 1)
                with act.Fori(0, T // U) as i:
                    for u in range(U):
                        s = i * U + u
                        act.wait_ge(h_saved, s + 1)
                        act.wait_ge(h_psum, s + 1)
                        nc.scalar.activation(h_ring[:, u, :], acc[:, u % 2, 0:B], ACT.Tanh).then_inc(h_ready, 1)

            @block.vector
            def _(dve):
                for c in range(NCHUNK):
                    dve.wait_ge(xw_psum, c + 1)
                    nc.vector.tensor_scalar(xw_by_seq[:, BC * c:BC * (c + 1), :],
                                            pre[:, c, :].rearrange("p (b t) -> p b t", t=T), bias, None,
                                            ALU.add).then_inc(xw_ready, 1)

            @block.gpsimd
            def _(pool):
                pool.sem_inc(h_saved, U)
                with pool.Fori(0, T // U) as i:
                    for u in range(U):
                        s = i * U + u
                        pool.wait_ge(h_ready, s + 2)
                        nc.gpsimd.tensor_copy(dst_by_step[:, bass.ds(s, 1), :], h_ring[:, u:u + 1, :]).then_inc(h_saved, 1)
HEADS2, N2 = 8, 32
HG = HEADS2 // 4
IQ = 4
IL = N2 // IQ
ROWS = HG * IL
TC = 64
NTC = T // TC
KN_EPS = 1e-6


def delta_stage(nc, tag, src, x, w_in, w_k, w_q, w_vb, b_vb, w_out, head_sum):
    with ExitStack() as stack:
        mem = Memory(nc, stack, tag)
        xp_sig = mem.sb("xp_sig", [P, CHUNK])
        xp = mem.sb("xp", [P, CHUNK])
        k_sq = mem.sb("k_sq", [P, HG, CHUNK])
        k_norm = mem.sb("k_norm", [P, HG, CHUNK])
        kn_f = mem.sb("kn_f", [P, HG, CHUNK])
        q_f = mem.sb("q_f", [P, HG, CHUNK])
        vb_f = mem.sb("vb_f", [P, TC, B, IQ])
        kn_t = mem.sb("kn_t", [P, TC, HG, N2])
        q_t = mem.sb("q_t", [P, TC, HG, N2])
        vb_t = mem.sb("vb_t", [P, TC, 2 * ROWS])
        state = mem.sb("state", [P, 2, ROWS, N2])
        s_kn = mem.sb("s_kn", [P, ROWS, N2])
        beta_s = mem.sb("beta_s", [P, ROWS, N2])
        dk = mem.sb("dk", [P, ROWS, N2])
        pre = mem.sb("pre", [P, ROWS, N2])
        s_q = mem.sb("s_q", [P, ROWS, N2])
        got = mem.sb("got", [P, ROWS])
        dlt = mem.sb("dlt", [P, ROWS])
        sq = mem.sb("sq", [P, TC, 2 * ROWS])
        sq_sig = mem.sb("sq_sig", [P, TC, ROWS])
        sq_sq = mem.sb("sq_sq", [P, TC, ROWS])
        cell_f = vb_f[:, :, :, :].rearrange("p t b q -> p (t b) q")
        ps = [mem.ps(f"ps{n}", [P, CHUNK]) for n in range(8)]
        k_ps, q_ps, vb_ps, ssq_ps, x_ps = ps[0:2], ps[2:4], ps[4:6], ps[6], ps[7]

        xin_psum, xp_sig_ready, xp_ready = mem.sem("xin_psum"), mem.sem("xp_sig_ready"), mem.sem("xp_ready")
        k_psum, k_sq_ready, ssq_psum = mem.sem("k_psum"), mem.sem("k_sq_ready"), mem.sem("ssq_psum")
        k_norm_ready, kn_chain = mem.sem("k_norm_ready"), mem.sem("kn_chain")
        q_psum, q_ready = mem.sem("q_psum"), mem.sem("q_ready")
        vb_psum, vb_ready = mem.sem("vb_psum"), mem.sem("vb_ready")
        turned, beta_ready = mem.sem("turned"), mem.sem("beta_ready")
        step_chain, bs_ready, pre_ready = mem.sem("step_chain"), mem.sem("bs_ready"), mem.sem("pre_ready")
        state_ready, s_q_ready, sq_ready = mem.sem("state_ready"), mem.sem("s_q_ready"), mem.sem("sq_ready")
        sq_sig_ready, cell_chain, cell_turned = mem.sem("sq_sig_ready"), mem.sem("cell_chain"), mem.sem("cell_turned")
        out_psum, x_added, cleared = mem.sem("out_psum"), mem.sem("x_added"), mem.sem("cleared")

        src_b = src.rearrange("p (b t) -> p b t", t=T)
        x_t = x.rearrange("p (b t) -> p t b", t=T)

        def repeated(ap):
            return ap.rearrange("p (b t) -> p t b", t=TC).unsqueeze(3).broadcast_to([P, TC, B, IQ])

        def over_rows(ap):
            return ap.unsqueeze(3).broadcast_to([P, HG, N2, IL]).rearrange("p g j i -> p g i j")

        def over_cols(ap):
            return ap.unsqueeze(2).broadcast_to([P, ROWS, N2])

        def by_group(ap):
            return ap.rearrange("p (g i) j -> p g i j", g=HG)

        with nc.Block() as block:

            @block.tensor
            def _(pe):
                with pe.Fori(0, NTC) as c:
                    pe.wait_ge(x_added, c + 1)
                    nc.tensor.matmul(x_ps[:, :].rearrange("p (b t) -> p b t", t=TC), w_in,
                                     src_b[:, :, bass.ds(c * TC, TC)], start=True, stop=True).then_inc(xin_psum, 1)
                    pe.wait_ge(xp_ready, c + 1)
                    for g in range(HG):
                        nc.tensor.matmul(k_ps[g][:, :], w_k[:, g * P:(g + 1) * P], xp[:, :],
                                         start=True, stop=True).then_inc(k_psum, 1)
                    for g in range(HG):
                        nc.tensor.matmul(q_ps[g][:, :], w_q[:, g * P:(g + 1) * P], xp[:, :],
                                         start=True, stop=True).then_inc(q_psum, 1)
                    for n in range(IQ):
                        if n >= 2:
                            pe.wait_ge(vb_ready, IQ * c + n - 1)
                        nc.tensor.matmul(vb_ps[n % 2][:, :], w_vb[:, n, :], xp[:, :],
                                         start=True, stop=True).then_inc(vb_psum, 1)
                    for g in range(HG):
                        pe.wait_ge(k_sq_ready, HG * c + g + 1)
                        if g >= 1:
                            pe.wait_ge(k_norm_ready, HG * c + g)
                        nc.tensor.matmul(ssq_ps[:, :], head_sum, k_sq[:, g, :],
                                         start=True, stop=True).then_inc(ssq_psum, 1)
                    pe.wait_ge(cell_turned, c + 1)
                    for n in range(IQ):
                        last = nc.tensor.matmul(x_ps[:, :], w_out[:, n, :], cell_f[:, :, n],
                                                start=(n == 0), stop=(n == IQ - 1))
                    last.then_inc(out_psum, 1)

            @block.scalar
            def _(act):
                def step(n, u):
                    act.wait_ge(pre_ready, n + 1)
                    nc.scalar.activation(state[:, u, :, :], pre[:, :, :], ACT.Tanh).then_inc(state_ready, 1)

                with act.Fori(0, NTC) as c:
                    act.wait_ge(xin_psum, c + 1)
                    nc.scalar.activation(xp_sig[:, :], x_ps[:, :], ACT.Sigmoid).then_inc(xp_sig_ready, 1)
                    for g in range(HG):
                        act.wait_ge(k_psum, HG * c + g + 1)
                        nc.scalar.activation(k_sq[:, g, :], k_ps[g][:, :], ACT.Square).then_inc(k_sq_ready, 1)
                    for g in range(HG):
                        act.wait_ge(q_psum, HG * c + g + 1)
                        nc.scalar.activation(q_f[:, g, :], q_ps[g][:, :], ACT.Identity).then_inc(q_ready, 1)
                    for n in range(IQ):
                        act.wait_ge(vb_psum, IQ * c + n + 1)
                        nc.scalar.activation(vb_f[:, :, :, n].rearrange("p t b -> p b t"),
                                             vb_ps[n % 2][:, :].rearrange("p (b t) -> p b t", t=TC), ACT.Identity,
                                             bias=b_vb[:, n:n + 1]).then_inc(vb_ready, 1)
                    for g in range(HG):
                        act.wait_ge(ssq_psum, HG * c + g + 1)
                        nc.scalar.activation(k_norm[:, g, :], ssq_ps[:, :], ACT.Sqrt).then_inc(k_norm_ready, 1)
                    act.wait_ge(turned, (2 * HG + 1) * (c + 1))
                    nc.scalar.activation(vb_t[:, :, ROWS:2 * ROWS], vb_t[:, :, ROWS:2 * ROWS],
                                         ACT.Sigmoid).then_inc(beta_ready, 1)
                    with act.Fori(0, TC // 2) as i:
                        for u in range(2):
                            step(c * TC + i * 2 + u, u)
                    act.wait_ge(sq_ready, TC * (c + 1) + 1)
                    nc.scalar.activation(sq_sig[:, :, :], sq[:, :, 0:ROWS], ACT.Sigmoid).then_inc(sq_sig_ready, 1)

            @block.gpsimd
            def _(pool):
                nc.gpsimd.memset(state[:, 1, :, :], 0.0).then_inc(state_ready, 1)
                nc.gpsimd.memset(sq[:, :, ROWS:2 * ROWS], 0.0).then_inc(cleared, 1)

                def step(c, s, u):
                    n = c * TC + s
                    pool.wait_ge(beta_ready, c + 1)
                    pool.wait_ge(state_ready, n + 1)
                    nc.gpsimd.tensor_tensor(beta_s[:, :, :], state[:, 1 - u, :, :],
                                            over_cols(vb_t[:, bass.ds(s, 1), ROWS:2 * ROWS].squeeze(1)),
                                            ALU.mult).then_inc(bs_ready, 1)
                    pool.wait_ge(state_ready, n + 2)
                    pool.wait_ge(sq_ready, n + 1)
                    nc.gpsimd.tensor_tensor(by_group(s_q[:, :, :]), by_group(state[:, u, :, :]),
                                            over_rows(q_t[:, bass.ds(s, 1), :, :].squeeze(1)),
                                            ALU.mult).then_inc(s_q_ready, 1)

                with pool.Fori(0, NTC) as c:
                    with pool.Fori(0, TC // 2) as i:
                        for u in range(2):
                            step(c, i * 2 + u, u)

            @block.vector
            def _(dve):
                dve.sem_inc(x_added, 1)
                dve.sem_inc(sq_ready, 1)
                dve.wait_ge(cleared, 1)

                def step(c, s, u, behind):
                    n = c * TC + s
                    kn = over_rows(kn_t[:, bass.ds(s, 1), :, :].squeeze(1))
                    dve.wait_ge(state_ready, n + 1)
                    nc.vector.tensor_tensor(by_group(s_kn[:, :, :]), by_group(state[:, 1 - u, :, :]), kn,
                                            ALU.mult).then_inc(step_chain, 1)
                    dve.wait_ge(step_chain, 4 * n + 1)
                    nc.vector.tensor_reduce(got[:, :], s_kn[:, :, :], AX_X, ALU.add).then_inc(step_chain, 1)
                    dve.wait_ge(step_chain, 4 * n + 2)
                    nc.vector.tensor_tensor(dlt[:, :], vb_t[:, bass.ds(s, 1), 0:ROWS].squeeze(1), got[:, :],
                                            ALU.subtract).then_inc(step_chain, 1)
                    dve.wait_ge(step_chain, 4 * n + 3)
                    nc.vector.tensor_tensor(by_group(dk[:, :, :]), by_group(over_cols(dlt[:, :])), kn,
                                            ALU.mult).then_inc(step_chain, 1)
                    dve.wait_ge(step_chain, 4 * n + 4)
                    dve.wait_ge(bs_ready, n + 1)
                    nc.vector.tensor_tensor(pre[:, :, :], dk[:, :, :], beta_s[:, :, :], ALU.add).then_inc(pre_ready, 1)
                    if behind:
                        q_sum(c, s - 1)

                def q_sum(c, s):
                    dve.wait_ge(s_q_ready, c * TC + s + 1)
                    nc.vector.tensor_reduce(sq[:, bass.ds(s, 1), 0:ROWS].squeeze(1), s_q[:, :, :], AX_X,
                                            ALU.add).then_inc(sq_ready, 1)

                with dve.Fori(0, NTC) as c:
                    dve.wait_ge(xp_sig_ready, c + 1)
                    nc.vector.tensor_tensor(xp[:, :], xp_sig[:, :], x_ps[:, :], ALU.mult).then_inc(xp_ready, 1)
                    for g in range(HG):
                        dve.wait_ge(q_ready, HG * c + g + 1)
                        nc.vector.transpose(q_t[:, :, g, :], repeated(q_f[:, g, :])).then_inc(turned, 1)
                    dve.wait_ge(vb_ready, IQ * (c + 1))
                    nc.vector.transpose(vb_t[:, :, :], vb_f[:, :, :, :]).then_inc(turned, 1)
                    for g in range(HG):
                        m = HG * c + g
                        dve.wait_ge(k_norm_ready, m + 1)
                        nc.vector.tensor_scalar(k_norm[:, g, :], k_norm[:, g, :], KN_EPS, None,
                                                ALU.add).then_inc(kn_chain, 1)
                        dve.wait_ge(kn_chain, 3 * m + 1)
                        nc.vector.reciprocal(k_sq[:, g, :], k_norm[:, g, :]).then_inc(kn_chain, 1)
                        dve.wait_ge(kn_chain, 3 * m + 2)
                        nc.vector.tensor_tensor(kn_f[:, g, :], k_sq[:, g, :], k_ps[g][:, :],
                                                ALU.mult).then_inc(kn_chain, 1)
                        dve.wait_ge(kn_chain, 3 * m + 3)
                        nc.vector.transpose(kn_t[:, :, g, :], repeated(kn_f[:, g, :])).then_inc(turned, 1)
                    dve.wait_ge(turned, (2 * HG + 1) * (c + 1))
                    step(c, 0, 0, False)
                    step(c, 1, 1, True)
                    with dve.Fori(1, TC // 2) as i:
                        for u in range(2):
                            step(c, i * 2 + u, u, True)
                    q_sum(c, TC - 1)
                    dve.wait_ge(sq_ready, TC * (c + 1) + 1)
                    nc.vector.tensor_tensor(sq_sq[:, :, :], sq[:, :, 0:ROWS], sq[:, :, 0:ROWS],
                                            ALU.mult).then_inc(cell_chain, 1)
                    dve.wait_ge(sq_sig_ready, c + 1)
                    dve.wait_ge(cell_chain, 2 * c + 1)
                    nc.vector.tensor_tensor(sq[:, :, 0:ROWS], sq_sq[:, :, :], sq_sig[:, :, :],
                                            ALU.mult).then_inc(cell_chain, 1)
                    dve.wait_ge(cell_chain, 2 * c + 2)
                    nc.vector.transpose(cell_f.rearrange("p n q -> p (n q)"),
                                        sq[:, :, :].rearrange("p t r -> p (t r)")).then_inc(cell_turned, 1)
                    dve.wait_ge(out_psum, c + 1)
                    out_x = x_t[:, bass.ds(c * TC, TC), :]
                    nc.vector.tensor_tensor(out_x, x_ps[:, :].rearrange("p (t b) -> p t b", b=B), out_x,
                                            ALU.add).then_inc(x_added, 1)


def delta_weights(i):
    def heads(w):
        return w.reshape(HG, 4, IQ, IL, -1)

    vb = np.zeros((IQ, 4, 2, HG, IL, D), np.float32)
    vb[:, :, 0] = heads(i["L2_attn_W_v"]).transpose(2, 1, 0, 3, 4)
    vb[:, :, 1] = heads(i["L2_attn_W_beta"]).transpose(2, 1, 0, 3, 4)
    bias = np.zeros((IQ, 4, 2, HG, IL), np.float32)
    bias[:, :, 1] = heads(i["L2_attn_b_beta"].reshape(-1, 1)).transpose(2, 1, 0, 3, 4)[..., 0]
    out = np.zeros((IQ, 4, 2, HG, IL, D), np.float32)
    out[:, :, 0] = heads(np.ascontiguousarray(i["L2_attn_W_out"].T)).transpose(2, 1, 0, 3, 4)
    return {
        "w_in": i["L2_attn_W_in"].T,
        "w_k": i["L2_attn_W_k"].T,
        "w_q": i["L2_attn_W_q"].T,
        "w_vb": vb.reshape(IQ, P, D).transpose(2, 0, 1),
        "b_vb": bias.reshape(IQ, P).T,
        "w_out": out.reshape(IQ, P, D).transpose(1, 0, 2),
    }
NHEAD, HD = 16, 8
QUAD = 32
NQUAD = 4
RUNS = NHEAD // NQUAD
HALF = T // 2
SPAN = HALF + T
NBLK = 3


def attention_stage(nc, tag, src, x, wq, wk, wv, wo, cos, sin, ident, ident_bf, mask_bf, kv_heads):
    krun = kv_heads // NQUAD
    vc = kv_heads * HD
    scale = float(HD) ** -0.5
    with ExitStack() as stack:
        mem = Memory(nc, stack, tag)
        y = mem.sb("y", [P, T])
        q_cos, q_sin = mem.sb("q_cos", [P, RUNS, T]), mem.sb("q_sin", [P, RUNS, T])
        k_cos, k_sin = mem.sb("k_cos", [P, krun, T]), mem.sb("k_sin", [P, krun, T])
        q, k = mem.sb("q", [P, RUNS, T]), mem.sb("k", [P, krun, T])
        v1 = mem.sb("v1", [P, 2, kv_heads, HD + 1])
        top = mem.sb("top", [P, 2, NQUAD])
        prob = mem.sb("prob", [P, 2, NQUAD * SPAN])
        prob_t = mem.sb("prob_t", [P, 2, NBLK * NQUAD, HALF])
        inv = mem.sb("inv", [P, 2, NHEAD])
        heads = mem.sb("heads", [P, 2, NHEAD * HD])
        heads_t = mem.sb("heads_t", [P, T])
        s_ps = mem.ps("s_ps", [P, NQUAD, CHUNK])
        t_ps = mem.ps("t_ps", [P, NBLK, CHUNK])
        o_ps = mem.ps("o_ps", [P, CHUNK])
        out_heads = o_ps[:, 0:2 * NHEAD * (HD + 1)].rearrange("p (a h e) -> p a h e", a=2, e=HD + 1)
        t_blocks = t_ps[:, :, :].rearrange("p n (m k) -> p (n m) k", k=HALF)
        v_ps = t_ps[:, 0, 0:2 * vc].rearrange("p (a h e) -> p a h e", a=2, e=HD)

        def wide(bank):
            return s_ps[:, bank:bank + 2, :].rearrange("p n (r t) -> p (n r) t", t=T)

        k_wide = [wide(0), wide(2)] if krun > 1 else [t_ps[:, 1, 0:T].unsqueeze(1), t_ps[:, 2, 0:T].unsqueeze(1)]

        y_ready, ones_ready = mem.sem("y_ready"), mem.sem("ones_ready")
        q_psum, q_turned, q_ready = mem.sem("q_psum"), mem.sem("q_turned"), mem.sem("q_ready")
        k_psum, k_turned, k_ready = mem.sem("k_psum"), mem.sem("k_turned"), mem.sem("k_ready")
        v_psum, v_ready = mem.sem("v_psum"), mem.sem("v_ready")
        s_psum, top_ready, s_ready = mem.sem("s_psum"), mem.sem("top_ready"), mem.sem("s_ready")
        p_ready, t_psum, t_ready = mem.sem("p_ready"), mem.sem("t_psum"), mem.sem("t_ready")
        o_psum, inv_ready, o_ready = mem.sem("o_psum"), mem.sem("inv_ready"), mem.sem("o_ready")
        ot_psum, ot_ready = mem.sem("ot_psum"), mem.sem("ot_ready")
        out_psum, x_added = mem.sem("out_psum"), mem.sem("x_added")

        def block_of(half, g, n):
            return g if half == 0 else NQUAD + 2 * g + n

        def span(half):
            return half * NQUAD * HALF, NQUAD * HALF * (half + 1)

        with nc.Block() as block:

            @block.gpsimd
            def _(pool):
                nc.gpsimd.memset(v1[:, :, :, HD:HD + 1], 1.0).then_inc(ones_ready, 1)
                pool.sem_inc(k_psum, 1)
                with pool.Fori(0, B) as b:
                    pool.wait_ge(k_psum, b + 1)
                    nc.gpsimd.tensor_copy(y[:, :], src[:, bass.ds(b * T, T)]).then_inc(y_ready, 1)
                    pool.wait_ge(q_turned, 2 * b + 2)
                    nc.gpsimd.tensor_tensor(q[:, :, :], q_cos[:, :, :], q_sin[:, :, :], ALU.add).then_inc(q_ready, 1)
                    pool.wait_ge(k_turned, 2 * b + 2)
                    nc.gpsimd.tensor_tensor(k[:, :, :], k_cos[:, :, :], k_sin[:, :, :], ALU.add).then_inc(k_ready, 1)

            @block.tensor
            def _(pe):
                def scores(b, r):
                    if r >= 1:
                        pe.wait_ge(s_ready, RUNS * b + r)
                    for half in range(2):
                        keys = (half + 1) * HALF
                        for g in range(NQUAD):
                            quad = slice(QUAD * g, QUAD * (g + 1))
                            nc.tensor.matmul(s_ps[:, g, half * T:half * T + keys],
                                             q[quad, r, half * HALF:(half + 1) * HALF], k[quad, r % krun, 0:keys],
                                             start=True, stop=False)
                        for g in range(NQUAD):
                            last = nc.tensor.matmul(s_ps[:, g, half * (T + HALF):half * (T + HALF) + HALF],
                                                    ident_bf, mask_bf, start=False, stop=True)
                    last.then_inc(s_psum, 1)

                def turns(b, r):
                    pe.wait_ge(p_ready, RUNS * b + r + 1)
                    if r >= 1:
                        pe.wait_ge(t_ready, RUNS * b + r)
                    for n in range(NBLK * NQUAD):
                        last = nc.tensor.transpose(t_blocks[:, n, :], prob[:, r % 2, n * HALF:(n + 1) * HALF], ident)
                    last.then_inc(t_psum, 1)

                def values(b, r):
                    pe.wait_ge(t_ready, RUNS * b + r + 1)
                    for half in range(2):
                        for g in range(NQUAD):
                            hv = g if krun == 1 else NQUAD * g + r
                            for n in range(half + 1):
                                last = nc.tensor.matmul(out_heads[:, half, NQUAD * g + r, :],
                                                        prob_t[:, r % 2, block_of(half, g, n), :], v1[:, n, hv, :],
                                                        start=(n == 0), stop=(n == half))
                    last.then_inc(o_psum, 1)

                with pe.Fori(0, B) as b:
                    pe.wait_ge(y_ready, b + 1)
                    for part in range(2):
                        for r in range(RUNS):
                            last = nc.tensor.matmul(wide(2 * part)[:, r, :], wq[:, part, r, :], y[:, :],
                                                    start=True, stop=True)
                    last.then_inc(q_psum, 1)
                    for n in range(2):
                        last = nc.tensor.matmul(t_ps[:, 0, n * vc:(n + 1) * vc], y[:, n * HALF:(n + 1) * HALF], wv,
                                                start=True, stop=True)
                    last.then_inc(v_psum, 1)
                    if krun > 1:
                        pe.wait_ge(q_turned, 2 * b + 2)
                    pe.wait_ge(x_added, b + 1)
                    for part in range(2):
                        for r in range(krun):
                            last = nc.tensor.matmul(k_wide[part][:, r, :], wk[:, part, r, :], y[:, :],
                                                    start=True, stop=True)
                    last.then_inc(k_psum, 1)
                    pe.wait_ge(q_ready, b + 1)
                    pe.wait_ge(k_ready, b + 1)
                    scores(b, 0)
                    pe.wait_ge(v_ready, b + 1)
                    for r in range(RUNS):
                        if r + 1 < RUNS:
                            scores(b, r + 1)
                        turns(b, r)
                        values(b, r)
                    pe.wait_ge(o_ready, b + 1)
                    for half in range(2):
                        last = nc.tensor.transpose(t_ps[:, 0, half * HALF:(half + 1) * HALF], heads[:, half, :], ident)
                    last.then_inc(ot_psum, 1)
                    pe.wait_ge(ot_ready, b + 1)
                    nc.tensor.matmul(t_ps[:, 1, 0:T], wo, heads_t[:, :], start=True, stop=True).then_inc(out_psum, 1)

            @block.scalar
            def _(act):
                def exps(b, r):
                    act.wait_ge(s_ready, RUNS * b + r + 1)
                    nc.scalar.activation(prob[:, r % 2, :], prob[:, r % 2, :], ACT.Exp, scale=scale).then_inc(p_ready, 1)

                act.wait_ge(ones_ready, 1)
                with act.Fori(0, B) as b:
                    act.wait_ge(v_psum, b + 1)
                    nc.scalar.activation(v1[:, :, :, 0:HD], v_ps, ACT.Identity).then_inc(v_ready, 1)
                    exps(b, 0)
                    for r in range(RUNS):
                        if r + 1 < RUNS:
                            exps(b, r + 1)
                        act.wait_ge(t_psum, RUNS * b + r + 1)
                        nc.scalar.activation(prob_t[:, r % 2, :, :], t_blocks, ACT.Identity).then_inc(t_ready, 1)
                    act.wait_ge(ot_psum, b + 1)
                    nc.scalar.activation(heads_t[:, :], t_ps[:, 0, 0:T], ACT.Identity).then_inc(ot_ready, 1)

            @block.vector
            def _(dve):
                def rotate(ps, table, out, runs, done):
                    nc.vector.tensor_tensor(out, ps, table.unsqueeze(1).broadcast_to([P, runs, T]),
                                            ALU.mult).then_inc(done, 1)

                dve.sem_inc(x_added, 1)
                with dve.Fori(0, B) as b:
                    dve.wait_ge(q_psum, b + 1)
                    rotate(wide(0), cos, q_cos[:, :, :], RUNS, q_turned)
                    rotate(wide(2), sin, q_sin[:, :, :], RUNS, q_turned)
                    dve.wait_ge(k_psum, b + 2)
                    rotate(k_wide[0], cos, k_cos[:, :, :], krun, k_turned)
                    rotate(k_wide[1], sin, k_sin[:, :, :], krun, k_turned)
                    for r in range(RUNS):
                        n = RUNS * b + r
                        dve.wait_ge(s_psum, n + 1)
                        nc.vector.tensor_reduce(top[:, 0, :], s_ps[:, :, 0:HALF], AX_X, ALU.max)
                        nc.vector.tensor_reduce(top[:, 1, :], s_ps[:, :, T:2 * T], AX_X, ALU.max).then_inc(top_ready, 1)
                        dve.wait_ge(top_ready, n + 1)
                        if r >= 2:
                            dve.wait_ge(t_psum, n - 1)
                        for half in range(2):
                            lo, size = span(half)
                            keys = (half + 1) * HALF
                            last = nc.vector.tensor_tensor(
                                prob[:, r % 2, lo:lo + size].rearrange("p (g k) -> p g k", k=keys),
                                s_ps[:, :, half * T:half * T + keys],
                                top[:, half, :].unsqueeze(2).broadcast_to([P, NQUAD, keys]), ALU.subtract)
                        last.then_inc(s_ready, 1)
                    dve.wait_ge(o_psum, RUNS * (b + 1))
                    nc.vector.reciprocal(inv[:, :, :], out_heads[:, :, :, HD]).then_inc(inv_ready, 1)
                    dve.wait_ge(inv_ready, b + 1)
                    nc.vector.tensor_tensor(heads[:, :, :].rearrange("p a (h e) -> p a h e", e=HD),
                                            out_heads[:, :, :, 0:HD],
                                            inv[:, :, :].unsqueeze(3).broadcast_to([P, 2, NHEAD, HD]),
                                            ALU.mult).then_inc(o_ready, 1)
                    dve.wait_ge(out_psum, b + 1)
                    here = x[:, bass.ds(b * T, T)]
                    nc.vector.tensor_tensor(here, t_ps[:, 1, 0:T], here, ALU.add).then_inc(x_added, 1)


def cond_gate_stage(nc, tag, x, dst, cond, w1, b1, w2, b2):
    with ExitStack() as stack:
        mem = Memory(nc, stack, tag)
        ps = mem.ps("ps", [P, 2, B])
        z, sig, h, gate = (mem.sb(n, [P, B]) for n in ("z", "sig", "h", "gate"))
        z_psum, sig_ready, z_ready, h_ready = (mem.sem(n) for n in ("z_psum", "sig_ready", "z_ready", "h_ready"))
        gate_psum, gate_ready, factor_ready, done = (mem.sem(n) for n in ("gate_psum", "gate_ready", "factor_ready", "done"))
        with nc.Block() as block:

            @block.tensor
            def _(pe):
                nc.tensor.matmul(ps[:, 0, :], w1, cond, start=True, stop=True).then_inc(z_psum, 1)
                pe.wait_ge(h_ready, 1)
                nc.tensor.matmul(ps[:, 1, :], w2, h[:, :], start=True, stop=True).then_inc(gate_psum, 1)

            @block.scalar
            def _(act):
                act.wait_ge(z_psum, 1)
                nc.scalar.activation(sig[:, :], ps[:, 0, :], ACT.Sigmoid, bias=b1).then_inc(sig_ready, 1)
                act.wait_ge(gate_psum, 1)
                nc.scalar.activation(gate[:, :], ps[:, 1, :], ACT.Sigmoid, bias=b2).then_inc(gate_ready, 1)

            @block.vector
            def _(dve):
                dve.wait_ge(sig_ready, 1)
                nc.vector.tensor_scalar(z[:, :], ps[:, 0, :], b1, None, ALU.add).then_inc(z_ready, 1)
                dve.wait_ge(z_ready, 1)
                nc.vector.tensor_tensor(h[:, :], z[:, :], sig[:, :], ALU.mult).then_inc(h_ready, 1)
                dve.wait_ge(gate_ready, 1)
                nc.vector.tensor_scalar(sig[:, :], gate[:, :], 1.0, None, ALU.add).then_inc(factor_ready, 1)
                dve.wait_ge(factor_ready, 1)
                nc.vector.tensor_tensor(dst.rearrange("p (b t) -> p b t", t=T), x.rearrange("p (b t) -> p b t", t=T),
                                        sig[:, :].unsqueeze(2).broadcast_to([P, B, T]), ALU.mult).then_inc(done, 1)


def attention_weights(w, heads, rotated):
    runs = heads // NQUAD
    cols = w.reshape(D, NQUAD, runs, HD)
    out = np.zeros((D, 2 if rotated else 1, runs, NQUAD, QUAD), np.float32)
    out[:, 0, :, :, :HD] = cols.transpose(0, 2, 1, 3)
    if rotated:
        half = HD // 2
        out[:, 1, :, :, :HD] = np.concatenate([cols[..., half:], cols[..., :half]], -1).transpose(0, 2, 1, 3)
    return out.reshape(D, -1, runs, P)


def rope_tables(repeat):
    half = HD // 2
    freq = (1.0 / 10000.0 ** (np.arange(half, dtype=np.float32) / half)).astype(np.float32)
    angle = np.arange(T, dtype=np.float32)[:, None] * freq[None, :]
    dims = np.repeat(np.arange(half), 2) if repeat else np.tile(np.arange(half), 2)
    sign = np.where(np.arange(HD) < half, -1.0, 1.0)
    cos, sin = np.zeros((2, NQUAD, QUAD, T), np.float32)
    cos[:, :HD] = np.cos(angle).T[dims]
    sin[:, :HD] = np.sin(angle).T[dims] * sign[:, None]
    return cos.reshape(P, T), sin.reshape(P, T)
NEXP = 8
TILES = CHUNK // P
FAR = 3.0e38
MAGIC = 1.5 * 2.0 ** 23


def over_experts(ap):
    return ap.unsqueeze(2).broadcast_to([P, TILES, NEXP])


def over_tiles(ap):
    return ap.unsqueeze(1).broadcast_to([P, TILES, NEXP])


def top2(nc, dve, score, rank, buf, one, picked, chain, at):
    best, buf2 = one
    for n in range(2):
        k = at + 5 * n
        hit = picked if n == 0 else buf2
        nc.vector.tensor_reduce(best, score, AX_X, ALU.max).then_inc(chain, 1)
        dve.wait_ge(chain, k + 1)
        nc.vector.tensor_tensor(buf, score, over_experts(best), ALU.is_equal).then_inc(chain, 1)
        dve.wait_ge(chain, k + 2)
        nc.vector.tensor_tensor(buf, buf, over_tiles(rank), ALU.mult).then_inc(chain, 1)
        dve.wait_ge(chain, k + 3)
        nc.vector.tensor_reduce(best, buf, AX_X, ALU.max).then_inc(chain, 1)
        dve.wait_ge(chain, k + 4)
        last = nc.vector.tensor_tensor(hit, buf, over_experts(best), ALU.is_equal)
        if n == 0:
            last.then_inc(chain, 1)
            dve.wait_ge(chain, k + 5)
            nc.vector.scalar_tensor_tensor(score, picked, -FAR, score, ALU.mult, ALU.add).then_inc(chain, 1)
            at += 1
            dve.wait_ge(chain, k + 6)
        else:
            last.then_inc(chain, 1)
            dve.wait_ge(chain, k + 5)
            nc.vector.tensor_tensor(picked, picked, buf2, ALU.add).then_inc(chain, 1)


TOP2_OPS = 12


def expert_stage(nc, tag, src, x, router, w_gate, b_gate, w_up, b_up, w_down, b_down, rank, ident):
    glu = w_up is not None
    with ExitStack() as stack:
        mem = Memory(nc, stack, tag)
        y = mem.sb("y", [P, CHUNK])
        small = {n: mem.sb(n, [P, TILES, NEXP]) for n in ("prob", "buf", "buf2", "picked", "share", "score")}
        best, norm = mem.sb("best", [P, TILES]), mem.sb("norm", [P, TILES])
        prob, buf, buf2, picked, share, score = (small[n][:, :, :] for n in small)
        share_t = mem.sb("share_t", [NEXP, CHUNK])
        sig, part = mem.sb("sig", [P, 2, CHUNK]), mem.sb("part", [P, 2, CHUNK])
        hidden = mem.sb("hidden", [P, 2, 2, CHUNK])
        acc = mem.sb("acc", [P, TILES, P])
        h_ps = mem.ps("h_ps", [P, 4, CHUNK])
        out_ps = mem.ps("out_ps", [P, 2, TILES, P])
        log_ps, turn_ps = mem.ps("log_ps", [P, CHUNK]), mem.ps("turn_ps", [P, CHUNK])
        logits = log_ps[:, 0:TILES * NEXP].rearrange("p (a e) -> p a e", e=NEXP)
        names = ("y_ready", "log_psum", "chain", "exp_in", "exp_ready", "share_ready", "share_psum", "share_t_ready",
                 "bias_psum", "bias_ready", "h_psum", "sig_ready", "part_ready", "h_ready", "out_psum", "acc_ready",
                 "turn_psum", "x_added")
        s = {n: mem.sem(n) for n in names}
        ROUTE = 5 + TOP2_OPS + (5 if glu else 1)

        with nc.Block() as block:

            @block.gpsimd
            def _(pool):
                pool.sem_inc(s["turn_psum"], 1)
                with pool.Fori(0, NCHUNK) as c:
                    pool.wait_ge(s["turn_psum"], c + 1)
                    nc.gpsimd.tensor_copy(y[:, :], src[:, bass.ds(c * CHUNK, CHUNK)]).then_inc(s["y_ready"], 1)

            @block.tensor
            def _(pe):
                def first_layer(c, e):
                    for n in range(2):
                        unit = 2 * NEXP * c + 2 * e + n
                        if glu:
                            pe.wait_ge(s["h_ready"], unit + 1)
                            nc.tensor.matmul(h_ps[:, 2 * n, :], w_gate[:, e, n * P:(n + 1) * P], y[:, :],
                                             start=True, stop=True)
                            nc.tensor.matmul(h_ps[:, 2 * n + 1, :], w_up[:, e, n * P:(n + 1) * P], y[:, :],
                                             start=True, stop=True).then_inc(s["h_psum"], 1)
                        else:
                            if e >= 2:
                                pe.wait_ge(s["h_ready"], unit - 1)
                            nc.tensor.matmul(h_ps[:, 2 * (e % 2) + n, :], w_gate[:, e, n * P:(n + 1) * P], y[:, :],
                                             start=True, stop=True).then_inc(s["h_psum"], 1)

                def second_layer(c, e):
                    pe.wait_ge(s["h_ready"], 2 * NEXP * c + 2 * e + (4 if glu else 2))
                    if e >= 2:
                        pe.wait_ge(s["acc_ready"], TILES * (NEXP * c + e - 1))
                    for a in range(TILES):
                        for n in range(2):
                            last = nc.tensor.matmul(out_ps[:, e % 2, a, :], hidden[:, e % 2, n, a * P:(a + 1) * P],
                                                    w_down[:, e, n, :], start=(n == 0), stop=(n == 1))
                    last.then_inc(s["out_psum"], 1)

                with pe.Fori(0, NCHUNK) as c:
                    pe.wait_ge(s["y_ready"], c + 1)
                    for a in range(TILES):
                        last = nc.tensor.matmul(logits[:, a, :], y[:, a * P:(a + 1) * P], router, start=True, stop=True)
                    last.then_inc(s["log_psum"], 1)
                    first_layer(c, 0)
                    first_layer(c, 1) if not glu else None
                    pe.wait_ge(s["share_ready"], c + 1)
                    pe.wait_ge(s["x_added"], c + 1)
                    for a in range(TILES):
                        last = nc.tensor.transpose(turn_ps[0:NEXP, a * P:(a + 1) * P], share[:, a, :], ident)
                    last.then_inc(s["share_psum"], 1)
                    pe.wait_ge(s["share_t_ready"], c + 1)
                    for a in range(TILES):
                        last = nc.tensor.matmul(log_ps[:, a * P:(a + 1) * P], share_t[:, a * P:(a + 1) * P], b_down,
                                                start=True, stop=True)
                    last.then_inc(s["bias_psum"], 1)
                    for e in range(NEXP):
                        if glu and e + 1 < NEXP:
                            first_layer(c, e + 1)
                        second_layer(c, e)
                        if not glu and e + 2 < NEXP:
                            first_layer(c, e + 2)
                    pe.wait_ge(s["acc_ready"], TILES * NEXP * (c + 1))
                    for a in range(TILES):
                        last = nc.tensor.transpose(turn_ps[:, a * P:(a + 1) * P], acc[:, a, :], ident)
                    last.then_inc(s["turn_psum"], 1)

            @block.scalar
            def _(act):
                with act.Fori(0, NCHUNK) as c:
                    act.wait_ge(s["exp_in"], c + 1)
                    nc.scalar.activation(prob, score, ACT.Exp).then_inc(s["exp_ready"], 1)
                    for e in range(NEXP):
                        for n in range(2):
                            unit = 2 * NEXP * c + 2 * e + n
                            act.wait_ge(s["h_psum"], unit + 1)
                            if glu:
                                nc.scalar.activation(sig[:, n, :], h_ps[:, 2 * n, :], ACT.Sigmoid,
                                                     bias=b_gate[:, e, n:n + 1]).then_inc(s["sig_ready"], 1)
                            else:
                                if e >= 2:
                                    act.wait_ge(s["out_psum"], NEXP * c + e - 1)
                                nc.scalar.activation(hidden[:, e % 2, n, :], h_ps[:, 2 * (e % 2) + n, :], ACT.Relu,
                                                     bias=b_gate[:, e, n:n + 1]).then_inc(s["h_ready"], 1)

            @block.vector
            def _(dve):
                dve.sem_inc(s["x_added"], 1)
                if glu:
                    dve.sem_inc(s["h_ready"], 2)
                chain = s["chain"]

                def route(c):
                    at = ROUTE * c
                    dve.wait_ge(s["log_psum"], c + 1)
                    nc.vector.tensor_reduce(best[:, :], logits, AX_X, ALU.max).then_inc(chain, 1)
                    dve.wait_ge(chain, at + 1)
                    nc.vector.tensor_tensor(score, logits, over_experts(best[:, :]), ALU.subtract).then_inc(s["exp_in"], 1)
                    dve.wait_ge(s["exp_ready"], c + 1)
                    nc.vector.tensor_reduce(norm[:, :], prob, AX_X, ALU.add).then_inc(chain, 1)
                    dve.wait_ge(chain, at + 2)
                    nc.vector.reciprocal(best[:, :], norm[:, :]).then_inc(chain, 1)
                    dve.wait_ge(chain, at + 3)
                    nc.vector.tensor_tensor(prob, prob, over_experts(best[:, :]), ALU.mult).then_inc(chain, 1)
                    dve.wait_ge(chain, at + 4)
                    nc.vector.tensor_copy(score, prob).then_inc(chain, 1)
                    dve.wait_ge(chain, at + 5)
                    top2(nc, dve, score, rank, buf, (best[:, :], buf2), picked, chain, at + 5)
                    at = at + 5 + TOP2_OPS
                    dve.wait_ge(chain, at)
                    if glu:
                        nc.vector.tensor_tensor(buf, prob, picked, ALU.mult).then_inc(chain, 1)
                        dve.wait_ge(chain, at + 1)
                        nc.vector.tensor_reduce(norm[:, :], buf, AX_X, ALU.add).then_inc(chain, 1)
                        dve.wait_ge(chain, at + 2)
                        nc.vector.tensor_scalar(norm[:, :], norm[:, :], 1e-9, None, ALU.add).then_inc(chain, 1)
                        dve.wait_ge(chain, at + 3)
                        nc.vector.reciprocal(best[:, :], norm[:, :]).then_inc(chain, 1)
                        dve.wait_ge(chain, at + 4)
                        nc.vector.tensor_tensor(share, buf, over_experts(best[:, :]), ALU.mult).then_inc(s["share_ready"], 1)
                        nc.vector.sem_inc(chain, 1)
                    else:
                        nc.vector.tensor_tensor(share, prob, picked, ALU.mult).then_inc(s["share_ready"], 1)
                        nc.vector.sem_inc(chain, 1)
                    dve.wait_ge(s["share_psum"], c + 1)
                    nc.vector.tensor_copy(share_t[:, :], turn_ps[0:NEXP, :]).then_inc(s["share_t_ready"], 1)
                    dve.wait_ge(s["bias_psum"], c + 1)
                    nc.vector.tensor_copy(acc[:, :, :].rearrange("p a d -> p (a d)"), log_ps[:, :]).then_inc(s["bias_ready"], 1)

                def hidden_layer(c, e):
                    for n in range(2):
                        unit = 2 * NEXP * c + 2 * e + n
                        dve.wait_ge(s["sig_ready"], unit + 1)
                        nc.vector.scalar_tensor_tensor(part[:, n, :], h_ps[:, 2 * n, :], b_gate[:, e, n:n + 1],
                                                       sig[:, n, :], ALU.add, ALU.mult).then_inc(s["part_ready"], 1)
                        dve.wait_ge(s["part_ready"], unit + 1)
                        if e >= 2:
                            dve.wait_ge(s["out_psum"], NEXP * c + e - 1)
                        nc.vector.scalar_tensor_tensor(hidden[:, e % 2, n, :], h_ps[:, 2 * n + 1, :],
                                                       b_up[:, e, n:n + 1], part[:, n, :], ALU.add,
                                                       ALU.mult).then_inc(s["h_ready"], 1)

                def add_expert(c, e):
                    dve.wait_ge(s["out_psum"], NEXP * c + e + 1)
                    if e == 0:
                        dve.wait_ge(s["bias_ready"], c + 1)
                    else:
                        dve.wait_ge(s["acc_ready"], TILES * (NEXP * c + e))
                    for a in range(TILES):
                        nc.vector.scalar_tensor_tensor(acc[:, a, :], out_ps[:, e % 2, a, :], share[:, a, e:e + 1],
                                                       acc[:, a, :], ALU.mult, ALU.add).then_inc(s["acc_ready"], 1)

                with dve.Fori(0, NCHUNK) as c:
                    route(c)
                    if glu:
                        hidden_layer(c, 0)
                    for e in range(NEXP):
                        if glu and e + 1 < NEXP:
                            hidden_layer(c, e + 1)
                        add_expert(c, e)
                    dve.wait_ge(s["turn_psum"], c + 2)
                    here = x[:, bass.ds(c * CHUNK, CHUNK)]
                    nc.vector.tensor_tensor(here, turn_ps[:, :], here, ALU.add).then_inc(s["x_added"], 1)


def routed_cond_stage(nc, tag, src, dst, cond, router, router_t, router_bias, sw1, sw3, sw2, rw1, rw2, rank, ones, ident):
    with ExitStack() as stack:
        mem = Memory(nc, stack, tag)
        cond_w = mem.sb("cond_w", [P, B, NEXP])
        t_bias = mem.sb("t_bias", [P, B, NEXP])
        y = mem.sb("y", [P, CHUNK])
        small = {n: mem.sb(n, [P, TILES, NEXP]) for n in ("prob", "buf", "buf2", "picked", "share", "score")}
        prob, buf, buf2, picked, share, score = (small[n][:, :, :] for n in small)
        best, norm, have, even = (mem.sb(n, [P, TILES]) for n in ("best", "norm", "have", "even"))
        sig, part = mem.sb("sig", [P, 2, CHUNK]), mem.sb("part", [P, 2, CHUNK])
        shared = mem.sb("shared", [P, 2, CHUNK])
        routed = mem.sb("routed", [P, NEXP // 2, CHUNK])
        acc = mem.sb("acc", [P, TILES, P])
        h_ps = mem.ps("h_ps", [P, 4, CHUNK])
        out_ps = mem.ps("out_ps", [P, 2, TILES, P])
        log_ps, turn_ps = mem.ps("log_ps", [P, CHUNK]), mem.ps("turn_ps", [P, CHUNK])
        logits = log_ps[:, 0:TILES * NEXP].rearrange("p (a e) -> p a e", e=NEXP)
        names = ("cond_w_ready", "t_psum", "t_bias_ready", "y_ready", "log_psum", "chain", "score_in", "prob_ready",
                 "s_psum", "sig_ready", "part_ready", "shared_ready", "r_psum", "routed_ready", "out_psum", "acc_ready",
                 "turn_psum", "dst_ready")
        s = {n: mem.sem(n) for n in names}
        ROUTE = TOP2_OPS + 9

        with nc.Block() as block:

            @block.gpsimd
            def _(pool):
                pool.sem_inc(s["turn_psum"], 1)
                with pool.Fori(0, NCHUNK) as c:
                    pool.wait_ge(s["turn_psum"], c + 1)
                    nc.gpsimd.tensor_copy(y[:, :], src[:, bass.ds(c * CHUNK, CHUNK)]).then_inc(s["y_ready"], 1)

            @block.tensor
            def _(pe):
                pe.wait_ge(s["cond_w_ready"], 1)
                nc.tensor.matmul(log_ps[:, 0:B * NEXP], ones, cond_w[:, :, :], start=True, stop=True).then_inc(s["t_psum"], 1)
                pe.wait_ge(s["t_bias_ready"], 1)
                with pe.Fori(0, NCHUNK) as c:
                    pe.wait_ge(s["y_ready"], c + 1)
                    for a in range(TILES):
                        last = nc.tensor.matmul(logits[:, a, :], y[:, a * P:(a + 1) * P], router, start=True, stop=True)
                    last.then_inc(s["log_psum"], 1)
                    for n in range(2):
                        nc.tensor.matmul(h_ps[:, 2 * n, :], sw1[:, n * P:(n + 1) * P], y[:, :], start=True, stop=True)
                        nc.tensor.matmul(h_ps[:, 2 * n + 1, :], sw3[:, n * P:(n + 1) * P], y[:, :],
                                         start=True, stop=True).then_inc(s["s_psum"], 1)
                    pe.wait_ge(s["shared_ready"], 2 * c + 2)
                    for m in range(NEXP // 2):
                        nc.tensor.matmul(h_ps[:, m, :], rw1[:, m * P:(m + 1) * P], y[:, :],
                                         start=True, stop=True).then_inc(s["r_psum"], 1)
                    for a in range(TILES):
                        for n in range(2):
                            last = nc.tensor.matmul(out_ps[:, 0, a, :], shared[:, n, a * P:(a + 1) * P], sw2[:, n, :],
                                                    start=(n == 0), stop=(n == 1))
                    last.then_inc(s["out_psum"], 1)
                    for e in range(NEXP):
                        k = (NEXP + 1) * c + e + 1
                        rows = slice(P // 2 * (e % 2), P // 2 * (e % 2 + 1))
                        pe.wait_ge(s["routed_ready"], NEXP // 2 * c + e // 2 + 1)
                        if e >= 1:
                            pe.wait_ge(s["acc_ready"], TILES * (k - 1))
                        for a in range(TILES):
                            last = nc.tensor.matmul(out_ps[:, (e + 1) % 2, a, :], routed[rows, e // 2, a * P:(a + 1) * P],
                                                    rw2[rows, e // 2, :], start=True, stop=True)
                        last.then_inc(s["out_psum"], 1)
                    pe.wait_ge(s["acc_ready"], TILES * (NEXP + 1) * (c + 1))
                    for a in range(TILES):
                        last = nc.tensor.transpose(turn_ps[:, a * P:(a + 1) * P], acc[:, a, :], ident)
                    last.then_inc(s["turn_psum"], 1)

            @block.scalar
            def _(act):
                with act.Fori(0, NCHUNK) as c:
                    act.wait_ge(s["score_in"], c + 1)
                    nc.scalar.activation(prob, score, ACT.Sigmoid).then_inc(s["prob_ready"], 1)
                    for n in range(2):
                        act.wait_ge(s["s_psum"], 2 * c + n + 1)
                        nc.scalar.activation(sig[:, n, :], h_ps[:, 2 * n, :], ACT.Sigmoid).then_inc(s["sig_ready"], 1)
                    for m in range(NEXP // 2):
                        act.wait_ge(s["r_psum"], NEXP // 2 * c + m + 1)
                        nc.scalar.activation(routed[:, m, :], h_ps[:, m, :], ACT.Gelu).then_inc(s["routed_ready"], 1)
                    act.wait_ge(s["turn_psum"], c + 2)
                    nc.scalar.activation(dst[:, bass.ds(c * CHUNK, CHUNK)], turn_ps[:, :], ACT.Identity,
                                         scale=1.0 / 3.0).then_inc(s["dst_ready"], 1)

            @block.vector
            def _(dve):
                chain = s["chain"]
                nc.vector.tensor_tensor(cond_w[:, :, :], cond.unsqueeze(2).broadcast_to([P, B, NEXP]),
                                        router_t.unsqueeze(1).broadcast_to([P, B, NEXP]), ALU.mult).then_inc(s["cond_w_ready"], 1)
                dve.wait_ge(s["t_psum"], 1)
                nc.vector.tensor_copy(t_bias[:, :, :].rearrange("p b e -> p (b e)"),
                                      log_ps[:, 0:B * NEXP]).then_inc(s["t_bias_ready"], 1)
                dve.wait_ge(s["t_bias_ready"], 1)
                SEQS = CHUNK // T

                def route(c):
                    at = ROUTE * c
                    dve.wait_ge(s["log_psum"], c + 1)
                    for q in range(SEQS):
                        half = slice(q * TILES // SEQS, (q + 1) * TILES // SEQS)
                        last = nc.vector.tensor_tensor(score[:, half, :], logits[:, half, :],
                                                       t_bias[:, bass.ds(c * SEQS + q, 1), :].broadcast_to(
                                                           [P, TILES // SEQS, NEXP]), ALU.add)
                    last.then_inc(s["score_in"], 1)
                    dve.wait_ge(s["prob_ready"], c + 1)
                    nc.vector.tensor_tensor(score, prob, over_tiles(router_bias), ALU.add).then_inc(chain, 1)
                    dve.wait_ge(chain, at + 1)
                    top2(nc, dve, score, rank, buf, (best[:, :], buf2), picked, chain, at + 1)
                    at = at + 1 + TOP2_OPS
                    dve.wait_ge(chain, at)
                    nc.vector.tensor_tensor(buf, prob, picked, ALU.mult).then_inc(chain, 1)
                    dve.wait_ge(chain, at + 1)
                    nc.vector.tensor_reduce(norm[:, :], buf, AX_X, ALU.add).then_inc(chain, 1)
                    dve.wait_ge(chain, at + 2)
                    nc.vector.tensor_scalar(have[:, :], norm[:, :], 1e-9, None, ALU.is_gt).then_inc(chain, 1)
                    nc.vector.tensor_scalar(norm[:, :], norm[:, :], 1e-9, None, ALU.add).then_inc(chain, 1)
                    dve.wait_ge(chain, at + 4)
                    nc.vector.reciprocal(best[:, :], norm[:, :]).then_inc(chain, 1)
                    nc.vector.tensor_scalar(even[:, :], have[:, :], -0.5, 0.5, ALU.mult, ALU.add).then_inc(chain, 1)
                    dve.wait_ge(chain, at + 6)
                    nc.vector.tensor_tensor(norm[:, :], best[:, :], have[:, :], ALU.mult)
                    nc.vector.tensor_tensor(buf2, picked, over_experts(even[:, :]), ALU.mult).then_inc(chain, 1)
                    dve.wait_ge(chain, at + 7)
                    nc.vector.tensor_tensor(buf, buf, over_experts(norm[:, :]), ALU.mult).then_inc(chain, 1)
                    dve.wait_ge(chain, at + 8)
                    nc.vector.tensor_tensor(share, buf, buf2, ALU.add)

                with dve.Fori(0, NCHUNK) as c:
                    route(c)
                    for n in range(2):
                        m = 2 * c + n
                        dve.wait_ge(s["sig_ready"], m + 1)
                        nc.vector.tensor_tensor(part[:, n, :], h_ps[:, 2 * n, :], sig[:, n, :], ALU.mult).then_inc(s["part_ready"], 1)
                        dve.wait_ge(s["part_ready"], m + 1)
                        nc.vector.tensor_tensor(shared[:, n, :], h_ps[:, 2 * n + 1, :], part[:, n, :],
                                                ALU.mult).then_inc(s["shared_ready"], 1)
                    dve.wait_ge(s["out_psum"], (NEXP + 1) * c + 1)
                    nc.vector.tensor_copy(acc[:, :, :], out_ps[:, 0, :, :]).then_inc(s["acc_ready"], TILES)
                    for e in range(NEXP):
                        k = (NEXP + 1) * c + e + 1
                        dve.wait_ge(s["out_psum"], k + 1)
                        dve.wait_ge(s["acc_ready"], TILES * k)
                        for a in range(TILES):
                            nc.vector.scalar_tensor_tensor(acc[:, a, :], out_ps[:, (e + 1) % 2, a, :], share[:, a, e:e + 1],
                                                           acc[:, a, :], ALU.mult, ALU.add).then_inc(s["acc_ready"], 1)


def ternary_stage(nc, tag, src, x, w, bias):
    with ExitStack() as stack:
        mem = Memory(nc, stack, tag)
        most, size = mem.sb("most", [P, 1]), mem.sb("size", [P, 1])
        most_all, size_all = mem.sb("most_all", [P, 1]), mem.sb("size_all", [P, 1])
        step, inv, over, under, back = (mem.sb(n, [P, 1]) for n in ("step", "inv", "over", "under", "back"))
        below = mem.sb("below", [P, P])
        wq = mem.sb("wq", [P, P], BF16)
        num = mem.sb("num", [P, TOK])
        xq = mem.sb("xq", [P, TOK], BF16)
        out = mem.sb("out", [P, 2, CHUNK])
        ps = mem.ps("ps", [P, NCHUNK, CHUNK])
        sizes_ready, all_ready, chain = mem.sem("sizes_ready"), mem.sem("all_ready"), mem.sem("chain")
        out_psum, out_ready, x_added = mem.sem("out_psum"), mem.sem("out_ready"), mem.sem("x_added")

        with nc.Block() as block:

            @block.gpsimd
            def _(pool):
                pool.wait_ge(sizes_ready, 2)
                nc.gpsimd.partition_all_reduce(most_all[:, :], most[:, :], P, RMAX).then_inc(all_ready, 1)
                nc.gpsimd.partition_all_reduce(size_all[:, :], size[:, :], P, RADD).then_inc(all_ready, 1)

            @block.vector
            def _(dve):
                nc.vector.tensor_reduce(most[:, :], src, AX_X, ALU.max, apply_absolute_value=True).then_inc(sizes_ready, 1)
                nc.vector.tensor_reduce(size[:, :], w, AX_X, ALU.add, apply_absolute_value=True).then_inc(sizes_ready, 1)
                dve.wait_ge(all_ready, 2)
                nc.vector.tensor_scalar(step[:, :], most_all[:, :], 1.0 / 127.0, None, ALU.mult).then_inc(chain, 1)
                nc.vector.tensor_scalar(over[:, :], size_all[:, :], 0.5 / (P * P), None, ALU.mult).then_inc(chain, 1)
                nc.vector.tensor_scalar(under[:, :], size_all[:, :], -0.5 / (P * P), None, ALU.mult).then_inc(chain, 1)
                dve.wait_ge(chain, 3)
                nc.vector.reciprocal(inv[:, :], step[:, :]).then_inc(chain, 1)
                nc.vector.tensor_scalar(below[:, :], w, under[:, 0:1], None, ALU.is_lt).then_inc(chain, 1)
                nc.vector.scalar_tensor_tensor(back[:, :], over[:, :], 2.0, step[:, :], ALU.mult, ALU.mult).then_inc(chain, 1)
                dve.wait_ge(chain, 6)
                nc.vector.scalar_tensor_tensor(wq[:, :], w, over[:, 0:1], below[:, :], ALU.is_gt,
                                               ALU.subtract).then_inc(chain, 1)
                nc.vector.tensor_scalar(num[:, :], src, inv[:, 0:1], MAGIC, ALU.mult, ALU.add).then_inc(chain, 1)
                dve.wait_ge(chain, 8)
                nc.vector.tensor_scalar(num[:, :], num[:, :], MAGIC, 127.0, ALU.subtract, ALU.min).then_inc(chain, 1)
                dve.wait_ge(chain, 9)
                nc.vector.tensor_scalar(xq[:, :], num[:, :], -128.0, None, ALU.max).then_inc(chain, 1)
                for c in range(NCHUNK):
                    dve.wait_ge(out_psum, c + 1)
                    if c >= 2:
                        dve.wait_ge(x_added, c - 1)
                    nc.vector.tensor_scalar(out[:, c % 2, :], ps[:, c, :], back[:, 0:1], bias, ALU.mult,
                                            ALU.add).then_inc(out_ready, 1)
                    dve.wait_ge(out_ready, c + 1)
                    here = x[:, c * CHUNK:(c + 1) * CHUNK]
                    nc.vector.tensor_tensor(here, out[:, c % 2, :], here, ALU.add).then_inc(x_added, 1)

            @block.tensor
            def _(pe):
                pe.wait_ge(chain, 10)
                for c in range(NCHUNK):
                    nc.tensor.matmul(ps[:, c, :], wq[:, :], xq[:, c * CHUNK:(c + 1) * CHUNK],
                                     start=True, stop=True).then_inc(out_psum, 1)


BIT_INNER = 512
BIT_BLOCKS = BIT_INNER // P


def bit_ffn_stage(nc, tag, src, x, w, ident, ident_bf):
    with ExitStack() as stack:
        mem = Memory(nc, stack, tag)
        size, size_all, mean, winv = (mem.sb(n, [P, 3]) for n in ("size", "size_all", "mean", "winv"))
        wnum = mem.sb("wnum", [P, 3, BIT_INNER])
        wq = mem.sb("wq", [P, 3, BIT_INNER], BF16)
        y = mem.sb("y", [P, 2, P])
        top = mem.sb("top", [P, 2, 1])
        inv, quant = mem.sb("inv", [P, 2, 1]), mem.sb("quant", [P, 2, 1])
        back = mem.sb("back", [P, 3])
        num = mem.sb("num", [P, P])
        yq, yq_t = mem.sb("yq", [P, P], BF16), mem.sb("yq_t", [P, P], BF16)
        sig, act_gate = mem.sb("sig", [P, BIT_INNER]), mem.sb("act_gate", [P, BIT_INNER])
        prod, pnum = mem.sb("prod", [P, BIT_INNER]), mem.sb("pnum", [P, BIT_INNER])
        pq = mem.sb("pq", [P, BIT_INNER], BF16)
        pq_t = mem.sb("pq_t", [P, BIT_BLOCKS, P], BF16)
        out = mem.sb("out", [P, P])
        y_ps = mem.ps("y_ps", [P, CHUNK])
        yq_ps = mem.ps("yq_ps", [P, 2 * CHUNK], BF16)
        gate_ps, up_ps = mem.ps("gate_ps", [P, CHUNK]), mem.ps("up_ps", [P, CHUNK])
        pq_ps = mem.ps("pq_ps", [P, 2 * CHUNK], BF16)
        out_ps, turn_ps = mem.ps("out_ps", [P, CHUNK]), mem.ps("turn_ps", [P, CHUNK])
        pq_blocks = pq_ps[:, 0:BIT_INNER].rearrange("p (n k) -> p n k", k=P)
        names = ("size_ready", "all_ready", "wchain", "y_ready", "y_psum", "chain", "yq_ready", "yq_psum", "yq_t_ready",
                 "gate_psum", "up_psum", "sig_ready", "pq_ready", "pq_psum", "pq_t_ready", "out_psum", "out_ready", "turn_psum",
                 "x_added")
        s = {n: mem.sem(n) for n in names}
        STEPS = 14
        NT = TOK // P

        with nc.Block() as block:

            @block.gpsimd
            def _(pool):
                pool.wait_ge(s["size_ready"], 1)
                nc.gpsimd.partition_all_reduce(size_all[:, :], size[:, :], P, RADD).then_inc(s["all_ready"], 1)
                pool.sem_inc(s["y_psum"], 2)
                with pool.Fori(0, NT // 2) as i:
                    for u in range(2):
                        n = i * 2 + u
                        pool.wait_ge(s["y_psum"], n + 1)
                        nc.gpsimd.tensor_copy(y[:, u, :], src[:, bass.ds(n * P, P)]).then_inc(s["y_ready"], 1)

            @block.tensor
            def _(pe):
                with pe.Fori(0, NT // 2) as i:
                    for u in range(2):
                        n = i * 2 + u
                        pe.wait_ge(s["y_ready"], n + 1)
                        pe.wait_ge(s["yq_ready"], n + 1)
                        nc.tensor.transpose(y_ps[:, 0:P], y[:, u, :], ident).then_inc(s["y_psum"], 1)
                        pe.wait_ge(s["yq_ready"], n + 2)
                        nc.tensor.transpose(yq_ps[:, 0:P], yq[:, :], ident_bf).then_inc(s["yq_psum"], 1)
                        pe.wait_ge(s["yq_t_ready"], n + 1)
                        nc.tensor.matmul(gate_ps[:, :], yq_t[:, :], wq[:, 0, :], start=True, stop=True).then_inc(s["gate_psum"], 1)
                        nc.tensor.matmul(up_ps[:, :], yq_t[:, :], wq[:, 1, :], start=True, stop=True).then_inc(s["up_psum"], 1)
                        pe.wait_ge(s["pq_ready"], n + 1)
                        for m in range(BIT_BLOCKS):
                            last = nc.tensor.transpose(pq_blocks[:, m, :], pq[:, m * P:(m + 1) * P], ident_bf)
                        last.then_inc(s["pq_psum"], 1)
                        pe.wait_ge(s["pq_t_ready"], n + 1)
                        for m in range(BIT_BLOCKS):
                            last = nc.tensor.matmul(out_ps[:, 0:P], pq_t[:, m, :], wq[:, 2, m * P:(m + 1) * P],
                                                    start=(m == 0), stop=(m == BIT_BLOCKS - 1))
                        last.then_inc(s["out_psum"], 1)
                        pe.wait_ge(s["out_ready"], n + 1)
                        nc.tensor.transpose(turn_ps[:, 0:P], out[:, :], ident).then_inc(s["turn_psum"], 1)

            @block.scalar
            def _(act):
                with act.Fori(0, NT // 2) as i:
                    for u in range(2):
                        n = i * 2 + u
                        act.wait_ge(s["yq_psum"], n + 1)
                        nc.scalar.activation(yq_t[:, :], yq_ps[:, 0:P], ACT.Identity).then_inc(s["yq_t_ready"], 1)
                        act.wait_ge(s["gate_psum"], n + 1)
                        nc.scalar.activation(sig[:, :], gate_ps[:, :], ACT.Sigmoid, scale=back[:, 0:1]).then_inc(s["sig_ready"], 1)
                        act.wait_ge(s["pq_psum"], n + 1)
                        nc.scalar.activation(pq_t[:, :, :], pq_blocks, ACT.Identity).then_inc(s["pq_t_ready"], 1)
                        act.wait_ge(s["out_psum"], n + 1)
                        nc.scalar.activation(out[:, :], out_ps[:, 0:P], ACT.Identity, scale=back[:, 2:3]).then_inc(s["out_ready"], 1)

            @block.vector
            def _(dve):
                wchain, chain = s["wchain"], s["chain"]
                nc.vector.tensor_reduce(size[:, :], w, AX_X, ALU.add, apply_absolute_value=True).then_inc(s["size_ready"], 1)
                dve.wait_ge(s["all_ready"], 1)
                nc.vector.tensor_scalar(mean[:, :], size_all[:, :], 1.0 / (P * BIT_INNER), 1e-5, ALU.mult,
                                        ALU.max).then_inc(wchain, 1)
                dve.wait_ge(wchain, 1)
                nc.vector.reciprocal(winv[:, :], mean[:, :]).then_inc(wchain, 1)
                dve.wait_ge(wchain, 2)
                for m in range(3):
                    nc.vector.tensor_scalar(wnum[:, m, :], w[:, m, :], winv[:, m:m + 1], MAGIC, ALU.mult,
                                            ALU.add).then_inc(wchain, 1)
                dve.wait_ge(wchain, 5)
                nc.vector.tensor_scalar(wnum[:, :, :], wnum[:, :, :], MAGIC, 1.0, ALU.subtract, ALU.min).then_inc(wchain, 1)
                dve.wait_ge(wchain, 6)
                nc.vector.tensor_scalar(wq[:, :, :], wnum[:, :, :], -1.0, None, ALU.max).then_inc(s["yq_ready"], 1)

                def scales(which, at):
                    dve.wait_ge(chain, at + 1)
                    nc.vector.tensor_scalar(top[:, which, :], top[:, which, :], 1e-5, 1.0 / 127.0, ALU.max,
                                            ALU.mult).then_inc(chain, 1)
                    dve.wait_ge(chain, at + 2)
                    nc.vector.reciprocal(quant[:, which, :], top[:, which, :]).then_inc(chain, 1)

                with dve.Fori(0, NT) as n:
                    at = n * STEPS
                    dve.wait_ge(s["y_psum"], n + 3)
                    nc.vector.tensor_reduce(top[:, 0, :], y_ps[:, 0:P], AX_X, ALU.max,
                                            apply_absolute_value=True).then_inc(chain, 1)
                    scales(0, at)
                    dve.wait_ge(chain, at + 3)
                    nc.vector.tensor_scalar(num[:, :], y_ps[:, 0:P], quant[:, 0, :], MAGIC, ALU.mult, ALU.add).then_inc(chain, 1)
                    nc.vector.tensor_scalar(back[:, 0:2], mean[:, 0:2], top[:, 0, :], None, ALU.mult).then_inc(chain, 1)
                    dve.wait_ge(chain, at + 5)
                    nc.vector.tensor_scalar(num[:, :], num[:, :], MAGIC, 127.0, ALU.subtract, ALU.min).then_inc(chain, 1)
                    dve.wait_ge(chain, at + 6)
                    nc.vector.tensor_scalar(yq[:, :], num[:, :], -128.0, None, ALU.max).then_inc(s["yq_ready"], 1)
                    dve.wait_ge(s["sig_ready"], n + 1)
                    nc.vector.scalar_tensor_tensor(act_gate[:, :], gate_ps[:, :], back[:, 0:1], sig[:, :], ALU.mult,
                                                   ALU.mult).then_inc(chain, 1)
                    dve.wait_ge(chain, at + 7)
                    dve.wait_ge(s["up_psum"], n + 1)
                    nc.vector.scalar_tensor_tensor(prod[:, :], up_ps[:, :], back[:, 1:2], act_gate[:, :], ALU.mult,
                                                   ALU.mult).then_inc(chain, 1)
                    dve.wait_ge(chain, at + 8)
                    nc.vector.tensor_reduce(top[:, 1, :], prod[:, :], AX_X, ALU.max,
                                            apply_absolute_value=True).then_inc(chain, 1)
                    scales(1, at + 8)
                    dve.wait_ge(chain, at + 11)
                    nc.vector.tensor_scalar(pnum[:, :], prod[:, :], quant[:, 1, :], MAGIC, ALU.mult, ALU.add).then_inc(chain, 1)
                    nc.vector.tensor_scalar(back[:, 2:3], mean[:, 2:3], top[:, 1, :], None, ALU.mult).then_inc(chain, 1)
                    dve.wait_ge(chain, at + 13)
                    nc.vector.tensor_scalar(pnum[:, :], pnum[:, :], MAGIC, 127.0, ALU.subtract, ALU.min).then_inc(chain, 1)
                    dve.wait_ge(chain, at + 14)
                    nc.vector.tensor_scalar(pq[:, :], pnum[:, :], -128.0, None, ALU.max).then_inc(s["pq_ready"], 1)
                    dve.wait_ge(s["turn_psum"], n + 1)
                    here = x[:, bass.ds(n * P, P)]
                    nc.vector.tensor_tensor(here, turn_ps[:, 0:P], here, ALU.add).then_inc(s["x_added"], 1)


def threshold_stage(nc, tag, x, dst, draws):
    with ExitStack() as stack:
        mem = Memory(nc, stack, tag)
        size, p, cum, step = (mem.sb(n, [P, B, T]) for n in ("size", "p", "cum", "step"))
        zero = mem.sb("zero", [P, T])
        passed = mem.sb("passed", [P, B, T + 1])
        total, inv, bound = (mem.sb(n, [P, B]) for n in ("total", "inv", "bound"))
        chain, size_ready, p_ready, cum_ready, exp_ready = (mem.sem(n) for n in ("chain", "size_ready", "p_ready", "cum_ready", "exp_ready"))
        xb, db = x.rearrange("p (b t) -> p b t", t=T), dst.rearrange("p (b t) -> p b t", t=T)

        def over_time(ap):
            return ap.unsqueeze(2).broadcast_to([P, B, T])

        with nc.Block() as block:

            @block.scalar
            def _(act):
                nc.scalar.activation(size[:, :, :], xb, ACT.Abs).then_inc(size_ready, 1)
                act.wait_ge(p_ready, 1)
                nc.scalar.activation(p[:, :, :], p[:, :, :], ACT.Exp, scale=2.0).then_inc(exp_ready, 1)

            @block.vector
            def _(dve):
                nc.vector.memset(zero[:, :], 0.0).then_inc(chain, 1)
                nc.vector.memset(passed[:, :, 0:1], 1.0).then_inc(chain, 1)
                dve.wait_ge(size_ready, 1)
                nc.vector.tensor_reduce(total[:, :], size[:, :, :], AX_X, ALU.add).then_inc(chain, 1)
                dve.wait_ge(chain, 3)
                nc.vector.reciprocal(inv[:, :], total[:, :]).then_inc(chain, 1)
                dve.wait_ge(chain, 4)
                nc.vector.tensor_tensor(p[:, :, :], size[:, :, :], over_time(inv[:, :]), ALU.mult).then_inc(p_ready, 1)
                dve.wait_ge(exp_ready, 1)
                nc.vector.tensor_reduce(total[:, :], p[:, :, :], AX_X, ALU.add).then_inc(chain, 1)
                dve.wait_ge(chain, 5)
                nc.vector.reciprocal(inv[:, :], total[:, :]).then_inc(chain, 1)
                dve.wait_ge(chain, 6)
                nc.vector.tensor_tensor(p[:, :, :], p[:, :, :], over_time(inv[:, :]), ALU.mult).then_inc(chain, 1)
                dve.wait_ge(chain, 7)
                for b in range(B):
                    nc.vector.tensor_tensor_scan(cum[:, b, :], p[:, b, :], zero[:, :], 0.0, ALU.add,
                                                 ALU.add).then_inc(cum_ready, 1)
                dve.wait_ge(cum_ready, B)
                nc.vector.scalar_tensor_tensor(passed[:, :, 1:T + 1], cum[:, :, :], 0.001, over_time(draws), ALU.add,
                                               ALU.is_le).then_inc(chain, 1)
                dve.wait_ge(chain, 8)
                nc.vector.tensor_tensor(step[:, :, :], passed[:, :, 0:T], passed[:, :, 1:T + 1], ALU.subtract).then_inc(chain, 1)
                dve.wait_ge(chain, 9)
                nc.vector.tensor_tensor(step[:, :, :], step[:, :, :], size[:, :, :], ALU.mult).then_inc(chain, 1)
                dve.wait_ge(chain, 10)
                nc.vector.tensor_reduce(bound[:, :], step[:, :, :], AX_X, ALU.add).then_inc(chain, 1)
                dve.wait_ge(chain, 11)
                nc.vector.scalar_tensor_tensor(bound[:, :], passed[:, :, T:T + 1].squeeze(2), FAR, bound[:, :], ALU.mult,
                                               ALU.add).then_inc(chain, 1)
                dve.wait_ge(chain, 12)
                nc.vector.tensor_tensor(step[:, :, :], size[:, :, :], over_time(bound[:, :]), ALU.is_ge).then_inc(chain, 1)
                dve.wait_ge(chain, 13)
                nc.vector.tensor_tensor(db, xb, step[:, :, :], ALU.mult).then_inc(chain, 1)
RET_SCALE = float(D) ** -0.5
RET_EPS = 1e-6
RANK = 16


def low_rank_cond_stage(nc, tag, x, dst, w, u_all, v_all, pick, fc_bias, cond):
    with ExitStack() as stack:
        mem = Memory(nc, stack, tag)
        bias = mem.sb("bias", [P, B])
        z = mem.sb("z", [P, 2, T])
        z_ps, y_ps = mem.ps("z_ps", [P, 2, CHUNK]), mem.ps("y_ps", [P, 2, CHUNK])
        z_psum, z_ready, y_psum, dst_ready, bias_ready = (mem.sem(n) for n in ("z_psum", "z_ready", "y_psum", "dst_ready", "bias_ready"))
        with nc.Block() as block:

            @block.tensor
            def _(pe):
                with pe.Fori(0, B // 2) as i:
                    for u in range(2):
                        b = i * 2 + u
                        here = x[:, bass.ds(b * T, T)]
                        pe.wait_ge(z_ready, b + 1)
                        nc.tensor.matmul(z_ps[:, u, 0:T], v_all, here, start=True, stop=True).then_inc(z_psum, 1)
                        pe.wait_ge(dst_ready, b + 1)
                        nc.tensor.matmul(y_ps[:, u, 0:T], w, here, start=True, stop=False)
                        pe.wait_ge(z_ready, b + 3)
                        nc.tensor.matmul(y_ps[:, u, 0:T], u_all, z[:, u, :], start=False, stop=True).then_inc(y_psum, 1)

            @block.vector
            def _(dve):
                nc.vector.tensor_scalar(bias[:, :], cond, fc_bias, None, ALU.add).then_inc(bias_ready, 1)
                dve.sem_inc(z_ready, 2)
                dve.sem_inc(y_psum, 2)
                with dve.Fori(0, B // 2) as i:
                    for u in range(2):
                        b = i * 2 + u
                        dve.wait_ge(z_psum, b + 1)
                        dve.wait_ge(y_psum, b + 1)
                        nc.vector.tensor_scalar(z[:, u, :], z_ps[:, u, 0:T], pick[:, bass.ds(b, 1)], None,
                                                ALU.mult).then_inc(z_ready, 1)

            @block.scalar
            def _(act):
                act.sem_inc(dst_ready, 2)
                act.wait_ge(bias_ready, 1)
                with act.Fori(0, B // 2) as i:
                    for u in range(2):
                        b = i * 2 + u
                        act.wait_ge(y_psum, b + 3)
                        nc.scalar.activation(dst[:, bass.ds(b * T, T)], y_ps[:, u, 0:T], ACT.Gelu,
                                             bias=bias[:, bass.ds(b, 1)]).then_inc(dst_ready, 1)


def retention_stage(nc, tag, src, x, wq, wk, wv, wg, cos, sin, decay, ident, ones):
    W3 = T + HALF
    with ExitStack() as stack:
        mem = Memory(nc, stack, tag)
        y = mem.sb("y", [P, T])
        q_cos, q_sin = mem.sb("q_cos", [P, RUNS, T]), mem.sb("q_sin", [P, RUNS, T])
        q, k = mem.sb("q", [P, RUNS, T]), mem.sb("k", [P, RUNS, T])
        v = mem.sb("v", [P, 2, NHEAD * HD])
        silu_g = mem.sb("silu_g", [P, 2 * NHEAD, HD])
        part = mem.sb("part", [P, 2, NQUAD, W3])
        size = mem.sb("size", [P, 2, NQUAD, W3])
        den, inv, ms, rms, irms = (mem.sb(n, [P, 2 * NHEAD]) for n in ("den", "inv", "ms", "rms", "irms"))
        heads, square = mem.sb("heads", [P, 2 * NHEAD, HD]), mem.sb("square", [P, 2 * NHEAD, HD])
        s_ps = mem.ps("s_ps", [P, NQUAD, CHUNK])
        v_ps, g_ps = mem.ps("v_ps", [P, CHUNK]), mem.ps("g_ps", [P, CHUNK])
        o_ps, turn_ps = mem.ps("o_ps", [P, CHUNK]), mem.ps("turn_ps", [P, CHUNK])
        out_heads = o_ps[:, 0:2 * NHEAD * (HD + 1)].rearrange("p (h e) -> p h e", e=HD + 1)
        g_heads = g_ps[:, 0:T].rearrange("p (h e) -> p h e", e=HD)
        names = ("y_ready", "q_psum", "q_turned", "q_ready", "k_psum", "k_turned", "k_ready", "v_psum", "v_ready", "g_psum",
                 "sig_ready", "silu_ready", "s_psum", "part_ready", "size_ready", "o_psum", "chain", "rms_in", "rms_ready",
                 "o_ready", "turn_psum", "x_added")
        s = {n: mem.sem(n) for n in names}

        def wide(bank):
            return s_ps[:, bank:bank + 2, :].rearrange("p n (r t) -> p (n r) t", t=T)

        def each(ap):
            return ap.unsqueeze(2).broadcast_to([P, 2 * NHEAD, HD])

        with nc.Block() as block:

            @block.gpsimd
            def _(pool):
                pool.sem_inc(s["k_psum"], 1)
                with pool.Fori(0, B) as b:
                    pool.wait_ge(s["k_psum"], b + 1)
                    nc.gpsimd.tensor_copy(y[:, :], src[:, bass.ds(b * T, T)]).then_inc(s["y_ready"], 1)
                    pool.wait_ge(s["q_turned"], 2 * b + 2)
                    nc.gpsimd.tensor_tensor(q[:, :, :], q_cos[:, :, :], q_sin[:, :, :], ALU.add).then_inc(s["q_ready"], 1)
                    pool.wait_ge(s["k_turned"], 2 * b + 2)
                    nc.gpsimd.tensor_tensor(k[:, :, :], q_cos[:, :, :], q_sin[:, :, :], ALU.add).then_inc(s["k_ready"], 1)

            @block.tensor
            def _(pe):
                def scores(b, r):
                    if r >= 1:
                        pe.wait_ge(s["part_ready"], RUNS * b + r)
                    for half in range(2):
                        for g in range(NQUAD):
                            quad = slice(QUAD * g, QUAD * (g + 1))
                            last = nc.tensor.matmul(s_ps[:, g, half * T:half * T + T - half * HALF],
                                                    k[quad, r, half * HALF:(half + 1) * HALF],
                                                    q[quad, r, half * HALF:T], start=True, stop=True)
                    last.then_inc(s["s_psum"], 1)

                def values(b, r):
                    pe.wait_ge(s["size_ready"], RUNS * b + r + 1)
                    for half in range(2):
                        for g in range(NQUAD):
                            head = NQUAD * g + r
                            for rows, rhs, lo, hi in ((part, v, 0, HD), (size, None, HD, HD + 1)):
                                for n in range(half + 1):
                                    at = half * HALF if n == 0 else T
                                    last = nc.tensor.matmul(out_heads[:, NHEAD * half + head, lo:hi],
                                                            rows[:, r % 2, g, at:at + HALF],
                                                            ones[:, 0:1] if rhs is None else rhs[:, n, HD * head:HD * head + HD],
                                                            start=(n == 0), stop=(n == half))
                    last.then_inc(s["o_psum"], 1)

                with pe.Fori(0, B) as b:
                    pe.wait_ge(s["y_ready"], b + 1)
                    for p in range(2):
                        for r in range(RUNS):
                            last = nc.tensor.matmul(wide(2 * p)[:, r, :], wq[:, p, r, :], y[:, :], start=True, stop=True)
                    last.then_inc(s["q_psum"], 1)
                    for n in range(2):
                        last = nc.tensor.matmul(v_ps[:, n * P:(n + 1) * P], y[:, n * HALF:(n + 1) * HALF], wv, start=True, stop=True)
                    last.then_inc(s["v_psum"], 1)
                    for n in range(2):
                        last = nc.tensor.matmul(g_ps[:, n * P:(n + 1) * P], y[:, n * HALF:(n + 1) * HALF], wg, start=True, stop=True)
                    last.then_inc(s["g_psum"], 1)
                    pe.wait_ge(s["q_turned"], 2 * b + 2)
                    for p in range(2):
                        for r in range(RUNS):
                            last = nc.tensor.matmul(wide(2 * p)[:, r, :], wk[:, p, r, :], y[:, :], start=True, stop=True)
                    last.then_inc(s["k_psum"], 1)
                    pe.wait_ge(s["q_ready"], b + 1)
                    pe.wait_ge(s["k_ready"], b + 1)
                    scores(b, 0)
                    pe.wait_ge(s["v_ready"], b + 1)
                    for r in range(RUNS):
                        if r + 1 < RUNS:
                            scores(b, r + 1)
                        values(b, r)
                    pe.wait_ge(s["o_ready"], b + 1)
                    pe.wait_ge(s["x_added"], b + 1)
                    for n in range(2):
                        last = nc.tensor.transpose(turn_ps[:, n * P:(n + 1) * P],
                                                   square[:, n * NHEAD:(n + 1) * NHEAD, :].rearrange("p h e -> p (h e)"), ident)
                    last.then_inc(s["turn_psum"], 1)

            @block.scalar
            def _(act):
                with act.Fori(0, B) as b:
                    act.wait_ge(s["v_psum"], b + 1)
                    nc.scalar.activation(v[:, :, :].rearrange("p a d -> p (a d)"), v_ps[:, 0:T], ACT.Identity).then_inc(s["v_ready"], 1)
                    act.wait_ge(s["g_psum"], b + 1)
                    act.wait_ge(s["x_added"], b + 1)
                    nc.scalar.activation(silu_g[:, :, :], g_heads, ACT.Sigmoid).then_inc(s["sig_ready"], 1)
                    for r in range(RUNS):
                        act.wait_ge(s["part_ready"], RUNS * b + r + 1)
                        if r >= 2:
                            act.wait_ge(s["o_psum"], RUNS * b + r - 1)
                        nc.scalar.activation(size[:, r % 2, :, :], part[:, r % 2, :, :], ACT.Abs).then_inc(s["size_ready"], 1)
                    act.wait_ge(s["rms_in"], b + 1)
                    nc.scalar.activation(rms[:, :], ms[:, :], ACT.Sqrt).then_inc(s["rms_ready"], 1)

            @block.vector
            def _(dve):
                chain = s["chain"]

                def rotate(ps, table, out, done):
                    nc.vector.tensor_tensor(out, ps, table.unsqueeze(1).broadcast_to([P, RUNS, T]),
                                            ALU.mult).then_inc(done, 1)

                dve.sem_inc(s["x_added"], 1)
                with dve.Fori(0, B) as b:
                    at = 7 * b
                    dve.wait_ge(s["q_psum"], b + 1)
                    rotate(wide(0), cos[:, 0, :], q_cos[:, :, :], s["q_turned"])
                    rotate(wide(2), sin[:, 0, :], q_sin[:, :, :], s["q_turned"])
                    dve.wait_ge(s["k_psum"], b + 2)
                    dve.wait_ge(s["q_ready"], b + 1)
                    rotate(wide(0), cos[:, 1, :], q_cos[:, :, :], s["k_turned"])
                    rotate(wide(2), sin[:, 1, :], q_sin[:, :, :], s["k_turned"])
                    dve.wait_ge(s["sig_ready"], b + 1)
                    nc.vector.tensor_tensor(silu_g[:, :, :], silu_g[:, :, :], g_heads, ALU.mult).then_inc(s["silu_ready"], 1)
                    for r in range(RUNS):
                        dve.wait_ge(s["s_psum"], RUNS * b + r + 1)
                        if r >= 2:
                            dve.wait_ge(s["o_psum"], RUNS * b + r - 1)
                        nc.vector.tensor_tensor(part[:, r % 2, :, :], s_ps[:, :, 0:W3], decay[:, r, :, :],
                                                ALU.mult).then_inc(s["part_ready"], 1)
                    dve.wait_ge(s["o_psum"], RUNS * (b + 1))
                    nc.vector.tensor_scalar(den[:, :], out_heads[:, :, HD], 1.0, 50000.0, ALU.max, ALU.min).then_inc(chain, 1)
                    dve.wait_ge(chain, at + 1)
                    nc.vector.reciprocal(inv[:, :], den[:, :]).then_inc(chain, 1)
                    dve.wait_ge(chain, at + 2)
                    nc.vector.tensor_tensor(heads[:, :, :], out_heads[:, :, 0:HD], each(inv[:, :]), ALU.mult).then_inc(chain, 1)
                    dve.wait_ge(chain, at + 3)
                    nc.vector.tensor_tensor(square[:, :, :], heads[:, :, :], heads[:, :, :], ALU.mult).then_inc(chain, 1)
                    dve.wait_ge(chain, at + 4)
                    nc.vector.tensor_reduce(den[:, :], square[:, :, :], AX_X, ALU.add).then_inc(chain, 1)
                    dve.wait_ge(chain, at + 5)
                    nc.vector.tensor_scalar(ms[:, :], den[:, :], 1.0 / HD, RET_EPS, ALU.mult, ALU.add).then_inc(s["rms_in"], 1)
                    dve.wait_ge(s["silu_ready"], b + 1)
                    nc.vector.tensor_tensor(heads[:, :, :], heads[:, :, :], silu_g[:, :, :], ALU.mult).then_inc(chain, 1)
                    dve.wait_ge(s["rms_ready"], b + 1)
                    nc.vector.reciprocal(irms[:, :], rms[:, :]).then_inc(chain, 1)
                    dve.wait_ge(chain, at + 7)
                    nc.vector.tensor_tensor(square[:, :, :], heads[:, :, :], each(irms[:, :]), ALU.mult).then_inc(s["o_ready"], 1)
                    dve.wait_ge(s["turn_psum"], b + 1)
                    here = x[:, bass.ds(b * T, T)]
                    nc.vector.tensor_tensor(here, turn_ps[:, 0:T], here, ALU.add).then_inc(s["x_added"], 1)


def retention_weights(w):
    cols = w.reshape(D, NQUAD, RUNS, HD)
    out = np.zeros((D, 2, RUNS, NQUAD, QUAD), np.float32)
    out[:, 0, :, :, :HD] = cols.transpose(0, 2, 1, 3)
    out[:, 1, :, :, :HD] = cols.reshape(D, NQUAD, RUNS, HD // 2, 2)[..., ::-1].reshape(cols.shape).transpose(0, 2, 1, 3)
    return out.reshape(D, 2, RUNS, P)


def retention_tables():
    f = np.float32
    angle = np.repeat(1.0 / f(10000.0) ** np.linspace(0.0, 1.0, HD // 2, dtype=f), 2).astype(f)
    turn = (np.arange(T, dtype=f)[:, None] * angle[None, :]).astype(f)
    cos, sin = np.zeros((2, NQUAD, QUAD, 2, T), f)
    sign = np.where(np.arange(HD) % 2 == 0, -1.0, 1.0)
    for n, by in enumerate((1.0, RET_SCALE)):
        cos[:, :HD, n] = np.cos(turn).T * by
        sin[:, :HD, n] = np.sin(turn).T * sign[:, None] * by
    rate = np.log(1.0 - 2.0 ** (-5.0 - np.arange(NHEAD, dtype=f))).astype(f)
    lag = np.arange(T)[:, None] - np.arange(T)[None, :]
    mask = np.where(lag >= 0, np.exp(np.maximum(lag, 0).astype(f) * rate[:, None, None]), 0.0).astype(f)
    mask = (mask / np.sqrt(mask.sum(-1, keepdims=True, dtype=f))).astype(f)
    keys = mask.transpose(0, 2, 1).reshape(NQUAD, RUNS, T, T)
    decay = np.concatenate([keys[:, :, :HALF], keys[:, :, HALF:, HALF:]], -1)
    return cos.reshape(P, 2, T), sin.reshape(P, 2, T), decay.transpose(2, 1, 0, 3)


def packs(i):
    cos0, sin0 = rope_tables(False)
    cos1, sin1 = rope_tables(True)
    cos3, sin3, decay = retention_tables()
    qkv = i["L1_attn_w_qkv"]
    fside = i["fside_Bx1x1024x16_0"][:, 0]
    inch = 1.0 / (D * RANK)
    base = {
        "cond": i["cond_1024"].T,
        "ident": np.eye(P, dtype=np.float32), "mask": np.where(np.tril(np.ones((P, P))), 0.0, -1e30).astype(np.float32),
        "ones": np.ones((P, P), np.float32),
        "rank": np.tile(np.arange(NEXP, 0, -1, dtype=np.float32), (P, 1)),
    }
    l0 = {
        "c_w1": i["L0_cond_W1"].T, "c_b1": i["L0_cond_b1"][:, None],
        "c_w2": i["L0_cond_W2"].T, "c_b2": i["L0_cond_b2"][:, None],
        "wq": attention_weights(i["L0_attn_Wq"], NHEAD, True), "wk": attention_weights(i["L0_attn_Wk"], NQUAD, True),
        "wv": i["L0_attn_Wv"], "wo": i["L0_attn_Wo"], "cos": cos0, "sin": sin0,
        "wx": i["L0_cond2_Wx"], "wh": i["L0_cond2_Wh"], "b": i["L0_cond2_b"].reshape(4, P).T,
        "f_w": i["L0_ffn_weight"].T, "f_b": i["L0_ffn_bias"][:, None],
    }
    l1 = {
        "wq": attention_weights(qkv[:, :D], NHEAD, True), "wk": attention_weights(qkv[:, D:2 * D], NHEAD, True),
        "wv": qkv[:, 2 * D:], "wo": i["L1_attn_w_proj"], "cos": cos1, "sin": sin1,
        "r_w": i["L1_cond2_router_w"].T, "r_t": i["L1_cond2_router_t_w"].T,
        "r_b": np.tile(i["L1_cond2_router_bias"], (P, 1)),
        "sw1": i["L1_cond2_sw1"].T, "sw3": i["L1_cond2_sw3"].T,
        "sw2": i["L1_cond2_sw2"].T.reshape(2, P, D).transpose(1, 0, 2),
        "rw1": i["L1_cond2_rw1"].reshape(NEXP * P // 2, D).T,
        "rw2": i["L1_cond2_rw2"].transpose(0, 2, 1).reshape(NEXP // 2, P, D).transpose(1, 0, 2),
        "f_r": i["L1_ffn_Wg"], "f_w1": i["L1_ffn_W1"].transpose(1, 0, 2),
        "f_b1": i["L1_ffn_b1"].reshape(NEXP, 2, P).transpose(2, 0, 1),
        "f_w2": i["L1_ffn_W2"].reshape(NEXP, 2, P, D).transpose(2, 0, 1, 3), "f_b2": i["L1_ffn_b2"],
    }
    l2 = {
        "wx": i["L2_cond_Wx"], "wh": i["L2_cond_Wh"], "b": i["L2_cond_b"].reshape(4, P).T,
        **delta_weights(i), "head_sum": np.kron(np.eye(P // N2, dtype=np.float32), np.ones((N2, N2), np.float32)),
        "r_wx": i["L2_cond2_Wx"], "r_wh": i["L2_cond2_Wh"], "r_b": i["L2_cond2_b"][:, None],
        "f_w": np.stack([i["L2_ffn_w_gate"].T, i["L2_ffn_w_up"].T,
                         i["L2_ffn_w_down"].T.reshape(BIT_BLOCKS, P, D).transpose(1, 0, 2).reshape(P, -1)], 1),
    }
    l3 = {
        "c_w": i["L3_cond_W"].T, "c_b": i["L3_cond_fc_bias"][:, None],
        "u_all": fside.transpose(0, 2, 1).reshape(P, D), "v_all": fside.transpose(1, 0, 2).reshape(D, P),
        "pick": np.kron(np.eye(B, dtype=np.float32), np.full((RANK, 1), inch, np.float32)),
        "wq": retention_weights(i["L3_attn_Wq"]), "wk": retention_weights(i["L3_attn_Wk"]),
        "wv": i["L3_attn_Wv"], "wg": i["L3_attn_Wg"], "cos": cos3, "sin": sin3,
        "wx": i["L3_cond2_Wx"], "wh": i["L3_cond2_Wh"], "b": i["L3_cond2_b"].reshape(4, P).T,
        "f_r": i["L3_ffn_router_w"].T,
        "f_wg": i["L3_ffn_gate_w"].transpose(1, 0, 2), "f_bg": i["L3_ffn_gate_b"].reshape(NEXP, 2, P).transpose(2, 0, 1),
        "f_wu": i["L3_ffn_up_w"].transpose(1, 0, 2), "f_bu": i["L3_ffn_up_b"].reshape(NEXP, 2, P).transpose(2, 0, 1),
        "f_wd": i["L3_ffn_down_w"].reshape(NEXP, 2, P, D).transpose(2, 0, 1, 3), "f_bd": i["L3_ffn_down_b"],
    }
    return {"base": base, "l0": l0, "l1": l1, "l2": l2, "l3": l3}, decay


def packed(pack):
    total = sum(int(np.prod(a.shape[1:])) for a in pack.values())
    whole = np.zeros((P, total), np.float32)
    places, at = {}, 0
    for name, a in pack.items():
        size = int(np.prod(a.shape[1:]))
        whole[:a.shape[0], at:at + size] = a.reshape(a.shape[0], size)
        places[name] = (at, a.shape)
        at += size
    return whole, places


def views(buffer, places):
    letters = "abc"
    out = {}
    for name, (at, shape) in places.items():
        part = buffer[0:shape[0], at:at + int(np.prod(shape[1:]))]
        if len(shape) > 2:
            dims = letters[:len(shape) - 1]
            part = part.rearrange(f"p ({' '.join(dims)}) -> p {' '.join(dims)}", **dict(zip(dims, shape[1:])))
        out[name] = part
    return out


def program(nc, dram, out, places, first=0, last=8):
    STAGE_SEMAPHORES.clear()
    with ExitStack() as stack:
        mem = Memory(nc, stack, "main")
        widths = {name: max(at + int(np.prod(shape[1:])) for at, shape in p.values()) for name, p in places.items()}
        x_buf, y_buf = mem.sb("x", [P, TOK]), mem.sb("y", [P, TOK])
        x, y = x_buf[:, :], y_buf[:, :]
        base_buf = mem.sb("base", [P, widths["base"]])
        ident_bf_buf, mask_bf_buf = mem.sb("ident_bf", [P, P], BF16), mem.sb("mask_bf", [P, P], BF16)
        even_buf = mem.sb("even_layers", [P, max(widths["l0"], widths["l2"])])
        odd_buf = mem.sb("odd_layers", [P, max(widths["l1"], widths["l3"])])
        base = views(base_buf, places["base"])
        l0, l2 = views(even_buf, places["l0"]), views(even_buf, places["l2"])
        l1, l3 = views(odd_buf, places["l1"]), views(odd_buf, places["l3"])
        ident, ones, rank, cond = base["ident"], base["ones"], base["rank"], base["cond"]
        ident_bf, mask_bf = ident_bf_buf[:, :], mask_bf_buf[:, :]
        loaded = {n: mem.sem(f"loaded_{n}") for n in ("start", "l1", "l2", "l3", "decay")}
        stored = mem.sem("stored")

        def between(load=(), need=None):
            with nc.Block() as block:

                @block.gpsimd
                def _(pool):
                    if STAGE_SEMAPHORES:
                        nc.clear_and_free_semaphores(list(STAGE_SEMAPHORES))
                        STAGE_SEMAPHORES.clear()

                @block.sync
                def _(sp):
                    for dst, src, name in load:
                        sp.dma_start(dst, src).then_inc(loaded[name], 16)
                    if need:
                        sp.wait_ge(loaded[need[0]], 16 * need[1])

        between([(x, dram["x"], "start"), (base_buf[:, :], dram["base"], "start"),
                 (even_buf[:, 0:widths["l0"]], dram["l0"], "start"), (odd_buf[:, 0:widths["l1"]], dram["l1"], "l1")], ("start", 3))
        with nc.Block() as block:

            @block.vector
            def _(dve):
                nc.vector.tensor_copy(ident_bf, ident)
                nc.vector.tensor_copy(mask_bf, base["mask"])

        if first <= 0 < last:
            cond_gate_stage(nc, "l0c", x, y, cond, l0["c_w1"], l0["c_b1"], l0["c_w2"], l0["c_b2"])
            attention_stage(nc, "l0a", y, x, l0["wq"], l0["wk"], l0["wv"], l0["wo"], l0["cos"], l0["sin"], ident,
                            ident_bf, mask_bf, NQUAD)
        if first <= 1 < last:
            lstm_stage(nc, "l0r", x, y, l0["wx"], l0["wh"], l0["b"], cond, ident)
            ternary_stage(nc, "l0f", y, x, l0["f_w"], l0["f_b"])
        between([(even_buf[:, 0:widths["l2"]], dram["l2"], "l2")], ("l1", 1))
        if first <= 2 < last:
            threshold_stage(nc, "l1c", x, y, cond)
            attention_stage(nc, "l1a", y, x, l1["wq"], l1["wk"], l1["wv"], l1["wo"], l1["cos"], l1["sin"], ident,
                            ident_bf, mask_bf, NHEAD)
        if first <= 3 < last:
            routed_cond_stage(nc, "l1r", x, y, cond, l1["r_w"], l1["r_t"], l1["r_b"], l1["sw1"], l1["sw3"], l1["sw2"],
                              l1["rw1"], l1["rw2"], rank, ones, ident)
            expert_stage(nc, "l1f", y, x, l1["f_r"], l1["f_w1"], l1["f_b1"], None, None, l1["f_w2"], l1["f_b2"], rank, ident)
        between([(odd_buf[:, 0:widths["l3"]], dram["l3"], "l3")], ("l2", 1))
        if first <= 4 < last:
            lstm_stage(nc, "l2r", x, y, l2["wx"], l2["wh"], l2["b"], cond, ident)
            delta_stage(nc, "l2a", y, x, l2["w_in"], l2["w_k"], l2["w_q"], l2["w_vb"], l2["b_vb"], l2["w_out"], l2["head_sum"])
        decay_buf = mem.sb("decay", [P, RUNS, NQUAD, T + HALF])
        decay = decay_buf[:, :, :, :]
        between([(decay, dram["decay"], "decay")])
        if first <= 5 < last:
            rnn_stage(nc, "l2s", x, y, l2["r_wx"], l2["r_wh"], l2["r_b"], cond, ident)
            bit_ffn_stage(nc, "l2f", y, x, l2["f_w"], ident, ident_bf)
        between((), ("l3", 1))
        between((), ("decay", 1))
        if first <= 6 < last:
            low_rank_cond_stage(nc, "l3c", x, y, l3["c_w"], l3["u_all"], l3["v_all"], l3["pick"], l3["c_b"], cond)
            retention_stage(nc, "l3a", y, x, l3["wq"], l3["wk"], l3["wv"], l3["wg"], l3["cos"], l3["sin"], decay, ident, ones)
        if first <= 7 < last:
            lstm_stage(nc, "l3r", x, y, l3["wx"], l3["wh"], l3["b"], cond, ident)
            expert_stage(nc, "l3f", y, x, l3["f_r"], l3["f_wg"], l3["f_bg"], l3["f_wu"], l3["f_bu"], l3["f_wd"], l3["f_bd"],
                         rank, ident)
        with nc.Block() as block:

            @block.sync
            def _(sp):
                sp.dma_start(out, x).then_inc(stored, 16)
                sp.wait_ge(stored, 16)


def host_arrays(inputs):
    i = {name: np.asarray(a) for name, a in inputs.items()}
    layers, decay = packs(i)
    arrays, places = {"x": np.ascontiguousarray(i["x"].transpose(2, 0, 1).reshape(D, TOK))}, {}
    for name, pack in layers.items():
        arrays[name], places[name] = packed(pack)
    arrays["decay"] = np.ascontiguousarray(decay)
    return arrays, places


def kernel(**inputs):
    import concourse.bacc as bacc
    from concourse.bass_utils import run_bass_kernel_spmd

    nc = bacc.Bacc("TRN2", target_bir_lowering=False, num_devices=1)
    arrays, places = host_arrays(inputs)
    dram = {name: nc.dram_tensor(f"in_{name}", a.shape, mybir.dt.from_np(a.dtype), kind="ExternalInput").ap()
            for name, a in arrays.items()}
    out = nc.dram_tensor("out", (D, TOK), F32, kind="ExternalOutput").ap()
    program(nc, dram, out, places)
    got = run_bass_kernel_spmd(nc, [{f"in_{name}": a for name, a in arrays.items()}], core_ids=[0])
    return np.ascontiguousarray(got.results[0]["out"].reshape(D, B, T).transpose(1, 2, 0))
```

```python
from contextlib import ExitStack

import numpy as np

import concourse.bass as bass
from concourse import mybir

F32 = mybir.dt.float32
BF16 = mybir.dt.bfloat16
ALU = mybir.AluOpType
ACT = mybir.ActivationFunctionType
AX_X = mybir.AxisListType.X
RMAX = bass.bass_isa.ReduceOp.max
RADD = bass.bass_isa.ReduceOp.add

B, T, D = 8, 256, 128
TOK = B * T
P = 128
CHUNK = 512
NCHUNK = TOK // CHUNK


def high(ap):
    dims = "abcd"[:ap.ndim - 1]
    return ap.bitcast(BF16).rearrange(f"{' '.join(dims)} (n two) -> {' '.join(dims)} two n", two=2)[
        tuple(slice(None) for _ in dims) + (1,)]


STAGE_SEMAPHORES = []


class Memory:

    def __init__(self, nc, stack, tag):
        self.nc, self.stack, self.tag = nc, stack, tag

    def sb(self, name, shape, dt=F32):
        return self.stack.enter_context(self.nc.sbuf_tensor(f"{self.tag}_{name}", shape, dt))

    def ps(self, name, shape, dt=F32):
        return self.stack.enter_context(self.nc.psum_tensor(f"{self.tag}_{name}", shape, dt))

    def sem(self, name):
        sem = self.nc.alloc_semaphore(f"{self.tag}_{name}")
        if self.tag != "main":
            STAGE_SEMAPHORES.append(sem)
        return sem


def clear_stage_semaphores(nc):
    with nc.Block() as block:

        @block.gpsimd
        def _(pool):
            nc.clear_and_free_semaphores(list(STAGE_SEMAPHORES))
            STAGE_SEMAPHORES.clear()
STEPS_IN_BODY = 4


def lstm_stage(nc, tag, src, dst, wx, wh, bias, h0, ident):
    with ExitStack() as stack:
        mem = Memory(nc, stack, tag)
        xw = mem.sb("xw", [P, T * 4 * B])
        gates = mem.sb("gates", [P, 2 * B])
        both = mem.sb("both", [P, 2 * B])
        tanh_c = mem.sb("tanh_c", [P, B])
        h_ring = mem.sb("h_ring", [P, STEPS_IN_BODY, B])
        h_rest, h_low = mem.sb("h_rest", [P, B]), mem.sb("h_low", [P, B], BF16)
        w_part = [mem.sb(f"w_part{n}", [P, 4 * P], BF16) for n in range(3)]
        w_rest = mem.sb("w_rest", [P, 4 * P])
        pre = mem.ps("pre", [P, 4, CHUNK])
        acc = mem.ps("acc", [P, 2, CHUNK])
        acc_o = mem.ps("acc_o", [P, 2, CHUNK])
        out_gate = mem.sb("out_gate", [P, B])
        o_psum = mem.sem("o_psum")
        cand_cell = pre[:, 3, 0:2 * B]
        xw_psum, xw_act, xw_dve = mem.sem("xw_psum"), mem.sem("xw_act"), mem.sem("xw_dve")
        w_split = mem.sem("w_split")
        gates_psum, gates_ready = mem.sem("gates_psum"), mem.sem("gates_ready")
        mul_ready, cell_ready, tanh_ready = mem.sem("mul_ready"), mem.sem("cell_ready"), mem.sem("tanh_ready")
        h_ready, rest_ready, low_ready = mem.sem("h_ready"), mem.sem("rest_ready"), mem.sem("low_ready")
        table_ready, h_saved = mem.sem("table_ready"), mem.sem("h_saved")
        FIRST, LAST = (0, 1, 3), (2,)
        SLOT = (0, 1, 3, 2)
        xw_by_gate = xw[:, :].rearrange("p (t g b) -> p g b t", g=4, b=B)
        dst_by_step = dst.rearrange("p (b t) -> p t b", t=T)
        U = STEPS_IN_BODY
        BC = CHUNK // T

        with nc.Block() as block:

            @block.tensor
            def _(pe):
                for c in range(NCHUNK):
                    for g in range(4):
                        if c >= 1 and g == 0:
                            pe.wait_ge(xw_act, 2 * c)
                        if c >= 1 and g == 2:
                            pe.wait_ge(xw_dve, 2 * c)
                        nc.tensor.matmul(pre[:, g, :], wx[:, g * P:(g + 1) * P], src[:, c * CHUNK:(c + 1) * CHUNK],
                                         start=True, stop=True).then_inc(xw_psum, 1)
                pe.wait_ge(xw_act, 2 * NCHUNK)
                pe.wait_ge(xw_dve, 2 * NCHUNK)
                pe.wait_ge(w_split, 4)
                with pe.Fori(0, T // U) as i:
                    for u in range(U):
                        s = i * U + u

                        def products(into, which, parts, h, end=False):
                            for at, g in enumerate(which):
                                for n in range(parts):
                                    last = nc.tensor.matmul(into[:, u % 2, at * B:(at + 1) * B],
                                                            w_part[n][:, g * P:(g + 1) * P], h, start=False,
                                                            stop=(end and g == which[-1]))
                            return last

                        h_parts = high(h_ring[:, (u - 1) % U, :]), high(h_rest[:, :]), h_low[:, :]
                        nc.tensor.matmul(acc[:, u % 2, 0:3 * B], ident, xw[:, bass.ds(s * 4 * B, 3 * B)], start=True,
                                         stop=False)
                        pe.wait_ge(h_ready, s + 1)
                        products(acc, FIRST, 3, h_parts[0])
                        pe.wait_ge(rest_ready, s + 1)
                        products(acc, FIRST, 2, h_parts[1])
                        pe.wait_ge(low_ready, s + 1)
                        products(acc, FIRST, 1, h_parts[2], True).then_inc(gates_psum, 1)
                        nc.tensor.matmul(acc_o[:, u % 2, 0:B], ident, xw[:, bass.ds(s * 4 * B + 3 * B, B)], start=True,
                                         stop=False)
                        for n in range(3):
                            last = products(acc_o, LAST, 3 - n, h_parts[n], n == 2)
                        last.then_inc(o_psum, 1)

            @block.scalar
            def _(act):
                for c in range(NCHUNK):
                    for g in range(2):
                        act.wait_ge(xw_psum, 4 * c + g + 1)
                        nc.scalar.activation(xw_by_gate[:, SLOT[g], BC * c:BC * (c + 1), :],
                                             pre[:, g, :].rearrange("p (b t) -> p b t", t=T), ACT.Identity,
                                             bias=bias[:, g:g + 1]).then_inc(xw_act, 1)
                act.wait_ge(cell_ready, 1)
                nc.scalar.activation(tanh_c[:, :], cand_cell[:, B:2 * B], ACT.Sigmoid).then_inc(table_ready, 1)
                act.wait_ge(table_ready, 1)
                with act.Fori(0, T // U) as i:
                    for u in range(U):
                        s = i * U + u
                        act.wait_ge(gates_psum, s + 1)
                        nc.scalar.activation(gates[:, :], acc[:, u % 2, 0:2 * B], ACT.Sigmoid)
                        nc.scalar.activation(cand_cell[:, 0:B], acc[:, u % 2, 2 * B:3 * B],
                                             ACT.Tanh).then_inc(gates_ready, 1)
                        act.wait_ge(o_psum, s + 1)
                        nc.scalar.activation(out_gate[:, :], acc_o[:, u % 2, 0:B], ACT.Sigmoid)
                        act.wait_ge(cell_ready, s + 2)
                        nc.scalar.activation(tanh_c[:, :], cand_cell[:, B:2 * B], ACT.Tanh).then_inc(tanh_ready, 1)

            @block.vector
            def _(dve):
                def split(u, s):
                    h = h_ring[:, u, :]
                    dve.wait_ge(h_ready, s)
                    nc.vector.tensor_tensor(h_rest[:, :], h, high(h), ALU.subtract).then_inc(rest_ready, 1)
                    dve.wait_ge(rest_ready, s)
                    nc.vector.tensor_tensor(h_low[:, :], h_rest[:, :], high(h_rest[:, :]), ALU.subtract).then_inc(low_ready, 1)

                nc.vector.tensor_copy(h_ring[:, U - 1, :], h0).then_inc(h_ready, 1)
                split(U - 1, 1)
                for c in range(NCHUNK):
                    for g in range(2, 4):
                        dve.wait_ge(xw_psum, 4 * c + g + 1)
                        nc.vector.tensor_scalar(xw_by_gate[:, SLOT[g], BC * c:BC * (c + 1), :],
                                                pre[:, g, :].rearrange("p (b t) -> p b t", t=T),
                                                bias[:, g:g + 1], None, ALU.add).then_inc(xw_dve, 1)
                dve.wait_ge(xw_dve, 2 * NCHUNK)
                nc.vector.memset(cand_cell[:, B:2 * B], 0.0).then_inc(cell_ready, 1)
                dve.wait_ge(cell_ready, 1)
                with dve.Fori(0, T // U) as i:
                    for u in range(U):
                        s = i * U + u
                        dve.wait_ge(gates_ready, s + 1)
                        nc.vector.tensor_tensor(both[:, :], gates[:, :], cand_cell, ALU.mult).then_inc(mul_ready, 1)
                        dve.wait_ge(mul_ready, s + 1)
                        nc.vector.tensor_tensor(cand_cell[:, B:2 * B], both[:, 0:B], both[:, B:2 * B],
                                                ALU.add).then_inc(cell_ready, 1)
                        dve.wait_ge(h_saved, s + 1)
                        dve.wait_ge(tanh_ready, s + 1)
                        nc.vector.tensor_tensor(h_ring[:, u, :], out_gate[:, :], tanh_c[:, :],
                                                ALU.mult).then_inc(h_ready, 1)
                        split(u, s + 2)

            @block.gpsimd
            def _(pool):
                nc.gpsimd.tensor_copy(w_part[0][:, :], wh).then_inc(w_split, 1)
                pool.wait_ge(w_split, 1)
                nc.gpsimd.tensor_tensor(w_rest[:, :], wh, w_part[0][:, :], ALU.subtract).then_inc(w_split, 1)
                pool.wait_ge(w_split, 2)
                nc.gpsimd.tensor_copy(w_part[1][:, :], w_rest[:, :]).then_inc(w_split, 1)
                pool.wait_ge(w_split, 3)
                nc.gpsimd.tensor_tensor(w_part[2][:, :], w_rest[:, :], w_part[1][:, :], ALU.subtract).then_inc(w_split, 1)
                pool.sem_inc(h_saved, U)
                with pool.Fori(0, T // U) as i:
                    for u in range(U):
                        s = i * U + u
                        pool.wait_ge(h_ready, s + 2)
                        nc.gpsimd.tensor_copy(dst_by_step[:, bass.ds(s, 1), :], h_ring[:, u:u + 1, :]).then_inc(h_saved, 1)



HEADS2, N2 = 8, 32
HG = HEADS2 // 4
IQ = 4
IL = N2 // IQ
ROWS = HG * IL
TC = 32
NTC = T // TC
CH = TC * B
KN_EPS = 1e-6


def recurrent_stages(nc, tag, x, y, wx, wh, bias, w_in, w_k, w_q, w_vb, b_vb, w_out, head_sum, r_wx, r_wh, r_bias, h0, ident):
    with ExitStack() as stack:
        mem = Memory(nc, stack, tag)
        xw = mem.sb("xw", [P, T * 4 * B])
        gates = mem.sb("gates", [P, 3 * B])
        cand_cell = mem.sb("cand_cell", [P, 2 * B])
        both = mem.sb("both", [P, 2 * B])
        tanh_c = mem.sb("tanh_c", [P, B])
        h_ring = mem.sb("h_ring", [P, 2, B])
        xp_sig = mem.sb("xp_sig", [P, CH])
        xp = mem.sb("xp", [P, CH])
        k_sq = mem.sb("k_sq", [P, HG, CH])
        k_norm = mem.sb("k_norm", [P, HG, CH])
        kn_f = mem.sb("kn_f", [P, HG, CH])
        q_f = mem.sb("q_f", [P, HG, CH])
        vb_f = mem.sb("vb_f", [P, TC, B, IQ])
        kn_t = mem.sb("kn_t", [P, TC, HG, N2])
        q_t = mem.sb("q_t", [P, TC, HG, N2])
        vb_t = mem.sb("vb_t", [P, TC, 2 * ROWS])
        state = mem.sb("state", [P, 2, ROWS, N2])
        s_kn = mem.sb("s_kn", [P, ROWS, N2])
        beta_s = mem.sb("beta_s", [P, ROWS, N2])
        dk = mem.sb("dk", [P, ROWS, N2])
        pre = mem.sb("pre", [P, ROWS, N2])
        s_q = mem.sb("s_q", [P, ROWS, N2])
        got = mem.sb("got", [P, ROWS])
        dlt = mem.sb("dlt", [P, ROWS])
        sq = mem.sb("sq", [P, TC, 2 * ROWS])
        sq_sig = mem.sb("sq_sig", [P, TC, ROWS])
        sq_sq = mem.sb("sq_sq", [P, TC, ROWS])
        cell_f = mem.sb("cell_f", [P, CH, IQ])
        rxw = mem.sb("rxw", [P, CH])
        r_ring = mem.sb("r_ring", [P, 2, B])
        banks = [mem.ps(f"bank{n}", [P, CHUNK]) for n in range(8)]
        acc, r_ps, x_ps = banks[0:2], banks[2], banks[3]
        k_ps, q_ps, vb_ps = banks[4], banks[5], banks[6:8]
        ssq_ps = x_ps
        out_ps = q_ps
        xw_ps = banks[4:8]

        xw_by_gate = xw[:, :].rearrange("p (t g b) -> p g b t", g=4, b=B)
        rxw_by_seq = rxw[:, :].rearrange("p (t b) -> p b t", b=B)
        y_b, x_b = y.rearrange("p (b t) -> p b t", t=T), x.rearrange("p (b t) -> p b t", t=T)
        y_t, x_t = y.rearrange("p (b t) -> p t b", t=T), x.rearrange("p (b t) -> p t b", t=T)
        BC = CHUNK // T

        def halves(bank):
            return bank[:, :].rearrange("p (g n) -> p g n", g=2)

        def repeated(ap):
            return ap.rearrange("p (b t) -> p t b", t=TC).unsqueeze(3).broadcast_to([P, TC, B, IQ])

        def over_rows(ap):
            return ap.unsqueeze(3).broadcast_to([P, HG, N2, IL]).rearrange("p g j i -> p g i j")

        def over_cols(ap):
            return ap.unsqueeze(2).broadcast_to([P, ROWS, N2])

        def by_group(ap):
            return ap.rearrange("p (g i) j -> p g i j", g=HG)

        def start():
            xw_psum, xw_act, xw_dve = mem.sem("xw_psum"), mem.sem("xw_act"), mem.sem("xw_dve")
            with nc.Block() as block:

                @block.tensor
                def _(pe):
                    for c in range(NCHUNK):
                        for g in range(4):
                            if c >= 1 and g == 0:
                                pe.wait_ge(xw_act, 2 * c)
                            if c >= 1 and g == 2:
                                pe.wait_ge(xw_dve, 2 * c)
                            nc.tensor.matmul(xw_ps[g][:, :], wx[:, g * P:(g + 1) * P], x[:, c * CHUNK:(c + 1) * CHUNK],
                                             start=True, stop=True).then_inc(xw_psum, 1)

                @block.scalar
                def _(act):
                    for c in range(NCHUNK):
                        for g in range(2):
                            act.wait_ge(xw_psum, 4 * c + g + 1)
                            nc.scalar.activation(xw_by_gate[:, g, BC * c:BC * (c + 1), :],
                                                 xw_ps[g][:, :].rearrange("p (b t) -> p b t", t=T), ACT.Identity,
                                                 bias=bias[:, g:g + 1]).then_inc(xw_act, 1)

                @block.vector
                def _(dve):
                    nc.vector.tensor_copy(h_ring[:, 1, :], h0)
                    nc.vector.tensor_copy(r_ring[:, 1, :], h0)
                    nc.vector.memset(cand_cell[:, B:2 * B], 0.0)
                    for c in range(NCHUNK):
                        for g in range(2, 4):
                            dve.wait_ge(xw_psum, 4 * c + g + 1)
                            nc.vector.tensor_scalar(xw_by_gate[:, g, BC * c:BC * (c + 1), :],
                                                    xw_ps[g][:, :].rearrange("p (b t) -> p b t", t=T),
                                                    bias[:, g:g + 1], None, ALU.add).then_inc(xw_dve, 1)

                @block.gpsimd
                def _(pool):
                    nc.gpsimd.memset(state[:, 1, :, :], 0.0)
                    nc.gpsimd.memset(sq[:, :, ROWS:2 * ROWS], 0.0)

        def waves(name, count, lstm, delta, rnn):
            L, DELTA, R = lstm is not None, delta is not None, rnn is not None
            sem = Memory(nc, stack, f"{tag}{name}").sem
            gates_psum, gates_ready, mul_ready = sem("gates_psum"), sem("gates_ready"), sem("mul_ready")
            cell_ready, tanh_ready, h_ready, h_saved = sem("cell_ready"), sem("tanh_ready"), sem("h_ready"), sem("h_saved")
            xin_psum, xp_sig_ready, xp_ready = sem("xin_psum"), sem("xp_sig_ready"), sem("xp_ready")
            k_psum, k_sq_ready, ssq_psum = sem("k_psum"), sem("k_sq_ready"), sem("ssq_psum")
            k_norm_ready, kn_chain = sem("k_norm_ready"), sem("kn_chain")
            q_psum, q_ready = sem("q_psum"), sem("q_ready")
            vb_psum, vb_ready = sem("vb_psum"), sem("vb_ready")
            turned, beta_ready = sem("turned"), sem("beta_ready")
            step_chain, bs_ready, pre_ready = sem("step_chain"), sem("bs_ready"), sem("pre_ready")
            state_ready, s_q_ready, sq_ready = sem("state_ready"), sem("s_q_ready"), sem("sq_ready")
            sq_sig_ready, cell_chain, cell_turned = sem("sq_sig_ready"), sem("cell_chain"), sem("cell_turned")
            out_psum, x_added, table_ready = sem("out_psum"), sem("x_added"), sem("table_ready")
            rx_psum, rxw_ready, r_psum, r_ready, r_saved = (sem(n) for n in ("rx_psum", "rxw_ready", "r_psum", "r_ready", "r_saved"))

            with nc.Block() as block:

                @block.tensor
                def _(pe):
                    def project(w):
                        c = w + delta
                        pe.wait_ge(k_norm_ready, w + 1)
                        if L:
                            pe.wait_ge(h_saved, w * TC + 2)
                        nc.tensor.matmul(x_ps[:, 0:CH].rearrange("p (b t) -> p b t", t=TC), w_in,
                                         y_b[:, :, bass.ds(c * TC, TC)], start=True, stop=True).then_inc(xin_psum, 1)
                        pe.wait_ge(xp_ready, w + 1)
                        for g in range(HG):
                            nc.tensor.matmul(halves(k_ps)[:, g, :], w_k[:, g * P:(g + 1) * P], xp[:, :],
                                             start=True, stop=True).then_inc(k_psum, 1)
                        for g in range(HG):
                            nc.tensor.matmul(halves(q_ps)[:, g, :], w_q[:, g * P:(g + 1) * P], xp[:, :],
                                             start=True, stop=True).then_inc(q_psum, 1)
                        pe.wait_ge(k_sq_ready, w + 1)
                        for g in range(HG):
                            nc.tensor.matmul(halves(ssq_ps)[:, g, :], head_sum, k_sq[:, g, :],
                                             start=True, stop=True).then_inc(ssq_psum, 1)

                    def project_values(w):
                        for n in range(IQ):
                            nc.tensor.matmul(halves(vb_ps[n // 2])[:, n % 2, :], w_vb[:, n, :], xp[:, :],
                                             start=True, stop=True).then_inc(vb_psum, 1)

                    def output(w):
                        if DELTA:
                            pe.wait_ge(q_ready, w + 1)
                        pe.wait_ge(cell_turned, w + 1)
                        for n in range(IQ):
                            last = nc.tensor.matmul(out_ps[:, 0:CH], w_out[:, n, :], cell_f[:, :, n],
                                                    start=(n == 0), stop=(n == IQ - 1))
                        last.then_inc(out_psum, 1)

                    def project_rnn(w):
                        pe.wait_ge(x_added, w + 1)
                        nc.tensor.matmul(r_ps[:, 0:CH].rearrange("p (b t) -> p b t", t=TC), r_wx,
                                         x_b[:, :, bass.ds((w + rnn) * TC, TC)], start=True, stop=True).then_inc(rx_psum, 1)

                    def step(w, s, u):
                        n = w * TC + s
                        if L:
                            nc.tensor.matmul(acc[u][:, 0:4 * B], ident, xw[:, bass.ds((n + lstm * TC) * 4 * B, 4 * B)],
                                             start=True, stop=False)
                        if R:
                            pe.wait_ge(rxw_ready, w + 1)
                            pe.wait_ge(r_ready, n + 1)
                            nc.tensor.matmul(r_ps[:, 0:B], ident, rxw[:, bass.ds(s * B, B)], start=True, stop=False)
                            nc.tensor.matmul(r_ps[:, 0:B], r_wh, r_ring[:, 1 - u, :], start=False, stop=True).then_inc(r_psum, 1)
                        if L:
                            pe.wait_ge(h_ready, n + 1)
                            for g in range(4):
                                last = nc.tensor.matmul(acc[u][:, g * B:(g + 1) * B], wh[:, g * P:(g + 1) * P],
                                                        h_ring[:, 1 - u, :], start=False, stop=(g == 3))
                            last.then_inc(gates_psum, 1)

                    with pe.Fori(0, count) as w:
                        if DELTA:
                            project(w)
                        if R:
                            output(w)
                        if DELTA:
                            project_values(w)
                        if R:
                            project_rnn(w)
                        if L or R:
                            with pe.Fori(0, TC // 2) as i:
                                for u in range(2):
                                    step(w, i * 2 + u, u)

                @block.scalar
                def _(act):
                    if R:
                        act.sem_inc(r_ready, 1)
                    if DELTA:
                        act.sem_inc(k_norm_ready, 1)
                    nc.scalar.activation(sq_sig[:, 0, 0:1], ident[:, 0:1], ACT.Sigmoid).then_inc(table_ready, 1)
                    act.wait_ge(table_ready, 1)

                    def output(w):
                        if DELTA:
                            act.wait_ge(sq_ready, TC * w + 1)
                        nc.scalar.activation(sq_sig[:, :, :], sq[:, :, 0:ROWS], ACT.Sigmoid).then_inc(sq_sig_ready, 1)

                    def project(w):
                        act.wait_ge(xin_psum, w + 1)
                        nc.scalar.activation(xp_sig[:, :], x_ps[:, 0:CH], ACT.Sigmoid).then_inc(xp_sig_ready, 1)
                        if R:
                            output(w)
                        act.wait_ge(k_psum, HG * (w + 1))
                        nc.scalar.activation(k_sq[:, :, :], halves(k_ps), ACT.Square).then_inc(k_sq_ready, 1)
                        act.wait_ge(q_psum, HG * (w + 1))
                        nc.scalar.activation(q_f[:, :, :], halves(q_ps), ACT.Identity).then_inc(q_ready, 1)
                        act.wait_ge(ssq_psum, HG * (w + 1))
                        nc.scalar.activation(k_norm[:, :, :], halves(ssq_ps), ACT.Sqrt).then_inc(k_norm_ready, 1)
                        for n in range(IQ):
                            act.wait_ge(vb_psum, IQ * w + 2 * (n // 2) + 2)
                            nc.scalar.activation(vb_f[:, :, :, n].rearrange("p t b -> p b t"),
                                                 halves(vb_ps[n // 2])[:, n % 2, :].rearrange("p (b t) -> p b t", t=TC),
                                                 ACT.Identity, bias=b_vb[:, n:n + 1]).then_inc(vb_ready, 1)
                        act.wait_ge(turned, (2 * HG + 1) * (w + 1))
                        nc.scalar.activation(vb_t[:, :, ROWS:2 * ROWS], vb_t[:, :, ROWS:2 * ROWS],
                                             ACT.Sigmoid).then_inc(beta_ready, 1)

                    def step(w, s, u):
                        n = w * TC + s
                        if L:
                            act.wait_ge(gates_psum, n + 1)
                            nc.scalar.activation(gates[:, :], acc[u][:, 0:3 * B], ACT.Sigmoid)
                            nc.scalar.activation(cand_cell[:, 0:B], acc[u][:, 3 * B:4 * B], ACT.Tanh).then_inc(gates_ready, 1)
                            act.wait_ge(cell_ready, n + 1)
                            nc.scalar.activation(tanh_c[:, :], cand_cell[:, B:2 * B], ACT.Tanh).then_inc(tanh_ready, 1)
                        if R:
                            act.wait_ge(r_saved, n + 1)
                            act.wait_ge(r_psum, n + 1)
                            nc.scalar.activation(r_ring[:, u, :], r_ps[:, 0:B], ACT.Tanh).then_inc(r_ready, 1)
                        if DELTA:
                            for g in range(HG):
                                act.wait_ge(pre_ready, HG * n + g + 1)
                                nc.scalar.activation(state[:, u, g * IL:(g + 1) * IL, :], pre[:, g * IL:(g + 1) * IL, :],
                                                     ACT.Tanh).then_inc(state_ready, 1)

                    with act.Fori(0, count) as w:
                        if DELTA:
                            project(w)
                        elif R:
                            output(w)
                        with act.Fori(0, TC // 2) as i:
                            for u in range(2):
                                step(w, i * 2 + u, u)

                @block.gpsimd
                def _(pool):
                    if L:
                        pool.sem_inc(h_saved, 2)
                    if R:
                        pool.sem_inc(r_saved, 2)
                    if DELTA:
                        pool.sem_inc(state_ready, HG)

                    def step(w, s, u):
                        n = w * TC + s
                        if DELTA:
                            pool.wait_ge(beta_ready, w + 1)
                            pool.wait_ge(state_ready, HG * (n + 1))
                            nc.gpsimd.tensor_tensor(beta_s[:, :, :], state[:, 1 - u, :, :],
                                                    over_cols(vb_t[:, bass.ds(s, 1), ROWS:2 * ROWS].squeeze(1)),
                                                    ALU.mult).then_inc(bs_ready, 1)
                        if R:
                            pool.wait_ge(r_ready, n + 2)
                            nc.gpsimd.tensor_copy(y_t[:, bass.ds(s + (w + rnn) * TC, 1), :],
                                                  r_ring[:, u:u + 1, :]).then_inc(r_saved, 1)
                        if L:
                            pool.wait_ge(h_ready, n + 2)
                            nc.gpsimd.tensor_copy(y_t[:, bass.ds(s + (w + lstm) * TC, 1), :],
                                                  h_ring[:, u:u + 1, :]).then_inc(h_saved, 1)
                        if DELTA:
                            pool.wait_ge(state_ready, HG * (n + 2))
                            pool.wait_ge(sq_ready, n + 1)
                            nc.gpsimd.tensor_tensor(by_group(s_q[:, :, :]), by_group(state[:, u, :, :]),
                                                    over_rows(q_t[:, bass.ds(s, 1), :, :].squeeze(1)),
                                                    ALU.mult).then_inc(s_q_ready, 1)

                    with pool.Fori(0, count) as w:
                        with pool.Fori(0, TC // 2) as i:
                            for u in range(2):
                                step(w, i * 2 + u, u)

                @block.vector
                def _(dve):
                    if L:
                        dve.sem_inc(h_ready, 1)
                    if DELTA:
                        dve.sem_inc(sq_ready, 1)

                    def project(w):
                        dve.wait_ge(xp_sig_ready, w + 1)
                        nc.vector.tensor_tensor(xp[:, :], xp_sig[:, :], x_ps[:, 0:CH], ALU.mult).then_inc(xp_ready, 1)
                        if R:
                            cell_output(w)
                        dve.wait_ge(q_ready, w + 1)
                        for g in range(HG):
                            nc.vector.transpose(q_t[:, :, g, :], repeated(q_f[:, g, :])).then_inc(turned, 1)
                        dve.wait_ge(vb_ready, IQ * (w + 1))
                        nc.vector.transpose(vb_t[:, :, :], vb_f[:, :, :, :]).then_inc(turned, 1)
                        dve.wait_ge(k_norm_ready, w + 2)
                        nc.vector.tensor_scalar(k_norm[:, :, :], k_norm[:, :, :], KN_EPS, None, ALU.add).then_inc(kn_chain, 1)
                        dve.wait_ge(kn_chain, 3 * w + 1)
                        nc.vector.reciprocal(k_sq[:, :, :], k_norm[:, :, :]).then_inc(kn_chain, 1)
                        dve.wait_ge(kn_chain, 3 * w + 2)
                        nc.vector.tensor_tensor(kn_f[:, :, :], k_sq[:, :, :], halves(k_ps), ALU.mult).then_inc(kn_chain, 1)
                        if R:
                            add_output(w)
                        dve.wait_ge(kn_chain, 3 * w + 3)
                        for g in range(HG):
                            nc.vector.transpose(kn_t[:, :, g, :], repeated(kn_f[:, g, :])).then_inc(turned, 1)
                        dve.wait_ge(turned, (2 * HG + 1) * (w + 1))

                    def lstm_products(n):
                        dve.wait_ge(gates_ready, n + 1)
                        nc.vector.tensor_tensor(both[:, :], gates[:, 0:2 * B], cand_cell[:, :], ALU.mult).then_inc(mul_ready, 1)

                    def lstm_cell(n):
                        dve.wait_ge(mul_ready, n + 1)
                        nc.vector.tensor_tensor(cand_cell[:, B:2 * B], both[:, 0:B], both[:, B:2 * B],
                                                ALU.add).then_inc(cell_ready, 1)

                    def lstm_out(n, u):
                        dve.wait_ge(h_saved, n + 1)
                        dve.wait_ge(tanh_ready, n + 1)
                        nc.vector.tensor_tensor(h_ring[:, u, :], gates[:, 2 * B:3 * B], tanh_c[:, :],
                                                ALU.mult).then_inc(h_ready, 1)

                    def q_sum(w, s):
                        dve.wait_ge(s_q_ready, w * TC + s + 1)
                        nc.vector.tensor_reduce(sq[:, bass.ds(s, 1), 0:ROWS].squeeze(1), s_q[:, :, :], AX_X,
                                                ALU.add).then_inc(sq_ready, 1)

                    def step(w, s, u, behind):
                        n = w * TC + s
                        if DELTA:
                            kn = over_rows(kn_t[:, bass.ds(s, 1), :, :].squeeze(1))
                            dve.wait_ge(state_ready, HG * (n + 1))
                            nc.vector.tensor_tensor(by_group(s_kn[:, :, :]), by_group(state[:, 1 - u, :, :]), kn,
                                                    ALU.mult).then_inc(step_chain, 1)
                            dve.wait_ge(step_chain, 4 * n + 1)
                            nc.vector.tensor_reduce(got[:, :], s_kn[:, :, :], AX_X, ALU.add).then_inc(step_chain, 1)
                        if L:
                            lstm_products(n)
                        if DELTA:
                            dve.wait_ge(step_chain, 4 * n + 2)
                            nc.vector.tensor_tensor(dlt[:, :], vb_t[:, bass.ds(s, 1), 0:ROWS].squeeze(1), got[:, :],
                                                    ALU.subtract).then_inc(step_chain, 1)
                        if L:
                            lstm_cell(n)
                        if DELTA:
                            dve.wait_ge(step_chain, 4 * n + 3)
                            nc.vector.tensor_tensor(by_group(dk[:, :, :]), by_group(over_cols(dlt[:, :])), kn,
                                                    ALU.mult).then_inc(step_chain, 1)
                        if L:
                            lstm_out(n, u)
                        if DELTA:
                            dve.wait_ge(step_chain, 4 * n + 4)
                            dve.wait_ge(bs_ready, n + 1)
                            for g in range(HG):
                                half = slice(g * IL, (g + 1) * IL)
                                nc.vector.tensor_tensor(pre[:, half, :], dk[:, half, :], beta_s[:, half, :],
                                                        ALU.add).then_inc(pre_ready, 1)
                            if behind:
                                q_sum(w, s - 1)

                    def cell_output(w):
                        if DELTA:
                            dve.wait_ge(sq_ready, TC * w + 1)
                        nc.vector.tensor_tensor(sq_sq[:, :, :], sq[:, :, 0:ROWS], sq[:, :, 0:ROWS],
                                                ALU.mult).then_inc(cell_chain, 1)
                        dve.wait_ge(sq_sig_ready, w + 1)
                        dve.wait_ge(cell_chain, 2 * w + 1)
                        nc.vector.tensor_tensor(sq[:, :, 0:ROWS], sq_sq[:, :, :], sq_sig[:, :, :],
                                                ALU.mult).then_inc(cell_chain, 1)
                        dve.wait_ge(cell_chain, 2 * w + 2)
                        nc.vector.transpose(cell_f[:, :, :].rearrange("p n q -> p (n q)"),
                                            sq[:, :, :].rearrange("p t r -> p (t r)")).then_inc(cell_turned, 1)

                    def add_output(w):
                        dve.wait_ge(out_psum, w + 1)
                        out_x = x_t[:, bass.ds((w + rnn) * TC, TC), :]
                        nc.vector.tensor_tensor(out_x, out_ps[:, 0:CH].rearrange("p (t b) -> p t b", b=B), out_x,
                                                ALU.add).then_inc(x_added, 1)
                        dve.wait_ge(rx_psum, w + 1)
                        nc.vector.tensor_scalar(rxw_by_seq, r_ps[:, 0:CH].rearrange("p (b t) -> p b t", t=TC), r_bias,
                                                None, ALU.add).then_inc(rxw_ready, 1)

                    with dve.Fori(0, count) as w:
                        if DELTA:
                            project(w)
                        elif R:
                            cell_output(w)
                            add_output(w)
                        if DELTA or L:
                            step(w, 0, 0, False)
                            step(w, 1, 1, True)
                            with dve.Fori(1, TC // 2) as i:
                                for u in range(2):
                                    step(w, i * 2 + u, u, True)
                        if DELTA:
                            q_sum(w, TC - 1)

            clear_stage_semaphores(nc)

        start()
        waves("first", 1, 0, None, None)
        waves("second", 1, 1, 0, None)
        waves("all", NTC - 2, 2, 1, 0)
        waves("late", 1, None, NTC - 1, NTC - 2)
        waves("last", 1, None, None, NTC - 1)


def delta_weights(i):
    def heads(w):
        return w.reshape(HG, 4, IQ, IL, -1)

    vb = np.zeros((IQ, 4, 2, HG, IL, D), np.float32)
    vb[:, :, 0] = heads(i["L2_attn_W_v"]).transpose(2, 1, 0, 3, 4)
    vb[:, :, 1] = heads(i["L2_attn_W_beta"]).transpose(2, 1, 0, 3, 4)
    bias = np.zeros((IQ, 4, 2, HG, IL), np.float32)
    bias[:, :, 1] = heads(i["L2_attn_b_beta"].reshape(-1, 1)).transpose(2, 1, 0, 3, 4)[..., 0]
    out = np.zeros((IQ, 4, 2, HG, IL, D), np.float32)
    out[:, :, 0] = heads(np.ascontiguousarray(i["L2_attn_W_out"].T)).transpose(2, 1, 0, 3, 4)
    return {
        "w_in": i["L2_attn_W_in"].T,
        "w_k": i["L2_attn_W_k"].T,
        "w_q": i["L2_attn_W_q"].T,
        "w_vb": vb.reshape(IQ, P, D).transpose(2, 0, 1),
        "b_vb": bias.reshape(IQ, P).T,
        "w_out": out.reshape(IQ, P, D).transpose(1, 0, 2),
    }
NHEAD, HD = 16, 8
QUAD = 32
NQUAD = 4
RUNS = NHEAD // NQUAD
HALF = T // 2
SPAN = HALF + T
UNITS = NHEAD // 2
UBLK = 6


def attention_stage(nc, tag, src, x, wq, wk, wv, wo, cos, sin, ident, ident_bf, mask_bf, kv_heads):
    krun = kv_heads // NQUAD
    vc = kv_heads * HD
    scale = float(HD) ** -0.5
    with ExitStack() as stack:
        mem = Memory(nc, stack, tag)
        y = mem.sb("y", [P, T])
        q_cos, q_sin = mem.sb("q_cos", [P, RUNS, T]), mem.sb("q_sin", [P, RUNS, T])
        k_cos, k_sin = mem.sb("k_cos", [P, krun, T]), mem.sb("k_sin", [P, krun, T])
        q, k = mem.sb("q", [P, RUNS, T]), mem.sb("k", [P, krun, T])
        v_top, v_low = mem.sb("v_top", [P, 2, kv_heads, HD + 1], BF16), mem.sb("v_low", [P, 2, kv_heads, HD + 1], BF16)
        v_rest = mem.sb("v_rest", [P, 2, kv_heads, HD + 1])
        v_part = v_top[:, :, :, :], high(v_rest[:, :, :, :]), v_low[:, :, :, :]
        top = mem.sb("top", [P, 2, 2, 2])
        prob = mem.sb("prob", [P, 2, 2 * SPAN])
        prob_t = mem.sb("prob_t", [P, 2, UBLK, HALF])
        rest_t = mem.sb("rest_t", [P, 2, UBLK, HALF])
        low_t = mem.sb("low_t", [P, 2, UBLK, HALF], BF16)
        inv = mem.sb("inv", [P, 2, NHEAD])
        heads = mem.sb("heads", [P, 2, NHEAD * HD])
        heads_t = mem.sb("heads_t", [P, T])
        s_ps = mem.ps("s_ps", [P, NQUAD, CHUNK])
        t_ps = mem.ps("t_ps", [P, 2, CHUNK])
        v_bank = mem.ps("v_bank", [P, CHUNK])
        o_ps = mem.ps("o_ps", [P, CHUNK])
        out_heads = o_ps[:, 0:2 * NHEAD * (HD + 1)].rearrange("p (a h e) -> p a h e", a=2, e=HD + 1)
        t_blocks = t_ps[:, :, 0:UBLK // 2 * HALF]
        v_ps = v_bank[:, 0:2 * vc].rearrange("p (a h e) -> p a h e", a=2, e=HD)

        def wide(bank):
            return s_ps[:, bank:bank + 2, :].rearrange("p n (r t) -> p (n r) t", t=T)

        k_wide = [wide(0), wide(2)] if krun > 1 else [t_ps[:, 0, 0:T].unsqueeze(1), t_ps[:, 1, 0:T].unsqueeze(1)]

        y_ready, ones_ready = mem.sem("y_ready"), mem.sem("ones_ready")
        q_psum, q_turned, q_ready = mem.sem("q_psum"), mem.sem("q_turned"), mem.sem("q_ready")
        k_psum, k_turned, k_ready = mem.sem("k_psum"), mem.sem("k_turned"), mem.sem("k_ready")
        v_psum, v_ready = mem.sem("v_psum"), mem.sem("v_ready")
        s_psum, top_ready, s_ready = mem.sem("s_psum"), mem.sem("top_ready"), mem.sem("s_ready")
        p_ready, t_psum, t_ready = mem.sem("p_ready"), mem.sem("t_psum"), mem.sem("t_ready")
        o_psum, inv_ready, o_ready = mem.sem("o_psum"), mem.sem("inv_ready"), mem.sem("o_ready")
        ot_psum, ot_ready = mem.sem("ot_psum"), mem.sem("ot_ready")
        out_psum, x_added = mem.sem("out_psum"), mem.sem("x_added")
        table_ready, v_split = mem.sem("table_ready"), mem.sem("v_split")
        rest_ready, low_ready = mem.sem("rest_ready"), mem.sem("low_ready")

        def quadrants(u):
            return range(u % 2 * 2, u % 2 * 2 + 2)

        def block_of(half, g, n):
            return g % 2 if half == 0 else 2 + 2 * (g % 2) + n

        def span(half):
            return half * 2 * HALF, 2 * HALF * (half + 1)

        with nc.Block() as block:

            @block.gpsimd
            def _(pool):
                nc.gpsimd.memset(v_top[:, :, :, HD:HD + 1], 1.0).then_inc(ones_ready, 1)
                nc.gpsimd.memset(v_rest[:, :, :, HD:HD + 1], 0.0).then_inc(ones_ready, 1)

                def project(n):
                    nc.gpsimd.tensor_copy(y[:, :], src[:, bass.ds(n * T, T)]).then_inc(y_ready, 1)
                    pool.wait_ge(q_turned, 2 * n + 2)
                    nc.gpsimd.tensor_tensor(q[:, :, :], q_cos[:, :, :], q_sin[:, :, :], ALU.add).then_inc(q_ready, 1)
                    pool.wait_ge(k_turned, 2 * n + 2)
                    nc.gpsimd.tensor_tensor(k[:, :, :], k_cos[:, :, :], k_sin[:, :, :], ALU.add).then_inc(k_ready, 1)
                    pool.wait_ge(v_split, 2 * n + 2)
                    nc.gpsimd.tensor_tensor(v_low[:, :, :, :], v_rest[:, :, :, :], v_part[1], ALU.subtract).then_inc(v_ready, 1)

                project(0)
                with pool.Fori(0, B - 1) as b:
                    pool.wait_ge(k_psum, b + 1)
                    project(b + 1)

            @block.tensor
            def _(pe):
                def project_q(n):
                    pe.wait_ge(y_ready, n + 1)
                    for part in range(2):
                        for r in range(RUNS):
                            last = nc.tensor.matmul(wide(2 * part)[:, r, :], wq[:, part, r, :], y[:, :],
                                                    start=True, stop=True)
                    last.then_inc(q_psum, 1)

                def project_kv(n):
                    for a in range(2):
                        last = nc.tensor.matmul(v_bank[:, a * vc:(a + 1) * vc], y[:, a * HALF:(a + 1) * HALF], wv,
                                                start=True, stop=True)
                    last.then_inc(v_psum, 1)
                    if krun > 1:
                        pe.wait_ge(q_turned, 2 * n + 2)
                    for part in range(2):
                        for r in range(krun):
                            last = nc.tensor.matmul(k_wide[part][:, r, :], wk[:, part, r, :], y[:, :],
                                                    start=True, stop=True)
                    last.then_inc(k_psum, 1)

                def scores(b, u):
                    for half in range(2):
                        keys = (half + 1) * HALF
                        for g in quadrants(u):
                            quad = slice(QUAD * g, QUAD * (g + 1))
                            nc.tensor.matmul(s_ps[:, g, half * T:half * T + keys],
                                             q[quad, u // 2, half * HALF:(half + 1) * HALF], k[quad, u // 2 % krun, 0:keys],
                                             start=True, stop=False)
                        for g in quadrants(u):
                            last = nc.tensor.matmul(s_ps[:, g, half * (T + HALF):half * (T + HALF) + HALF],
                                                    ident_bf, mask_bf, start=False, stop=True)
                    last.then_inc(s_psum, 1)

                def first_scores(n):
                    pe.wait_ge(q_ready, n + 1)
                    pe.wait_ge(k_ready, n + 1)
                    scores(n, 0)

                def turns(b, u):
                    pe.wait_ge(p_ready, UNITS * b + u + 1)
                    if u >= 1:
                        pe.wait_ge(t_ready, UNITS * b + u)
                    for n in range(UBLK):
                        at = n % (UBLK // 2) * HALF
                        last = nc.tensor.transpose(t_ps[:, n // (UBLK // 2), at:at + HALF],
                                                   prob[:, u % 2, n * HALF:(n + 1) * HALF], ident)
                    last.then_inc(t_psum, 1)

                def values(b, u):
                    if u == 0:
                        pe.wait_ge(x_added, b + 1)
                        pe.wait_ge(v_ready, b + 1)
                    pe.wait_ge(low_ready, UNITS * b + u + 1)
                    rows = high(prob_t[:, u % 2, :, :]), high(rest_t[:, u % 2, :, :]), low_t[:, u % 2, :, :]
                    for half in range(2):
                        for g in quadrants(u):
                            head = NQUAD * g + u // 2
                            hv = g if krun == 1 else head
                            terms = [(rows[i][:, block_of(half, g, n), :], v_part[j][:, n, hv, :])
                                     for n in range(half + 1) for i in range(3) for j in range(3 - i)]
                            for m, (keys_first, columns) in enumerate(terms):
                                last = nc.tensor.matmul(out_heads[:, half, head, :], keys_first, columns,
                                                        start=(m == 0), stop=(m == len(terms) - 1))
                    last.then_inc(o_psum, 1)

                def sequence(b, more):
                    for u in range(UNITS):
                        if u + 1 < UNITS:
                            if u >= 1:
                                pe.wait_ge(s_ready, UNITS * b + u)
                            scores(b, u + 1)
                        elif more:
                            pe.wait_ge(s_ready, UNITS * b + u + 1)
                            project_q(b + 1)
                        turns(b, u)
                        if u >= 1:
                            values(b, u - 1)
                    values(b, UNITS - 1)
                    if more:
                        project_kv(b + 1)
                        pe.wait_ge(v_split, 2 * b + 4)
                    pe.wait_ge(o_ready, b + 1)
                    for half in range(2):
                        last = nc.tensor.transpose(v_bank[:, half * HALF:(half + 1) * HALF], heads[:, half, :], ident)
                    last.then_inc(ot_psum, 1)
                    pe.wait_ge(ot_ready, b + 1)
                    nc.tensor.matmul(o_ps[:, 0:T], wo, heads_t[:, :], start=True, stop=True).then_inc(out_psum, 1)
                    if more:
                        first_scores(b + 1)

                project_q(0)
                project_kv(0)
                first_scores(0)
                with pe.Fori(0, B - 1) as b:
                    sequence(b, True)
                sequence(B - 1, False)

            @block.scalar
            def _(act):
                def exps(b, u):
                    act.wait_ge(s_ready, UNITS * b + u + 1)
                    nc.scalar.activation(prob[:, u % 2, :], prob[:, u % 2, :], ACT.Exp, scale=scale).then_inc(p_ready, 1)

                def read_v(n):
                    act.wait_ge(v_psum, n + 1)
                    nc.scalar.activation(v_top[:, :, :, 0:HD], v_ps, ACT.Identity).then_inc(v_split, 1)

                def sequence(b, more):
                    exps(b, 0)
                    for u in range(UNITS):
                        act.wait_ge(t_psum, UNITS * b + u + 1)
                        nc.scalar.activation(prob_t[:, u % 2, :, :].rearrange("p (n m) k -> p n (m k)", n=2), t_blocks,
                                             ACT.Identity).then_inc(t_ready, 1)
                        if u + 1 < UNITS:
                            exps(b, u + 1)
                    if more:
                        read_v(b + 1)
                    act.wait_ge(ot_psum, b + 1)
                    nc.scalar.activation(heads_t[:, :], v_bank[:, 0:T], ACT.Identity).then_inc(ot_ready, 1)

                nc.scalar.activation(inv[:, 0, 0:1], ident[:, 0:1], ACT.Exp).then_inc(table_ready, 1)
                act.wait_ge(table_ready, 1)
                act.wait_ge(ones_ready, 2)
                read_v(0)
                with act.Fori(0, B - 1) as b:
                    sequence(b, True)
                sequence(B - 1, False)

            @block.vector
            def _(dve):
                def rotate(ps, table, out, runs, done):
                    nc.vector.tensor_tensor(out, ps, table.unsqueeze(1).broadcast_to([P, runs, T]),
                                            ALU.mult).then_inc(done, 1)

                def rotate_q(n):
                    dve.wait_ge(q_psum, n + 1)
                    rotate(wide(0), cos, q_cos[:, :, :], RUNS, q_turned)
                    rotate(wide(2), sin, q_sin[:, :, :], RUNS, q_turned)

                def rotate_k(n):
                    dve.wait_ge(k_psum, n + 1)
                    rotate(k_wide[0], cos, k_cos[:, :, :], krun, k_turned)
                    rotate(k_wide[1], sin, k_sin[:, :, :], krun, k_turned)

                def split_v(n):
                    dve.wait_ge(v_split, 2 * n + 1)
                    nc.vector.tensor_tensor(v_rest[:, :, :, 0:HD], v_ps, v_top[:, :, :, 0:HD], ALU.subtract).then_inc(v_split, 1)

                def less_top(b, u):
                    n = UNITS * b + u
                    mine = slice(quadrants(u)[0], quadrants(u)[-1] + 1)
                    dve.wait_ge(s_psum, n + 1)
                    nc.vector.tensor_reduce(top[:, u % 2, 0, :], s_ps[:, mine, 0:HALF], AX_X, ALU.max)
                    nc.vector.tensor_reduce(top[:, u % 2, 1, :], s_ps[:, mine, T:2 * T], AX_X, ALU.max).then_inc(top_ready, 1)
                    dve.wait_ge(top_ready, n + 1)
                    if u >= 2:
                        dve.wait_ge(t_psum, n - 1)
                    for half in range(2):
                        lo, size = span(half)
                        keys = (half + 1) * HALF
                        last = nc.vector.tensor_tensor(
                            prob[:, u % 2, lo:lo + size].rearrange("p (g k) -> p g k", k=keys),
                            s_ps[:, mine, half * T:half * T + keys],
                            top[:, u % 2, half, :].unsqueeze(2).broadcast_to([P, 2, keys]), ALU.subtract)
                    last.then_inc(s_ready, 1)

                def split_probabilities(b, u):
                    n = UNITS * b + u
                    dve.wait_ge(t_ready, n + 1)
                    nc.vector.tensor_tensor(rest_t[:, u % 2, :, :], prob_t[:, u % 2, :, :], high(prob_t[:, u % 2, :, :]),
                                            ALU.subtract).then_inc(rest_ready, 1)
                    dve.wait_ge(rest_ready, n + 1)
                    nc.vector.tensor_tensor(low_t[:, u % 2, :, :], rest_t[:, u % 2, :, :], high(rest_t[:, u % 2, :, :]),
                                            ALU.subtract).then_inc(low_ready, 1)

                def sequence(b, more):
                    less_top(b, 0)
                    for u in range(UNITS):
                        if u + 1 < UNITS:
                            less_top(b, u + 1)
                        elif more:
                            rotate_q(b + 1)
                        split_probabilities(b, u)
                    dve.wait_ge(o_psum, UNITS * (b + 1))
                    nc.vector.reciprocal(inv[:, :, :], out_heads[:, :, :, HD]).then_inc(inv_ready, 1)
                    dve.wait_ge(inv_ready, b + 1)
                    nc.vector.tensor_tensor(heads[:, :, :].rearrange("p a (h e) -> p a h e", e=HD),
                                            out_heads[:, :, :, 0:HD],
                                            inv[:, :, :].unsqueeze(3).broadcast_to([P, 2, NHEAD, HD]),
                                            ALU.mult).then_inc(o_ready, 1)
                    if more:
                        split_v(b + 1)
                        rotate_k(b + 1)
                    dve.wait_ge(out_psum, b + 1)
                    here = x[:, bass.ds(b * T, T)]
                    nc.vector.tensor_tensor(here, o_ps[:, 0:T], here, ALU.add).then_inc(x_added, 1)

                dve.sem_inc(x_added, 1)
                dve.wait_ge(table_ready, 1)
                rotate_q(0)
                split_v(0)
                rotate_k(0)
                with dve.Fori(0, B - 1) as b:
                    sequence(b, True)
                sequence(B - 1, False)


def cond_gate_stage(nc, tag, x, dst, cond, w1, b1, w2, b2):
    with ExitStack() as stack:
        mem = Memory(nc, stack, tag)
        ps = mem.ps("ps", [P, 2, B])
        z, sig, h, gate = (mem.sb(n, [P, B]) for n in ("z", "sig", "h", "gate"))
        z_psum, sig_ready, z_ready, h_ready = (mem.sem(n) for n in ("z_psum", "sig_ready", "z_ready", "h_ready"))
        gate_psum, gate_ready, factor_ready, done = (mem.sem(n) for n in ("gate_psum", "gate_ready", "factor_ready", "done"))
        with nc.Block() as block:

            @block.tensor
            def _(pe):
                nc.tensor.matmul(ps[:, 0, :], w1, cond, start=True, stop=True).then_inc(z_psum, 1)
                pe.wait_ge(h_ready, 1)
                nc.tensor.matmul(ps[:, 1, :], w2, h[:, :], start=True, stop=True).then_inc(gate_psum, 1)

            @block.scalar
            def _(act):
                act.wait_ge(z_psum, 1)
                nc.scalar.activation(sig[:, :], ps[:, 0, :], ACT.Sigmoid, bias=b1).then_inc(sig_ready, 1)
                act.wait_ge(gate_psum, 1)
                nc.scalar.activation(gate[:, :], ps[:, 1, :], ACT.Sigmoid, bias=b2).then_inc(gate_ready, 1)

            @block.vector
            def _(dve):
                dve.wait_ge(sig_ready, 1)
                nc.vector.tensor_scalar(z[:, :], ps[:, 0, :], b1, None, ALU.add).then_inc(z_ready, 1)
                dve.wait_ge(z_ready, 1)
                nc.vector.tensor_tensor(h[:, :], z[:, :], sig[:, :], ALU.mult).then_inc(h_ready, 1)
                dve.wait_ge(gate_ready, 1)
                nc.vector.tensor_scalar(sig[:, :], gate[:, :], 1.0, None, ALU.add).then_inc(factor_ready, 1)
                dve.wait_ge(factor_ready, 1)
                nc.vector.tensor_tensor(dst.rearrange("p (b t) -> p b t", t=T), x.rearrange("p (b t) -> p b t", t=T),
                                        sig[:, :].unsqueeze(2).broadcast_to([P, B, T]), ALU.mult).then_inc(done, 1)


def attention_weights(w, heads, rotated):
    runs = heads // NQUAD
    cols = w.reshape(D, NQUAD, runs, HD)
    out = np.zeros((D, 2 if rotated else 1, runs, NQUAD, QUAD), np.float32)
    out[:, 0, :, :, :HD] = cols.transpose(0, 2, 1, 3)
    if rotated:
        half = HD // 2
        out[:, 1, :, :, :HD] = np.concatenate([cols[..., half:], cols[..., :half]], -1).transpose(0, 2, 1, 3)
    return out.reshape(D, -1, runs, P)


def rope_tables(repeat):
    half = HD // 2
    freq = (1.0 / 10000.0 ** (np.arange(half, dtype=np.float32) / half)).astype(np.float32)
    angle = np.arange(T, dtype=np.float32)[:, None] * freq[None, :]
    dims = np.repeat(np.arange(half), 2) if repeat else np.tile(np.arange(half), 2)
    sign = np.where(np.arange(HD) < half, -1.0, 1.0)
    cos, sin = np.zeros((2, NQUAD, QUAD, T), np.float32)
    cos[:, :HD] = np.cos(angle).T[dims]
    sin[:, :HD] = np.sin(angle).T[dims] * sign[:, None]
    return cos.reshape(P, T), sin.reshape(P, T)
NEXP = 8
TILES = CHUNK // P
FAR = 3.0e38
MAGIC = 1.5 * 2.0 ** 23


def over_experts(ap):
    return ap.unsqueeze(2).broadcast_to([P, TILES, NEXP])


def over_tiles(ap):
    return ap.unsqueeze(1).broadcast_to([P, TILES, NEXP])


def top2(nc, dve, score, rank, buf, one, picked, chain, at):
    best, buf2 = one
    for n in range(2):
        k = at + 5 * n
        hit = picked if n == 0 else buf2
        nc.vector.tensor_reduce(best, score, AX_X, ALU.max).then_inc(chain, 1)
        dve.wait_ge(chain, k + 1)
        nc.vector.tensor_tensor(buf, score, over_experts(best), ALU.is_equal).then_inc(chain, 1)
        dve.wait_ge(chain, k + 2)
        nc.vector.tensor_tensor(buf, buf, over_tiles(rank), ALU.mult).then_inc(chain, 1)
        dve.wait_ge(chain, k + 3)
        nc.vector.tensor_reduce(best, buf, AX_X, ALU.max).then_inc(chain, 1)
        dve.wait_ge(chain, k + 4)
        last = nc.vector.tensor_tensor(hit, buf, over_experts(best), ALU.is_equal)
        if n == 0:
            last.then_inc(chain, 1)
            dve.wait_ge(chain, k + 5)
            nc.vector.scalar_tensor_tensor(score, picked, -FAR, score, ALU.mult, ALU.add).then_inc(chain, 1)
            at += 1
            dve.wait_ge(chain, k + 6)
        else:
            last.then_inc(chain, 1)
            dve.wait_ge(chain, k + 5)
            nc.vector.tensor_tensor(picked, picked, buf2, ALU.add).then_inc(chain, 1)


TOP2_OPS = 12


def expert_stage(nc, tag, src, x, router, w_gate, b_gate, w_up, b_up, w_down, b_down, rank, ident):
    glu = w_up is not None
    with ExitStack() as stack:
        mem = Memory(nc, stack, tag)
        y = mem.sb("y", [P, CHUNK])
        small = {n: mem.sb(n, [P, TILES, NEXP]) for n in ("prob", "buf", "buf2", "picked", "share", "score")}
        best, norm = mem.sb("best", [P, TILES]), mem.sb("norm", [P, TILES])
        prob, buf, buf2, picked, share, score = (small[n][:, :, :] for n in small)
        share_t = mem.sb("share_t", [NEXP, CHUNK])
        sig, part = mem.sb("sig", [P, 2, CHUNK]), mem.sb("part", [P, 2, CHUNK])
        hidden = mem.sb("hidden", [P, 2, 2, CHUNK])
        acc = mem.sb("acc", [P, TILES, P])
        h_ps = mem.ps("h_ps", [P, 4, CHUNK])
        out_ps = mem.ps("out_ps", [P, 2, TILES, P])
        log_ps, turn_ps = mem.ps("log_ps", [P, CHUNK]), mem.ps("turn_ps", [P, CHUNK])
        logits = log_ps[:, 0:TILES * NEXP].rearrange("p (a e) -> p a e", e=NEXP)
        names = ("y_ready", "log_psum", "chain", "exp_in", "exp_ready", "share_ready", "share_psum", "share_t_ready",
                 "bias_psum", "bias_ready", "h_psum", "sig_ready", "part_ready", "h_ready", "out_psum", "acc_ready",
                 "turn_psum", "x_added")
        s = {n: mem.sem(n) for n in names}
        ROUTE = 5 + TOP2_OPS + (5 if glu else 1)

        with nc.Block() as block:

            @block.gpsimd
            def _(pool):
                pool.sem_inc(s["turn_psum"], 1)
                with pool.Fori(0, NCHUNK) as c:
                    pool.wait_ge(s["turn_psum"], c + 1)
                    nc.gpsimd.tensor_copy(y[:, :], src[:, bass.ds(c * CHUNK, CHUNK)]).then_inc(s["y_ready"], 1)

            @block.tensor
            def _(pe):
                def first_layer(c, e):
                    for n in range(2):
                        unit = 2 * NEXP * c + 2 * e + n
                        if glu:
                            pe.wait_ge(s["h_ready"], unit + 1)
                            nc.tensor.matmul(h_ps[:, 2 * n, :], w_gate[:, e, n * P:(n + 1) * P], y[:, :],
                                             start=True, stop=True)
                            nc.tensor.matmul(h_ps[:, 2 * n + 1, :], w_up[:, e, n * P:(n + 1) * P], y[:, :],
                                             start=True, stop=True).then_inc(s["h_psum"], 1)
                        else:
                            if e >= 2:
                                pe.wait_ge(s["h_ready"], unit - 1)
                            nc.tensor.matmul(h_ps[:, 2 * (e % 2) + n, :], w_gate[:, e, n * P:(n + 1) * P], y[:, :],
                                             start=True, stop=True).then_inc(s["h_psum"], 1)

                def second_layer(c, e):
                    pe.wait_ge(s["h_ready"], 2 * NEXP * c + 2 * e + (4 if glu else 2))
                    if e >= 2:
                        pe.wait_ge(s["acc_ready"], TILES * (NEXP * c + e - 1))
                    for a in range(TILES):
                        for n in range(2):
                            last = nc.tensor.matmul(out_ps[:, e % 2, a, :], hidden[:, e % 2, n, a * P:(a + 1) * P],
                                                    w_down[:, e, n, :], start=(n == 0), stop=(n == 1))
                    last.then_inc(s["out_psum"], 1)

                with pe.Fori(0, NCHUNK) as c:
                    pe.wait_ge(s["y_ready"], c + 1)
                    for a in range(TILES):
                        last = nc.tensor.matmul(logits[:, a, :], y[:, a * P:(a + 1) * P], router, start=True, stop=True)
                    last.then_inc(s["log_psum"], 1)
                    first_layer(c, 0)
                    first_layer(c, 1) if not glu else None
                    pe.wait_ge(s["share_ready"], c + 1)
                    pe.wait_ge(s["x_added"], c + 1)
                    for a in range(TILES):
                        last = nc.tensor.transpose(turn_ps[0:NEXP, a * P:(a + 1) * P], share[:, a, :], ident)
                    last.then_inc(s["share_psum"], 1)
                    pe.wait_ge(s["share_t_ready"], c + 1)
                    for a in range(TILES):
                        last = nc.tensor.matmul(log_ps[:, a * P:(a + 1) * P], share_t[:, a * P:(a + 1) * P], b_down,
                                                start=True, stop=True)
                    last.then_inc(s["bias_psum"], 1)
                    for e in range(NEXP):
                        if glu and e + 1 < NEXP:
                            first_layer(c, e + 1)
                        second_layer(c, e)
                        if not glu and e + 2 < NEXP:
                            first_layer(c, e + 2)
                    pe.wait_ge(s["acc_ready"], TILES * NEXP * (c + 1))
                    for a in range(TILES):
                        last = nc.tensor.transpose(turn_ps[:, a * P:(a + 1) * P], acc[:, a, :], ident)
                    last.then_inc(s["turn_psum"], 1)

            @block.scalar
            def _(act):
                with act.Fori(0, NCHUNK) as c:
                    act.wait_ge(s["exp_in"], c + 1)
                    nc.scalar.activation(prob, score, ACT.Exp).then_inc(s["exp_ready"], 1)
                    for e in range(NEXP):
                        for n in range(2):
                            unit = 2 * NEXP * c + 2 * e + n
                            act.wait_ge(s["h_psum"], unit + 1)
                            if glu:
                                nc.scalar.activation(sig[:, n, :], h_ps[:, 2 * n, :], ACT.Sigmoid,
                                                     bias=b_gate[:, e, n:n + 1]).then_inc(s["sig_ready"], 1)
                            else:
                                if e >= 2:
                                    act.wait_ge(s["out_psum"], NEXP * c + e - 1)
                                nc.scalar.activation(hidden[:, e % 2, n, :], h_ps[:, 2 * (e % 2) + n, :], ACT.Relu,
                                                     bias=b_gate[:, e, n:n + 1]).then_inc(s["h_ready"], 1)

            @block.vector
            def _(dve):
                dve.sem_inc(s["x_added"], 1)
                if glu:
                    dve.sem_inc(s["h_ready"], 2)
                chain = s["chain"]

                def route(c):
                    at = ROUTE * c
                    dve.wait_ge(s["log_psum"], c + 1)
                    nc.vector.tensor_reduce(best[:, :], logits, AX_X, ALU.max).then_inc(chain, 1)
                    dve.wait_ge(chain, at + 1)
                    nc.vector.tensor_tensor(score, logits, over_experts(best[:, :]), ALU.subtract).then_inc(s["exp_in"], 1)
                    dve.wait_ge(s["exp_ready"], c + 1)
                    nc.vector.tensor_reduce(norm[:, :], prob, AX_X, ALU.add).then_inc(chain, 1)
                    dve.wait_ge(chain, at + 2)
                    nc.vector.reciprocal(best[:, :], norm[:, :]).then_inc(chain, 1)
                    dve.wait_ge(chain, at + 3)
                    nc.vector.tensor_tensor(prob, prob, over_experts(best[:, :]), ALU.mult).then_inc(chain, 1)
                    dve.wait_ge(chain, at + 4)
                    nc.vector.tensor_copy(score, prob).then_inc(chain, 1)
                    dve.wait_ge(chain, at + 5)
                    top2(nc, dve, score, rank, buf, (best[:, :], buf2), picked, chain, at + 5)
                    at = at + 5 + TOP2_OPS
                    dve.wait_ge(chain, at)
                    if glu:
                        nc.vector.tensor_tensor(buf, prob, picked, ALU.mult).then_inc(chain, 1)
                        dve.wait_ge(chain, at + 1)
                        nc.vector.tensor_reduce(norm[:, :], buf, AX_X, ALU.add).then_inc(chain, 1)
                        dve.wait_ge(chain, at + 2)
                        nc.vector.tensor_scalar(norm[:, :], norm[:, :], 1e-9, None, ALU.add).then_inc(chain, 1)
                        dve.wait_ge(chain, at + 3)
                        nc.vector.reciprocal(best[:, :], norm[:, :]).then_inc(chain, 1)
                        dve.wait_ge(chain, at + 4)
                        nc.vector.tensor_tensor(share, buf, over_experts(best[:, :]), ALU.mult).then_inc(s["share_ready"], 1)
                        nc.vector.sem_inc(chain, 1)
                    else:
                        nc.vector.tensor_tensor(share, prob, picked, ALU.mult).then_inc(s["share_ready"], 1)
                        nc.vector.sem_inc(chain, 1)
                    dve.wait_ge(s["share_psum"], c + 1)
                    nc.vector.tensor_copy(share_t[:, :], turn_ps[0:NEXP, :]).then_inc(s["share_t_ready"], 1)
                    dve.wait_ge(s["bias_psum"], c + 1)
                    nc.vector.tensor_copy(acc[:, :, :].rearrange("p a d -> p (a d)"), log_ps[:, :]).then_inc(s["bias_ready"], 1)

                def hidden_layer(c, e):
                    for n in range(2):
                        unit = 2 * NEXP * c + 2 * e + n
                        dve.wait_ge(s["sig_ready"], unit + 1)
                        nc.vector.scalar_tensor_tensor(part[:, n, :], h_ps[:, 2 * n, :], b_gate[:, e, n:n + 1],
                                                       sig[:, n, :], ALU.add, ALU.mult).then_inc(s["part_ready"], 1)
                        dve.wait_ge(s["part_ready"], unit + 1)
                        if e >= 2:
                            dve.wait_ge(s["out_psum"], NEXP * c + e - 1)
                        nc.vector.scalar_tensor_tensor(hidden[:, e % 2, n, :], h_ps[:, 2 * n + 1, :],
                                                       b_up[:, e, n:n + 1], part[:, n, :], ALU.add,
                                                       ALU.mult).then_inc(s["h_ready"], 1)

                def add_expert(c, e):
                    dve.wait_ge(s["out_psum"], NEXP * c + e + 1)
                    if e == 0:
                        dve.wait_ge(s["bias_ready"], c + 1)
                    else:
                        dve.wait_ge(s["acc_ready"], TILES * (NEXP * c + e))
                    for a in range(TILES):
                        nc.vector.scalar_tensor_tensor(acc[:, a, :], out_ps[:, e % 2, a, :], share[:, a, e:e + 1],
                                                       acc[:, a, :], ALU.mult, ALU.add).then_inc(s["acc_ready"], 1)

                with dve.Fori(0, NCHUNK) as c:
                    route(c)
                    if glu:
                        hidden_layer(c, 0)
                    for e in range(NEXP):
                        if glu and e + 1 < NEXP:
                            hidden_layer(c, e + 1)
                        add_expert(c, e)
                    dve.wait_ge(s["turn_psum"], c + 2)
                    here = x[:, bass.ds(c * CHUNK, CHUNK)]
                    nc.vector.tensor_tensor(here, turn_ps[:, :], here, ALU.add).then_inc(s["x_added"], 1)


def routed_cond_stage(nc, tag, src, dst, cond, router, router_t, router_bias, sw1, sw3, sw2, rw1, rw2, rank, ones, ident):
    with ExitStack() as stack:
        mem = Memory(nc, stack, tag)
        cond_w = mem.sb("cond_w", [P, B, NEXP])
        t_bias = mem.sb("t_bias", [P, B, NEXP])
        y = mem.sb("y", [P, CHUNK])
        small = {n: mem.sb(n, [P, TILES, NEXP]) for n in ("prob", "buf", "buf2", "picked", "share", "score")}
        prob, buf, buf2, picked, share, score = (small[n][:, :, :] for n in small)
        best, norm, have, even = (mem.sb(n, [P, TILES]) for n in ("best", "norm", "have", "even"))
        sig, part = mem.sb("sig", [P, 2, CHUNK]), mem.sb("part", [P, 2, CHUNK])
        shared = mem.sb("shared", [P, 2, CHUNK])
        routed = mem.sb("routed", [P, NEXP // 2, CHUNK])
        acc = mem.sb("acc", [P, TILES, P])
        h_ps = mem.ps("h_ps", [P, 4, CHUNK])
        out_ps = mem.ps("out_ps", [P, 2, TILES, P])
        log_ps, turn_ps = mem.ps("log_ps", [P, CHUNK]), mem.ps("turn_ps", [P, CHUNK])
        logits = log_ps[:, 0:TILES * NEXP].rearrange("p (a e) -> p a e", e=NEXP)
        names = ("cond_w_ready", "t_psum", "t_bias_ready", "y_ready", "log_psum", "chain", "score_in", "prob_ready",
                 "s_psum", "sig_ready", "part_ready", "shared_ready", "r_psum", "routed_ready", "out_psum", "acc_ready",
                 "turn_psum", "dst_ready")
        s = {n: mem.sem(n) for n in names}
        ROUTE = TOP2_OPS + 9

        with nc.Block() as block:

            @block.gpsimd
            def _(pool):
                pool.sem_inc(s["turn_psum"], 1)
                with pool.Fori(0, NCHUNK) as c:
                    pool.wait_ge(s["turn_psum"], c + 1)
                    nc.gpsimd.tensor_copy(y[:, :], src[:, bass.ds(c * CHUNK, CHUNK)]).then_inc(s["y_ready"], 1)

            @block.tensor
            def _(pe):
                pe.wait_ge(s["cond_w_ready"], 1)
                nc.tensor.matmul(log_ps[:, 0:B * NEXP], ones, cond_w[:, :, :], start=True, stop=True).then_inc(s["t_psum"], 1)
                pe.wait_ge(s["t_bias_ready"], 1)
                with pe.Fori(0, NCHUNK) as c:
                    pe.wait_ge(s["y_ready"], c + 1)
                    for a in range(TILES):
                        last = nc.tensor.matmul(logits[:, a, :], y[:, a * P:(a + 1) * P], router, start=True, stop=True)
                    last.then_inc(s["log_psum"], 1)
                    for n in range(2):
                        nc.tensor.matmul(h_ps[:, 2 * n, :], sw1[:, n * P:(n + 1) * P], y[:, :], start=True, stop=True)
                        nc.tensor.matmul(h_ps[:, 2 * n + 1, :], sw3[:, n * P:(n + 1) * P], y[:, :],
                                         start=True, stop=True).then_inc(s["s_psum"], 1)
                    pe.wait_ge(s["shared_ready"], 2 * c + 2)
                    for m in range(NEXP // 2):
                        nc.tensor.matmul(h_ps[:, m, :], rw1[:, m * P:(m + 1) * P], y[:, :],
                                         start=True, stop=True).then_inc(s["r_psum"], 1)
                    for a in range(TILES):
                        for n in range(2):
                            last = nc.tensor.matmul(out_ps[:, 0, a, :], shared[:, n, a * P:(a + 1) * P], sw2[:, n, :],
                                                    start=(n == 0), stop=(n == 1))
                    last.then_inc(s["out_psum"], 1)
                    for e in range(NEXP):
                        k = (NEXP + 1) * c + e + 1
                        rows = slice(P // 2 * (e % 2), P // 2 * (e % 2 + 1))
                        pe.wait_ge(s["routed_ready"], NEXP // 2 * c + e // 2 + 1)
                        if e >= 1:
                            pe.wait_ge(s["acc_ready"], TILES * (k - 1))
                        for a in range(TILES):
                            last = nc.tensor.matmul(out_ps[:, (e + 1) % 2, a, :], routed[rows, e // 2, a * P:(a + 1) * P],
                                                    rw2[rows, e // 2, :], start=True, stop=True)
                        last.then_inc(s["out_psum"], 1)
                    pe.wait_ge(s["acc_ready"], TILES * (NEXP + 1) * (c + 1))
                    for a in range(TILES):
                        last = nc.tensor.transpose(turn_ps[:, a * P:(a + 1) * P], acc[:, a, :], ident)
                    last.then_inc(s["turn_psum"], 1)

            @block.scalar
            def _(act):
                with act.Fori(0, NCHUNK) as c:
                    act.wait_ge(s["score_in"], c + 1)
                    nc.scalar.activation(prob, score, ACT.Sigmoid).then_inc(s["prob_ready"], 1)
                    for n in range(2):
                        act.wait_ge(s["s_psum"], 2 * c + n + 1)
                        nc.scalar.activation(sig[:, n, :], h_ps[:, 2 * n, :], ACT.Sigmoid).then_inc(s["sig_ready"], 1)
                    for m in range(NEXP // 2):
                        act.wait_ge(s["r_psum"], NEXP // 2 * c + m + 1)
                        nc.scalar.activation(routed[:, m, :], h_ps[:, m, :], ACT.Gelu).then_inc(s["routed_ready"], 1)
                    act.wait_ge(s["turn_psum"], c + 2)
                    nc.scalar.activation(dst[:, bass.ds(c * CHUNK, CHUNK)], turn_ps[:, :], ACT.Identity,
                                         scale=1.0 / 3.0).then_inc(s["dst_ready"], 1)

            @block.vector
            def _(dve):
                chain = s["chain"]
                nc.vector.tensor_tensor(cond_w[:, :, :], cond.unsqueeze(2).broadcast_to([P, B, NEXP]),
                                        router_t.unsqueeze(1).broadcast_to([P, B, NEXP]), ALU.mult).then_inc(s["cond_w_ready"], 1)
                dve.wait_ge(s["t_psum"], 1)
                nc.vector.tensor_copy(t_bias[:, :, :].rearrange("p b e -> p (b e)"),
                                      log_ps[:, 0:B * NEXP]).then_inc(s["t_bias_ready"], 1)
                dve.wait_ge(s["t_bias_ready"], 1)
                SEQS = CHUNK // T

                def route(c):
                    at = ROUTE * c
                    dve.wait_ge(s["log_psum"], c + 1)
                    for q in range(SEQS):
                        half = slice(q * TILES // SEQS, (q + 1) * TILES // SEQS)
                        last = nc.vector.tensor_tensor(score[:, half, :], logits[:, half, :],
                                                       t_bias[:, bass.ds(c * SEQS + q, 1), :].broadcast_to(
                                                           [P, TILES // SEQS, NEXP]), ALU.add)
                    last.then_inc(s["score_in"], 1)
                    dve.wait_ge(s["prob_ready"], c + 1)
                    nc.vector.tensor_tensor(score, prob, over_tiles(router_bias), ALU.add).then_inc(chain, 1)
                    dve.wait_ge(chain, at + 1)
                    top2(nc, dve, score, rank, buf, (best[:, :], buf2), picked, chain, at + 1)
                    at = at + 1 + TOP2_OPS
                    dve.wait_ge(chain, at)
                    nc.vector.tensor_tensor(buf, prob, picked, ALU.mult).then_inc(chain, 1)
                    dve.wait_ge(chain, at + 1)
                    nc.vector.tensor_reduce(norm[:, :], buf, AX_X, ALU.add).then_inc(chain, 1)
                    dve.wait_ge(chain, at + 2)
                    nc.vector.tensor_scalar(have[:, :], norm[:, :], 1e-9, None, ALU.is_gt).then_inc(chain, 1)
                    nc.vector.tensor_scalar(norm[:, :], norm[:, :], 1e-9, None, ALU.add).then_inc(chain, 1)
                    dve.wait_ge(chain, at + 4)
                    nc.vector.reciprocal(best[:, :], norm[:, :]).then_inc(chain, 1)
                    nc.vector.tensor_scalar(even[:, :], have[:, :], -0.5, 0.5, ALU.mult, ALU.add).then_inc(chain, 1)
                    dve.wait_ge(chain, at + 6)
                    nc.vector.tensor_tensor(norm[:, :], best[:, :], have[:, :], ALU.mult)
                    nc.vector.tensor_tensor(buf2, picked, over_experts(even[:, :]), ALU.mult).then_inc(chain, 1)
                    dve.wait_ge(chain, at + 7)
                    nc.vector.tensor_tensor(buf, buf, over_experts(norm[:, :]), ALU.mult).then_inc(chain, 1)
                    dve.wait_ge(chain, at + 8)
                    nc.vector.tensor_tensor(share, buf, buf2, ALU.add)

                with dve.Fori(0, NCHUNK) as c:
                    route(c)
                    for n in range(2):
                        m = 2 * c + n
                        dve.wait_ge(s["sig_ready"], m + 1)
                        nc.vector.tensor_tensor(part[:, n, :], h_ps[:, 2 * n, :], sig[:, n, :], ALU.mult).then_inc(s["part_ready"], 1)
                        dve.wait_ge(s["part_ready"], m + 1)
                        nc.vector.tensor_tensor(shared[:, n, :], h_ps[:, 2 * n + 1, :], part[:, n, :],
                                                ALU.mult).then_inc(s["shared_ready"], 1)
                    dve.wait_ge(s["out_psum"], (NEXP + 1) * c + 1)
                    nc.vector.tensor_copy(acc[:, :, :], out_ps[:, 0, :, :]).then_inc(s["acc_ready"], TILES)
                    for e in range(NEXP):
                        k = (NEXP + 1) * c + e + 1
                        dve.wait_ge(s["out_psum"], k + 1)
                        dve.wait_ge(s["acc_ready"], TILES * k)
                        for a in range(TILES):
                            nc.vector.scalar_tensor_tensor(acc[:, a, :], out_ps[:, (e + 1) % 2, a, :], share[:, a, e:e + 1],
                                                           acc[:, a, :], ALU.mult, ALU.add).then_inc(s["acc_ready"], 1)


def ternary_stage(nc, tag, src, x, w, bias):
    with ExitStack() as stack:
        mem = Memory(nc, stack, tag)
        most, size = mem.sb("most", [P, 1]), mem.sb("size", [P, 1])
        most_all, size_all = mem.sb("most_all", [P, 1]), mem.sb("size_all", [P, 1])
        step, inv, over, under, back = (mem.sb(n, [P, 1]) for n in ("step", "inv", "over", "under", "back"))
        below = mem.sb("below", [P, P])
        wq = mem.sb("wq", [P, P], BF16)
        num = mem.sb("num", [P, TOK])
        xq = mem.sb("xq", [P, TOK], BF16)
        out = mem.sb("out", [P, 2, CHUNK])
        ps = mem.ps("ps", [P, NCHUNK, CHUNK])
        sizes_ready, all_ready, chain = mem.sem("sizes_ready"), mem.sem("all_ready"), mem.sem("chain")
        out_psum, out_ready, x_added = mem.sem("out_psum"), mem.sem("out_ready"), mem.sem("x_added")

        with nc.Block() as block:

            @block.gpsimd
            def _(pool):
                pool.wait_ge(sizes_ready, 2)
                nc.gpsimd.partition_all_reduce(most_all[:, :], most[:, :], P, RMAX).then_inc(all_ready, 1)
                nc.gpsimd.partition_all_reduce(size_all[:, :], size[:, :], P, RADD).then_inc(all_ready, 1)

            @block.vector
            def _(dve):
                nc.vector.tensor_reduce(most[:, :], src, AX_X, ALU.max, apply_absolute_value=True).then_inc(sizes_ready, 1)
                nc.vector.tensor_reduce(size[:, :], w, AX_X, ALU.add, apply_absolute_value=True).then_inc(sizes_ready, 1)
                dve.wait_ge(all_ready, 2)
                nc.vector.tensor_scalar(step[:, :], most_all[:, :], 1.0 / 127.0, None, ALU.mult).then_inc(chain, 1)
                nc.vector.tensor_scalar(over[:, :], size_all[:, :], 0.5 / (P * P), None, ALU.mult).then_inc(chain, 1)
                nc.vector.tensor_scalar(under[:, :], size_all[:, :], -0.5 / (P * P), None, ALU.mult).then_inc(chain, 1)
                dve.wait_ge(chain, 3)
                nc.vector.reciprocal(inv[:, :], step[:, :]).then_inc(chain, 1)
                nc.vector.tensor_scalar(below[:, :], w, under[:, 0:1], None, ALU.is_lt).then_inc(chain, 1)
                nc.vector.scalar_tensor_tensor(back[:, :], over[:, :], 2.0, step[:, :], ALU.mult, ALU.mult).then_inc(chain, 1)
                dve.wait_ge(chain, 6)
                nc.vector.scalar_tensor_tensor(wq[:, :], w, over[:, 0:1], below[:, :], ALU.is_gt,
                                               ALU.subtract).then_inc(chain, 1)
                nc.vector.tensor_scalar(num[:, :], src, inv[:, 0:1], MAGIC, ALU.mult, ALU.add).then_inc(chain, 1)
                dve.wait_ge(chain, 8)
                nc.vector.tensor_scalar(num[:, :], num[:, :], MAGIC, 127.0, ALU.subtract, ALU.min).then_inc(chain, 1)
                dve.wait_ge(chain, 9)
                nc.vector.tensor_scalar(xq[:, :], num[:, :], -128.0, None, ALU.max).then_inc(chain, 1)
                for c in range(NCHUNK):
                    dve.wait_ge(out_psum, c + 1)
                    if c >= 2:
                        dve.wait_ge(x_added, c - 1)
                    nc.vector.tensor_scalar(out[:, c % 2, :], ps[:, c, :], back[:, 0:1], bias, ALU.mult,
                                            ALU.add).then_inc(out_ready, 1)
                    dve.wait_ge(out_ready, c + 1)
                    here = x[:, c * CHUNK:(c + 1) * CHUNK]
                    nc.vector.tensor_tensor(here, out[:, c % 2, :], here, ALU.add).then_inc(x_added, 1)

            @block.tensor
            def _(pe):
                pe.wait_ge(chain, 10)
                for c in range(NCHUNK):
                    nc.tensor.matmul(ps[:, c, :], wq[:, :], xq[:, c * CHUNK:(c + 1) * CHUNK],
                                     start=True, stop=True).then_inc(out_psum, 1)


BIT_INNER = 512
BIT_BLOCKS = BIT_INNER // P


def bit_ffn_stage(nc, tag, src, x, w, ident, ident_bf):
    with ExitStack() as stack:
        mem = Memory(nc, stack, tag)
        size, size_all, mean, winv = (mem.sb(n, [P, 3]) for n in ("size", "size_all", "mean", "winv"))
        wnum = mem.sb("wnum", [P, 3, BIT_INNER])
        wq = mem.sb("wq", [P, 3, BIT_INNER], BF16)
        y = mem.sb("y", [P, 2, P])
        top, quant, back = mem.sb("top", [P, 2, 1]), mem.sb("quant", [P, 2, 1]), mem.sb("back", [P, 2, 2])
        top_p, quant_p, back_p = mem.sb("top_p", [P, 1]), mem.sb("quant_p", [P, 1]), mem.sb("back_p", [P, 2, 1])
        num = mem.sb("num", [P, P])
        yq, yq_t = mem.sb("yq", [P, P], BF16), mem.sb("yq_t", [P, P], BF16)
        sig, act_gate = mem.sb("sig", [P, 2, BIT_INNER]), mem.sb("act_gate", [P, BIT_INNER])
        prod, pnum = mem.sb("prod", [P, BIT_INNER]), mem.sb("pnum", [P, BIT_INNER])
        pq = mem.sb("pq", [P, BIT_INNER], BF16)
        pq_t = mem.sb("pq_t", [P, BIT_BLOCKS, P], BF16)
        out = mem.sb("out", [P, P])
        y_ps, turned_ps = mem.ps("y_ps", [P, CHUNK]), mem.ps("turned_ps", [P, 2 * CHUNK], BF16)
        gate_ps, up_ps = mem.ps("gate_ps", [P, 2, CHUNK]), mem.ps("up_ps", [P, 2, CHUNK])
        out_ps, turn_ps = mem.ps("out_ps", [P, CHUNK]), mem.ps("turn_ps", [P, CHUNK])
        pq_blocks = turned_ps[:, 0:BIT_INNER].rearrange("p (n k) -> p n k", k=P)
        yq_ps = turned_ps[:, BIT_INNER:BIT_INNER + P]
        names = ("size_ready", "all_ready", "wchain", "y_ready", "y_psum", "first_chain", "second_chain", "yq_ready", "yq_psum",
                 "yq_t_ready", "gate_psum", "up_psum", "sig_ready", "pq_ready", "pq_psum", "pq_t_ready", "out_psum",
                 "out_ready", "turn_psum", "x_added")
        s = {n: mem.sem(n) for n in names}
        NT = TOK // P

        def tiles(engine, tile):
            with engine.Fori(0, NT // 2 - 1) as i:
                for u in range(2):
                    tile(i * 2 + u, u, 2)
            tile(NT - 2, 0, 1)
            tile(NT - 1, 1, 0)

        with nc.Block() as block:

            @block.gpsimd
            def _(pool):
                pool.wait_ge(s["size_ready"], 1)
                nc.gpsimd.partition_all_reduce(size_all[:, :], size[:, :], P, RADD).then_inc(s["all_ready"], 1)
                pool.sem_inc(s["y_psum"], 2)
                with pool.Fori(0, NT // 2) as i:
                    for u in range(2):
                        n = i * 2 + u
                        pool.wait_ge(s["y_psum"], n + 1)
                        nc.gpsimd.tensor_copy(y[:, u, :], src[:, bass.ds(n * P, P)]).then_inc(s["y_ready"], 1)

            @block.tensor
            def _(pe):
                def turn_input(n, u):
                    pe.wait_ge(s["y_ready"], n + 1)
                    nc.tensor.transpose(y_ps[:, 0:P], y[:, u, :], ident).then_inc(s["y_psum"], 1)

                def turn_integers(n):
                    pe.wait_ge(s["yq_ready"], n + 2)
                    nc.tensor.transpose(yq_ps, yq[:, :], ident_bf).then_inc(s["yq_psum"], 1)

                def gate_and_up(n, u):
                    pe.wait_ge(s["yq_t_ready"], n + 1)
                    nc.tensor.matmul(gate_ps[:, u, :], yq_t[:, :], wq[:, 0, :], start=True, stop=True).then_inc(s["gate_psum"], 1)
                    nc.tensor.matmul(up_ps[:, u, :], yq_t[:, :], wq[:, 1, :], start=True, stop=True).then_inc(s["up_psum"], 1)

                def down(n):
                    pe.wait_ge(s["pq_ready"], n + 1)
                    for m in range(BIT_BLOCKS):
                        last = nc.tensor.transpose(pq_blocks[:, m, :], pq[:, m * P:(m + 1) * P], ident_bf)
                    last.then_inc(s["pq_psum"], 1)
                    pe.wait_ge(s["pq_t_ready"], n + 1)
                    for m in range(BIT_BLOCKS):
                        last = nc.tensor.matmul(out_ps[:, 0:P], pq_t[:, m, :], wq[:, 2, m * P:(m + 1) * P],
                                                start=(m == 0), stop=(m == BIT_BLOCKS - 1))
                    last.then_inc(s["out_psum"], 1)
                    pe.wait_ge(s["out_ready"], n + 1)
                    pe.wait_ge(s["x_added"], n + 1)
                    nc.tensor.transpose(turn_ps[:, 0:P], out[:, :], ident).then_inc(s["turn_psum"], 1)

                def tile(n, u, more):
                    if more:
                        turn_integers(n + 1)
                        if more > 1:
                            turn_input(n + 2, u)
                        gate_and_up(n + 1, 1 - u)
                    down(n)

                turn_input(0, 0)
                turn_integers(0)
                turn_input(1, 1)
                gate_and_up(0, 0)
                tiles(pe, tile)

            @block.scalar
            def _(act):
                def first_half(n, u):
                    act.wait_ge(s["yq_psum"], n + 1)
                    nc.scalar.activation(yq_t[:, :], yq_ps, ACT.Identity).then_inc(s["yq_t_ready"], 1)
                    act.wait_ge(s["gate_psum"], n + 1)
                    nc.scalar.activation(sig[:, u, :], gate_ps[:, u, :], ACT.Sigmoid, scale=back[:, u, 0:1]).then_inc(s["sig_ready"], 1)

                def tile(n, u, more):
                    if more:
                        first_half(n + 1, 1 - u)
                    act.wait_ge(s["pq_psum"], n + 1)
                    nc.scalar.activation(pq_t[:, :, :], pq_blocks, ACT.Identity).then_inc(s["pq_t_ready"], 1)
                    act.wait_ge(s["out_psum"], n + 1)
                    nc.scalar.activation(out[:, :], out_ps[:, 0:P], ACT.Identity, scale=back_p[:, u, :]).then_inc(s["out_ready"], 1)

                first_half(0, 0)
                tiles(act, tile)

            @block.vector
            def _(dve):
                wchain, chain, pchain = s["wchain"], s["first_chain"], s["second_chain"]
                nc.vector.tensor_reduce(size[:, :], w, AX_X, ALU.add, apply_absolute_value=True).then_inc(s["size_ready"], 1)
                dve.sem_inc(s["x_added"], 1)
                dve.wait_ge(s["all_ready"], 1)
                nc.vector.tensor_scalar(mean[:, :], size_all[:, :], 1.0 / (P * BIT_INNER), 1e-5, ALU.mult,
                                        ALU.max).then_inc(wchain, 1)
                dve.wait_ge(wchain, 1)
                nc.vector.reciprocal(winv[:, :], mean[:, :]).then_inc(wchain, 1)
                dve.wait_ge(wchain, 2)
                for m in range(3):
                    nc.vector.tensor_scalar(wnum[:, m, :], w[:, m, :], winv[:, m:m + 1], MAGIC, ALU.mult,
                                            ALU.add).then_inc(wchain, 1)
                dve.wait_ge(wchain, 5)
                nc.vector.tensor_scalar(wnum[:, :, :], wnum[:, :, :], MAGIC, 1.0, ALU.subtract, ALU.min).then_inc(wchain, 1)
                dve.wait_ge(wchain, 6)
                nc.vector.tensor_scalar(wq[:, :, :], wnum[:, :, :], -1.0, None, ALU.max).then_inc(s["yq_ready"], 1)

                def first_half(n, u, first=False):
                    at = n * 6
                    dve.wait_ge(s["y_psum"], n + 3)
                    nc.vector.tensor_reduce(top[:, u, :], y_ps[:, 0:P], AX_X, ALU.max,
                                            apply_absolute_value=True).then_inc(chain, 1)
                    dve.wait_ge(chain, at + 1)
                    nc.vector.tensor_scalar(top[:, u, :], top[:, u, :], 1e-5, 1.0 / 127.0, ALU.max, ALU.mult).then_inc(chain, 1)
                    dve.wait_ge(chain, at + 2)
                    nc.vector.reciprocal(quant[:, u, :], top[:, u, :]).then_inc(chain, 1)
                    dve.wait_ge(chain, at + 3)
                    nc.vector.tensor_scalar(num[:, :], y_ps[:, 0:P], quant[:, u, :], MAGIC, ALU.mult, ALU.add).then_inc(chain, 1)
                    nc.vector.tensor_scalar(back[:, u, :], mean[:, 0:2], top[:, u, :], None, ALU.mult).then_inc(chain, 1)
                    dve.wait_ge(chain, at + 5)
                    nc.vector.tensor_scalar(num[:, :], num[:, :], MAGIC, 127.0, ALU.subtract, ALU.min).then_inc(chain, 1)
                    dve.wait_ge(chain, at + 6)
                    if not first:
                        dve.wait_ge(s["yq_psum"], n)
                    nc.vector.tensor_scalar(yq[:, :], num[:, :], -128.0, None, ALU.max).then_inc(s["yq_ready"], 1)

                def second_half(n, u):
                    at = n * 8
                    dve.wait_ge(s["sig_ready"], n + 1)
                    nc.vector.scalar_tensor_tensor(act_gate[:, :], gate_ps[:, u, :], back[:, u, 0:1], sig[:, u, :], ALU.mult,
                                                   ALU.mult).then_inc(pchain, 1)
                    dve.wait_ge(pchain, at + 1)
                    dve.wait_ge(s["up_psum"], n + 1)
                    nc.vector.scalar_tensor_tensor(prod[:, :], up_ps[:, u, :], back[:, u, 1:2], act_gate[:, :], ALU.mult,
                                                   ALU.mult).then_inc(pchain, 1)
                    dve.wait_ge(pchain, at + 2)
                    nc.vector.tensor_reduce(top_p[:, :], prod[:, :], AX_X, ALU.max,
                                            apply_absolute_value=True).then_inc(pchain, 1)
                    dve.wait_ge(pchain, at + 3)
                    nc.vector.tensor_scalar(top_p[:, :], top_p[:, :], 1e-5, 1.0 / 127.0, ALU.max, ALU.mult).then_inc(pchain, 1)
                    dve.wait_ge(pchain, at + 4)
                    nc.vector.reciprocal(quant_p[:, :], top_p[:, :]).then_inc(pchain, 1)
                    dve.wait_ge(pchain, at + 5)
                    nc.vector.tensor_scalar(pnum[:, :], prod[:, :], quant_p[:, :], MAGIC, ALU.mult, ALU.add).then_inc(pchain, 1)
                    nc.vector.tensor_scalar(back_p[:, u, :], mean[:, 2:3], top_p[:, :], None, ALU.mult).then_inc(pchain, 1)
                    dve.wait_ge(pchain, at + 7)
                    nc.vector.tensor_scalar(pnum[:, :], pnum[:, :], MAGIC, 127.0, ALU.subtract, ALU.min).then_inc(pchain, 1)
                    dve.wait_ge(pchain, at + 8)
                    nc.vector.tensor_scalar(pq[:, :], pnum[:, :], -128.0, None, ALU.max).then_inc(s["pq_ready"], 1)

                def add_output(n):
                    dve.wait_ge(s["turn_psum"], n + 1)
                    here = x[:, bass.ds(n * P, P)]
                    nc.vector.tensor_tensor(here, turn_ps[:, 0:P], here, ALU.add).then_inc(s["x_added"], 1)

                first_half(0, 0, True)
                first_half(1, 1)
                second_half(0, 0)
                with dve.Fori(0, NT // 2 - 1) as i:
                    for u in range(2):
                        n = i * 2 + u
                        first_half(n + 2, u)
                        add_output(n)
                        second_half(n + 1, 1 - u)
                add_output(NT - 2)
                second_half(NT - 1, 1)
                add_output(NT - 1)


def threshold_stage(nc, tag, x, dst, draws):
    with ExitStack() as stack:
        mem = Memory(nc, stack, tag)
        size, p, cum, step = (mem.sb(n, [P, B, T]) for n in ("size", "p", "cum", "step"))
        zero = mem.sb("zero", [P, T])
        passed = mem.sb("passed", [P, B, T + 1])
        total, inv, bound = (mem.sb(n, [P, B]) for n in ("total", "inv", "bound"))
        chain, size_ready, p_ready, cum_ready, exp_ready = (mem.sem(n) for n in ("chain", "size_ready", "p_ready", "cum_ready", "exp_ready"))
        xb, db = x.rearrange("p (b t) -> p b t", t=T), dst.rearrange("p (b t) -> p b t", t=T)

        def over_time(ap):
            return ap.unsqueeze(2).broadcast_to([P, B, T])

        with nc.Block() as block:

            @block.scalar
            def _(act):
                nc.scalar.activation(size[:, :, :], xb, ACT.Abs).then_inc(size_ready, 1)
                act.wait_ge(p_ready, 1)
                nc.scalar.activation(p[:, :, :], p[:, :, :], ACT.Exp, scale=2.0).then_inc(exp_ready, 1)

            @block.vector
            def _(dve):
                nc.vector.memset(zero[:, :], 0.0).then_inc(chain, 1)
                nc.vector.memset(passed[:, :, 0:1], 1.0).then_inc(chain, 1)
                dve.wait_ge(size_ready, 1)
                nc.vector.tensor_reduce(total[:, :], size[:, :, :], AX_X, ALU.add).then_inc(chain, 1)
                dve.wait_ge(chain, 3)
                nc.vector.reciprocal(inv[:, :], total[:, :]).then_inc(chain, 1)
                dve.wait_ge(chain, 4)
                nc.vector.tensor_tensor(p[:, :, :], size[:, :, :], over_time(inv[:, :]), ALU.mult).then_inc(p_ready, 1)
                dve.wait_ge(exp_ready, 1)
                nc.vector.tensor_reduce(total[:, :], p[:, :, :], AX_X, ALU.add).then_inc(chain, 1)
                dve.wait_ge(chain, 5)
                nc.vector.reciprocal(inv[:, :], total[:, :]).then_inc(chain, 1)
                dve.wait_ge(chain, 6)
                nc.vector.tensor_tensor(p[:, :, :], p[:, :, :], over_time(inv[:, :]), ALU.mult).then_inc(chain, 1)
                dve.wait_ge(chain, 7)
                for b in range(B):
                    nc.vector.tensor_tensor_scan(cum[:, b, :], p[:, b, :], zero[:, :], 0.0, ALU.add,
                                                 ALU.add).then_inc(cum_ready, 1)
                dve.wait_ge(cum_ready, B)
                nc.vector.scalar_tensor_tensor(passed[:, :, 1:T + 1], cum[:, :, :], 0.001, over_time(draws), ALU.add,
                                               ALU.is_le).then_inc(chain, 1)
                dve.wait_ge(chain, 8)
                nc.vector.tensor_tensor(step[:, :, :], passed[:, :, 0:T], passed[:, :, 1:T + 1], ALU.subtract).then_inc(chain, 1)
                dve.wait_ge(chain, 9)
                nc.vector.tensor_tensor(step[:, :, :], step[:, :, :], size[:, :, :], ALU.mult).then_inc(chain, 1)
                dve.wait_ge(chain, 10)
                nc.vector.tensor_reduce(bound[:, :], step[:, :, :], AX_X, ALU.add).then_inc(chain, 1)
                dve.wait_ge(chain, 11)
                nc.vector.scalar_tensor_tensor(bound[:, :], passed[:, :, T:T + 1].squeeze(2), FAR, bound[:, :], ALU.mult,
                                               ALU.add).then_inc(chain, 1)
                dve.wait_ge(chain, 12)
                nc.vector.tensor_tensor(step[:, :, :], size[:, :, :], over_time(bound[:, :]), ALU.is_ge).then_inc(chain, 1)
                dve.wait_ge(chain, 13)
                nc.vector.tensor_tensor(db, xb, step[:, :, :], ALU.mult).then_inc(chain, 1)
RET_SCALE = float(D) ** -0.5
RET_EPS = 1e-6
RANK = 16


def low_rank_cond_stage(nc, tag, x, dst, w, u_all, v_all, pick, fc_bias, cond):
    with ExitStack() as stack:
        mem = Memory(nc, stack, tag)
        bias = mem.sb("bias", [P, B])
        z = mem.sb("z", [P, 2, T])
        z_ps, y_ps = mem.ps("z_ps", [P, 2, CHUNK]), mem.ps("y_ps", [P, 2, CHUNK])
        z_psum, z_ready, y_psum, dst_ready, bias_ready = (mem.sem(n) for n in ("z_psum", "z_ready", "y_psum", "dst_ready", "bias_ready"))
        with nc.Block() as block:

            @block.tensor
            def _(pe):
                with pe.Fori(0, B // 2) as i:
                    for u in range(2):
                        b = i * 2 + u
                        here = x[:, bass.ds(b * T, T)]
                        pe.wait_ge(z_ready, b + 1)
                        nc.tensor.matmul(z_ps[:, u, 0:T], v_all, here, start=True, stop=True).then_inc(z_psum, 1)
                        pe.wait_ge(dst_ready, b + 1)
                        nc.tensor.matmul(y_ps[:, u, 0:T], w, here, start=True, stop=False)
                        pe.wait_ge(z_ready, b + 3)
                        nc.tensor.matmul(y_ps[:, u, 0:T], u_all, z[:, u, :], start=False, stop=True).then_inc(y_psum, 1)

            @block.vector
            def _(dve):
                nc.vector.tensor_scalar(bias[:, :], cond, fc_bias, None, ALU.add).then_inc(bias_ready, 1)
                dve.sem_inc(z_ready, 2)
                dve.sem_inc(y_psum, 2)
                with dve.Fori(0, B // 2) as i:
                    for u in range(2):
                        b = i * 2 + u
                        dve.wait_ge(z_psum, b + 1)
                        dve.wait_ge(y_psum, b + 1)
                        nc.vector.tensor_scalar(z[:, u, :], z_ps[:, u, 0:T], pick[:, bass.ds(b, 1)], None,
                                                ALU.mult).then_inc(z_ready, 1)

            @block.scalar
            def _(act):
                act.sem_inc(dst_ready, 2)
                act.wait_ge(bias_ready, 1)
                with act.Fori(0, B // 2) as i:
                    for u in range(2):
                        b = i * 2 + u
                        act.wait_ge(y_psum, b + 3)
                        nc.scalar.activation(dst[:, bass.ds(b * T, T)], y_ps[:, u, 0:T], ACT.Gelu,
                                             bias=bias[:, bass.ds(b, 1)]).then_inc(dst_ready, 1)


def retention_stage(nc, tag, src, x, wq, wk, wv, wg, cos, sin, decay, ident, ones_bf):
    W3 = T + HALF
    with ExitStack() as stack:
        mem = Memory(nc, stack, tag)
        y = mem.sb("y", [P, T])
        q_cos, q_sin = mem.sb("q_cos", [P, RUNS, T]), mem.sb("q_sin", [P, RUNS, T])
        q, k = mem.sb("q", [P, RUNS, T]), mem.sb("k", [P, RUNS, T])
        v_top, v_low = mem.sb("v_top", [P, 2 * NHEAD * HD], BF16), mem.sb("v_low", [P, 2 * NHEAD * HD], BF16)
        v_rest = mem.sb("v_rest", [P, 2 * NHEAD * HD])
        v_part = v_top[:, :], high(v_rest[:, :]), v_low[:, :]
        silu_g = mem.sb("silu_g", [P, 2 * NHEAD, HD])
        part, rest = mem.sb("part", [P, 2, NQUAD, W3]), mem.sb("rest", [P, 2, NQUAD, W3])
        low = mem.sb("low", [P, 2, NQUAD, W3], BF16)
        size, size_rest = mem.sb("size", [P, 2, NQUAD, W3]), mem.sb("size_rest", [P, 2, NQUAD, W3])
        size_low = mem.sb("size_low", [P, 2, NQUAD, W3], BF16)
        den, inv, ms, rms, irms = (mem.sb(n, [P, 2 * NHEAD]) for n in ("den", "inv", "ms", "rms", "irms"))
        heads, square = mem.sb("heads", [P, 2 * NHEAD, HD]), mem.sb("square", [P, 2 * NHEAD, HD])
        s_ps = mem.ps("s_ps", [P, NQUAD, CHUNK])
        v_ps, g_ps = mem.ps("v_ps", [P, CHUNK]), mem.ps("g_ps", [P, CHUNK])
        o_ps, turn_ps = mem.ps("o_ps", [P, CHUNK]), mem.ps("turn_ps", [P, CHUNK])
        out_heads = o_ps[:, 0:2 * NHEAD * (HD + 1)].rearrange("p (h e) -> p h e", e=HD + 1)
        g_heads = g_ps[:, 0:T].rearrange("p (h e) -> p h e", e=HD)
        names = ("y_ready", "q_psum", "q_turned", "q_ready", "k_psum", "k_turned", "k_ready", "v_psum", "v_split", "v_ready",
                 "g_psum", "sig_ready", "silu_ready", "s_psum", "part_ready", "rest_ready", "low_ready", "size_ready",
                 "o_psum", "chain", "rms_in", "rms_ready", "o_ready", "turn_psum", "x_added")
        s = {n: mem.sem(n) for n in names}

        def wide(bank):
            return s_ps[:, bank:bank + 2, :].rearrange("p n (r t) -> p (n r) t", t=T)

        def each(ap):
            return ap.unsqueeze(2).broadcast_to([P, 2 * NHEAD, HD])

        with nc.Block() as block:

            @block.gpsimd
            def _(pool):
                def project(n):
                    nc.gpsimd.tensor_copy(y[:, :], src[:, bass.ds(n * T, T)]).then_inc(s["y_ready"], 1)
                    pool.wait_ge(s["q_turned"], 2 * n + 2)
                    nc.gpsimd.tensor_tensor(q[:, :, :], q_cos[:, :, :], q_sin[:, :, :], ALU.add).then_inc(s["q_ready"], 1)
                    pool.wait_ge(s["k_turned"], 2 * n + 2)
                    nc.gpsimd.tensor_tensor(k[:, :, :], q_cos[:, :, :], q_sin[:, :, :], ALU.add).then_inc(s["k_ready"], 1)
                    pool.wait_ge(s["v_split"], 2 * n + 2)
                    nc.gpsimd.tensor_tensor(v_low[:, :], v_rest[:, :], high(v_rest[:, :]), ALU.subtract).then_inc(s["v_ready"], 1)

                project(0)
                with pool.Fori(0, B - 1) as b:
                    pool.wait_ge(s["g_psum"], b + 1)
                    project(b + 1)

            @block.tensor
            def _(pe):
                def project_q(n):
                    pe.wait_ge(s["y_ready"], n + 1)
                    for p in range(2):
                        for r in range(RUNS):
                            last = nc.tensor.matmul(wide(2 * p)[:, r, :], wq[:, p, r, :], y[:, :], start=True, stop=True)
                    last.then_inc(s["q_psum"], 1)

                def project_kvg(n):
                    pe.wait_ge(s["q_turned"], 2 * n + 2)
                    for p in range(2):
                        for r in range(RUNS):
                            last = nc.tensor.matmul(wide(2 * p)[:, r, :], wk[:, p, r, :], y[:, :], start=True, stop=True)
                    last.then_inc(s["k_psum"], 1)
                    for a in range(2):
                        last = nc.tensor.matmul(v_ps[:, a * P:(a + 1) * P], y[:, a * HALF:(a + 1) * HALF], wv, start=True, stop=True)
                    last.then_inc(s["v_psum"], 1)
                    for a in range(2):
                        last = nc.tensor.matmul(g_ps[:, a * P:(a + 1) * P], y[:, a * HALF:(a + 1) * HALF], wg, start=True, stop=True)
                    last.then_inc(s["g_psum"], 1)

                def scores(b, r):
                    for half in range(2):
                        for g in range(NQUAD):
                            quad = slice(QUAD * g, QUAD * (g + 1))
                            last = nc.tensor.matmul(s_ps[:, g, half * T:half * T + T - half * HALF],
                                                    k[quad, r, half * HALF:(half + 1) * HALF],
                                                    q[quad, r, half * HALF:T], start=True, stop=True)
                    last.then_inc(s["s_psum"], 1)

                def first_scores(n):
                    pe.wait_ge(s["q_ready"], n + 1)
                    pe.wait_ge(s["k_ready"], n + 1)
                    scores(n, 0)

                def values(b, r):
                    if r == 0:
                        pe.wait_ge(s["v_ready"], b + 1)
                    pe.wait_ge(s["low_ready"], RUNS * b + r + 1)
                    pe.wait_ge(s["size_ready"], RUNS * b + r + 1)
                    rows = high(part[:, r % 2, :, :]), high(rest[:, r % 2, :, :]), low[:, r % 2, :, :]
                    sizes = high(size[:, r % 2, :, :]), high(size_rest[:, r % 2, :, :]), size_low[:, r % 2, :, :]
                    for half in range(2):
                        for g in range(NQUAD):
                            head = NQUAD * g + r
                            at = NHEAD * half + head
                            blocks = [(n, half * HALF if n == 0 else T) for n in range(half + 1)]
                            terms = [(rows[i][:, g, lo:lo + HALF],
                                      v_part[j][:, n * P + HD * head:n * P + HD * (head + 1)])
                                     for n, lo in blocks for i in range(3) for j in range(3 - i)]
                            for m, (keys_first, columns) in enumerate(terms):
                                nc.tensor.matmul(out_heads[:, at, 0:HD], keys_first, columns,
                                                 start=(m == 0), stop=(m == len(terms) - 1))
                            terms = [sizes[i][:, g, lo:lo + HALF] for n, lo in blocks for i in range(3)]
                            for m, keys_first in enumerate(terms):
                                last = nc.tensor.matmul(out_heads[:, at, HD:HD + 1], keys_first, ones_bf[:, 0:1],
                                                        start=(m == 0), stop=(m == len(terms) - 1))
                    last.then_inc(s["o_psum"], 1)

                def sequence(b, more):
                    for r in range(RUNS):
                        pe.wait_ge(s["part_ready"], RUNS * b + r + 1)
                        if r + 1 < RUNS:
                            scores(b, r + 1)
                        elif more:
                            project_q(b + 1)
                        values(b, r)
                    if more:
                        project_kvg(b + 1)
                    pe.wait_ge(s["o_ready"], b + 1)
                    pe.wait_ge(s["x_added"], b + 1)
                    for n in range(2):
                        last = nc.tensor.transpose(turn_ps[:, n * P:(n + 1) * P],
                                                   square[:, n * NHEAD:(n + 1) * NHEAD, :].rearrange("p h e -> p (h e)"), ident)
                    last.then_inc(s["turn_psum"], 1)
                    if more:
                        first_scores(b + 1)

                project_q(0)
                project_kvg(0)
                first_scores(0)
                with pe.Fori(0, B - 1) as b:
                    sequence(b, True)
                sequence(B - 1, False)

            @block.scalar
            def _(act):
                def gate_and_v(n):
                    act.wait_ge(s["v_psum"], n + 1)
                    nc.scalar.activation(v_top[:, :], v_ps[:, 0:T], ACT.Identity).then_inc(s["v_split"], 1)
                    act.wait_ge(s["g_psum"], n + 1)
                    nc.scalar.activation(silu_g[:, :, :], g_heads, ACT.Sigmoid).then_inc(s["sig_ready"], 1)

                def sequence(b, more):
                    for r in range(RUNS):
                        n = RUNS * b + r
                        if r >= 2:
                            act.wait_ge(s["o_psum"], n - 1)
                        act.wait_ge(s["part_ready"], n + 1)
                        nc.scalar.activation(size[:, r % 2, :, :], part[:, r % 2, :, :], ACT.Abs)
                        act.wait_ge(s["rest_ready"], n + 1)
                        nc.scalar.activation(size_rest[:, r % 2, :, :], rest[:, r % 2, :, :], ACT.Abs)
                        act.wait_ge(s["low_ready"], n + 1)
                        nc.scalar.activation(size_low[:, r % 2, :, :], low[:, r % 2, :, :], ACT.Abs).then_inc(s["size_ready"], 1)
                    act.wait_ge(s["rms_in"], b + 1)
                    nc.scalar.activation(rms[:, :], ms[:, :], ACT.Sqrt).then_inc(s["rms_ready"], 1)
                    if more:
                        act.wait_ge(s["o_ready"], b + 1)
                        gate_and_v(b + 1)

                gate_and_v(0)
                with act.Fori(0, B - 1) as b:
                    sequence(b, True)
                sequence(B - 1, False)

            @block.vector
            def _(dve):
                chain = s["chain"]

                def rotate(ps, table, out, done):
                    nc.vector.tensor_tensor(out, ps, table.unsqueeze(1).broadcast_to([P, RUNS, T]),
                                            ALU.mult).then_inc(done, 1)

                def rotate_q(n):
                    dve.wait_ge(s["q_psum"], n + 1)
                    rotate(wide(0), cos[:, 0, :], q_cos[:, :, :], s["q_turned"])
                    rotate(wide(2), sin[:, 0, :], q_sin[:, :, :], s["q_turned"])

                def rotate_k(n):
                    dve.wait_ge(s["k_psum"], n + 1)
                    dve.wait_ge(s["q_ready"], n + 1)
                    rotate(wide(0), cos[:, 1, :], q_cos[:, :, :], s["k_turned"])
                    rotate(wide(2), sin[:, 1, :], q_sin[:, :, :], s["k_turned"])

                def gate_and_v(n):
                    dve.wait_ge(s["v_split"], 2 * n + 1)
                    nc.vector.tensor_tensor(v_rest[:, :], v_ps[:, 0:T], v_top[:, :], ALU.subtract).then_inc(s["v_split"], 1)
                    dve.wait_ge(s["sig_ready"], n + 1)
                    nc.vector.tensor_tensor(silu_g[:, :, :], silu_g[:, :, :], g_heads, ALU.mult).then_inc(s["silu_ready"], 1)

                def sequence(b, more):
                    at = 7 * b
                    for r in range(RUNS):
                        n = RUNS * b + r
                        dve.wait_ge(s["s_psum"], n + 1)
                        if r >= 2:
                            dve.wait_ge(s["o_psum"], n - 1)
                        nc.vector.tensor_tensor(part[:, r % 2, :, :], s_ps[:, :, 0:W3], decay[:, r, :, :],
                                                ALU.mult).then_inc(s["part_ready"], 1)
                        dve.wait_ge(s["part_ready"], n + 1)
                        nc.vector.tensor_tensor(rest[:, r % 2, :, :], part[:, r % 2, :, :], high(part[:, r % 2, :, :]),
                                                ALU.subtract).then_inc(s["rest_ready"], 1)
                        dve.wait_ge(s["rest_ready"], n + 1)
                        nc.vector.tensor_tensor(low[:, r % 2, :, :], rest[:, r % 2, :, :], high(rest[:, r % 2, :, :]),
                                                ALU.subtract).then_inc(s["low_ready"], 1)
                    if more:
                        rotate_q(b + 1)
                    dve.wait_ge(s["o_psum"], RUNS * (b + 1))
                    nc.vector.tensor_scalar(den[:, :], out_heads[:, :, HD], 1.0, 50000.0, ALU.max, ALU.min).then_inc(chain, 1)
                    dve.wait_ge(chain, at + 1)
                    nc.vector.reciprocal(inv[:, :], den[:, :]).then_inc(chain, 1)
                    dve.wait_ge(chain, at + 2)
                    nc.vector.tensor_tensor(heads[:, :, :], out_heads[:, :, 0:HD], each(inv[:, :]), ALU.mult).then_inc(chain, 1)
                    dve.wait_ge(chain, at + 3)
                    nc.vector.tensor_tensor(square[:, :, :], heads[:, :, :], heads[:, :, :], ALU.mult).then_inc(chain, 1)
                    dve.wait_ge(chain, at + 4)
                    nc.vector.tensor_reduce(den[:, :], square[:, :, :], AX_X, ALU.add).then_inc(chain, 1)
                    dve.wait_ge(chain, at + 5)
                    nc.vector.tensor_scalar(ms[:, :], den[:, :], 1.0 / HD, RET_EPS, ALU.mult, ALU.add).then_inc(s["rms_in"], 1)
                    dve.wait_ge(s["silu_ready"], b + 1)
                    nc.vector.tensor_tensor(heads[:, :, :], heads[:, :, :], silu_g[:, :, :], ALU.mult).then_inc(chain, 1)
                    dve.wait_ge(s["rms_ready"], b + 1)
                    nc.vector.reciprocal(irms[:, :], rms[:, :]).then_inc(chain, 1)
                    dve.wait_ge(chain, at + 7)
                    nc.vector.tensor_tensor(square[:, :, :], heads[:, :, :], each(irms[:, :]), ALU.mult).then_inc(s["o_ready"], 1)
                    if more:
                        rotate_k(b + 1)
                    dve.wait_ge(s["turn_psum"], b + 1)
                    here = x[:, bass.ds(b * T, T)]
                    nc.vector.tensor_tensor(here, turn_ps[:, 0:T], here, ALU.add).then_inc(s["x_added"], 1)
                    if more:
                        gate_and_v(b + 1)

                dve.sem_inc(s["x_added"], 1)
                rotate_q(0)
                rotate_k(0)
                gate_and_v(0)
                with dve.Fori(0, B - 1) as b:
                    sequence(b, True)
                sequence(B - 1, False)


def retention_weights(w):
    cols = w.reshape(D, NQUAD, RUNS, HD)
    out = np.zeros((D, 2, RUNS, NQUAD, QUAD), np.float32)
    out[:, 0, :, :, :HD] = cols.transpose(0, 2, 1, 3)
    out[:, 1, :, :, :HD] = cols.reshape(D, NQUAD, RUNS, HD // 2, 2)[..., ::-1].reshape(cols.shape).transpose(0, 2, 1, 3)
    return out.reshape(D, 2, RUNS, P)


def retention_tables():
    f = np.float32
    angle = np.repeat(1.0 / f(10000.0) ** np.linspace(0.0, 1.0, HD // 2, dtype=f), 2).astype(f)
    turn = (np.arange(T, dtype=f)[:, None] * angle[None, :]).astype(f)
    cos, sin = np.zeros((2, NQUAD, QUAD, 2, T), f)
    sign = np.where(np.arange(HD) % 2 == 0, -1.0, 1.0)
    for n, by in enumerate((1.0, RET_SCALE)):
        cos[:, :HD, n] = np.cos(turn).T * by
        sin[:, :HD, n] = np.sin(turn).T * sign[:, None] * by
    rate = np.log(1.0 - 2.0 ** (-5.0 - np.arange(NHEAD, dtype=f))).astype(f)
    lag = np.arange(T)[:, None] - np.arange(T)[None, :]
    mask = np.where(lag >= 0, np.exp(np.maximum(lag, 0).astype(f) * rate[:, None, None]), 0.0).astype(f)
    mask = (mask / np.sqrt(mask.sum(-1, keepdims=True, dtype=f))).astype(f)
    keys = mask.transpose(0, 2, 1).reshape(NQUAD, RUNS, T, T)
    decay = np.concatenate([keys[:, :, :HALF], keys[:, :, HALF:, HALF:]], -1)
    return cos.reshape(P, 2, T), sin.reshape(P, 2, T), decay.transpose(2, 1, 0, 3)


def packs(i):
    cos0, sin0 = rope_tables(False)
    cos1, sin1 = rope_tables(True)
    cos3, sin3, decay = retention_tables()
    qkv = i["L1_attn_w_qkv"]
    fside = i["fside_Bx1x1024x16_0"][:, 0]
    inch = 1.0 / (D * RANK)
    base = {
        "cond": i["cond_1024"].T,
        "ident": np.eye(P, dtype=np.float32), "mask": np.where(np.tril(np.ones((P, P))), 0.0, -1e30).astype(np.float32),
        "ones": np.ones((P, P), np.float32),
        "rank": np.tile(np.arange(NEXP, 0, -1, dtype=np.float32), (P, 1)),
    }
    l0 = {
        "c_w1": i["L0_cond_W1"].T, "c_b1": i["L0_cond_b1"][:, None],
        "c_w2": i["L0_cond_W2"].T, "c_b2": i["L0_cond_b2"][:, None],
        "wq": attention_weights(i["L0_attn_Wq"], NHEAD, True), "wk": attention_weights(i["L0_attn_Wk"], NQUAD, True),
        "wv": i["L0_attn_Wv"], "wo": i["L0_attn_Wo"], "cos": cos0, "sin": sin0,
        "wx": i["L0_cond2_Wx"], "wh": i["L0_cond2_Wh"], "b": i["L0_cond2_b"].reshape(4, P).T,
        "f_w": i["L0_ffn_weight"].T, "f_b": i["L0_ffn_bias"][:, None],
    }
    l1 = {
        "wq": attention_weights(qkv[:, :D], NHEAD, True), "wk": attention_weights(qkv[:, D:2 * D], NHEAD, True),
        "wv": qkv[:, 2 * D:], "wo": i["L1_attn_w_proj"], "cos": cos1, "sin": sin1,
        "r_w": i["L1_cond2_router_w"].T, "r_t": i["L1_cond2_router_t_w"].T,
        "r_b": np.tile(i["L1_cond2_router_bias"], (P, 1)),
        "sw1": i["L1_cond2_sw1"].T, "sw3": i["L1_cond2_sw3"].T,
        "sw2": i["L1_cond2_sw2"].T.reshape(2, P, D).transpose(1, 0, 2),
        "rw1": i["L1_cond2_rw1"].reshape(NEXP * P // 2, D).T,
        "rw2": i["L1_cond2_rw2"].transpose(0, 2, 1).reshape(NEXP // 2, P, D).transpose(1, 0, 2),
        "f_r": i["L1_ffn_Wg"], "f_w1": i["L1_ffn_W1"].transpose(1, 0, 2),
        "f_b1": i["L1_ffn_b1"].reshape(NEXP, 2, P).transpose(2, 0, 1),
        "f_w2": i["L1_ffn_W2"].reshape(NEXP, 2, P, D).transpose(2, 0, 1, 3), "f_b2": i["L1_ffn_b2"],
    }
    l2 = {
        "wx": i["L2_cond_Wx"], "wh": i["L2_cond_Wh"], "b": i["L2_cond_b"].reshape(4, P).T,
        **delta_weights(i), "head_sum": np.kron(np.eye(P // N2, dtype=np.float32), np.ones((N2, N2), np.float32)),
        "r_wx": i["L2_cond2_Wx"], "r_wh": i["L2_cond2_Wh"], "r_b": i["L2_cond2_b"][:, None],
        "f_w": np.stack([i["L2_ffn_w_gate"].T, i["L2_ffn_w_up"].T,
                         i["L2_ffn_w_down"].T.reshape(BIT_BLOCKS, P, D).transpose(1, 0, 2).reshape(P, -1)], 1),
    }
    l3 = {
        "c_w": i["L3_cond_W"].T, "c_b": i["L3_cond_fc_bias"][:, None],
        "u_all": fside.transpose(0, 2, 1).reshape(P, D), "v_all": fside.transpose(1, 0, 2).reshape(D, P),
        "pick": np.kron(np.eye(B, dtype=np.float32), np.full((RANK, 1), inch, np.float32)),
        "wq": retention_weights(i["L3_attn_Wq"]), "wk": retention_weights(i["L3_attn_Wk"]),
        "wv": i["L3_attn_Wv"], "wg": i["L3_attn_Wg"], "cos": cos3, "sin": sin3,
        "wx": i["L3_cond2_Wx"], "wh": i["L3_cond2_Wh"], "b": i["L3_cond2_b"].reshape(4, P).T,
        "f_r": i["L3_ffn_router_w"].T,
        "f_wg": i["L3_ffn_gate_w"].transpose(1, 0, 2), "f_bg": i["L3_ffn_gate_b"].reshape(NEXP, 2, P).transpose(2, 0, 1),
        "f_wu": i["L3_ffn_up_w"].transpose(1, 0, 2), "f_bu": i["L3_ffn_up_b"].reshape(NEXP, 2, P).transpose(2, 0, 1),
        "f_wd": i["L3_ffn_down_w"].reshape(NEXP, 2, P, D).transpose(2, 0, 1, 3), "f_bd": i["L3_ffn_down_b"],
    }
    return {"base": base, "l0": l0, "l1": l1, "l2": l2, "l3": l3}, decay


def packed(pack):
    total = sum(int(np.prod(a.shape[1:])) for a in pack.values())
    whole = np.zeros((P, total), np.float32)
    places, at = {}, 0
    for name, a in pack.items():
        size = int(np.prod(a.shape[1:]))
        whole[:a.shape[0], at:at + size] = a.reshape(a.shape[0], size)
        places[name] = (at, a.shape)
        at += size
    return whole, places


def views(buffer, places):
    letters = "abc"
    out = {}
    for name, (at, shape) in places.items():
        part = buffer[0:shape[0], at:at + int(np.prod(shape[1:]))]
        if len(shape) > 2:
            dims = letters[:len(shape) - 1]
            part = part.rearrange(f"p ({' '.join(dims)}) -> p {' '.join(dims)}", **dict(zip(dims, shape[1:])))
        out[name] = part
    return out


def program(nc, dram, out, places, first=0, last=8):
    STAGE_SEMAPHORES.clear()
    with ExitStack() as stack:
        mem = Memory(nc, stack, "main")
        widths = {name: max(at + int(np.prod(shape[1:])) for at, shape in p.values()) for name, p in places.items()}
        x_buf, y_buf = mem.sb("x", [P, TOK]), mem.sb("y", [P, TOK])
        x, y = x_buf[:, :], y_buf[:, :]
        base_buf = mem.sb("base", [P, widths["base"]])
        ident_bf_buf, mask_bf_buf = mem.sb("ident_bf", [P, P], BF16), mem.sb("mask_bf", [P, P], BF16)
        even_buf = mem.sb("even_layers", [P, max(widths["l0"], widths["l2"])])
        odd_buf = mem.sb("odd_layers", [P, max(widths["l1"], widths["l3"])])
        base = views(base_buf, places["base"])
        l0, l2 = views(even_buf, places["l0"]), views(even_buf, places["l2"])
        l1, l3 = views(odd_buf, places["l1"]), views(odd_buf, places["l3"])
        ident, ones, rank, cond = base["ident"], base["ones"], base["rank"], base["cond"]
        ones_bf_buf = mem.sb("ones_bf", [P, 1], BF16)
        ident_bf, mask_bf, ones_bf = ident_bf_buf[:, :], mask_bf_buf[:, :], ones_bf_buf[:, :]
        loaded = {n: mem.sem(f"loaded_{n}") for n in ("start", "l1", "l2", "l3", "decay")}
        stored = mem.sem("stored")

        def between(load=(), need=None):
            with nc.Block() as block:

                @block.gpsimd
                def _(pool):
                    if STAGE_SEMAPHORES:
                        nc.clear_and_free_semaphores(list(STAGE_SEMAPHORES))
                        STAGE_SEMAPHORES.clear()

                @block.sync
                def _(sp):
                    for dst, src, name in load:
                        sp.dma_start(dst, src).then_inc(loaded[name], 16)
                    if need:
                        sp.wait_ge(loaded[need[0]], 16 * need[1])

        between([(x, dram["x"], "start"), (base_buf[:, :], dram["base"], "start"),
                 (even_buf[:, 0:widths["l0"]], dram["l0"], "start"), (odd_buf[:, 0:widths["l1"]], dram["l1"], "l1")], ("start", 3))
        with nc.Block() as block:

            @block.vector
            def _(dve):
                nc.vector.tensor_copy(ident_bf, ident)
                nc.vector.tensor_copy(mask_bf, base["mask"])
                nc.vector.tensor_copy(ones_bf, ones[:, 0:1])

        if first <= 0 < last:
            cond_gate_stage(nc, "l0c", x, y, cond, l0["c_w1"], l0["c_b1"], l0["c_w2"], l0["c_b2"])
            attention_stage(nc, "l0a", y, x, l0["wq"], l0["wk"], l0["wv"], l0["wo"], l0["cos"], l0["sin"], ident,
                            ident_bf, mask_bf, NQUAD)
        if first <= 1 < last:
            lstm_stage(nc, "l0r", x, y, l0["wx"], l0["wh"], l0["b"], cond, ident)
            ternary_stage(nc, "l0f", y, x, l0["f_w"], l0["f_b"])
        between([(even_buf[:, 0:widths["l2"]], dram["l2"], "l2")], ("l1", 1))
        if first <= 2 < last:
            threshold_stage(nc, "l1c", x, y, cond)
            attention_stage(nc, "l1a", y, x, l1["wq"], l1["wk"], l1["wv"], l1["wo"], l1["cos"], l1["sin"], ident,
                            ident_bf, mask_bf, NHEAD)
        if first <= 3 < last:
            routed_cond_stage(nc, "l1r", x, y, cond, l1["r_w"], l1["r_t"], l1["r_b"], l1["sw1"], l1["sw3"], l1["sw2"],
                              l1["rw1"], l1["rw2"], rank, ones, ident)
            expert_stage(nc, "l1f", y, x, l1["f_r"], l1["f_w1"], l1["f_b1"], None, None, l1["f_w2"], l1["f_b2"], rank, ident)
        between([(odd_buf[:, 0:widths["l3"]], dram["l3"], "l3")], ("l2", 1))
        if first <= 4 < last:
            recurrent_stages(nc, "l2r", x, y, l2["wx"], l2["wh"], l2["b"], l2["w_in"], l2["w_k"], l2["w_q"], l2["w_vb"],
                             l2["b_vb"], l2["w_out"], l2["head_sum"], l2["r_wx"], l2["r_wh"], l2["r_b"], cond, ident)
        decay_buf = mem.sb("decay", [P, RUNS, NQUAD, T + HALF])
        decay = decay_buf[:, :, :, :]
        between([(decay, dram["decay"], "decay")])
        if first <= 5 < last:
            bit_ffn_stage(nc, "l2f", y, x, l2["f_w"], ident, ident_bf)
        between((), ("l3", 1))
        between((), ("decay", 1))
        if first <= 6 < last:
            low_rank_cond_stage(nc, "l3c", x, y, l3["c_w"], l3["u_all"], l3["v_all"], l3["pick"], l3["c_b"], cond)
            retention_stage(nc, "l3a", y, x, l3["wq"], l3["wk"], l3["wv"], l3["wg"], l3["cos"], l3["sin"], decay, ident, ones_bf)
        if first <= 7 < last:
            lstm_stage(nc, "l3r", x, y, l3["wx"], l3["wh"], l3["b"], cond, ident)
            expert_stage(nc, "l3f", y, x, l3["f_r"], l3["f_wg"], l3["f_bg"], l3["f_wu"], l3["f_bu"], l3["f_wd"], l3["f_bd"],
                         rank, ident)
        with nc.Block() as block:

            @block.sync
            def _(sp):
                sp.dma_start(out, x).then_inc(stored, 16)
                sp.wait_ge(stored, 16)


def host_arrays(inputs):
    i = {name: np.asarray(a) for name, a in inputs.items()}
    layers, decay = packs(i)
    arrays, places = {"x": np.ascontiguousarray(i["x"].transpose(2, 0, 1).reshape(D, TOK))}, {}
    for name, pack in layers.items():
        arrays[name], places[name] = packed(pack)
    arrays["decay"] = np.ascontiguousarray(decay)
    return arrays, places


def kernel(**inputs):
    import concourse.bacc as bacc
    from concourse.bass_utils import run_bass_kernel_spmd

    nc = bacc.Bacc("TRN2", target_bir_lowering=False, num_devices=1)
    arrays, places = host_arrays(inputs)
    dram = {name: nc.dram_tensor(f"in_{name}", a.shape, mybir.dt.from_np(a.dtype), kind="ExternalInput").ap()
            for name, a in arrays.items()}
    out = nc.dram_tensor("out", (D, TOK), F32, kind="ExternalOutput").ap()
    program(nc, dram, out, places)
    got = run_bass_kernel_spmd(nc, [{f"in_{name}": a for name, a in arrays.items()}], core_ids=[0])
    return np.ascontiguousarray(got.results[0]["out"].reshape(D, B, T).transpose(1, 2, 0))
```

```python
from contextlib import ExitStack

import numpy as np

import concourse.bass as bass
from concourse import mybir

F32 = mybir.dt.float32
BF16 = mybir.dt.bfloat16
ALU = mybir.AluOpType
ACT = mybir.ActivationFunctionType
AX_X = mybir.AxisListType.X
RMAX = bass.bass_isa.ReduceOp.max
RADD = bass.bass_isa.ReduceOp.add

B, T, D = 8, 256, 128
TOK = B * T
P = 128
CHUNK = 512
NCHUNK = TOK // CHUNK


def high(ap):
    dims = "abcd"[:ap.ndim - 1]
    return ap.bitcast(BF16).rearrange(f"{' '.join(dims)} (n two) -> {' '.join(dims)} two n", two=2)[
        tuple(slice(None) for _ in dims) + (1,)]


STAGE_SEMAPHORES = []


class Memory:

    def __init__(self, nc, stack, tag):
        self.nc, self.stack, self.tag = nc, stack, tag

    def sb(self, name, shape, dt=F32):
        return self.stack.enter_context(self.nc.sbuf_tensor(f"{self.tag}_{name}", shape, dt))

    def ps(self, name, shape, dt=F32):
        return self.stack.enter_context(self.nc.psum_tensor(f"{self.tag}_{name}", shape, dt))

    def sem(self, name):
        sem = self.nc.alloc_semaphore(f"{self.tag}_{name}")
        if self.tag != "main":
            STAGE_SEMAPHORES.append(sem)
        return sem


def clear_stage_semaphores(nc):
    with nc.Block() as block:

        @block.gpsimd
        def _(pool):
            nc.clear_and_free_semaphores(list(STAGE_SEMAPHORES))
            STAGE_SEMAPHORES.clear()
STEPS_IN_BODY = 4


def lstm_stage(nc, tag, src, dst, wx, wh, bias, h0, ident):
    with ExitStack() as stack:
        mem = Memory(nc, stack, tag)
        xw = mem.sb("xw", [P, T * 4 * B])
        gates = mem.sb("gates", [P, 2 * B])
        both = mem.sb("both", [P, 2 * B])
        h_ring = mem.sb("h_ring", [P, STEPS_IN_BODY, B])
        h_rest, h_low = mem.sb("h_rest", [P, B]), mem.sb("h_low", [P, B], BF16)
        w_part = [mem.sb(f"w_part{n}", [P, 4 * P], BF16) for n in range(3)]
        w_rest = mem.sb("w_rest", [P, 4 * P])
        pre = mem.ps("pre", [P, 4, CHUNK])
        acc = mem.ps("acc", [P, 2, CHUNK])
        acc_o = mem.ps("acc_o", [P, 2, CHUNK])
        out_gate = mem.sb("out_gate", [P, B])
        o_psum = mem.sem("o_psum")
        cand_cell, tanh_c = pre[:, 3, 0:2 * B], pre[:, 3, 2 * B:3 * B]
        xw_psum, xw_act, xw_dve = mem.sem("xw_psum"), mem.sem("xw_act"), mem.sem("xw_dve")
        w_split = mem.sem("w_split")
        gates_psum, gates_ready = mem.sem("gates_psum"), mem.sem("gates_ready")
        mul_ready, cell_ready, tanh_ready = mem.sem("mul_ready"), mem.sem("cell_ready"), mem.sem("tanh_ready")
        h_ready, rest_ready, low_ready = mem.sem("h_ready"), mem.sem("rest_ready"), mem.sem("low_ready")
        table_ready, h_saved = mem.sem("table_ready"), mem.sem("h_saved")
        FIRST, LAST = (0, 1, 3), (2,)
        SLOT = (0, 1, 3, 2)
        xw_by_gate = xw[:, :].rearrange("p (t g b) -> p g b t", g=4, b=B)
        dst_by_step = dst.rearrange("p (b t) -> p t b", t=T)
        U = STEPS_IN_BODY
        BC = CHUNK // T

        with nc.Block() as block:

            @block.tensor
            def _(pe):
                for c in range(NCHUNK):
                    for g in range(4):
                        if c >= 1 and g == 0:
                            pe.wait_ge(xw_act, 2 * c)
                        if c >= 1 and g == 2:
                            pe.wait_ge(xw_dve, 2 * c)
                        nc.tensor.matmul(pre[:, g, :], wx[:, g * P:(g + 1) * P], src[:, c * CHUNK:(c + 1) * CHUNK],
                                         start=True, stop=True).then_inc(xw_psum, 1)
                pe.wait_ge(xw_act, 2 * NCHUNK)
                pe.wait_ge(xw_dve, 2 * NCHUNK)
                pe.wait_ge(w_split, 4)
                with pe.Fori(0, T // U) as i:
                    for u in range(U):
                        s = i * U + u

                        def products(into, which, parts, h, end=False):
                            for at, g in enumerate(which):
                                for n in range(parts):
                                    last = nc.tensor.matmul(into[:, u % 2, at * B:(at + 1) * B],
                                                            w_part[n][:, g * P:(g + 1) * P], h, start=False,
                                                            stop=(end and g == which[-1]))
                            return last

                        h_parts = high(h_ring[:, (u - 1) % U, :]), high(h_rest[:, :]), h_low[:, :]
                        pe.wait_ge(h_saved, s + 1)
                        nc.tensor.matmul(acc[:, u % 2, 0:3 * B], ident, xw[:, bass.ds(s * 4 * B, 3 * B)], start=True,
                                         stop=False)
                        pe.wait_ge(h_ready, s + 1)
                        products(acc, FIRST, 3, h_parts[0])
                        pe.wait_ge(rest_ready, s + 1)
                        products(acc, FIRST, 2, h_parts[1])
                        pe.wait_ge(low_ready, s + 1)
                        products(acc, FIRST, 1, h_parts[2], True).then_inc(gates_psum, 1)
                        nc.tensor.matmul(acc_o[:, u % 2, 0:B], ident, xw[:, bass.ds(s * 4 * B + 3 * B, B)], start=True,
                                         stop=False)
                        for n in range(3):
                            last = products(acc_o, LAST, 3 - n, h_parts[n], n == 2)
                        last.then_inc(o_psum, 1)

            @block.scalar
            def _(act):
                for c in range(NCHUNK):
                    for g in range(2):
                        act.wait_ge(xw_psum, 4 * c + g + 1)
                        nc.scalar.activation(xw_by_gate[:, SLOT[g], BC * c:BC * (c + 1), :],
                                             pre[:, g, :].rearrange("p (b t) -> p b t", t=T), ACT.Identity,
                                             bias=bias[:, g:g + 1]).then_inc(xw_act, 1)
                act.wait_ge(cell_ready, 1)
                nc.scalar.activation(tanh_c, cand_cell[:, B:2 * B], ACT.Sigmoid).then_inc(table_ready, 1)
                act.wait_ge(table_ready, 1)
                with act.Fori(0, T // U) as i:
                    for u in range(U):
                        s = i * U + u
                        act.wait_ge(gates_psum, s + 1)
                        nc.scalar.activation(gates[:, :], acc[:, u % 2, 0:2 * B], ACT.Sigmoid)
                        nc.scalar.activation(cand_cell[:, 0:B], acc[:, u % 2, 2 * B:3 * B],
                                             ACT.Tanh).then_inc(gates_ready, 1)
                        act.wait_ge(o_psum, s + 1)
                        nc.scalar.activation(out_gate[:, :], acc_o[:, u % 2, 0:B], ACT.Sigmoid)
                        act.wait_ge(cell_ready, s + 2)
                        nc.scalar.activation(tanh_c, cand_cell[:, B:2 * B], ACT.Tanh).then_inc(tanh_ready, 1)

            @block.vector
            def _(dve):
                def split(u, s):
                    h = h_ring[:, u, :]
                    dve.wait_ge(h_ready, s)
                    nc.vector.tensor_tensor(h_rest[:, :], h, high(h), ALU.subtract).then_inc(rest_ready, 1)
                    dve.wait_ge(rest_ready, s)
                    nc.vector.tensor_tensor(h_low[:, :], h_rest[:, :], high(h_rest[:, :]), ALU.subtract).then_inc(low_ready, 1)

                nc.vector.tensor_copy(h_ring[:, U - 1, :], h0).then_inc(h_ready, 1)
                split(U - 1, 1)
                for c in range(NCHUNK):
                    for g in range(2, 4):
                        dve.wait_ge(xw_psum, 4 * c + g + 1)
                        nc.vector.tensor_scalar(xw_by_gate[:, SLOT[g], BC * c:BC * (c + 1), :],
                                                pre[:, g, :].rearrange("p (b t) -> p b t", t=T),
                                                bias[:, g:g + 1], None, ALU.add).then_inc(xw_dve, 1)
                dve.wait_ge(xw_dve, 2 * NCHUNK)
                nc.vector.memset(cand_cell[:, B:2 * B], 0.0).then_inc(cell_ready, 1)
                dve.wait_ge(cell_ready, 1)
                with dve.Fori(0, T // U) as i:
                    for u in range(U):
                        s = i * U + u
                        dve.wait_ge(gates_ready, s + 1)
                        nc.vector.tensor_tensor(both[:, :], gates[:, :], cand_cell, ALU.mult).then_inc(mul_ready, 1)
                        dve.wait_ge(mul_ready, s + 1)
                        nc.vector.tensor_tensor(cand_cell[:, B:2 * B], both[:, 0:B], both[:, B:2 * B],
                                                ALU.add).then_inc(cell_ready, 1)
                        dve.wait_ge(tanh_ready, s + 1)
                        nc.vector.tensor_tensor(h_ring[:, u, :], out_gate[:, :], tanh_c,
                                                ALU.mult).then_inc(h_ready, 1)
                        split(u, s + 2)

            @block.gpsimd
            def _(pool):
                nc.gpsimd.tensor_copy(w_part[0][:, :], wh).then_inc(w_split, 1)
                pool.wait_ge(w_split, 1)
                nc.gpsimd.tensor_tensor(w_rest[:, :], wh, w_part[0][:, :], ALU.subtract).then_inc(w_split, 1)
                pool.wait_ge(w_split, 2)
                nc.gpsimd.tensor_copy(w_part[1][:, :], w_rest[:, :]).then_inc(w_split, 1)
                pool.wait_ge(w_split, 3)
                nc.gpsimd.tensor_tensor(w_part[2][:, :], w_rest[:, :], w_part[1][:, :], ALU.subtract).then_inc(w_split, 1)
                pool.sem_inc(h_saved, U)
                with pool.Fori(0, T // U) as i:
                    for u in range(U):
                        s = i * U + u
                        pool.wait_ge(h_ready, s + 2)
                        nc.gpsimd.tensor_copy(dst_by_step[:, bass.ds(s, 1), :], h_ring[:, u:u + 1, :]).then_inc(h_saved, 1)



HEADS2, N2 = 8, 32
HG = HEADS2 // 4
IQ = 4
IL = N2 // IQ
ROWS = HG * IL
TC = 16
NTC = T // TC
CH = TC * B
KN_EPS = 1e-6


def recurrent_stages(nc, tag, x, y, wx, wh, bias, w_in, w_k, w_q, w_vb, b_vb, w_out, head_sum, r_wx, r_wh, r_bias, h0, ident):
    with ExitStack() as stack:
        mem = Memory(nc, stack, tag)
        xw = mem.sb("xw", [P, T * 4 * B])
        gates = mem.sb("gates", [P, 3 * B])
        cand_cell = mem.sb("cand_cell", [P, 2 * B])
        both = mem.sb("both", [P, 2 * B])
        tanh_c = mem.sb("tanh_c", [P, B])
        h_ring = mem.sb("h_ring", [P, 2, B])
        h_rest, h_low = mem.sb("h_rest", [P, B]), mem.sb("h_low", [P, B], BF16)
        w_part = [mem.sb(f"w_part{n}", [P, 4 * P], BF16) for n in range(3)]
        w_rest = mem.sb("w_rest", [P, 4 * P])
        xp_sig = mem.sb("xp_sig", [P, CH])
        xp = mem.sb("xp", [P, CH])
        k_sq = mem.sb("k_sq", [P, HG, CH])
        k_norm = mem.sb("k_norm", [P, HG, CH])
        kn_f = mem.sb("kn_f", [P, HG, CH])
        vb_f = mem.sb("vb_f", [P, TC, B, IQ])
        kn_t = mem.sb("kn_t", [P, TC, HG, N2])
        q_t = mem.sb("q_t", [P, TC, HG, N2])
        vb_t = mem.sb("vb_t", [P, TC, 2 * ROWS])
        state = mem.sb("state", [P, 2, ROWS, N2])
        s_kn = mem.sb("s_kn", [P, ROWS, N2])
        beta_s = mem.sb("beta_s", [P, ROWS, N2])
        dk = mem.sb("dk", [P, ROWS, N2])
        pre = mem.sb("pre", [P, ROWS, N2])
        s_q = mem.sb("s_q", [P, ROWS, N2])
        got = mem.sb("got", [P, ROWS])
        dlt = mem.sb("dlt", [P, ROWS])
        sq = mem.sb("sq", [P, TC, 2 * ROWS])
        sq_sig = mem.sb("sq_sig", [P, TC, ROWS])
        sq_sq = mem.sb("sq_sq", [P, TC, ROWS])
        cell_f = mem.sb("cell_f", [P, CH, IQ])
        rxw = mem.sb("rxw", [P, CH])
        r_ring = mem.sb("r_ring", [P, 2, B])
        banks = [mem.ps(f"bank{n}", [P, CHUNK]) for n in range(8)]
        acc, r_ps, x_ps = banks[0:2], banks[2], banks[3]
        k_ps, q_ps, vb_ps = banks[4], banks[5], banks[6:8]
        ssq_ps = x_ps
        out_ps = r_ps[:, 0:CH]
        xw_ps = banks[4:8]

        xw_by_gate = xw[:, :].rearrange("p (t g b) -> p g b t", g=4, b=B)
        rxw_by_seq = rxw[:, :].rearrange("p (t b) -> p b t", b=B)
        y_b, x_b = y.rearrange("p (b t) -> p b t", t=T), x.rearrange("p (b t) -> p b t", t=T)
        y_t, x_t = y.rearrange("p (b t) -> p t b", t=T), x.rearrange("p (b t) -> p t b", t=T)
        BC = CHUNK // T

        def halves(bank):
            return bank[:, 0:2 * CH].rearrange("p (g n) -> p g n", g=2)

        def repeated(ap):
            return ap.rearrange("p (b t) -> p t b", t=TC).unsqueeze(3).broadcast_to([P, TC, B, IQ])

        def over_rows(ap):
            return ap.unsqueeze(3).broadcast_to([P, HG, N2, IL]).rearrange("p g j i -> p g i j")

        def over_cols(ap):
            return ap.unsqueeze(2).broadcast_to([P, ROWS, N2])

        def by_group(ap):
            return ap.rearrange("p (g i) j -> p g i j", g=HG)

        def start():
            xw_psum, xw_act, xw_dve = mem.sem("xw_psum"), mem.sem("xw_act"), mem.sem("xw_dve")
            w_split = mem.sem("w_split")
            with nc.Block() as block:

                @block.tensor
                def _(pe):
                    for c in range(NCHUNK):
                        for g in range(4):
                            if c >= 1 and g == 0:
                                pe.wait_ge(xw_act, 2 * c)
                            if c >= 1 and g == 2:
                                pe.wait_ge(xw_dve, 2 * c)
                            nc.tensor.matmul(xw_ps[g][:, :], wx[:, g * P:(g + 1) * P], x[:, c * CHUNK:(c + 1) * CHUNK],
                                             start=True, stop=True).then_inc(xw_psum, 1)

                @block.scalar
                def _(act):
                    for c in range(NCHUNK):
                        for g in range(2):
                            act.wait_ge(xw_psum, 4 * c + g + 1)
                            nc.scalar.activation(xw_by_gate[:, g, BC * c:BC * (c + 1), :],
                                                 xw_ps[g][:, :].rearrange("p (b t) -> p b t", t=T), ACT.Identity,
                                                 bias=bias[:, g:g + 1]).then_inc(xw_act, 1)

                @block.vector
                def _(dve):
                    nc.vector.tensor_copy(h_ring[:, 1, :], h0)
                    nc.vector.tensor_copy(r_ring[:, 1, :], h0)
                    nc.vector.memset(cand_cell[:, B:2 * B], 0.0)
                    for c in range(NCHUNK):
                        for g in range(2, 4):
                            dve.wait_ge(xw_psum, 4 * c + g + 1)
                            nc.vector.tensor_scalar(xw_by_gate[:, g, BC * c:BC * (c + 1), :],
                                                    xw_ps[g][:, :].rearrange("p (b t) -> p b t", t=T),
                                                    bias[:, g:g + 1], None, ALU.add).then_inc(xw_dve, 1)

                @block.gpsimd
                def _(pool):
                    nc.gpsimd.tensor_copy(w_part[0][:, :], wh).then_inc(w_split, 1)
                    pool.wait_ge(w_split, 1)
                    nc.gpsimd.tensor_tensor(w_rest[:, :], wh, w_part[0][:, :], ALU.subtract).then_inc(w_split, 1)
                    pool.wait_ge(w_split, 2)
                    nc.gpsimd.tensor_copy(w_part[1][:, :], w_rest[:, :]).then_inc(w_split, 1)
                    pool.wait_ge(w_split, 3)
                    nc.gpsimd.tensor_tensor(w_part[2][:, :], w_rest[:, :], w_part[1][:, :], ALU.subtract).then_inc(w_split, 1)
                    nc.gpsimd.memset(state[:, 1, :, :], 0.0)
                    nc.gpsimd.memset(sq[:, :, ROWS:2 * ROWS], 0.0)

        def waves(name, count, lstm, delta, rnn):
            L, DELTA, R = lstm is not None, delta is not None, rnn is not None
            ALONE = L and not DELTA and not R
            sem = Memory(nc, stack, f"{tag}{name}").sem
            gates_psum, gates_ready, mul_ready = sem("gates_psum"), sem("gates_ready"), sem("mul_ready")
            rest_ready, low_ready = sem("rest_ready"), sem("low_ready")
            cell_ready, tanh_ready, h_ready, h_saved = sem("cell_ready"), sem("tanh_ready"), sem("h_ready"), sem("h_saved")
            xin_psum, xp_sig_ready, xp_ready = sem("xin_psum"), sem("xp_sig_ready"), sem("xp_ready")
            k_psum, k_sq_ready, ssq_psum = sem("k_psum"), sem("k_sq_ready"), sem("ssq_psum")
            k_norm_ready, kn_chain = sem("k_norm_ready"), sem("kn_chain")
            q_psum, q_turned = sem("q_psum"), sem("q_turned")
            vb_psum, vb_ready = sem("vb_psum"), sem("vb_ready")
            turned, beta_ready = sem("turned"), sem("beta_ready")
            s_kn_ready, got_ready, dlt_ready, dk_ready = sem("s_kn_ready"), sem("got_ready"), sem("dlt_ready"), sem("dk_ready")
            bs_ready, pre_ready = sem("bs_ready"), sem("pre_ready")
            state_ready, s_q_ready, sq_ready = sem("state_ready"), sem("s_q_ready"), sem("sq_ready")
            sq_sig_ready, cell_chain, cell_turned = sem("sq_sig_ready"), sem("cell_chain"), sem("cell_turned")
            out_psum, x_added, table_ready = sem("out_psum"), sem("x_added"), sem("table_ready")
            rx_psum, rxw_ready, r_psum, r_ready, r_saved = (sem(n) for n in ("rx_psum", "rxw_ready", "r_psum", "r_ready", "r_saved"))

            with nc.Block() as block:

                @block.tensor
                def _(pe):
                    def project(w):
                        c = w + delta
                        pe.wait_ge(k_norm_ready, w + 1)
                        if L:
                            pe.wait_ge(h_saved, w * TC + 2)
                        nc.tensor.matmul(x_ps[:, 0:CH].rearrange("p (b t) -> p b t", t=TC), w_in,
                                         y_b[:, :, bass.ds(c * TC, TC)], start=True, stop=True).then_inc(xin_psum, 1)
                        pe.wait_ge(xp_ready, w + 1)
                        for g in range(HG):
                            nc.tensor.matmul(halves(k_ps)[:, g, :], w_k[:, g * P:(g + 1) * P], xp[:, :],
                                             start=True, stop=True).then_inc(k_psum, 1)
                        for g in range(HG):
                            nc.tensor.matmul(halves(q_ps)[:, g, :], w_q[:, g * P:(g + 1) * P], xp[:, :],
                                             start=True, stop=True).then_inc(q_psum, 1)
                        pe.wait_ge(k_sq_ready, w + 1)
                        for g in range(HG):
                            nc.tensor.matmul(halves(ssq_ps)[:, g, :], head_sum, k_sq[:, g, :],
                                             start=True, stop=True).then_inc(ssq_psum, 1)

                    def project_values(w):
                        for n in range(IQ):
                            nc.tensor.matmul(halves(vb_ps[n // 2])[:, n % 2, :], w_vb[:, n, :], xp[:, :],
                                             start=True, stop=True).then_inc(vb_psum, 1)

                    def output(w):
                        pe.wait_ge(r_ready, w * TC + 1)
                        pe.wait_ge(cell_turned, w + 1)
                        for n in range(IQ):
                            last = nc.tensor.matmul(out_ps, w_out[:, n, :], cell_f[:, :, n],
                                                    start=(n == 0), stop=(n == IQ - 1))
                        last.then_inc(out_psum, 1)

                    def project_rnn(w):
                        pe.wait_ge(x_added, w + 1)
                        nc.tensor.matmul(r_ps[:, 0:CH].rearrange("p (b t) -> p b t", t=TC), r_wx,
                                         x_b[:, :, bass.ds((w + rnn) * TC, TC)], start=True, stop=True).then_inc(rx_psum, 1)

                    def step(w, s, u):
                        n = w * TC + s
                        if L:
                            nc.tensor.matmul(acc[u][:, 0:4 * B], ident, xw[:, bass.ds((n + lstm * TC) * 4 * B, 4 * B)],
                                             start=True, stop=False)
                        if L:
                            pe.wait_ge(h_ready, n + 1)
                            if ALONE:
                                h_parts = high(h_ring[:, 1 - u, :]), high(h_rest[:, :]), h_low[:, :]
                                for m in range(3):
                                    if m == 1:
                                        pe.wait_ge(rest_ready, n + 1)
                                    if m == 2:
                                        pe.wait_ge(low_ready, n + 1)
                                    for g in range(4):
                                        for k in range(3 - m):
                                            last = nc.tensor.matmul(acc[u][:, g * B:(g + 1) * B],
                                                                    w_part[k][:, g * P:(g + 1) * P], h_parts[m],
                                                                    start=False, stop=(m == 2 and g == 3))
                            else:
                                for g in range(4):
                                    last = nc.tensor.matmul(acc[u][:, g * B:(g + 1) * B], wh[:, g * P:(g + 1) * P],
                                                            h_ring[:, 1 - u, :], start=False, stop=(g == 3))
                            last.then_inc(gates_psum, 1)
                        if R:
                            pe.wait_ge(rxw_ready, w + 1)
                            pe.wait_ge(r_ready, n + 1)
                            nc.tensor.matmul(r_ps[:, 0:B], ident, rxw[:, bass.ds(s * B, B)], start=True, stop=False)
                            nc.tensor.matmul(r_ps[:, 0:B], r_wh, r_ring[:, 1 - u, :], start=False, stop=True).then_inc(r_psum, 1)

                    with pe.Fori(0, count) as w:
                        if DELTA:
                            project(w)
                        if R:
                            output(w)
                        if DELTA:
                            project_values(w)
                        if R:
                            project_rnn(w)
                        if L or R:
                            with pe.Fori(0, TC // 2) as i:
                                for u in range(2):
                                    step(w, i * 2 + u, u)

                @block.scalar
                def _(act):
                    if R:
                        act.sem_inc(r_ready, 1)
                    if DELTA:
                        act.sem_inc(k_norm_ready, 1)
                    nc.scalar.activation(sq_sig[:, 0, 0:1], ident[:, 0:1], ACT.Sigmoid).then_inc(table_ready, 1)
                    act.wait_ge(table_ready, 1)

                    def output(w):
                        if DELTA:
                            act.wait_ge(sq_ready, TC * w + 1)
                        nc.scalar.activation(sq_sig[:, :, :], sq[:, :, 0:ROWS], ACT.Sigmoid).then_inc(sq_sig_ready, 1)

                    def project(w):
                        act.wait_ge(xin_psum, w + 1)
                        nc.scalar.activation(xp_sig[:, :], x_ps[:, 0:CH], ACT.Sigmoid).then_inc(xp_sig_ready, 1)
                        if R:
                            output(w)
                        act.wait_ge(k_psum, HG * (w + 1))
                        nc.scalar.activation(k_sq[:, :, :], halves(k_ps), ACT.Square).then_inc(k_sq_ready, 1)
                        act.wait_ge(ssq_psum, HG * (w + 1))
                        nc.scalar.activation(k_norm[:, :, :], halves(ssq_ps), ACT.Sqrt).then_inc(k_norm_ready, 1)
                        for n in range(IQ):
                            act.wait_ge(vb_psum, IQ * w + 2 * (n // 2) + 2)
                            nc.scalar.activation(vb_f[:, :, :, n].rearrange("p t b -> p b t"),
                                                 halves(vb_ps[n // 2])[:, n % 2, :].rearrange("p (b t) -> p b t", t=TC),
                                                 ACT.Identity, bias=b_vb[:, n:n + 1]).then_inc(vb_ready, 1)
                        act.wait_ge(turned, (HG + 1) * (w + 1))
                        nc.scalar.activation(vb_t[:, :, ROWS:2 * ROWS], vb_t[:, :, ROWS:2 * ROWS],
                                             ACT.Sigmoid).then_inc(beta_ready, 1)

                    def step(w, s, u):
                        n = w * TC + s
                        if L:
                            act.wait_ge(gates_psum, n + 1)
                            nc.scalar.activation(gates[:, :], acc[u][:, 0:3 * B], ACT.Sigmoid)
                            nc.scalar.activation(cand_cell[:, 0:B], acc[u][:, 3 * B:4 * B], ACT.Tanh).then_inc(gates_ready, 1)
                            act.wait_ge(cell_ready, n + 1)
                            nc.scalar.activation(tanh_c[:, :], cand_cell[:, B:2 * B], ACT.Tanh).then_inc(tanh_ready, 1)
                        if R:
                            act.wait_ge(r_saved, n + 1)
                            act.wait_ge(r_psum, n + 1)
                            nc.scalar.activation(r_ring[:, u, :], r_ps[:, 0:B], ACT.Tanh).then_inc(r_ready, 1)
                        if DELTA:
                            for g in range(HG):
                                act.wait_ge(pre_ready, HG * n + g + 1)
                                nc.scalar.activation(state[:, u, g * IL:(g + 1) * IL, :], pre[:, g * IL:(g + 1) * IL, :],
                                                     ACT.Tanh).then_inc(state_ready, 1)

                    with act.Fori(0, count) as w:
                        if DELTA:
                            project(w)
                        elif R:
                            output(w)
                        with act.Fori(0, TC // 2) as i:
                            for u in range(2):
                                step(w, i * 2 + u, u)

                @block.gpsimd
                def _(pool):
                    if L:
                        pool.sem_inc(h_ready, 1)
                        pool.sem_inc(h_saved, 2)
                    if R:
                        pool.sem_inc(r_saved, 2)
                    if DELTA:
                        pool.sem_inc(state_ready, HG)

                    def q_products(w, s, u):
                        n = w * TC + s
                        pool.wait_ge(state_ready, HG * (n + 2))
                        pool.wait_ge(sq_ready, n + 1)
                        nc.gpsimd.tensor_tensor(by_group(s_q[:, :, :]), by_group(state[:, u, :, :]),
                                                over_rows(q_t[:, bass.ds(s, 1), :, :].squeeze(1)),
                                                ALU.mult).then_inc(s_q_ready, 1)

                    def step(w, s, u, behind):
                        n = w * TC + s
                        if DELTA:
                            pool.wait_ge(beta_ready, w + 1)
                            pool.wait_ge(state_ready, HG * (n + 1))
                            nc.gpsimd.tensor_tensor(beta_s[:, :, :], state[:, 1 - u, :, :],
                                                    over_cols(vb_t[:, bass.ds(s, 1), ROWS:2 * ROWS].squeeze(1)),
                                                    ALU.mult).then_inc(bs_ready, 1)
                            if behind:
                                q_products(w, s - 1, 1 - u)
                        if L:
                            pool.wait_ge(h_saved, n + 1)
                            pool.wait_ge(tanh_ready, n + 1)
                            nc.gpsimd.tensor_tensor(h_ring[:, u, :], gates[:, 2 * B:3 * B], tanh_c[:, :],
                                                    ALU.mult).then_inc(h_ready, 1)
                        if R:
                            pool.wait_ge(r_ready, n + 2)
                            nc.gpsimd.tensor_copy(y_t[:, bass.ds(s + (w + rnn) * TC, 1), :],
                                                  r_ring[:, u:u + 1, :]).then_inc(r_saved, 1)
                        if L:
                            pool.wait_ge(h_ready, n + 2)
                            nc.gpsimd.tensor_copy(y_t[:, bass.ds(s + (w + lstm) * TC, 1), :],
                                                  h_ring[:, u:u + 1, :]).then_inc(h_saved, 1)

                    with pool.Fori(0, count) as w:
                        for u in range(2):
                            step(w, u, u, u >= 1)
                        with pool.Fori(1, TC // 2) as i:
                            for u in range(2):
                                step(w, i * 2 + u, u, True)
                        if DELTA:
                            q_products(w, TC - 1, (TC - 1) % 2)

                @block.vector
                def _(dve):
                    if DELTA:
                        dve.sem_inc(sq_ready, 1)

                    def project_input(w):
                        dve.wait_ge(xp_sig_ready, w + 1)
                        nc.vector.tensor_tensor(xp[:, :], xp_sig[:, :], x_ps[:, 0:CH], ALU.mult).then_inc(xp_ready, 1)

                    def project(w):
                        if R:
                            cell_output(w)
                        dve.wait_ge(q_psum, HG * (w + 1))
                        for g in range(HG):
                            nc.vector.transpose(q_t[:, :, g, :], repeated(halves(q_ps)[:, g, :])).then_inc(q_turned, 1)
                        dve.wait_ge(k_norm_ready, w + 2)
                        nc.vector.tensor_scalar(k_norm[:, :, :], k_norm[:, :, :], KN_EPS, None, ALU.add).then_inc(kn_chain, 1)
                        dve.wait_ge(kn_chain, 3 * w + 1)
                        nc.vector.reciprocal(k_sq[:, :, :], k_norm[:, :, :]).then_inc(kn_chain, 1)
                        dve.wait_ge(kn_chain, 3 * w + 2)
                        nc.vector.tensor_tensor(kn_f[:, :, :], k_sq[:, :, :], halves(k_ps), ALU.mult).then_inc(kn_chain, 1)
                        if R:
                            add_output(w)
                        dve.wait_ge(kn_chain, 3 * w + 3)
                        for g in range(HG):
                            nc.vector.transpose(kn_t[:, :, g, :], repeated(kn_f[:, g, :])).then_inc(turned, 1)
                        dve.wait_ge(vb_ready, IQ * (w + 1))
                        nc.vector.transpose(vb_t[:, :, :], vb_f[:, :, :, :]).then_inc(turned, 1)
                        if R:
                            rnn_input(w)
                        dve.wait_ge(q_turned, HG * (w + 1))
                        dve.wait_ge(turned, (HG + 1) * (w + 1))

                    def lstm_products(n):
                        dve.wait_ge(gates_ready, n + 1)
                        nc.vector.tensor_tensor(both[:, :], gates[:, 0:2 * B], cand_cell[:, :], ALU.mult).then_inc(mul_ready, 1)

                    def lstm_cell(n):
                        dve.wait_ge(mul_ready, n + 1)
                        nc.vector.tensor_tensor(cand_cell[:, B:2 * B], both[:, 0:B], both[:, B:2 * B],
                                                ALU.add).then_inc(cell_ready, 1)

                    def q_sum(w, s):
                        dve.wait_ge(s_q_ready, w * TC + s + 1)
                        nc.vector.tensor_reduce(sq[:, bass.ds(s, 1), 0:ROWS].squeeze(1), s_q[:, :, :], AX_X,
                                                ALU.add).then_inc(sq_ready, 1)

                    def step(w, s, u, behind):
                        n = w * TC + s
                        half = [slice(g * IL, (g + 1) * IL) for g in range(HG)]
                        if DELTA:
                            kn = [kn_t[:, bass.ds(s, 1), g, :].broadcast_to([P, IL, N2]) for g in range(HG)]
                            for g in range(HG):
                                dve.wait_ge(state_ready, HG * n + g + 1)
                                nc.vector.tensor_tensor(s_kn[:, half[g], :], state[:, 1 - u, half[g], :], kn[g],
                                                        ALU.mult).then_inc(s_kn_ready, 1)
                            for g in range(HG):
                                dve.wait_ge(s_kn_ready, HG * n + g + 1)
                                nc.vector.tensor_reduce(got[:, half[g]], s_kn[:, half[g], :], AX_X, ALU.add).then_inc(got_ready, 1)
                            for g in range(HG):
                                if L and g == 1:
                                    lstm_products(n)
                                dve.wait_ge(got_ready, HG * n + g + 1)
                                nc.vector.tensor_tensor(dlt[:, half[g]], vb_t[:, bass.ds(s, 1), half[g]].squeeze(1), got[:, half[g]],
                                                        ALU.subtract).then_inc(dlt_ready, 1)
                            for g in range(HG):
                                if L and g == 1:
                                    lstm_cell(n)
                                dve.wait_ge(dlt_ready, HG * n + g + 1)
                                nc.vector.tensor_tensor(dk[:, half[g], :], dlt[:, half[g]].unsqueeze(2).broadcast_to([P, IL, N2]), kn[g],
                                                        ALU.mult).then_inc(dk_ready, 1)
                            for g in range(HG):
                                dve.wait_ge(dk_ready, HG * n + g + 1)
                                dve.wait_ge(bs_ready, n + 1)
                                nc.vector.tensor_tensor(pre[:, half[g], :], dk[:, half[g], :], beta_s[:, half[g], :],
                                                        ALU.add).then_inc(pre_ready, 1)
                            if behind:
                                q_sum(w, s - 1)
                        elif L:
                            if ALONE:
                                before = h_ring[:, 1 - u, :]
                                dve.wait_ge(h_ready, n + 1)
                                nc.vector.tensor_tensor(h_rest[:, :], before, high(before), ALU.subtract).then_inc(rest_ready, 1)
                                dve.wait_ge(rest_ready, n + 1)
                                nc.vector.tensor_tensor(h_low[:, :], h_rest[:, :], high(h_rest[:, :]),
                                                        ALU.subtract).then_inc(low_ready, 1)
                            lstm_products(n)
                            lstm_cell(n)

                    def cell_output(w):
                        if DELTA:
                            dve.wait_ge(sq_ready, TC * w + 1)
                        nc.vector.tensor_tensor(sq_sq[:, :, :], sq[:, :, 0:ROWS], sq[:, :, 0:ROWS],
                                                ALU.mult).then_inc(cell_chain, 1)
                        dve.wait_ge(sq_sig_ready, w + 1)
                        dve.wait_ge(cell_chain, 2 * w + 1)
                        nc.vector.tensor_tensor(sq[:, :, 0:ROWS], sq_sq[:, :, :], sq_sig[:, :, :],
                                                ALU.mult).then_inc(cell_chain, 1)
                        dve.wait_ge(cell_chain, 2 * w + 2)
                        nc.vector.transpose(cell_f[:, :, :].rearrange("p n q -> p (n q)"),
                                            sq[:, :, :].rearrange("p t r -> p (t r)")).then_inc(cell_turned, 1)

                    def add_output(w):
                        dve.wait_ge(out_psum, w + 1)
                        out_x = x_t[:, bass.ds((w + rnn) * TC, TC), :]
                        nc.vector.tensor_tensor(out_x, out_ps.rearrange("p (t b) -> p t b", b=B), out_x,
                                                ALU.add).then_inc(x_added, 1)

                    def rnn_input(w):
                        dve.wait_ge(rx_psum, w + 1)
                        nc.vector.tensor_scalar(rxw_by_seq, r_ps[:, 0:CH].rearrange("p (b t) -> p b t", t=TC), r_bias,
                                                None, ALU.add).then_inc(rxw_ready, 1)

                    def wave(w, more):
                        if DELTA:
                            project(w)
                        elif R:
                            cell_output(w)
                            add_output(w)
                            rnn_input(w)
                        if DELTA or L:
                            step(w, 0, 0, False)
                            step(w, 1, 1, True)
                            with dve.Fori(1, TC // 2) as i:
                                for u in range(2):
                                    step(w, i * 2 + u, u, True)
                        if DELTA:
                            if more:
                                project_input(w + 1)
                            q_sum(w, TC - 1)

                    if DELTA:
                        project_input(0)
                    if count > 1:
                        with dve.Fori(0, count - 1) as w:
                            wave(w, True)
                    wave(count - 1, False)

            clear_stage_semaphores(nc)

        start()
        waves("first", 1, 0, None, None)
        waves("second", 1, 1, 0, None)
        waves("all", NTC - 2, 2, 1, 0)
        waves("late", 1, None, NTC - 1, NTC - 2)
        waves("last", 1, None, None, NTC - 1)


def delta_weights(i):
    def heads(w):
        return w.reshape(HG, 4, IQ, IL, -1)

    vb = np.zeros((IQ, 4, 2, HG, IL, D), np.float32)
    vb[:, :, 0] = heads(i["L2_attn_W_v"]).transpose(2, 1, 0, 3, 4)
    vb[:, :, 1] = heads(i["L2_attn_W_beta"]).transpose(2, 1, 0, 3, 4)
    bias = np.zeros((IQ, 4, 2, HG, IL), np.float32)
    bias[:, :, 1] = heads(i["L2_attn_b_beta"].reshape(-1, 1)).transpose(2, 1, 0, 3, 4)[..., 0]
    out = np.zeros((IQ, 4, 2, HG, IL, D), np.float32)
    out[:, :, 0] = heads(np.ascontiguousarray(i["L2_attn_W_out"].T)).transpose(2, 1, 0, 3, 4)
    return {
        "w_in": i["L2_attn_W_in"].T,
        "w_k": i["L2_attn_W_k"].T,
        "w_q": i["L2_attn_W_q"].T,
        "w_vb": vb.reshape(IQ, P, D).transpose(2, 0, 1),
        "b_vb": bias.reshape(IQ, P).T,
        "w_out": out.reshape(IQ, P, D).transpose(1, 0, 2),
    }
NHEAD, HD = 16, 8
QUAD = 32
NQUAD = 4
RUNS = NHEAD // NQUAD
HALF = T // 2
SPAN = HALF + T
UNITS = NHEAD // 2
UBLK = 6


def attention_stage(nc, tag, src, x, wq, wk, wv, wo, cos, sin, ident, ident_bf, mask_bf, run_mask, kv_heads):
    krun = kv_heads // NQUAD
    vc = kv_heads * HD
    scale = float(HD) ** -0.5
    with ExitStack() as stack:
        mem = Memory(nc, stack, tag)
        y = mem.sb("y", [P, T])
        q_cos, q_sin = mem.sb("q_cos", [P, T]), mem.sb("q_sin", [P, T])
        k_cos, k_sin = mem.sb("k_cos", [P, T]), mem.sb("k_sin", [P, T])
        k_heads = mem.sb("k_heads", [P, T])
        q, k = mem.sb("q", [P, T]), mem.sb("k", [P, RUNS, T])
        v_top, v_low = mem.sb("v_top", [P, 2, kv_heads, HD + 1], BF16), mem.sb("v_low", [P, 2, kv_heads, HD + 1], BF16)
        v_rest = mem.sb("v_rest", [P, 2, kv_heads, HD + 1])
        v_part = v_top[:, :, :, :], high(v_rest[:, :, :, :]), v_low[:, :, :, :]
        top = mem.sb("top", [P, 2, 2, 2])
        prob = mem.sb("prob", [P, 2, 2 * SPAN])
        prob_t = mem.sb("prob_t", [P, 2, UBLK, HALF])
        rest_t = mem.sb("rest_t", [P, 2, UBLK, HALF])
        low_t = mem.sb("low_t", [P, 2, UBLK, HALF], BF16)
        inv = mem.sb("inv", [P, 2, NHEAD])
        heads = mem.sb("heads", [P, 2, NHEAD * HD])
        heads_t = mem.sb("heads_t", [P, T])
        s_ps = mem.ps("s_ps", [P, NQUAD, CHUNK])
        t_ps = mem.ps("t_ps", [P, 2, CHUNK])
        v_bank = mem.ps("v_bank", [P, CHUNK])
        o_ps = mem.ps("o_ps", [P, CHUNK])
        out_heads = o_ps[:, 0:2 * NHEAD * (HD + 1)].rearrange("p (a h e) -> p a h e", a=2, e=HD + 1)
        t_blocks = t_ps[:, :, 0:UBLK // 2 * HALF]
        v_ps = v_bank[:, 0:2 * vc].rearrange("p (a h e) -> p a h e", a=2, e=HD)

        q_ps, k_ps = (s_ps[:, n, :].rearrange("p (part t) -> p part t", t=T) for n in range(2))

        y_ready, ones_ready = mem.sem("y_ready"), mem.sem("ones_ready")
        q_psum, q_turned, q_ready = mem.sem("q_psum"), mem.sem("q_turned"), mem.sem("q_ready")
        k_psum, k_turned, k_ready = mem.sem("k_psum"), mem.sem("k_turned"), mem.sem("k_ready")
        v_psum, v_ready = mem.sem("v_psum"), mem.sem("v_ready")
        s_psum, top_ready, s_ready = mem.sem("s_psum"), mem.sem("top_ready"), mem.sem("s_ready")
        p_ready, t_psum, t_ready = mem.sem("p_ready"), mem.sem("t_psum"), mem.sem("t_ready")
        o_psum, inv_ready, o_ready = mem.sem("o_psum"), mem.sem("inv_ready"), mem.sem("o_ready")
        ot_psum, ot_ready = mem.sem("ot_psum"), mem.sem("ot_ready")
        out_psum, x_added = mem.sem("out_psum"), mem.sem("x_added")
        table_ready, v_split = mem.sem("table_ready"), mem.sem("v_split")
        k_summed = mem.sem("k_summed")
        rest_ready, low_ready = mem.sem("rest_ready"), mem.sem("low_ready")

        def quadrants(u):
            return range(u % 2 * 2, u % 2 * 2 + 2)

        def block_of(half, g, n):
            return g % 2 if half == 0 else 2 + 2 * (g % 2) + n

        def span(half):
            return half * 2 * HALF, 2 * HALF * (half + 1)

        with nc.Block() as block:

            @block.gpsimd
            def _(pool):
                nc.gpsimd.memset(v_top[:, :, :, HD:HD + 1], 1.0).then_inc(ones_ready, 1)
                nc.gpsimd.memset(v_rest[:, :, :, HD:HD + 1], 0.0).then_inc(ones_ready, 1)

                def project(n):
                    nc.gpsimd.tensor_copy(y[:, :], src[:, bass.ds(n * T, T)]).then_inc(y_ready, 1)
                    pool.wait_ge(q_turned, 2 * n + 2)
                    nc.gpsimd.tensor_tensor(q[:, :], q_cos[:, :], q_sin[:, :], ALU.add).then_inc(q_ready, 1)
                    pool.wait_ge(v_split, 2 * n + 2)
                    nc.gpsimd.tensor_tensor(v_low[:, :, :, :], v_rest[:, :, :, :], v_part[1], ALU.subtract).then_inc(v_ready, 1)

                project(0)
                with pool.Fori(0, B - 1) as b:
                    pool.wait_ge(v_psum, b + 1)
                    project(b + 1)

            @block.tensor
            def _(pe):
                def project_qk(n):
                    pe.wait_ge(y_ready, n + 1)
                    for ps, weights, done in ((q_ps, wq, q_psum), (k_ps, wk, k_psum)):
                        for part in range(2):
                            last = nc.tensor.matmul(ps[:, part, :], weights[:, part, :], y[:, :], start=True, stop=True)
                        last.then_inc(done, 1)

                def project_v(n):
                    for a in range(2):
                        last = nc.tensor.matmul(v_bank[:, a * vc:(a + 1) * vc], y[:, a * HALF:(a + 1) * HALF], wv,
                                                start=True, stop=True)
                    last.then_inc(v_psum, 1)

                def scores(b, u):
                    for half in range(2):
                        keys = (half + 1) * HALF
                        for g in quadrants(u):
                            quad = slice(QUAD * g, QUAD * (g + 1))
                            nc.tensor.matmul(s_ps[:, g, half * T:half * T + keys],
                                             q[quad, half * HALF:(half + 1) * HALF], k[quad, u // 2, 0:keys],
                                             start=True, stop=False)
                        for g in quadrants(u):
                            last = nc.tensor.matmul(s_ps[:, g, half * (T + HALF):half * (T + HALF) + HALF],
                                                    ident_bf, mask_bf, start=False, stop=True)
                    last.then_inc(s_psum, 1)

                def first_scores(n):
                    pe.wait_ge(q_ready, n + 1)
                    pe.wait_ge(k_ready, RUNS * (n + 1))
                    scores(n, 0)

                def turns(b, u):
                    pe.wait_ge(p_ready, UNITS * b + u + 1)
                    if u >= 1:
                        pe.wait_ge(t_ready, UNITS * b + u)
                    for n in range(UBLK):
                        at = n % (UBLK // 2) * HALF
                        last = nc.tensor.transpose(t_ps[:, n // (UBLK // 2), at:at + HALF],
                                                   prob[:, u % 2, n * HALF:(n + 1) * HALF], ident)
                    last.then_inc(t_psum, 1)

                def values(b, u):
                    if u == 0:
                        pe.wait_ge(x_added, b + 1)
                        pe.wait_ge(v_ready, b + 1)
                    pe.wait_ge(low_ready, UNITS * b + u + 1)
                    rows = high(prob_t[:, u % 2, :, :]), high(rest_t[:, u % 2, :, :]), low_t[:, u % 2, :, :]
                    for half in range(2):
                        for g in quadrants(u):
                            head = NQUAD * g + u // 2
                            hv = g if krun == 1 else head
                            terms = [(rows[i][:, block_of(half, g, n), :], v_part[j][:, n, hv, :])
                                     for n in range(half + 1) for i in range(3) for j in range(3 - i)]
                            for m, (keys_first, columns) in enumerate(terms):
                                last = nc.tensor.matmul(out_heads[:, half, head, :], keys_first, columns,
                                                        start=(m == 0), stop=(m == len(terms) - 1))
                    last.then_inc(o_psum, 1)

                def sequence(b, more):
                    for u in range(UNITS):
                        if 1 <= u < UNITS - 1:
                            pe.wait_ge(s_ready, UNITS * b + u)
                            scores(b, u + 1)
                        elif u and more:
                            pe.wait_ge(s_ready, UNITS * b + u)
                            project_qk(b + 1)
                        turns(b, u)
                        if u >= 1:
                            values(b, u - 1)
                    if more:
                        first_scores(b + 1)
                    values(b, UNITS - 1)
                    if more:
                        project_v(b + 1)
                        scores(b + 1, 1)
                        pe.wait_ge(v_split, 2 * b + 4)
                    pe.wait_ge(o_ready, b + 1)
                    for half in range(2):
                        last = nc.tensor.transpose(v_bank[:, half * HALF:(half + 1) * HALF], heads[:, half, :], ident)
                    last.then_inc(ot_psum, 1)
                    pe.wait_ge(ot_ready, b + 1)
                    nc.tensor.matmul(o_ps[:, 0:T], wo, heads_t[:, :], start=True, stop=True).then_inc(out_psum, 1)

                project_qk(0)
                project_v(0)
                first_scores(0)
                scores(0, 1)
                with pe.Fori(0, B - 1) as b:
                    sequence(b, True)
                sequence(B - 1, False)

            @block.scalar
            def _(act):
                def exps(b, u):
                    act.wait_ge(s_ready, UNITS * b + u + 1)
                    nc.scalar.activation(prob[:, u % 2, :], prob[:, u % 2, :], ACT.Exp, scale=scale).then_inc(p_ready, 1)

                def read_v(n):
                    act.wait_ge(v_psum, n + 1)
                    nc.scalar.activation(v_top[:, :, :, 0:HD], v_ps, ACT.Identity).then_inc(v_split, 1)

                def sequence(b, more):
                    for u in range(UNITS):
                        act.wait_ge(t_psum, UNITS * b + u + 1)
                        nc.scalar.activation(prob_t[:, u % 2, :, :].rearrange("p (n m) k -> p n (m k)", n=2), t_blocks,
                                             ACT.Identity).then_inc(t_ready, 1)
                        if u + 1 < UNITS:
                            exps(b, u + 1)
                    if more:
                        exps(b + 1, 0)
                        read_v(b + 1)
                    act.wait_ge(ot_psum, b + 1)
                    nc.scalar.activation(heads_t[:, :], v_bank[:, 0:T], ACT.Identity).then_inc(ot_ready, 1)

                nc.scalar.activation(inv[:, 0, 0:1], ident[:, 0:1], ACT.Exp).then_inc(table_ready, 1)
                act.wait_ge(table_ready, 1)
                act.wait_ge(ones_ready, 2)
                read_v(0)
                exps(0, 0)
                with act.Fori(0, B - 1) as b:
                    sequence(b, True)
                sequence(B - 1, False)

            @block.vector
            def _(dve):
                def rotate_qk(n):
                    for ps, done, cos_part, sin_part, turned in ((q_ps, q_psum, q_cos, q_sin, q_turned),
                                                                 (k_ps, k_psum, k_cos, k_sin, k_turned)):
                        dve.wait_ge(done, n + 1)
                        nc.vector.tensor_tensor(cos_part[:, :], ps[:, 0, :], cos, ALU.mult).then_inc(turned, 1)
                        nc.vector.tensor_tensor(sin_part[:, :], ps[:, 1, :], sin, ALU.mult).then_inc(turned, 1)
                    dve.wait_ge(k_turned, 2 * n + 2)
                    nc.vector.tensor_tensor(k_heads[:, :], k_cos[:, :], k_sin[:, :], ALU.add).then_inc(k_summed, 1)
                    dve.wait_ge(k_summed, n + 1)
                    for r in range(RUNS):
                        nc.vector.tensor_scalar(k[:, r, :], k_heads[:, :], run_mask[:, r:r + 1], None, ALU.mult).then_inc(k_ready, 1)

                def split_v(n):
                    dve.wait_ge(v_split, 2 * n + 1)
                    nc.vector.tensor_tensor(v_rest[:, :, :, 0:HD], v_ps, v_top[:, :, :, 0:HD], ALU.subtract).then_inc(v_split, 1)

                def less_top(b, u):
                    n = UNITS * b + u
                    mine = slice(quadrants(u)[0], quadrants(u)[-1] + 1)
                    dve.wait_ge(s_psum, n + 1)
                    nc.vector.tensor_reduce(top[:, u % 2, 0, :], s_ps[:, mine, 0:HALF], AX_X, ALU.max)
                    nc.vector.tensor_reduce(top[:, u % 2, 1, :], s_ps[:, mine, T:2 * T], AX_X, ALU.max).then_inc(top_ready, 1)
                    dve.wait_ge(top_ready, n + 1)
                    if u >= 2:
                        dve.wait_ge(t_psum, n - 1)
                    for half in range(2):
                        lo, size = span(half)
                        keys = (half + 1) * HALF
                        last = nc.vector.tensor_tensor(
                            prob[:, u % 2, lo:lo + size].rearrange("p (g k) -> p g k", k=keys),
                            s_ps[:, mine, half * T:half * T + keys],
                            top[:, u % 2, half, :].unsqueeze(2).broadcast_to([P, 2, keys]), ALU.subtract)
                    last.then_inc(s_ready, 1)

                def split_probabilities(b, u):
                    n = UNITS * b + u
                    dve.wait_ge(t_ready, n + 1)
                    nc.vector.tensor_tensor(rest_t[:, u % 2, :, :], prob_t[:, u % 2, :, :], high(prob_t[:, u % 2, :, :]),
                                            ALU.subtract).then_inc(rest_ready, 1)
                    dve.wait_ge(rest_ready, n + 1)
                    nc.vector.tensor_tensor(low_t[:, u % 2, :, :], rest_t[:, u % 2, :, :], high(rest_t[:, u % 2, :, :]),
                                            ALU.subtract).then_inc(low_ready, 1)

                def sequence(b, more):
                    for u in range(UNITS):
                        if u + 1 < UNITS:
                            less_top(b, u + 1)
                        elif more:
                            rotate_qk(b + 1)
                        split_probabilities(b, u)
                    if more:
                        less_top(b + 1, 0)
                    dve.wait_ge(o_psum, UNITS * (b + 1))
                    nc.vector.reciprocal(inv[:, :, :], out_heads[:, :, :, HD]).then_inc(inv_ready, 1)
                    dve.wait_ge(inv_ready, b + 1)
                    nc.vector.tensor_tensor(heads[:, :, :].rearrange("p a (h e) -> p a h e", e=HD),
                                            out_heads[:, :, :, 0:HD],
                                            inv[:, :, :].unsqueeze(3).broadcast_to([P, 2, NHEAD, HD]),
                                            ALU.mult).then_inc(o_ready, 1)
                    if more:
                        split_v(b + 1)
                    dve.wait_ge(out_psum, b + 1)
                    here = x[:, bass.ds(b * T, T)]
                    nc.vector.tensor_tensor(here, o_ps[:, 0:T], here, ALU.add).then_inc(x_added, 1)

                dve.sem_inc(x_added, 1)
                dve.wait_ge(table_ready, 1)
                rotate_qk(0)
                split_v(0)
                less_top(0, 0)
                with dve.Fori(0, B - 1) as b:
                    sequence(b, True)
                sequence(B - 1, False)


def cond_gate_stage(nc, tag, x, dst, cond, w1, b1, w2, b2):
    with ExitStack() as stack:
        mem = Memory(nc, stack, tag)
        ps = mem.ps("ps", [P, 2, B])
        z, sig, h, gate = (mem.sb(n, [P, B]) for n in ("z", "sig", "h", "gate"))
        z_psum, sig_ready, z_ready, h_ready = (mem.sem(n) for n in ("z_psum", "sig_ready", "z_ready", "h_ready"))
        gate_psum, gate_ready, factor_ready, done = (mem.sem(n) for n in ("gate_psum", "gate_ready", "factor_ready", "done"))
        with nc.Block() as block:

            @block.tensor
            def _(pe):
                nc.tensor.matmul(ps[:, 0, :], w1, cond, start=True, stop=True).then_inc(z_psum, 1)
                pe.wait_ge(h_ready, 1)
                nc.tensor.matmul(ps[:, 1, :], w2, h[:, :], start=True, stop=True).then_inc(gate_psum, 1)

            @block.scalar
            def _(act):
                act.wait_ge(z_psum, 1)
                nc.scalar.activation(sig[:, :], ps[:, 0, :], ACT.Sigmoid, bias=b1).then_inc(sig_ready, 1)
                act.wait_ge(gate_psum, 1)
                nc.scalar.activation(gate[:, :], ps[:, 1, :], ACT.Sigmoid, bias=b2).then_inc(gate_ready, 1)

            @block.vector
            def _(dve):
                dve.wait_ge(sig_ready, 1)
                nc.vector.tensor_scalar(z[:, :], ps[:, 0, :], b1, None, ALU.add).then_inc(z_ready, 1)
                dve.wait_ge(z_ready, 1)
                nc.vector.tensor_tensor(h[:, :], z[:, :], sig[:, :], ALU.mult).then_inc(h_ready, 1)
                dve.wait_ge(gate_ready, 1)
                nc.vector.tensor_scalar(sig[:, :], gate[:, :], 1.0, None, ALU.add).then_inc(factor_ready, 1)
                dve.wait_ge(factor_ready, 1)
                nc.vector.tensor_tensor(dst.rearrange("p (b t) -> p b t", t=T), x.rearrange("p (b t) -> p b t", t=T),
                                        sig[:, :].unsqueeze(2).broadcast_to([P, B, T]), ALU.mult).then_inc(done, 1)


def attention_weights(w, heads):
    cols = np.repeat(w.reshape(D, heads, HD), NHEAD // heads, 1)
    half = HD // 2
    both = np.stack([cols, np.concatenate([cols[..., half:], cols[..., :half]], -1)], 1)
    return both.reshape(D, 2, P)


def run_masks():
    return (np.arange(P)[:, None] // HD % RUNS == np.arange(RUNS)).astype(np.float32)


def rope_tables(repeat):
    half = HD // 2
    freq = (1.0 / 10000.0 ** (np.arange(half, dtype=np.float32) / half)).astype(np.float32)
    angle = np.arange(T, dtype=np.float32)[:, None] * freq[None, :]
    dims = np.repeat(np.arange(half), 2) if repeat else np.tile(np.arange(half), 2)
    sign = np.where(np.arange(HD) < half, -1.0, 1.0)
    cos = np.cos(angle).T[dims].astype(np.float32)
    sin = (np.sin(angle).T[dims] * sign[:, None]).astype(np.float32)
    return np.tile(cos, (NHEAD, 1)), np.tile(sin, (NHEAD, 1))
NEXP = 8
TILES = CHUNK // P
FAR = 3.0e38
MAGIC = 1.5 * 2.0 ** 23


def over_experts(ap):
    return ap.unsqueeze(2).broadcast_to([P, TILES, NEXP])


def over_tiles(ap):
    return ap.unsqueeze(1).broadcast_to([P, TILES, NEXP])


def top2(nc, dve, score, rank, buf, one, picked, chain, at):
    best, buf2 = one
    for n in range(2):
        k = at + 5 * n
        hit = picked if n == 0 else buf2
        nc.vector.tensor_reduce(best, score, AX_X, ALU.max).then_inc(chain, 1)
        dve.wait_ge(chain, k + 1)
        nc.vector.tensor_tensor(buf, score, over_experts(best), ALU.is_equal).then_inc(chain, 1)
        dve.wait_ge(chain, k + 2)
        nc.vector.tensor_tensor(buf, buf, over_tiles(rank), ALU.mult).then_inc(chain, 1)
        dve.wait_ge(chain, k + 3)
        nc.vector.tensor_reduce(best, buf, AX_X, ALU.max).then_inc(chain, 1)
        dve.wait_ge(chain, k + 4)
        last = nc.vector.tensor_tensor(hit, buf, over_experts(best), ALU.is_equal)
        if n == 0:
            last.then_inc(chain, 1)
            dve.wait_ge(chain, k + 5)
            nc.vector.scalar_tensor_tensor(score, picked, -FAR, score, ALU.mult, ALU.add).then_inc(chain, 1)
            at += 1
            dve.wait_ge(chain, k + 6)
        else:
            last.then_inc(chain, 1)
            dve.wait_ge(chain, k + 5)
            nc.vector.tensor_tensor(picked, picked, buf2, ALU.add).then_inc(chain, 1)


TOP2_OPS = 12


def expert_stage(nc, tag, src, x, router, w_gate, b_gate, w_up, b_up, w_down, b_down, rank, ident):
    glu = w_up is not None
    with ExitStack() as stack:
        mem = Memory(nc, stack, tag)
        y = mem.sb("y", [P, CHUNK])
        small = {n: mem.sb(n, [P, TILES, NEXP]) for n in ("prob", "buf", "buf2", "picked", "share", "score")}
        best, norm = mem.sb("best", [P, TILES]), mem.sb("norm", [P, TILES])
        prob, buf, buf2, picked, share, score = (small[n][:, :, :] for n in small)
        share_t = mem.sb("share_t", [NEXP, CHUNK])
        sig, part = mem.sb("sig", [P, 2, CHUNK]), mem.sb("part", [P, 2, CHUNK])
        hidden = mem.sb("hidden", [P, 2, 2, CHUNK])
        acc = mem.sb("acc", [P, TILES, P])
        h_ps = mem.ps("h_ps", [P, 4, CHUNK])
        out_ps = mem.ps("out_ps", [P, 2, TILES, P])
        log_ps, turn_ps = mem.ps("log_ps", [P, CHUNK]), mem.ps("turn_ps", [P, CHUNK])
        logits = log_ps[:, 0:TILES * NEXP].rearrange("p (a e) -> p a e", e=NEXP)
        names = ("y_ready", "log_psum", "chain", "exp_in", "exp_ready", "share_ready", "share_psum", "share_t_ready",
                 "bias_psum", "bias_ready", "h_psum", "sig_ready", "part_ready", "h_ready", "out_psum", "acc_ready",
                 "turn_psum", "x_added")
        s = {n: mem.sem(n) for n in names}
        ROUTE = 5 + TOP2_OPS + (5 if glu else 1)

        with nc.Block() as block:

            @block.gpsimd
            def _(pool):
                pool.sem_inc(s["log_psum"], 1)
                with pool.Fori(0, NCHUNK) as c:
                    pool.wait_ge(s["log_psum"], c + 1)
                    nc.gpsimd.tensor_copy(y[:, :], src[:, bass.ds(c * CHUNK, CHUNK)]).then_inc(s["y_ready"], 1)

            @block.tensor
            def _(pe):
                def first_layer(c, e):
                    here = src[:, bass.ds(c * CHUNK, CHUNK)]
                    for n in range(2):
                        unit = 2 * NEXP * c + 2 * e + n
                        if glu:
                            pe.wait_ge(s["h_ready"], unit + 1)
                            nc.tensor.matmul(h_ps[:, 2 * n, :], w_gate[:, e, n * P:(n + 1) * P], here,
                                             start=True, stop=True)
                            nc.tensor.matmul(h_ps[:, 2 * n + 1, :], w_up[:, e, n * P:(n + 1) * P], here,
                                             start=True, stop=True).then_inc(s["h_psum"], 1)
                        else:
                            if e >= 2:
                                pe.wait_ge(s["h_ready"], unit - 1)
                            nc.tensor.matmul(h_ps[:, 2 * (e % 2) + n, :], w_gate[:, e, n * P:(n + 1) * P], here,
                                             start=True, stop=True).then_inc(s["h_psum"], 1)

                def second_layer(c, e):
                    pe.wait_ge(s["h_ready"], 2 * NEXP * c + 2 * e + (4 if glu else 2))
                    if e >= 2:
                        pe.wait_ge(s["acc_ready"], TILES * (NEXP * c + e - 1))
                    for a in range(TILES):
                        for n in range(2):
                            last = nc.tensor.matmul(out_ps[:, e % 2, a, :], hidden[:, e % 2, n, a * P:(a + 1) * P],
                                                    w_down[:, e, n, :], start=(n == 0), stop=(n == 1))
                    last.then_inc(s["out_psum"], 1)

                with pe.Fori(0, NCHUNK) as c:
                    pe.wait_ge(s["y_ready"], c + 1)
                    for a in range(TILES):
                        last = nc.tensor.matmul(logits[:, a, :], y[:, a * P:(a + 1) * P], router, start=True, stop=True)
                    last.then_inc(s["log_psum"], 1)
                    first_layer(c, 0)
                    first_layer(c, 1) if not glu else None
                    pe.wait_ge(s["share_ready"], c + 1)
                    pe.wait_ge(s["x_added"], c + 1)
                    for a in range(TILES):
                        last = nc.tensor.transpose(turn_ps[0:NEXP, a * P:(a + 1) * P], share[:, a, :], ident)
                    last.then_inc(s["share_psum"], 1)
                    first_layer(c, 1) if glu else None
                    pe.wait_ge(s["share_t_ready"], c + 1)
                    for a in range(TILES):
                        last = nc.tensor.matmul(log_ps[:, a * P:(a + 1) * P], share_t[:, a * P:(a + 1) * P], b_down,
                                                start=True, stop=True)
                    last.then_inc(s["bias_psum"], 1)
                    for e in range(NEXP):
                        if glu and 1 <= e < NEXP - 1:
                            first_layer(c, e + 1)
                        second_layer(c, e)
                        if not glu and e + 2 < NEXP:
                            first_layer(c, e + 2)
                    pe.wait_ge(s["acc_ready"], TILES * NEXP * (c + 1))
                    for a in range(TILES):
                        last = nc.tensor.transpose(turn_ps[:, a * P:(a + 1) * P], acc[:, a, :], ident)
                    last.then_inc(s["turn_psum"], 1)

            @block.scalar
            def _(act):
                with act.Fori(0, NCHUNK) as c:
                    act.wait_ge(s["exp_in"], c + 1)
                    nc.scalar.activation(prob, score, ACT.Exp).then_inc(s["exp_ready"], 1)
                    for e in range(NEXP):
                        for n in range(2):
                            unit = 2 * NEXP * c + 2 * e + n
                            act.wait_ge(s["h_psum"], unit + 1)
                            if glu:
                                nc.scalar.activation(sig[:, n, :], h_ps[:, 2 * n, :], ACT.Sigmoid,
                                                     bias=b_gate[:, e, n:n + 1]).then_inc(s["sig_ready"], 1)
                            else:
                                if e >= 2:
                                    act.wait_ge(s["out_psum"], NEXP * c + e - 1)
                                nc.scalar.activation(hidden[:, e % 2, n, :], h_ps[:, 2 * (e % 2) + n, :], ACT.Relu,
                                                     bias=b_gate[:, e, n:n + 1]).then_inc(s["h_ready"], 1)

            @block.vector
            def _(dve):
                dve.sem_inc(s["x_added"], 1)
                if glu:
                    dve.sem_inc(s["h_ready"], 2)
                chain = s["chain"]

                def route(c):
                    at = ROUTE * c
                    dve.wait_ge(s["log_psum"], c + 2)
                    nc.vector.tensor_reduce(best[:, :], logits, AX_X, ALU.max).then_inc(chain, 1)
                    dve.wait_ge(chain, at + 1)
                    nc.vector.tensor_tensor(score, logits, over_experts(best[:, :]), ALU.subtract).then_inc(s["exp_in"], 1)
                    dve.wait_ge(s["exp_ready"], c + 1)
                    nc.vector.tensor_reduce(norm[:, :], prob, AX_X, ALU.add).then_inc(chain, 1)
                    dve.wait_ge(chain, at + 2)
                    nc.vector.reciprocal(best[:, :], norm[:, :]).then_inc(chain, 1)
                    dve.wait_ge(chain, at + 3)
                    nc.vector.tensor_tensor(prob, prob, over_experts(best[:, :]), ALU.mult).then_inc(chain, 1)
                    dve.wait_ge(chain, at + 4)
                    nc.vector.tensor_copy(score, prob).then_inc(chain, 1)
                    dve.wait_ge(chain, at + 5)
                    top2(nc, dve, score, rank, buf, (best[:, :], buf2), picked, chain, at + 5)
                    at = at + 5 + TOP2_OPS
                    dve.wait_ge(chain, at)
                    if glu:
                        nc.vector.tensor_tensor(buf, prob, picked, ALU.mult).then_inc(chain, 1)
                        dve.wait_ge(chain, at + 1)
                        nc.vector.tensor_reduce(norm[:, :], buf, AX_X, ALU.add).then_inc(chain, 1)
                        dve.wait_ge(chain, at + 2)
                        nc.vector.tensor_scalar(norm[:, :], norm[:, :], 1e-9, None, ALU.add).then_inc(chain, 1)
                        dve.wait_ge(chain, at + 3)
                        nc.vector.reciprocal(best[:, :], norm[:, :]).then_inc(chain, 1)
                        dve.wait_ge(chain, at + 4)
                        nc.vector.tensor_tensor(share, buf, over_experts(best[:, :]), ALU.mult).then_inc(s["share_ready"], 1)
                        nc.vector.sem_inc(chain, 1)
                    else:
                        nc.vector.tensor_tensor(share, prob, picked, ALU.mult).then_inc(s["share_ready"], 1)
                        nc.vector.sem_inc(chain, 1)

                def turned_shares(c):
                    dve.wait_ge(s["share_psum"], c + 1)
                    nc.vector.tensor_copy(share_t[:, :], turn_ps[0:NEXP, :]).then_inc(s["share_t_ready"], 1)

                def output_biases(c):
                    dve.wait_ge(s["bias_psum"], c + 1)
                    nc.vector.tensor_copy(acc[:, :, :].rearrange("p a d -> p (a d)"), log_ps[:, :]).then_inc(s["bias_ready"], 1)

                def hidden_layer(c, e):
                    for n in range(2):
                        unit = 2 * NEXP * c + 2 * e + n
                        dve.wait_ge(s["sig_ready"], unit + 1)
                        nc.vector.scalar_tensor_tensor(part[:, n, :], h_ps[:, 2 * n, :], b_gate[:, e, n:n + 1],
                                                       sig[:, n, :], ALU.add, ALU.mult).then_inc(s["part_ready"], 1)
                        dve.wait_ge(s["part_ready"], unit + 1)
                        if e >= 2:
                            dve.wait_ge(s["out_psum"], NEXP * c + e - 1)
                        nc.vector.scalar_tensor_tensor(hidden[:, e % 2, n, :], h_ps[:, 2 * n + 1, :],
                                                       b_up[:, e, n:n + 1], part[:, n, :], ALU.add,
                                                       ALU.mult).then_inc(s["h_ready"], 1)

                def add_expert(c, e):
                    dve.wait_ge(s["out_psum"], NEXP * c + e + 1)
                    if e == 0:
                        dve.wait_ge(s["bias_ready"], c + 1)
                    else:
                        dve.wait_ge(s["acc_ready"], TILES * (NEXP * c + e))
                    for a in range(TILES):
                        nc.vector.scalar_tensor_tensor(acc[:, a, :], out_ps[:, e % 2, a, :], share[:, a, e:e + 1],
                                                       acc[:, a, :], ALU.mult, ALU.add).then_inc(s["acc_ready"], 1)

                with dve.Fori(0, NCHUNK) as c:
                    route(c)
                    if glu:
                        hidden_layer(c, 0)
                    turned_shares(c)
                    if glu:
                        hidden_layer(c, 1)
                    output_biases(c)
                    for e in range(NEXP):
                        if glu and 1 <= e < NEXP - 1:
                            hidden_layer(c, e + 1)
                        add_expert(c, e)
                    dve.wait_ge(s["turn_psum"], c + 1)
                    here = x[:, bass.ds(c * CHUNK, CHUNK)]
                    nc.vector.tensor_tensor(here, turn_ps[:, :], here, ALU.add).then_inc(s["x_added"], 1)


def routed_cond_stage(nc, tag, src, dst, cond, router, router_t, router_bias, sw1, sw3, sw2, rw1, rw2, rank, ones, ident):
    with ExitStack() as stack:
        mem = Memory(nc, stack, tag)
        cond_w = mem.sb("cond_w", [P, B, NEXP])
        t_bias = mem.sb("t_bias", [P, B, NEXP])
        y = mem.sb("y", [P, CHUNK])
        small = {n: mem.sb(n, [P, TILES, NEXP]) for n in ("prob", "buf", "buf2", "picked", "share", "score")}
        prob, buf, buf2, picked, share, score = (small[n][:, :, :] for n in small)
        best, norm, have, even = (mem.sb(n, [P, TILES]) for n in ("best", "norm", "have", "even"))
        sig, part = mem.sb("sig", [P, 2, CHUNK]), mem.sb("part", [P, 2, CHUNK])
        shared = mem.sb("shared", [P, 2, CHUNK])
        routed = mem.sb("routed", [P, NEXP // 2, CHUNK])
        acc = mem.sb("acc", [P, TILES, P])
        h_ps = mem.ps("h_ps", [P, 4, CHUNK])
        out_ps = mem.ps("out_ps", [P, 2, TILES, P])
        log_ps, turn_ps = mem.ps("log_ps", [P, CHUNK]), mem.ps("turn_ps", [P, CHUNK])
        logits = log_ps[:, 0:TILES * NEXP].rearrange("p (a e) -> p a e", e=NEXP)
        names = ("cond_w_ready", "t_psum", "t_bias_ready", "y_ready", "log_psum", "chain", "score_in", "prob_ready",
                 "s_psum", "sig_ready", "part_ready", "shared_ready", "r_psum", "routed_ready", "out_psum", "acc_ready",
                 "turn_psum", "dst_ready")
        s = {n: mem.sem(n) for n in names}
        ROUTE = TOP2_OPS + 9

        with nc.Block() as block:

            @block.gpsimd
            def _(pool):
                pool.sem_inc(s["log_psum"], 1)
                with pool.Fori(0, NCHUNK) as c:
                    pool.wait_ge(s["log_psum"], c + 1)
                    nc.gpsimd.tensor_copy(y[:, :], src[:, bass.ds(c * CHUNK, CHUNK)]).then_inc(s["y_ready"], 1)

            @block.tensor
            def _(pe):
                pe.wait_ge(s["cond_w_ready"], 1)
                nc.tensor.matmul(log_ps[:, 0:B * NEXP], ones, cond_w[:, :, :], start=True, stop=True).then_inc(s["t_psum"], 1)
                pe.wait_ge(s["t_bias_ready"], 1)
                with pe.Fori(0, NCHUNK) as c:
                    here = src[:, bass.ds(c * CHUNK, CHUNK)]
                    pe.wait_ge(s["y_ready"], c + 1)
                    for a in range(TILES):
                        last = nc.tensor.matmul(logits[:, a, :], y[:, a * P:(a + 1) * P], router, start=True, stop=True)
                    last.then_inc(s["log_psum"], 1)
                    for n in range(2):
                        nc.tensor.matmul(h_ps[:, 2 * n, :], sw1[:, n * P:(n + 1) * P], here, start=True, stop=True)
                        nc.tensor.matmul(h_ps[:, 2 * n + 1, :], sw3[:, n * P:(n + 1) * P], here,
                                         start=True, stop=True).then_inc(s["s_psum"], 1)
                    pe.wait_ge(s["shared_ready"], 2 * c + 2)
                    for m in range(NEXP // 2):
                        nc.tensor.matmul(h_ps[:, m, :], rw1[:, m * P:(m + 1) * P], here,
                                         start=True, stop=True).then_inc(s["r_psum"], 1)
                    for a in range(TILES):
                        for n in range(2):
                            last = nc.tensor.matmul(out_ps[:, 0, a, :], shared[:, n, a * P:(a + 1) * P], sw2[:, n, :],
                                                    start=(n == 0), stop=(n == 1))
                    last.then_inc(s["out_psum"], 1)
                    for e in range(NEXP):
                        k = (NEXP + 1) * c + e + 1
                        rows = slice(P // 2 * (e % 2), P // 2 * (e % 2 + 1))
                        pe.wait_ge(s["routed_ready"], NEXP // 2 * c + e // 2 + 1)
                        if e >= 1:
                            pe.wait_ge(s["acc_ready"], TILES * (k - 1))
                        for a in range(TILES):
                            last = nc.tensor.matmul(out_ps[:, (e + 1) % 2, a, :], routed[rows, e // 2, a * P:(a + 1) * P],
                                                    rw2[rows, e // 2, :], start=True, stop=True)
                        last.then_inc(s["out_psum"], 1)
                    pe.wait_ge(s["acc_ready"], TILES * (NEXP + 1) * (c + 1))
                    for a in range(TILES):
                        last = nc.tensor.transpose(turn_ps[:, a * P:(a + 1) * P], acc[:, a, :], ident)
                    last.then_inc(s["turn_psum"], 1)

            @block.scalar
            def _(act):
                with act.Fori(0, NCHUNK) as c:
                    act.wait_ge(s["score_in"], c + 1)
                    nc.scalar.activation(prob, score, ACT.Sigmoid).then_inc(s["prob_ready"], 1)
                    for n in range(2):
                        act.wait_ge(s["s_psum"], 2 * c + n + 1)
                        nc.scalar.activation(sig[:, n, :], h_ps[:, 2 * n, :], ACT.Sigmoid).then_inc(s["sig_ready"], 1)
                    for m in range(NEXP // 2):
                        act.wait_ge(s["r_psum"], NEXP // 2 * c + m + 1)
                        nc.scalar.activation(routed[:, m, :], h_ps[:, m, :], ACT.Gelu).then_inc(s["routed_ready"], 1)
                    act.wait_ge(s["turn_psum"], c + 1)
                    nc.scalar.activation(dst[:, bass.ds(c * CHUNK, CHUNK)], turn_ps[:, :], ACT.Identity,
                                         scale=1.0 / 3.0).then_inc(s["dst_ready"], 1)

            @block.vector
            def _(dve):
                chain = s["chain"]
                nc.vector.tensor_tensor(cond_w[:, :, :], cond.unsqueeze(2).broadcast_to([P, B, NEXP]),
                                        router_t.unsqueeze(1).broadcast_to([P, B, NEXP]), ALU.mult).then_inc(s["cond_w_ready"], 1)
                dve.wait_ge(s["t_psum"], 1)
                nc.vector.tensor_copy(t_bias[:, :, :].rearrange("p b e -> p (b e)"),
                                      log_ps[:, 0:B * NEXP]).then_inc(s["t_bias_ready"], 1)
                dve.wait_ge(s["t_bias_ready"], 1)
                SEQS = CHUNK // T

                def route(c):
                    at = ROUTE * c
                    dve.wait_ge(s["log_psum"], c + 2)
                    for q in range(SEQS):
                        half = slice(q * TILES // SEQS, (q + 1) * TILES // SEQS)
                        last = nc.vector.tensor_tensor(score[:, half, :], logits[:, half, :],
                                                       t_bias[:, bass.ds(c * SEQS + q, 1), :].broadcast_to(
                                                           [P, TILES // SEQS, NEXP]), ALU.add)
                    last.then_inc(s["score_in"], 1)
                    dve.wait_ge(s["prob_ready"], c + 1)
                    nc.vector.tensor_tensor(score, prob, over_tiles(router_bias), ALU.add).then_inc(chain, 1)
                    dve.wait_ge(chain, at + 1)
                    top2(nc, dve, score, rank, buf, (best[:, :], buf2), picked, chain, at + 1)
                    at = at + 1 + TOP2_OPS
                    dve.wait_ge(chain, at)
                    nc.vector.tensor_tensor(buf, prob, picked, ALU.mult).then_inc(chain, 1)
                    dve.wait_ge(chain, at + 1)
                    nc.vector.tensor_reduce(norm[:, :], buf, AX_X, ALU.add).then_inc(chain, 1)
                    dve.wait_ge(chain, at + 2)
                    nc.vector.tensor_scalar(have[:, :], norm[:, :], 1e-9, None, ALU.is_gt).then_inc(chain, 1)
                    nc.vector.tensor_scalar(norm[:, :], norm[:, :], 1e-9, None, ALU.add).then_inc(chain, 1)
                    dve.wait_ge(chain, at + 4)
                    nc.vector.reciprocal(best[:, :], norm[:, :]).then_inc(chain, 1)
                    nc.vector.tensor_scalar(even[:, :], have[:, :], -0.5, 0.5, ALU.mult, ALU.add).then_inc(chain, 1)
                    dve.wait_ge(chain, at + 6)
                    nc.vector.tensor_tensor(norm[:, :], best[:, :], have[:, :], ALU.mult)
                    nc.vector.tensor_tensor(buf2, picked, over_experts(even[:, :]), ALU.mult).then_inc(chain, 1)
                    dve.wait_ge(chain, at + 7)
                    nc.vector.tensor_tensor(buf, buf, over_experts(norm[:, :]), ALU.mult).then_inc(chain, 1)
                    dve.wait_ge(chain, at + 8)
                    nc.vector.tensor_tensor(share, buf, buf2, ALU.add)

                with dve.Fori(0, NCHUNK) as c:
                    route(c)
                    for n in range(2):
                        m = 2 * c + n
                        dve.wait_ge(s["sig_ready"], m + 1)
                        nc.vector.tensor_tensor(part[:, n, :], h_ps[:, 2 * n, :], sig[:, n, :], ALU.mult).then_inc(s["part_ready"], 1)
                        dve.wait_ge(s["part_ready"], m + 1)
                        nc.vector.tensor_tensor(shared[:, n, :], h_ps[:, 2 * n + 1, :], part[:, n, :],
                                                ALU.mult).then_inc(s["shared_ready"], 1)
                    dve.wait_ge(s["out_psum"], (NEXP + 1) * c + 1)
                    nc.vector.tensor_copy(acc[:, :, :], out_ps[:, 0, :, :]).then_inc(s["acc_ready"], TILES)
                    for e in range(NEXP):
                        k = (NEXP + 1) * c + e + 1
                        dve.wait_ge(s["out_psum"], k + 1)
                        dve.wait_ge(s["acc_ready"], TILES * k)
                        for a in range(TILES):
                            nc.vector.scalar_tensor_tensor(acc[:, a, :], out_ps[:, (e + 1) % 2, a, :], share[:, a, e:e + 1],
                                                           acc[:, a, :], ALU.mult, ALU.add).then_inc(s["acc_ready"], 1)


def ternary_stage(nc, tag, src, x, w, bias):
    with ExitStack() as stack:
        mem = Memory(nc, stack, tag)
        most, size = mem.sb("most", [P, 1]), mem.sb("size", [P, 1])
        most_all, size_all = mem.sb("most_all", [P, 1]), mem.sb("size_all", [P, 1])
        step, inv, over, under, back = (mem.sb(n, [P, 1]) for n in ("step", "inv", "over", "under", "back"))
        below = mem.sb("below", [P, P])
        wq = mem.sb("wq", [P, P], BF16)
        num = mem.sb("num", [P, TOK])
        xq = mem.sb("xq", [P, TOK], BF16)
        out = mem.sb("out", [P, 2, CHUNK])
        ps = mem.ps("ps", [P, NCHUNK, CHUNK])
        sizes_ready, all_ready, chain = mem.sem("sizes_ready"), mem.sem("all_ready"), mem.sem("chain")
        out_psum, out_ready, x_added = mem.sem("out_psum"), mem.sem("out_ready"), mem.sem("x_added")

        with nc.Block() as block:

            @block.gpsimd
            def _(pool):
                pool.wait_ge(sizes_ready, 2)
                nc.gpsimd.partition_all_reduce(most_all[:, :], most[:, :], P, RMAX).then_inc(all_ready, 1)
                nc.gpsimd.partition_all_reduce(size_all[:, :], size[:, :], P, RADD).then_inc(all_ready, 1)

            @block.vector
            def _(dve):
                nc.vector.tensor_reduce(most[:, :], src, AX_X, ALU.max, apply_absolute_value=True).then_inc(sizes_ready, 1)
                nc.vector.tensor_reduce(size[:, :], w, AX_X, ALU.add, apply_absolute_value=True).then_inc(sizes_ready, 1)
                dve.wait_ge(all_ready, 2)
                nc.vector.tensor_scalar(step[:, :], most_all[:, :], 1.0 / 127.0, None, ALU.mult).then_inc(chain, 1)
                nc.vector.tensor_scalar(over[:, :], size_all[:, :], 0.5 / (P * P), None, ALU.mult).then_inc(chain, 1)
                nc.vector.tensor_scalar(under[:, :], size_all[:, :], -0.5 / (P * P), None, ALU.mult).then_inc(chain, 1)
                dve.wait_ge(chain, 3)
                nc.vector.reciprocal(inv[:, :], step[:, :]).then_inc(chain, 1)
                nc.vector.tensor_scalar(below[:, :], w, under[:, 0:1], None, ALU.is_lt).then_inc(chain, 1)
                nc.vector.scalar_tensor_tensor(back[:, :], over[:, :], 2.0, step[:, :], ALU.mult, ALU.mult).then_inc(chain, 1)
                dve.wait_ge(chain, 6)
                nc.vector.scalar_tensor_tensor(wq[:, :], w, over[:, 0:1], below[:, :], ALU.is_gt,
                                               ALU.subtract).then_inc(chain, 1)
                nc.vector.tensor_scalar(num[:, :], src, inv[:, 0:1], MAGIC, ALU.mult, ALU.add).then_inc(chain, 1)
                dve.wait_ge(chain, 8)
                nc.vector.tensor_scalar(num[:, :], num[:, :], MAGIC, 127.0, ALU.subtract, ALU.min).then_inc(chain, 1)
                dve.wait_ge(chain, 9)
                nc.vector.tensor_scalar(xq[:, :], num[:, :], -128.0, None, ALU.max).then_inc(chain, 1)
                for c in range(NCHUNK):
                    dve.wait_ge(out_psum, c + 1)
                    if c >= 2:
                        dve.wait_ge(x_added, c - 1)
                    nc.vector.tensor_scalar(out[:, c % 2, :], ps[:, c, :], back[:, 0:1], bias, ALU.mult,
                                            ALU.add).then_inc(out_ready, 1)
                    dve.wait_ge(out_ready, c + 1)
                    here = x[:, c * CHUNK:(c + 1) * CHUNK]
                    nc.vector.tensor_tensor(here, out[:, c % 2, :], here, ALU.add).then_inc(x_added, 1)

            @block.tensor
            def _(pe):
                pe.wait_ge(chain, 10)
                for c in range(NCHUNK):
                    nc.tensor.matmul(ps[:, c, :], wq[:, :], xq[:, c * CHUNK:(c + 1) * CHUNK],
                                     start=True, stop=True).then_inc(out_psum, 1)


BIT_INNER = 512
BIT_BLOCKS = BIT_INNER // P


def bit_ffn_stage(nc, tag, src, x, w, ident, ident_bf):
    with ExitStack() as stack:
        mem = Memory(nc, stack, tag)
        size, size_all, mean, winv = (mem.sb(n, [P, 3]) for n in ("size", "size_all", "mean", "winv"))
        wnum = mem.sb("wnum", [P, 3, BIT_INNER])
        wq = mem.sb("wq", [P, 3, BIT_INNER], BF16)
        y = mem.sb("y", [P, 2, P])
        top, quant, back = mem.sb("top", [P, 2, 1]), mem.sb("quant", [P, 2, 1]), mem.sb("back", [P, 2, 2])
        top_p, quant_p, back_p = mem.sb("top_p", [P, 1]), mem.sb("quant_p", [P, 1]), mem.sb("back_p", [P, 2, 1])
        num = mem.sb("num", [P, P])
        yq, yq_t = mem.sb("yq", [P, P], BF16), mem.sb("yq_t", [P, P], BF16)
        sig, act_gate = mem.sb("sig", [P, 2, BIT_INNER]), mem.sb("act_gate", [P, BIT_INNER])
        prod, pnum = mem.sb("prod", [P, BIT_INNER]), mem.sb("pnum", [P, BIT_INNER])
        pq = mem.sb("pq", [P, BIT_INNER], BF16)
        pq_t = mem.sb("pq_t", [P, BIT_BLOCKS, P], BF16)
        out = mem.sb("out", [P, P])
        y_ps, turned_ps = mem.ps("y_ps", [P, CHUNK]), mem.ps("turned_ps", [P, 2 * CHUNK], BF16)
        gate_ps, up_ps = mem.ps("gate_ps", [P, 2, CHUNK]), mem.ps("up_ps", [P, 2, CHUNK])
        out_ps, turn_ps = mem.ps("out_ps", [P, CHUNK]), mem.ps("turn_ps", [P, CHUNK])
        pq_blocks = turned_ps[:, 0:BIT_INNER].rearrange("p (n k) -> p n k", k=P)
        yq_ps = turned_ps[:, BIT_INNER:BIT_INNER + P]
        names = ("size_ready", "all_ready", "wchain", "y_ready", "y_psum", "first_chain", "second_chain", "yq_ready", "yq_psum",
                 "yq_t_ready", "gate_psum", "up_psum", "sig_ready", "pq_ready", "pq_psum", "pq_t_ready", "out_psum",
                 "out_ready", "turn_psum", "x_added")
        s = {n: mem.sem(n) for n in names}
        NT = TOK // P

        def tiles(engine, tile):
            with engine.Fori(0, NT // 2 - 1) as i:
                for u in range(2):
                    tile(i * 2 + u, u, 2)
            tile(NT - 2, 0, 1)
            tile(NT - 1, 1, 0)

        with nc.Block() as block:

            @block.gpsimd
            def _(pool):
                pool.wait_ge(s["size_ready"], 1)
                nc.gpsimd.partition_all_reduce(size_all[:, :], size[:, :], P, RADD).then_inc(s["all_ready"], 1)
                pool.sem_inc(s["y_psum"], 2)
                with pool.Fori(0, NT // 2) as i:
                    for u in range(2):
                        n = i * 2 + u
                        pool.wait_ge(s["y_psum"], n + 1)
                        nc.gpsimd.tensor_copy(y[:, u, :], src[:, bass.ds(n * P, P)]).then_inc(s["y_ready"], 1)

            @block.tensor
            def _(pe):
                def turn_input(n, u):
                    pe.wait_ge(s["y_ready"], n + 1)
                    nc.tensor.transpose(y_ps[:, 0:P], y[:, u, :], ident).then_inc(s["y_psum"], 1)

                def turn_integers(n):
                    pe.wait_ge(s["yq_ready"], n + 2)
                    nc.tensor.transpose(yq_ps, yq[:, :], ident_bf).then_inc(s["yq_psum"], 1)

                def gate_and_up(n, u):
                    pe.wait_ge(s["yq_t_ready"], n + 1)
                    nc.tensor.matmul(gate_ps[:, u, :], yq_t[:, :], wq[:, 0, :], start=True, stop=True).then_inc(s["gate_psum"], 1)
                    nc.tensor.matmul(up_ps[:, u, :], yq_t[:, :], wq[:, 1, :], start=True, stop=True).then_inc(s["up_psum"], 1)

                def down(n):
                    pe.wait_ge(s["pq_ready"], n + 1)
                    for m in range(BIT_BLOCKS):
                        last = nc.tensor.transpose(pq_blocks[:, m, :], pq[:, m * P:(m + 1) * P], ident_bf)
                    last.then_inc(s["pq_psum"], 1)
                    pe.wait_ge(s["pq_t_ready"], n + 1)
                    for m in range(BIT_BLOCKS):
                        last = nc.tensor.matmul(out_ps[:, 0:P], pq_t[:, m, :], wq[:, 2, m * P:(m + 1) * P],
                                                start=(m == 0), stop=(m == BIT_BLOCKS - 1))
                    last.then_inc(s["out_psum"], 1)
                    pe.wait_ge(s["out_ready"], n + 1)
                    pe.wait_ge(s["x_added"], n + 1)
                    nc.tensor.transpose(turn_ps[:, 0:P], out[:, :], ident).then_inc(s["turn_psum"], 1)

                def tile(n, u, more):
                    if more:
                        turn_integers(n + 1)
                        if more > 1:
                            turn_input(n + 2, u)
                        gate_and_up(n + 1, 1 - u)
                    down(n)

                turn_input(0, 0)
                turn_integers(0)
                turn_input(1, 1)
                gate_and_up(0, 0)
                tiles(pe, tile)

            @block.scalar
            def _(act):
                def first_half(n, u):
                    act.wait_ge(s["yq_psum"], n + 1)
                    nc.scalar.activation(yq_t[:, :], yq_ps, ACT.Identity).then_inc(s["yq_t_ready"], 1)
                    act.wait_ge(s["gate_psum"], n + 1)
                    nc.scalar.activation(sig[:, u, :], gate_ps[:, u, :], ACT.Sigmoid, scale=back[:, u, 0:1]).then_inc(s["sig_ready"], 1)

                def tile(n, u, more):
                    if more:
                        first_half(n + 1, 1 - u)
                    act.wait_ge(s["pq_psum"], n + 1)
                    nc.scalar.activation(pq_t[:, :, :], pq_blocks, ACT.Identity).then_inc(s["pq_t_ready"], 1)
                    act.wait_ge(s["out_psum"], n + 1)
                    nc.scalar.activation(out[:, :], out_ps[:, 0:P], ACT.Identity, scale=back_p[:, u, :]).then_inc(s["out_ready"], 1)

                first_half(0, 0)
                tiles(act, tile)

            @block.vector
            def _(dve):
                wchain, chain, pchain = s["wchain"], s["first_chain"], s["second_chain"]
                nc.vector.tensor_reduce(size[:, :], w, AX_X, ALU.add, apply_absolute_value=True).then_inc(s["size_ready"], 1)
                dve.sem_inc(s["x_added"], 1)
                dve.wait_ge(s["all_ready"], 1)
                nc.vector.tensor_scalar(mean[:, :], size_all[:, :], 1.0 / (P * BIT_INNER), 1e-5, ALU.mult,
                                        ALU.max).then_inc(wchain, 1)
                dve.wait_ge(wchain, 1)
                nc.vector.reciprocal(winv[:, :], mean[:, :]).then_inc(wchain, 1)
                dve.wait_ge(wchain, 2)
                for m in range(3):
                    nc.vector.tensor_scalar(wnum[:, m, :], w[:, m, :], winv[:, m:m + 1], MAGIC, ALU.mult,
                                            ALU.add).then_inc(wchain, 1)
                dve.wait_ge(wchain, 5)
                nc.vector.tensor_scalar(wnum[:, :, :], wnum[:, :, :], MAGIC, 1.0, ALU.subtract, ALU.min).then_inc(wchain, 1)
                dve.wait_ge(wchain, 6)
                nc.vector.tensor_scalar(wq[:, :, :], wnum[:, :, :], -1.0, None, ALU.max).then_inc(s["yq_ready"], 1)

                def first_half(n, u, first=False):
                    at = n * 6
                    dve.wait_ge(s["y_psum"], n + 3)
                    nc.vector.tensor_reduce(top[:, u, :], y_ps[:, 0:P], AX_X, ALU.max,
                                            apply_absolute_value=True).then_inc(chain, 1)
                    dve.wait_ge(chain, at + 1)
                    nc.vector.tensor_scalar(top[:, u, :], top[:, u, :], 1e-5, 1.0 / 127.0, ALU.max, ALU.mult).then_inc(chain, 1)
                    dve.wait_ge(chain, at + 2)
                    nc.vector.reciprocal(quant[:, u, :], top[:, u, :]).then_inc(chain, 1)
                    dve.wait_ge(chain, at + 3)
                    nc.vector.tensor_scalar(num[:, :], y_ps[:, 0:P], quant[:, u, :], MAGIC, ALU.mult, ALU.add).then_inc(chain, 1)
                    nc.vector.tensor_scalar(back[:, u, :], mean[:, 0:2], top[:, u, :], None, ALU.mult).then_inc(chain, 1)
                    dve.wait_ge(chain, at + 5)
                    nc.vector.tensor_scalar(num[:, :], num[:, :], MAGIC, 127.0, ALU.subtract, ALU.min).then_inc(chain, 1)
                    dve.wait_ge(chain, at + 6)
                    if not first:
                        dve.wait_ge(s["yq_psum"], n)
                    nc.vector.tensor_scalar(yq[:, :], num[:, :], -128.0, None, ALU.max).then_inc(s["yq_ready"], 1)

                def second_half(n, u):
                    at = n * 8
                    dve.wait_ge(s["sig_ready"], n + 1)
                    nc.vector.scalar_tensor_tensor(act_gate[:, :], gate_ps[:, u, :], back[:, u, 0:1], sig[:, u, :], ALU.mult,
                                                   ALU.mult).then_inc(pchain, 1)
                    dve.wait_ge(pchain, at + 1)
                    dve.wait_ge(s["up_psum"], n + 1)
                    nc.vector.scalar_tensor_tensor(prod[:, :], up_ps[:, u, :], back[:, u, 1:2], act_gate[:, :], ALU.mult,
                                                   ALU.mult).then_inc(pchain, 1)
                    dve.wait_ge(pchain, at + 2)
                    nc.vector.tensor_reduce(top_p[:, :], prod[:, :], AX_X, ALU.max,
                                            apply_absolute_value=True).then_inc(pchain, 1)
                    dve.wait_ge(pchain, at + 3)
                    nc.vector.tensor_scalar(top_p[:, :], top_p[:, :], 1e-5, 1.0 / 127.0, ALU.max, ALU.mult).then_inc(pchain, 1)
                    dve.wait_ge(pchain, at + 4)
                    nc.vector.reciprocal(quant_p[:, :], top_p[:, :]).then_inc(pchain, 1)
                    dve.wait_ge(pchain, at + 5)
                    nc.vector.tensor_scalar(pnum[:, :], prod[:, :], quant_p[:, :], MAGIC, ALU.mult, ALU.add).then_inc(pchain, 1)
                    nc.vector.tensor_scalar(back_p[:, u, :], mean[:, 2:3], top_p[:, :], None, ALU.mult).then_inc(pchain, 1)
                    dve.wait_ge(pchain, at + 7)
                    nc.vector.tensor_scalar(pnum[:, :], pnum[:, :], MAGIC, 127.0, ALU.subtract, ALU.min).then_inc(pchain, 1)
                    dve.wait_ge(pchain, at + 8)
                    nc.vector.tensor_scalar(pq[:, :], pnum[:, :], -128.0, None, ALU.max).then_inc(s["pq_ready"], 1)

                def add_output(n):
                    dve.wait_ge(s["turn_psum"], n + 1)
                    here = x[:, bass.ds(n * P, P)]
                    nc.vector.tensor_tensor(here, turn_ps[:, 0:P], here, ALU.add).then_inc(s["x_added"], 1)

                first_half(0, 0, True)
                first_half(1, 1)
                second_half(0, 0)
                with dve.Fori(0, NT // 2 - 1) as i:
                    for u in range(2):
                        n = i * 2 + u
                        first_half(n + 2, u)
                        add_output(n)
                        second_half(n + 1, 1 - u)
                add_output(NT - 2)
                second_half(NT - 1, 1)
                add_output(NT - 1)


def threshold_stage(nc, tag, x, dst, draws):
    with ExitStack() as stack:
        mem = Memory(nc, stack, tag)
        size, p, cum, step = (mem.sb(n, [P, B, T]) for n in ("size", "p", "cum", "step"))
        zero = mem.sb("zero", [P, T])
        passed = mem.sb("passed", [P, B, T + 1])
        total, inv, bound = (mem.sb(n, [P, B]) for n in ("total", "inv", "bound"))
        chain, size_ready, p_ready, cum_ready, exp_ready = (mem.sem(n) for n in ("chain", "size_ready", "p_ready", "cum_ready", "exp_ready"))
        xb, db = x.rearrange("p (b t) -> p b t", t=T), dst.rearrange("p (b t) -> p b t", t=T)

        def over_time(ap):
            return ap.unsqueeze(2).broadcast_to([P, B, T])

        with nc.Block() as block:

            @block.scalar
            def _(act):
                nc.scalar.activation(size[:, :, :], xb, ACT.Abs).then_inc(size_ready, 1)
                act.wait_ge(p_ready, 1)
                nc.scalar.activation(p[:, :, :], p[:, :, :], ACT.Exp, scale=2.0).then_inc(exp_ready, 1)

            @block.vector
            def _(dve):
                nc.vector.memset(zero[:, :], 0.0).then_inc(chain, 1)
                nc.vector.memset(passed[:, :, 0:1], 1.0).then_inc(chain, 1)
                dve.wait_ge(size_ready, 1)
                nc.vector.tensor_reduce(total[:, :], size[:, :, :], AX_X, ALU.add).then_inc(chain, 1)
                dve.wait_ge(chain, 3)
                nc.vector.reciprocal(inv[:, :], total[:, :]).then_inc(chain, 1)
                dve.wait_ge(chain, 4)
                nc.vector.tensor_tensor(p[:, :, :], size[:, :, :], over_time(inv[:, :]), ALU.mult).then_inc(p_ready, 1)
                dve.wait_ge(exp_ready, 1)
                nc.vector.tensor_reduce(total[:, :], p[:, :, :], AX_X, ALU.add).then_inc(chain, 1)
                dve.wait_ge(chain, 5)
                nc.vector.reciprocal(inv[:, :], total[:, :]).then_inc(chain, 1)
                dve.wait_ge(chain, 6)
                nc.vector.tensor_tensor(p[:, :, :], p[:, :, :], over_time(inv[:, :]), ALU.mult).then_inc(chain, 1)
                dve.wait_ge(chain, 7)
                for b in range(B):
                    nc.vector.tensor_tensor_scan(cum[:, b, :], p[:, b, :], zero[:, :], 0.0, ALU.add,
                                                 ALU.add).then_inc(cum_ready, 1)
                dve.wait_ge(cum_ready, B)
                nc.vector.scalar_tensor_tensor(passed[:, :, 1:T + 1], cum[:, :, :], 0.001, over_time(draws), ALU.add,
                                               ALU.is_le).then_inc(chain, 1)
                dve.wait_ge(chain, 8)
                nc.vector.tensor_tensor(step[:, :, :], passed[:, :, 0:T], passed[:, :, 1:T + 1], ALU.subtract).then_inc(chain, 1)
                dve.wait_ge(chain, 9)
                nc.vector.tensor_tensor(step[:, :, :], step[:, :, :], size[:, :, :], ALU.mult).then_inc(chain, 1)
                dve.wait_ge(chain, 10)
                nc.vector.tensor_reduce(bound[:, :], step[:, :, :], AX_X, ALU.add).then_inc(chain, 1)
                dve.wait_ge(chain, 11)
                nc.vector.scalar_tensor_tensor(bound[:, :], passed[:, :, T:T + 1].squeeze(2), FAR, bound[:, :], ALU.mult,
                                               ALU.add).then_inc(chain, 1)
                dve.wait_ge(chain, 12)
                nc.vector.tensor_tensor(step[:, :, :], size[:, :, :], over_time(bound[:, :]), ALU.is_ge).then_inc(chain, 1)
                dve.wait_ge(chain, 13)
                nc.vector.tensor_tensor(db, xb, step[:, :, :], ALU.mult).then_inc(chain, 1)
RET_SCALE = float(D) ** -0.5
RET_EPS = 1e-6
RANK = 16


def low_rank_cond_stage(nc, tag, x, dst, w, u_all, v_all, pick, fc_bias, cond):
    with ExitStack() as stack:
        mem = Memory(nc, stack, tag)
        bias = mem.sb("bias", [P, B])
        z = mem.sb("z", [P, 2, T])
        z_ps, y_ps = mem.ps("z_ps", [P, 2, CHUNK]), mem.ps("y_ps", [P, 2, CHUNK])
        z_psum, z_ready, y_psum, dst_ready, bias_ready = (mem.sem(n) for n in ("z_psum", "z_ready", "y_psum", "dst_ready", "bias_ready"))
        with nc.Block() as block:

            @block.tensor
            def _(pe):
                with pe.Fori(0, B // 2) as i:
                    for u in range(2):
                        b = i * 2 + u
                        here = x[:, bass.ds(b * T, T)]
                        pe.wait_ge(z_ready, b + 1)
                        nc.tensor.matmul(z_ps[:, u, 0:T], v_all, here, start=True, stop=True).then_inc(z_psum, 1)
                        pe.wait_ge(dst_ready, b + 1)
                        nc.tensor.matmul(y_ps[:, u, 0:T], w, here, start=True, stop=False)
                        pe.wait_ge(z_ready, b + 3)
                        nc.tensor.matmul(y_ps[:, u, 0:T], u_all, z[:, u, :], start=False, stop=True).then_inc(y_psum, 1)

            @block.vector
            def _(dve):
                nc.vector.tensor_scalar(bias[:, :], cond, fc_bias, None, ALU.add).then_inc(bias_ready, 1)
                dve.sem_inc(z_ready, 2)
                dve.sem_inc(y_psum, 2)
                with dve.Fori(0, B // 2) as i:
                    for u in range(2):
                        b = i * 2 + u
                        dve.wait_ge(z_psum, b + 1)
                        dve.wait_ge(y_psum, b + 1)
                        nc.vector.tensor_scalar(z[:, u, :], z_ps[:, u, 0:T], pick[:, bass.ds(b, 1)], None,
                                                ALU.mult).then_inc(z_ready, 1)

            @block.scalar
            def _(act):
                act.sem_inc(dst_ready, 2)
                act.wait_ge(bias_ready, 1)
                with act.Fori(0, B // 2) as i:
                    for u in range(2):
                        b = i * 2 + u
                        act.wait_ge(y_psum, b + 3)
                        nc.scalar.activation(dst[:, bass.ds(b * T, T)], y_ps[:, u, 0:T], ACT.Gelu,
                                             bias=bias[:, bass.ds(b, 1)]).then_inc(dst_ready, 1)


def retention_stage(nc, tag, src, x, wq, wk, wv, wg, cos, sin, decay, ident, ones_bf, run_mask):
    W3 = T + HALF
    with ExitStack() as stack:
        mem = Memory(nc, stack, tag)
        y = mem.sb("y", [P, T])
        q_cos, q_sin = mem.sb("q_cos", [P, T]), mem.sb("q_sin", [P, T])
        k_cos, k_sin, k_heads = mem.sb("k_cos", [P, T]), mem.sb("k_sin", [P, T]), mem.sb("k_heads", [P, T])
        q, k = mem.sb("q", [P, T]), mem.sb("k", [P, RUNS, T])
        v_top, v_low = mem.sb("v_top", [P, 2 * NHEAD * HD], BF16), mem.sb("v_low", [P, 2 * NHEAD * HD], BF16)
        v_rest = mem.sb("v_rest", [P, 2 * NHEAD * HD])
        v_part = v_top[:, :], high(v_rest[:, :]), v_low[:, :]
        silu_g = mem.sb("silu_g", [P, 2 * NHEAD, HD])
        part, rest = mem.sb("part", [P, 2, NQUAD, W3]), mem.sb("rest", [P, 2, NQUAD, W3])
        low = mem.sb("low", [P, 2, NQUAD, W3], BF16)
        size, size_rest = mem.sb("size", [P, 2, NQUAD, W3]), mem.sb("size_rest", [P, 2, NQUAD, W3])
        size_low = mem.sb("size_low", [P, 2, NQUAD, W3], BF16)
        den, inv, ms, rms, irms = (mem.sb(n, [P, 2 * NHEAD]) for n in ("den", "inv", "ms", "rms", "irms"))
        heads, square = mem.sb("heads", [P, 2 * NHEAD, HD]), mem.sb("square", [P, 2 * NHEAD, HD])
        s_ps = mem.ps("s_ps", [P, NQUAD, CHUNK])
        v_ps, g_ps = mem.ps("v_ps", [P, CHUNK]), mem.ps("g_ps", [P, CHUNK])
        o_ps, turn_ps = mem.ps("o_ps", [P, CHUNK]), mem.ps("turn_ps", [P, CHUNK])
        out_heads = o_ps[:, 0:2 * NHEAD * (HD + 1)].rearrange("p (h e) -> p h e", e=HD + 1)
        g_heads = g_ps[:, 0:T].rearrange("p (h e) -> p h e", e=HD)
        names = ("y_ready", "q_psum", "q_turned", "q_ready", "k_psum", "k_turned", "k_summed", "k_ready", "v_psum", "v_split", "v_ready",
                 "g_psum", "sig_ready", "silu_ready", "s_psum", "part_ready", "rest_ready", "low_ready", "size_ready",
                 "o_psum", "chain", "rms_in", "rms_ready", "o_ready", "turn_psum", "x_added")
        s = {n: mem.sem(n) for n in names}

        q_ps, k_ps = (s_ps[:, n, :].rearrange("p (part t) -> p part t", t=T) for n in range(2))

        def each(ap):
            return ap.unsqueeze(2).broadcast_to([P, 2 * NHEAD, HD])

        with nc.Block() as block:

            @block.gpsimd
            def _(pool):
                def project(n):
                    nc.gpsimd.tensor_copy(y[:, :], src[:, bass.ds(n * T, T)]).then_inc(s["y_ready"], 1)
                    pool.wait_ge(s["q_turned"], 2 * n + 2)
                    nc.gpsimd.tensor_tensor(q[:, :], q_cos[:, :], q_sin[:, :], ALU.add).then_inc(s["q_ready"], 1)
                    pool.wait_ge(s["v_split"], 2 * n + 2)
                    nc.gpsimd.tensor_tensor(v_low[:, :], v_rest[:, :], high(v_rest[:, :]), ALU.subtract).then_inc(s["v_ready"], 1)

                project(0)
                with pool.Fori(0, B - 1) as b:
                    pool.wait_ge(s["g_psum"], b + 1)
                    project(b + 1)

            @block.tensor
            def _(pe):
                def project_qk(n):
                    pe.wait_ge(s["y_ready"], n + 1)
                    for ps, weights, done in ((q_ps, wq, s["q_psum"]), (k_ps, wk, s["k_psum"])):
                        for p in range(2):
                            last = nc.tensor.matmul(ps[:, p, :], weights[:, p, :], y[:, :], start=True, stop=True)
                        last.then_inc(done, 1)

                def project_vg(n):
                    for a in range(2):
                        last = nc.tensor.matmul(v_ps[:, a * P:(a + 1) * P], y[:, a * HALF:(a + 1) * HALF], wv, start=True, stop=True)
                    last.then_inc(s["v_psum"], 1)
                    for a in range(2):
                        last = nc.tensor.matmul(g_ps[:, a * P:(a + 1) * P], y[:, a * HALF:(a + 1) * HALF], wg, start=True, stop=True)
                    last.then_inc(s["g_psum"], 1)

                def scores(b, r):
                    for half in range(2):
                        for g in range(NQUAD):
                            quad = slice(QUAD * g, QUAD * (g + 1))
                            last = nc.tensor.matmul(s_ps[:, g, half * T:half * T + T - half * HALF],
                                                    k[quad, r, half * HALF:(half + 1) * HALF],
                                                    q[quad, half * HALF:T], start=True, stop=True)
                    last.then_inc(s["s_psum"], 1)

                def first_scores(n):
                    pe.wait_ge(s["q_ready"], n + 1)
                    pe.wait_ge(s["k_ready"], RUNS * (n + 1))
                    scores(n, 0)

                def values(b, r):
                    if r == 0:
                        pe.wait_ge(s["v_ready"], b + 1)
                    pe.wait_ge(s["low_ready"], RUNS * b + r + 1)
                    pe.wait_ge(s["size_ready"], RUNS * b + r + 1)
                    rows = high(part[:, r % 2, :, :]), high(rest[:, r % 2, :, :]), low[:, r % 2, :, :]
                    sizes = high(size[:, r % 2, :, :]), high(size_rest[:, r % 2, :, :]), size_low[:, r % 2, :, :]
                    for half in range(2):
                        for g in range(NQUAD):
                            head = NQUAD * g + r
                            at = NHEAD * half + head
                            blocks = [(n, half * HALF if n == 0 else T) for n in range(half + 1)]
                            terms = [(rows[i][:, g, lo:lo + HALF],
                                      v_part[j][:, n * P + HD * head:n * P + HD * (head + 1)])
                                     for n, lo in blocks for i in range(3) for j in range(3 - i)]
                            for m, (keys_first, columns) in enumerate(terms):
                                nc.tensor.matmul(out_heads[:, at, 0:HD], keys_first, columns,
                                                 start=(m == 0), stop=(m == len(terms) - 1))
                            terms = [sizes[i][:, g, lo:lo + HALF] for n, lo in blocks for i in range(3)]
                            for m, keys_first in enumerate(terms):
                                last = nc.tensor.matmul(out_heads[:, at, HD:HD + 1], keys_first, ones_bf[:, 0:1],
                                                        start=(m == 0), stop=(m == len(terms) - 1))
                    last.then_inc(s["o_psum"], 1)

                def sequence(b, more):
                    for r in range(RUNS):
                        pe.wait_ge(s["part_ready"], RUNS * b + r + 1)
                        if r + 1 < RUNS:
                            scores(b, r + 1)
                        elif more:
                            project_qk(b + 1)
                        values(b, r)
                    if more:
                        first_scores(b + 1)
                        project_vg(b + 1)
                    pe.wait_ge(s["o_ready"], b + 1)
                    pe.wait_ge(s["x_added"], b + 1)
                    for n in range(2):
                        last = nc.tensor.transpose(turn_ps[:, n * P:(n + 1) * P],
                                                   square[:, n * NHEAD:(n + 1) * NHEAD, :].rearrange("p h e -> p (h e)"), ident)
                    last.then_inc(s["turn_psum"], 1)

                project_qk(0)
                project_vg(0)
                first_scores(0)
                with pe.Fori(0, B - 1) as b:
                    sequence(b, True)
                sequence(B - 1, False)

            @block.scalar
            def _(act):
                def gate_and_v(n):
                    act.wait_ge(s["v_psum"], n + 1)
                    nc.scalar.activation(v_top[:, :], v_ps[:, 0:T], ACT.Identity).then_inc(s["v_split"], 1)
                    act.wait_ge(s["g_psum"], n + 1)
                    nc.scalar.activation(silu_g[:, :, :], g_heads, ACT.Sigmoid).then_inc(s["sig_ready"], 1)

                def sizes(b, r):
                    n = RUNS * b + r
                    if r >= 2:
                        act.wait_ge(s["o_psum"], n - 1)
                    act.wait_ge(s["part_ready"], n + 1)
                    nc.scalar.activation(size[:, r % 2, :, :], part[:, r % 2, :, :], ACT.Abs)
                    act.wait_ge(s["rest_ready"], n + 1)
                    nc.scalar.activation(size_rest[:, r % 2, :, :], rest[:, r % 2, :, :], ACT.Abs)
                    act.wait_ge(s["low_ready"], n + 1)
                    nc.scalar.activation(size_low[:, r % 2, :, :], low[:, r % 2, :, :], ACT.Abs).then_inc(s["size_ready"], 1)

                def sequence(b, more):
                    for r in range(1, RUNS):
                        sizes(b, r)
                    act.wait_ge(s["rms_in"], b + 1)
                    nc.scalar.activation(rms[:, :], ms[:, :], ACT.Sqrt).then_inc(s["rms_ready"], 1)
                    if more:
                        sizes(b + 1, 0)
                        act.wait_ge(s["o_ready"], b + 1)
                        gate_and_v(b + 1)

                sizes(0, 0)
                gate_and_v(0)
                with act.Fori(0, B - 1) as b:
                    sequence(b, True)
                sequence(B - 1, False)

            @block.vector
            def _(dve):
                chain = s["chain"]

                def rotate_qk(n):
                    for i, (ps, done, cos_part, sin_part, turned) in enumerate((
                            (q_ps, s["q_psum"], q_cos, q_sin, s["q_turned"]), (k_ps, s["k_psum"], k_cos, k_sin, s["k_turned"]))):
                        dve.wait_ge(done, n + 1)
                        nc.vector.tensor_tensor(cos_part[:, :], ps[:, 0, :], cos[:, i, :], ALU.mult).then_inc(turned, 1)
                        nc.vector.tensor_tensor(sin_part[:, :], ps[:, 1, :], sin[:, i, :], ALU.mult).then_inc(turned, 1)
                    dve.wait_ge(s["k_turned"], 2 * n + 2)
                    nc.vector.tensor_tensor(k_heads[:, :], k_cos[:, :], k_sin[:, :], ALU.add).then_inc(s["k_summed"], 1)
                    dve.wait_ge(s["k_summed"], n + 1)
                    for r in range(RUNS):
                        nc.vector.tensor_scalar(k[:, r, :], k_heads[:, :], run_mask[:, r:r + 1], None,
                                                ALU.mult).then_inc(s["k_ready"], 1)

                def gate_and_v(n):
                    dve.wait_ge(s["v_split"], 2 * n + 1)
                    nc.vector.tensor_tensor(v_rest[:, :], v_ps[:, 0:T], v_top[:, :], ALU.subtract).then_inc(s["v_split"], 1)
                    dve.wait_ge(s["sig_ready"], n + 1)
                    nc.vector.tensor_tensor(silu_g[:, :, :], silu_g[:, :, :], g_heads, ALU.mult).then_inc(s["silu_ready"], 1)

                def decayed(b, r):
                    n = RUNS * b + r
                    dve.wait_ge(s["s_psum"], n + 1)
                    if r >= 2:
                        dve.wait_ge(s["o_psum"], n - 1)
                    nc.vector.tensor_tensor(part[:, r % 2, :, :], s_ps[:, :, 0:W3], decay[:, r, :, :],
                                            ALU.mult).then_inc(s["part_ready"], 1)
                    dve.wait_ge(s["part_ready"], n + 1)
                    nc.vector.tensor_tensor(rest[:, r % 2, :, :], part[:, r % 2, :, :], high(part[:, r % 2, :, :]),
                                            ALU.subtract).then_inc(s["rest_ready"], 1)
                    dve.wait_ge(s["rest_ready"], n + 1)
                    nc.vector.tensor_tensor(low[:, r % 2, :, :], rest[:, r % 2, :, :], high(rest[:, r % 2, :, :]),
                                            ALU.subtract).then_inc(s["low_ready"], 1)

                def sequence(b, more):
                    at = 7 * b
                    for r in range(1, RUNS):
                        decayed(b, r)
                    if more:
                        rotate_qk(b + 1)
                    dve.wait_ge(s["o_psum"], RUNS * (b + 1))
                    nc.vector.tensor_scalar(den[:, :], out_heads[:, :, HD], 1.0, 50000.0, ALU.max, ALU.min).then_inc(chain, 1)
                    dve.wait_ge(chain, at + 1)
                    nc.vector.reciprocal(inv[:, :], den[:, :]).then_inc(chain, 1)
                    dve.wait_ge(chain, at + 2)
                    nc.vector.tensor_tensor(heads[:, :, :], out_heads[:, :, 0:HD], each(inv[:, :]), ALU.mult).then_inc(chain, 1)
                    dve.wait_ge(chain, at + 3)
                    nc.vector.tensor_tensor(square[:, :, :], heads[:, :, :], heads[:, :, :], ALU.mult).then_inc(chain, 1)
                    dve.wait_ge(chain, at + 4)
                    nc.vector.tensor_reduce(den[:, :], square[:, :, :], AX_X, ALU.add).then_inc(chain, 1)
                    dve.wait_ge(chain, at + 5)
                    nc.vector.tensor_scalar(ms[:, :], den[:, :], 1.0 / HD, RET_EPS, ALU.mult, ALU.add).then_inc(s["rms_in"], 1)
                    dve.wait_ge(s["silu_ready"], b + 1)
                    nc.vector.tensor_tensor(heads[:, :, :], heads[:, :, :], silu_g[:, :, :], ALU.mult).then_inc(chain, 1)
                    dve.wait_ge(s["rms_ready"], b + 1)
                    nc.vector.reciprocal(irms[:, :], rms[:, :]).then_inc(chain, 1)
                    dve.wait_ge(chain, at + 7)
                    nc.vector.tensor_tensor(square[:, :, :], heads[:, :, :], each(irms[:, :]), ALU.mult).then_inc(s["o_ready"], 1)
                    if more:
                        decayed(b + 1, 0)
                    dve.wait_ge(s["turn_psum"], b + 1)
                    here = x[:, bass.ds(b * T, T)]
                    nc.vector.tensor_tensor(here, turn_ps[:, 0:T], here, ALU.add).then_inc(s["x_added"], 1)
                    if more:
                        gate_and_v(b + 1)

                dve.sem_inc(s["x_added"], 1)
                rotate_qk(0)
                decayed(0, 0)
                gate_and_v(0)
                with dve.Fori(0, B - 1) as b:
                    sequence(b, True)
                sequence(B - 1, False)


def retention_weights(w):
    return np.stack([w, w.reshape(D, D // 2, 2)[..., ::-1].reshape(D, D)], 1)


def retention_tables():
    f = np.float32
    angle = np.repeat(1.0 / f(10000.0) ** np.linspace(0.0, 1.0, HD // 2, dtype=f), 2).astype(f)
    turn = (np.arange(T, dtype=f)[:, None] * angle[None, :]).astype(f)
    cos, sin = np.zeros((2, HD, 2, T), f)
    sign = np.where(np.arange(HD) % 2 == 0, -1.0, 1.0)
    for n, by in enumerate((1.0, RET_SCALE)):
        cos[:, n] = np.cos(turn).T * by
        sin[:, n] = np.sin(turn).T * sign[:, None] * by
    cos, sin = np.tile(cos, (NHEAD, 1, 1)), np.tile(sin, (NHEAD, 1, 1))
    rate = np.log(1.0 - 2.0 ** (-5.0 - np.arange(NHEAD, dtype=f))).astype(f)
    lag = np.arange(T)[:, None] - np.arange(T)[None, :]
    mask = np.where(lag >= 0, np.exp(np.maximum(lag, 0).astype(f) * rate[:, None, None]), 0.0).astype(f)
    mask = (mask / np.sqrt(mask.sum(-1, keepdims=True, dtype=f))).astype(f)
    keys = mask.transpose(0, 2, 1).reshape(NQUAD, RUNS, T, T)
    decay = np.concatenate([keys[:, :, :HALF], keys[:, :, HALF:, HALF:]], -1)
    return cos, sin, decay.transpose(2, 1, 0, 3)


def packs(i):
    cos0, sin0 = rope_tables(False)
    cos1, sin1 = rope_tables(True)
    cos3, sin3, decay = retention_tables()
    qkv = i["L1_attn_w_qkv"]
    fside = i["fside_Bx1x1024x16_0"][:, 0]
    inch = 1.0 / (D * RANK)
    base = {
        "cond": i["cond_1024"].T,
        "run_mask": run_masks(),
        "ident": np.eye(P, dtype=np.float32), "mask": np.where(np.tril(np.ones((P, P))), 0.0, -1e30).astype(np.float32),
        "ones": np.ones((P, P), np.float32),
        "rank": np.tile(np.arange(NEXP, 0, -1, dtype=np.float32), (P, 1)),
    }
    l0 = {
        "c_w1": i["L0_cond_W1"].T, "c_b1": i["L0_cond_b1"][:, None],
        "c_w2": i["L0_cond_W2"].T, "c_b2": i["L0_cond_b2"][:, None],
        "wq": attention_weights(i["L0_attn_Wq"], NHEAD), "wk": attention_weights(i["L0_attn_Wk"], NQUAD),
        "wv": i["L0_attn_Wv"], "wo": i["L0_attn_Wo"], "cos": cos0, "sin": sin0,
        "wx": i["L0_cond2_Wx"], "wh": i["L0_cond2_Wh"], "b": i["L0_cond2_b"].reshape(4, P).T,
        "f_w": i["L0_ffn_weight"].T, "f_b": i["L0_ffn_bias"][:, None],
    }
    l1 = {
        "wq": attention_weights(qkv[:, :D], NHEAD), "wk": attention_weights(qkv[:, D:2 * D], NHEAD),
        "wv": qkv[:, 2 * D:], "wo": i["L1_attn_w_proj"], "cos": cos1, "sin": sin1,
        "r_w": i["L1_cond2_router_w"].T, "r_t": i["L1_cond2_router_t_w"].T,
        "r_b": np.tile(i["L1_cond2_router_bias"], (P, 1)),
        "sw1": i["L1_cond2_sw1"].T, "sw3": i["L1_cond2_sw3"].T,
        "sw2": i["L1_cond2_sw2"].T.reshape(2, P, D).transpose(1, 0, 2),
        "rw1": i["L1_cond2_rw1"].reshape(NEXP * P // 2, D).T,
        "rw2": i["L1_cond2_rw2"].transpose(0, 2, 1).reshape(NEXP // 2, P, D).transpose(1, 0, 2),
        "f_r": i["L1_ffn_Wg"], "f_w1": i["L1_ffn_W1"].transpose(1, 0, 2),
        "f_b1": i["L1_ffn_b1"].reshape(NEXP, 2, P).transpose(2, 0, 1),
        "f_w2": i["L1_ffn_W2"].reshape(NEXP, 2, P, D).transpose(2, 0, 1, 3), "f_b2": i["L1_ffn_b2"],
    }
    l2 = {
        "wx": i["L2_cond_Wx"], "wh": i["L2_cond_Wh"], "b": i["L2_cond_b"].reshape(4, P).T,
        **delta_weights(i), "head_sum": np.kron(np.eye(P // N2, dtype=np.float32), np.ones((N2, N2), np.float32)),
        "r_wx": i["L2_cond2_Wx"], "r_wh": i["L2_cond2_Wh"], "r_b": i["L2_cond2_b"][:, None],
        "f_w": np.stack([i["L2_ffn_w_gate"].T, i["L2_ffn_w_up"].T,
                         i["L2_ffn_w_down"].T.reshape(BIT_BLOCKS, P, D).transpose(1, 0, 2).reshape(P, -1)], 1),
    }
    l3 = {
        "c_w": i["L3_cond_W"].T, "c_b": i["L3_cond_fc_bias"][:, None],
        "u_all": fside.transpose(0, 2, 1).reshape(P, D), "v_all": fside.transpose(1, 0, 2).reshape(D, P),
        "pick": np.kron(np.eye(B, dtype=np.float32), np.full((RANK, 1), inch, np.float32)),
        "wq": retention_weights(i["L3_attn_Wq"]), "wk": retention_weights(i["L3_attn_Wk"]),
        "wv": i["L3_attn_Wv"], "wg": i["L3_attn_Wg"], "cos": cos3, "sin": sin3,
        "wx": i["L3_cond2_Wx"], "wh": i["L3_cond2_Wh"], "b": i["L3_cond2_b"].reshape(4, P).T,
        "f_r": i["L3_ffn_router_w"].T,
        "f_wg": i["L3_ffn_gate_w"].transpose(1, 0, 2), "f_bg": i["L3_ffn_gate_b"].reshape(NEXP, 2, P).transpose(2, 0, 1),
        "f_wu": i["L3_ffn_up_w"].transpose(1, 0, 2), "f_bu": i["L3_ffn_up_b"].reshape(NEXP, 2, P).transpose(2, 0, 1),
        "f_wd": i["L3_ffn_down_w"].reshape(NEXP, 2, P, D).transpose(2, 0, 1, 3), "f_bd": i["L3_ffn_down_b"],
    }
    return {"base": base, "l0": l0, "l1": l1, "l2": l2, "l3": l3}, decay


def packed(pack):
    total = sum(int(np.prod(a.shape[1:])) for a in pack.values())
    whole = np.zeros((P, total), np.float32)
    places, at = {}, 0
    for name, a in pack.items():
        size = int(np.prod(a.shape[1:]))
        whole[:a.shape[0], at:at + size] = a.reshape(a.shape[0], size)
        places[name] = (at, a.shape)
        at += size
    return whole, places


def views(buffer, places):
    letters = "abc"
    out = {}
    for name, (at, shape) in places.items():
        part = buffer[0:shape[0], at:at + int(np.prod(shape[1:]))]
        if len(shape) > 2:
            dims = letters[:len(shape) - 1]
            part = part.rearrange(f"p ({' '.join(dims)}) -> p {' '.join(dims)}", **dict(zip(dims, shape[1:])))
        out[name] = part
    return out


def program(nc, dram, out, places, first=0, last=8):
    STAGE_SEMAPHORES.clear()
    with ExitStack() as stack:
        mem = Memory(nc, stack, "main")
        widths = {name: max(at + int(np.prod(shape[1:])) for at, shape in p.values()) for name, p in places.items()}
        x_buf, y_buf = mem.sb("x", [P, TOK]), mem.sb("y", [P, TOK])
        x, y = x_buf[:, :], y_buf[:, :]
        base_buf = mem.sb("base", [P, widths["base"]])
        ident_bf_buf, mask_bf_buf = mem.sb("ident_bf", [P, P], BF16), mem.sb("mask_bf", [P, P], BF16)
        even_buf = mem.sb("even_layers", [P, max(widths["l0"], widths["l2"])])
        odd_buf = mem.sb("odd_layers", [P, max(widths["l1"], widths["l3"])])
        base = views(base_buf, places["base"])
        l0, l2 = views(even_buf, places["l0"]), views(even_buf, places["l2"])
        l1, l3 = views(odd_buf, places["l1"]), views(odd_buf, places["l3"])
        run_mask = base["run_mask"]
        ident, ones, rank, cond = base["ident"], base["ones"], base["rank"], base["cond"]
        ones_bf_buf = mem.sb("ones_bf", [P, 1], BF16)
        ident_bf, mask_bf, ones_bf = ident_bf_buf[:, :], mask_bf_buf[:, :], ones_bf_buf[:, :]
        loaded = {n: mem.sem(f"loaded_{n}") for n in ("start", "l1", "l2", "l3", "decay")}
        stored = mem.sem("stored")

        def between(load=(), need=None):
            with nc.Block() as block:

                @block.gpsimd
                def _(pool):
                    if STAGE_SEMAPHORES:
                        nc.clear_and_free_semaphores(list(STAGE_SEMAPHORES))
                        STAGE_SEMAPHORES.clear()

                @block.sync
                def _(sp):
                    for dst, src, name in load:
                        sp.dma_start(dst, src).then_inc(loaded[name], 16)
                    if need:
                        sp.wait_ge(loaded[need[0]], 16 * need[1])

        between([(x, dram["x"], "start"), (base_buf[:, :], dram["base"], "start"),
                 (even_buf[:, 0:widths["l0"]], dram["l0"], "start"), (odd_buf[:, 0:widths["l1"]], dram["l1"], "l1")], ("start", 3))
        with nc.Block() as block:

            @block.vector
            def _(dve):
                nc.vector.tensor_copy(ident_bf, ident)
                nc.vector.tensor_copy(mask_bf, base["mask"])
                nc.vector.tensor_copy(ones_bf, ones[:, 0:1])

        if first <= 0 < last:
            cond_gate_stage(nc, "l0c", x, y, cond, l0["c_w1"], l0["c_b1"], l0["c_w2"], l0["c_b2"])
            attention_stage(nc, "l0a", y, x, l0["wq"], l0["wk"], l0["wv"], l0["wo"], l0["cos"], l0["sin"], ident,
                            ident_bf, mask_bf, run_mask, NQUAD)
        if first <= 1 < last:
            lstm_stage(nc, "l0r", x, y, l0["wx"], l0["wh"], l0["b"], cond, ident)
            ternary_stage(nc, "l0f", y, x, l0["f_w"], l0["f_b"])
        between([(even_buf[:, 0:widths["l2"]], dram["l2"], "l2")], ("l1", 1))
        if first <= 2 < last:
            threshold_stage(nc, "l1c", x, y, cond)
            attention_stage(nc, "l1a", y, x, l1["wq"], l1["wk"], l1["wv"], l1["wo"], l1["cos"], l1["sin"], ident,
                            ident_bf, mask_bf, run_mask, NHEAD)
        if first <= 3 < last:
            routed_cond_stage(nc, "l1r", x, y, cond, l1["r_w"], l1["r_t"], l1["r_b"], l1["sw1"], l1["sw3"], l1["sw2"],
                              l1["rw1"], l1["rw2"], rank, ones, ident)
            expert_stage(nc, "l1f", y, x, l1["f_r"], l1["f_w1"], l1["f_b1"], None, None, l1["f_w2"], l1["f_b2"], rank, ident)
        between([(odd_buf[:, 0:widths["l3"]], dram["l3"], "l3")], ("l2", 1))
        if first <= 4 < last:
            recurrent_stages(nc, "l2r", x, y, l2["wx"], l2["wh"], l2["b"], l2["w_in"], l2["w_k"], l2["w_q"], l2["w_vb"],
                             l2["b_vb"], l2["w_out"], l2["head_sum"], l2["r_wx"], l2["r_wh"], l2["r_b"], cond, ident)
        decay_buf = mem.sb("decay", [P, RUNS, NQUAD, T + HALF])
        decay = decay_buf[:, :, :, :]
        between([(decay, dram["decay"], "decay")])
        if first <= 5 < last:
            bit_ffn_stage(nc, "l2f", y, x, l2["f_w"], ident, ident_bf)
        between((), ("l3", 1))
        between((), ("decay", 1))
        if first <= 6 < last:
            low_rank_cond_stage(nc, "l3c", x, y, l3["c_w"], l3["u_all"], l3["v_all"], l3["pick"], l3["c_b"], cond)
            retention_stage(nc, "l3a", y, x, l3["wq"], l3["wk"], l3["wv"], l3["wg"], l3["cos"], l3["sin"], decay, ident, ones_bf, run_mask)
        if first <= 7 < last:
            lstm_stage(nc, "l3r", x, y, l3["wx"], l3["wh"], l3["b"], cond, ident)
            expert_stage(nc, "l3f", y, x, l3["f_r"], l3["f_wg"], l3["f_bg"], l3["f_wu"], l3["f_bu"], l3["f_wd"], l3["f_bd"],
                         rank, ident)
        with nc.Block() as block:

            @block.sync
            def _(sp):
                sp.dma_start(out, x).then_inc(stored, 16)
                sp.wait_ge(stored, 16)


def host_arrays(inputs):
    i = {name: np.asarray(a) for name, a in inputs.items()}
    layers, decay = packs(i)
    arrays, places = {"x": np.ascontiguousarray(i["x"].transpose(2, 0, 1).reshape(D, TOK))}, {}
    for name, pack in layers.items():
        arrays[name], places[name] = packed(pack)
    arrays["decay"] = np.ascontiguousarray(decay)
    return arrays, places


def kernel(**inputs):
    import concourse.bacc as bacc
    from concourse.bass_utils import run_bass_kernel_spmd

    nc = bacc.Bacc("TRN2", target_bir_lowering=False, num_devices=1)
    arrays, places = host_arrays(inputs)
    dram = {name: nc.dram_tensor(f"in_{name}", a.shape, mybir.dt.from_np(a.dtype), kind="ExternalInput").ap()
            for name, a in arrays.items()}
    out = nc.dram_tensor("out", (D, TOK), F32, kind="ExternalOutput").ap()
    program(nc, dram, out, places)
    got = run_bass_kernel_spmd(nc, [{f"in_{name}": a for name, a in arrays.items()}], core_ids=[0])
    return np.ascontiguousarray(got.results[0]["out"].reshape(D, B, T).transpose(1, 2, 0))
```
